# Optimizing a Trainium2 kernel written in Bass

```python
import numpy as np
import jax
import jax.numpy as jnp

def _softmax(x, axis=-1):
    return jax.nn.softmax(x, axis=axis)

def _gelu(x):
    return jax.nn.gelu(x, approximate=True)

def _silu(x):
    return jax.nn.silu(x)

def _sigmoid(x):
    return jax.nn.sigmoid(x)

def _layernorm(x, axis=-1, eps=1e-05):
    m = jnp.mean(x, axis=axis, keepdims=True)
    v = jnp.var(x, axis=axis, keepdims=True)
    return (x - m) / jnp.sqrt(v + eps)

def _scatter_add(tgt, idx, src, axis=0):
    return tgt.at[idx].add(src)

def _segment_sum(src, seg, n):
    return jax.ops.segment_sum(src, seg, n)
kernel_name = 'mk_gnn_ffn_d4_gnn_r32_175677'

def setup_inputs(seed: int=0):
    np.random.seed(seed)
    _w = jnp.asarray

    def _rec_inputs():
        import jax
        import jax.numpy as jnp
        _gk = jax.random.key(seed)
        x = -0.000202 + 1 * jax.random.normal(jax.random.fold_in(_gk, 1), (3125, 256), jnp.float32)
        src = jax.random.randint(jax.random.fold_in(_gk, 2), (50000,), 0, 3125, jnp.int32)
        dst = jnp.minimum((3125 * jax.random.uniform(jax.random.fold_in(_gk, 3), (50000,)) ** 2.0).astype(jnp.int32), 99999)
        _o = jnp.argsort(dst, stable=True)
        src = src[_o]
        dst = dst[_o]
        edge_attr_128 = -5.16925e-05 + 1.00005 * jax.random.normal(jax.random.fold_in(_gk, 12), (50000, 128), jnp.float32)
        edge_attr_16 = 0.000398968 + 1.00027 * jax.random.normal(jax.random.fold_in(_gk, 13), (50000, 16), jnp.float32)
        edge_attr_64 = -5.3897e-05 + 0.999841 * jax.random.normal(jax.random.fold_in(_gk, 14), (50000, 64), jnp.float32)
        edge_weight1 = jax.random.uniform(jax.random.fold_in(_gk, 16), (50000, 1), jnp.float32, 0.0, 0.999998)
        return (x, src, dst, edge_attr_128, edge_attr_16, edge_attr_64, edge_weight1)
    x, src, dst, edge_attr_128, edge_attr_16, edge_attr_64, edge_weight1 = _rec_inputs()

    def _L0_gnn_setup():
        import jax, jax.numpy as jnp
        import numpy as np
        LOG2 = float(np.log(2.0))

        def ssp(x):
            return jax.nn.softplus(x) - LOG2
        N_ATOMS, N_EDGES, N_HF, N_RBF = (25000, 12500, 256, 64)
        key = jax.random.key(seed)
        ks = jax.random.split(key, 16)
        s = 1.0 / np.sqrt(N_HF)
        sr = 1.0 / np.sqrt(N_RBF)
        return {'x': jax.random.normal(ks[0], (N_ATOMS, N_HF), jnp.float32), 'rbf': jax.random.normal(ks[1], (N_EDGES, N_RBF), jnp.float32), 'dist_cut': jax.random.uniform(ks[2], (N_EDGES, 1), jnp.float32), 'idx_i': jax.random.randint(ks[3], (N_EDGES,), 0, N_ATOMS), 'idx_j': jax.random.randint(ks[4], (N_EDGES,), 0, N_ATOMS), 'W_in2f': jax.random.normal(ks[5], (N_HF, N_HF), jnp.float32) * s, 'Wf1': jax.random.normal(ks[6], (N_RBF, N_HF), jnp.float32) * sr, 'bf1': jnp.zeros((N_HF,), jnp.float32), 'Wf2': jax.random.normal(ks[7], (N_HF, N_HF), jnp.float32) * s, 'bf2': jnp.zeros((N_HF,), jnp.float32), 'Wo1': jax.random.normal(ks[8], (N_HF, N_HF), jnp.float32) * s, 'bo1': jnp.zeros((N_HF,), jnp.float32), 'Wo2': jax.random.normal(ks[9], (N_HF, N_HF), jnp.float32) * s, 'bo2': jnp.zeros((N_HF,), jnp.float32)}
    _L0_gnn_all = _L0_gnn_setup()
    _L0_gnn_in = {k: v for k, v in _L0_gnn_all.items() if k in ('W_in2f', 'Wf1', 'bf1', 'Wf2', 'bf2', 'Wo1', 'bo1', 'Wo2', 'bo2')}
    del _L0_gnn_all

    def _L0_ffn_setup():
        import jax, jax.numpy as jnp
        import numpy as np
        NUM_EXPERTS = 8
        TOP_K = 2
        B, S, D = (8, 256, 256)

        def _moe(tokens, router_w, w1, b1, w2, b2):
            N = tokens.shape[0]
            E = router_w.shape[0]
            logits = tokens.astype(jnp.float32) @ router_w.astype(jnp.float32).T
            probs = jax.nn.softmax(logits, axis=-1)
            rw, re = jax.lax.top_k(probs, TOP_K)
            if TOP_K > 1:
                rw = rw / jnp.maximum(rw.sum(-1, keepdims=True), 1e-12)
            rw = rw.astype(tokens.dtype)
            combine = jnp.zeros((N, E), tokens.dtype).at[jnp.arange(N)[:, None], re].set(rw)
            out = tokens
            for e in range(E):
                h = jax.nn.gelu(tokens @ w1[e] + b1[e], approximate=False)
                y = h @ w2[e] + b2[e]
                out = out + combine[:, e:e + 1] * y
            return out
        key = jax.random.key(seed)
        ks = jax.random.split(key, 4)
        scale = 1.0 / np.sqrt(D).astype(np.float32)
        return {'input_embeddings': jax.random.normal(ks[0], (B, S, D), jnp.float32), 'router_w': jax.random.normal(ks[1], (NUM_EXPERTS, D), jnp.float32) * scale, 'w1': jax.random.normal(ks[2], (NUM_EXPERTS, D, D), jnp.float32) * scale, 'b1': jnp.zeros((NUM_EXPERTS, D), jnp.float32), 'w2': jax.random.normal(ks[3], (NUM_EXPERTS, D, D), jnp.float32) * scale, 'b2': jnp.zeros((NUM_EXPERTS, D), jnp.float32)}
    _L0_ffn_all = _L0_ffn_setup()
    _L0_ffn_in = {k: v for k, v in _L0_ffn_all.items() if k in ('router_w', 'w1', 'b1', 'w2', 'b2')}
    del _L0_ffn_all

    def _L1_gnn_setup():
        import jax, jax.numpy as jnp
        import numpy as np
        N_NODES = 625
        N_EDGES = 10000
        IN_DIM = 256
        HEADS = 4
        OUT_C = 64
        HC = HEADS * OUT_C
        EDGE_DIM = 16
        NEG_SLOPE = 0.2
        key = jax.random.key(seed)
        ks = jax.random.split(key, 10)
        x = jax.random.normal(ks[0], (N_NODES, IN_DIM), dtype=jnp.float32)
        src = jax.random.randint(ks[1], (N_EDGES,), 0, N_NODES)
        off = jax.random.randint(ks[2], (N_EDGES,), 1, N_NODES)
        dst = (src + off) % N_NODES
        edge_index = jnp.stack([src, dst]).astype(jnp.int64)
        edge_attr = jax.random.normal(ks[3], (N_EDGES, EDGE_DIM), dtype=jnp.float32)
        s = 0.05
        return {'x': x, 'edge_index': edge_index, 'edge_attr': edge_attr, 'W_l': jax.random.normal(ks[4], (IN_DIM, HC), dtype=jnp.float32) * s, 'b_l': jnp.zeros((HC,), dtype=jnp.float32), 'W_r': jax.random.normal(ks[5], (IN_DIM, HC), dtype=jnp.float32) * s, 'b_r': jnp.zeros((HC,), dtype=jnp.float32), 'W_e': jax.random.normal(ks[6], (EDGE_DIM, HC), dtype=jnp.float32) * s, 'att': jax.random.normal(ks[7], (HEADS, OUT_C), dtype=jnp.float32) * s, 'W_res': jax.random.normal(ks[8], (IN_DIM, HC), dtype=jnp.float32) * s, 'bias': jnp.zeros((HC,), dtype=jnp.float32)}
    _L1_gnn_all = _L1_gnn_setup()
    _L1_gnn_in = {k: v for k, v in _L1_gnn_all.items() if k in ('W_l', 'b_l', 'W_r', 'b_r', 'W_e', 'att', 'W_res', 'bias')}
    del _L1_gnn_all

    def _L1_ffn_setup():
        import jax, jax.numpy as jnp
        import numpy as np
        TOP_K = 2
        key = jax.random.key(seed)
        ks = jax.random.split(key, 4)
        B, L, D, H, E = (8, 128, 256, 1024, 8)
        s = 0.02
        return {'x': jax.random.normal(ks[0], (B, L, D), jnp.float32), 'Wg': jax.random.normal(ks[1], (D, E), jnp.float32) * s, 'bg': jnp.zeros((E,), jnp.float32), 'W1': jax.random.normal(ks[2], (E, D, H), jnp.float32) * s, 'b1': jnp.zeros((E, H), jnp.float32), 'W2': jax.random.normal(ks[3], (E, H, D), jnp.float32) * s, 'b2': jnp.zeros((E, D), jnp.float32)}
    _L1_ffn_all = _L1_ffn_setup()
    _L1_ffn_in = {k: v for k, v in _L1_ffn_all.items() if k in ('Wg', 'bg', 'W1', 'b1', 'W2', 'b2')}
    del _L1_ffn_all

    def _L2_gnn_setup():
        import jax, jax.numpy as jnp
        import numpy as np
        N_NODES = 50000

        def _add_self_loops(src, dst, n):
            loop = jnp.arange(n, dtype=src.dtype)
            return (jnp.concatenate([src, loop]), jnp.concatenate([dst, loop]))

        def gcn_conv(x, src, dst, W, b, n):
            h = x @ W
            deg = jnp.zeros((n,), h.dtype).at[dst].add(1.0)
            dinv = jax.lax.rsqrt(jnp.maximum(deg, 1e-12))
            norm = dinv[src] * dinv[dst]
            msg = h[src] * norm[:, None]
            return jax.ops.segment_sum(msg, dst, num_segments=n) + b
        key = jax.random.key(seed)
        ks = jax.random.split(key, 10)
        num_features, hidden = (256, 64)
        x = jax.random.normal(ks[0], (N_NODES, num_features), jnp.float32)
        edge_index = jax.random.randint(ks[1], (2, 50000), 0, N_NODES, jnp.int64)

        def glorot(k, fi, fo):
            s = jnp.sqrt(6.0 / (fi + fo)).astype(jnp.float32)
            return jax.random.uniform(k, (fi, fo), jnp.float32, -s, s)
        dims = [(num_features, 2 * hidden), (2 * hidden, hidden), (hidden, 2 * hidden), (2 * hidden, num_features)]
        params = {}
        for i, (fi, fo) in enumerate(dims):
            params[f'W{i + 1}'] = glorot(ks[2 + i], fi, fo)
            params[f'b{i + 1}'] = jnp.zeros((fo,), jnp.float32)
        return {'x': x, 'edge_index': edge_index, **params}
    _L2_gnn_all = _L2_gnn_setup()
    _L2_gnn_in = {k: v for k, v in _L2_gnn_all.items() if k in ('W1', 'b1', 'W2', 'b2', 'W3', 'b3', 'W4', 'b4')}
    del _L2_gnn_all

    def _L2_ffn_setup():
        import jax, jax.numpy as jnp
        import numpy as np
        BN_EPS = 0.001

        def _bn(h, g, b, m, v):
            return g * (h - m) * jax.lax.rsqrt(v + BN_EPS) + b
        key = jax.random.key(seed)
        ks = jax.random.split(key, 8)
        B, F, Df = (256, 64, 256)
        E, H, D = (8, 256, 256)
        s1 = 1.0 / np.sqrt(Df)
        s2 = 1.0 / np.sqrt(H)
        return {'x': jax.random.normal(ks[0], (B, F, Df), jnp.float32), 'Wr': jax.random.normal(ks[1], (Df, E), jnp.float32) * s1, 'br': jnp.zeros((E,), jnp.float32), 'W1': jax.random.normal(ks[2], (E, Df, H), jnp.float32) * s1, 'b1': jnp.zeros((E, H), jnp.float32), 'g1': jnp.ones((E, H), jnp.float32), 'be1': jnp.zeros((E, H), jnp.float32), 'm1': jnp.zeros((E, H), jnp.float32), 'v1': jnp.ones((E, H), jnp.float32), 'W2': jax.random.normal(ks[3], (E, H, H), jnp.float32) * s2, 'b2': jnp.zeros((E, H), jnp.float32), 'g2': jnp.ones((E, H), jnp.float32), 'be2': jnp.zeros((E, H), jnp.float32), 'm2': jnp.zeros((E, H), jnp.float32), 'v2': jnp.ones((E, H), jnp.float32), 'Wo': jax.random.normal(ks[4], (E, H, D), jnp.float32) * s2, 'bo': jnp.zeros((E, D), jnp.float32)}
    _L2_ffn_all = _L2_ffn_setup()
    _L2_ffn_in = {k: v for k, v in _L2_ffn_all.items() if k in ('Wr', 'br', 'W1', 'b1', 'g1', 'be1', 'm1', 'v1', 'W2', 'b2', 'g2', 'be2', 'm2', 'v2', 'Wo', 'bo')}
    del _L2_ffn_all

    def _L3_gnn_setup():
        import jax, jax.numpy as jnp
        import numpy as np
        N_NODES = 50000
        N_EDGES = 25000
        IN_DIM = 256
        OUT_DIM = 256
        HEADS = 1
        EDGE_DIM = 128
        NEG_SLOPE = 0.01
        key = jax.random.key(seed)
        ks = jax.random.split(key, 8)
        x = jax.random.normal(ks[0], (N_NODES, IN_DIM), dtype=jnp.float32)
        edge_index = jax.random.randint(ks[1], (2, N_EDGES), 0, N_NODES, dtype=jnp.int64)
        edge_attr = jax.random.normal(ks[2], (N_EDGES, EDGE_DIM), dtype=jnp.float32)
        hc = HEADS * OUT_DIM
        Wn = jax.random.normal(ks[3], (hc, IN_DIM), dtype=jnp.float32) / np.sqrt(IN_DIM)
        bn = jnp.zeros((hc,), dtype=jnp.float32)
        We = jax.random.normal(ks[4], (hc, EDGE_DIM), dtype=jnp.float32) / np.sqrt(EDGE_DIM)
        be = jnp.zeros((hc,), dtype=jnp.float32)
        attn = jax.random.normal(ks[5], (1, HEADS, OUT_DIM), dtype=jnp.float32) * np.sqrt(2.0 / (HEADS * OUT_DIM + 1))
        return {'x': x, 'edge_index': edge_index, 'edge_attr': edge_attr, 'Wn': Wn, 'bn': bn, 'We': We, 'be': be, 'attn': attn}
    _L3_gnn_all = _L3_gnn_setup()
    _L3_gnn_in = {k: v for k, v in _L3_gnn_all.items() if k in ('Wn', 'bn', 'We', 'be', 'attn')}
    del _L3_gnn_all

    def _L3_ffn_setup():
        import math
        import jax, jax.numpy as jnp
        import numpy as np
        CAPACITY_FACTOR = 1.25
        key = jax.random.key(seed)
        ks = jax.random.split(key, 5)
        B, L, D, F, E = (8, 256, 256, 1024, 8)
        h = jax.random.normal(ks[0], (B, L, D), dtype=jnp.float32)
        gate_w = jax.random.normal(ks[1], (D, E), dtype=jnp.float32) * 0.02
        gate_b = jnp.zeros((E,), dtype=jnp.float32)
        w1 = jax.random.normal(ks[2], (E, D, F), dtype=jnp.float32) * (1.0 / math.sqrt(D))
        b1 = jnp.zeros((E, F), dtype=jnp.float32)
        w2 = jax.random.normal(ks[3], (E, F, D), dtype=jnp.float32) * (1.0 / math.sqrt(F))
        b2 = jnp.zeros((E, D), dtype=jnp.float32)
        return {'h': h, 'gate_w': gate_w, 'gate_b': gate_b, 'w1': w1, 'b1': b1, 'w2': w2, 'b2': b2}
    _L3_ffn_all = _L3_ffn_setup()
    _L3_ffn_in = {k: v for k, v in _L3_ffn_all.items() if k in ('gate_w', 'gate_b', 'w1', 'b1', 'w2', 'b2')}
    del _L3_ffn_all
    return {'x': x, 'src': src, 'dst': dst, 'edge_attr_128': edge_attr_128, 'edge_attr_16': edge_attr_16, 'edge_attr_64': edge_attr_64, 'edge_weight1': edge_weight1, 'L0_gnn_W_in2f': _L0_gnn_in['W_in2f'], 'L0_gnn_Wf1': _L0_gnn_in['Wf1'], 'L0_gnn_bf1': _L0_gnn_in['bf1'], 'L0_gnn_Wf2': _L0_gnn_in['Wf2'], 'L0_gnn_bf2': _L0_gnn_in['bf2'], 'L0_gnn_Wo1': _L0_gnn_in['Wo1'], 'L0_gnn_bo1': _L0_gnn_in['bo1'], 'L0_gnn_Wo2': _L0_gnn_in['Wo2'], 'L0_gnn_bo2': _L0_gnn_in['bo2'], 'L0_ffn_router_w': _L0_ffn_in['router_w'], 'L0_ffn_w1': _L0_ffn_in['w1'], 'L0_ffn_b1': _L0_ffn_in['b1'], 'L0_ffn_w2': _L0_ffn_in['w2'], 'L0_ffn_b2': _L0_ffn_in['b2'], 'L1_gnn_W_l': _L1_gnn_in['W_l'], 'L1_gnn_b_l': _L1_gnn_in['b_l'], 'L1_gnn_W_r': _L1_gnn_in['W_r'], 'L1_gnn_b_r': _L1_gnn_in['b_r'], 'L1_gnn_W_e': _L1_gnn_in['W_e'], 'L1_gnn_att': _L1_gnn_in['att'], 'L1_gnn_W_res': _L1_gnn_in['W_res'], 'L1_gnn_bias': _L1_gnn_in['bias'], 'L1_ffn_Wg': _L1_ffn_in['Wg'], 'L1_ffn_bg': _L1_ffn_in['bg'], 'L1_ffn_W1': _L1_ffn_in['W1'], 'L1_ffn_b1': _L1_ffn_in['b1'], 'L1_ffn_W2': _L1_ffn_in['W2'], 'L1_ffn_b2': _L1_ffn_in['b2'], 'L2_gnn_W1': _L2_gnn_in['W1'], 'L2_gnn_b1': _L2_gnn_in['b1'], 'L2_gnn_W2': _L2_gnn_in['W2'], 'L2_gnn_b2': _L2_gnn_in['b2'], 'L2_gnn_W3': _L2_gnn_in['W3'], 'L2_gnn_b3': _L2_gnn_in['b3'], 'L2_gnn_W4': _L2_gnn_in['W4'], 'L2_gnn_b4': _L2_gnn_in['b4'], 'L2_ffn_Wr': _L2_ffn_in['Wr'], 'L2_ffn_br': _L2_ffn_in['br'], 'L2_ffn_W1': _L2_ffn_in['W1'], 'L2_ffn_b1': _L2_ffn_in['b1'], 'L2_ffn_g1': _L2_ffn_in['g1'], 'L2_ffn_be1': _L2_ffn_in['be1'], 'L2_ffn_m1': _L2_ffn_in['m1'], 'L2_ffn_v1': _L2_ffn_in['v1'], 'L2_ffn_W2': _L2_ffn_in['W2'], 'L2_ffn_b2': _L2_ffn_in['b2'], 'L2_ffn_g2': _L2_ffn_in['g2'], 'L2_ffn_be2': _L2_ffn_in['be2'], 'L2_ffn_m2': _L2_ffn_in['m2'], 'L2_ffn_v2': _L2_ffn_in['v2'], 'L2_ffn_Wo': _L2_ffn_in['Wo'], 'L2_ffn_bo': _L2_ffn_in['bo'], 'L3_gnn_Wn': _L3_gnn_in['Wn'], 'L3_gnn_bn': _L3_gnn_in['bn'], 'L3_gnn_We': _L3_gnn_in['We'], 'L3_gnn_be': _L3_gnn_in['be'], 'L3_gnn_attn': _L3_gnn_in['attn'], 'L3_ffn_gate_w': _L3_ffn_in['gate_w'], 'L3_ffn_gate_b': _L3_ffn_in['gate_b'], 'L3_ffn_w1': _L3_ffn_in['w1'], 'L3_ffn_b1': _L3_ffn_in['b1'], 'L3_ffn_w2': _L3_ffn_in['w2'], 'L3_ffn_b2': _L3_ffn_in['b2']}

def reference(x, src, dst, edge_attr_128, edge_attr_16, edge_attr_64, edge_weight1, L0_gnn_W_in2f, L0_gnn_Wf1, L0_gnn_bf1, L0_gnn_Wf2, L0_gnn_bf2, L0_gnn_Wo1, L0_gnn_bo1, L0_gnn_Wo2, L0_gnn_bo2, L0_ffn_router_w, L0_ffn_w1, L0_ffn_b1, L0_ffn_w2, L0_ffn_b2, L1_gnn_W_l, L1_gnn_b_l, L1_gnn_W_r, L1_gnn_b_r, L1_gnn_W_e, L1_gnn_att, L1_gnn_W_res, L1_gnn_bias, L1_ffn_Wg, L1_ffn_bg, L1_ffn_W1, L1_ffn_b1, L1_ffn_W2, L1_ffn_b2, L2_gnn_W1, L2_gnn_b1, L2_gnn_W2, L2_gnn_b2, L2_gnn_W3, L2_gnn_b3, L2_gnn_W4, L2_gnn_b4, L2_ffn_Wr, L2_ffn_br, L2_ffn_W1, L2_ffn_b1, L2_ffn_g1, L2_ffn_be1, L2_ffn_m1, L2_ffn_v1, L2_ffn_W2, L2_ffn_b2, L2_ffn_g2, L2_ffn_be2, L2_ffn_m2, L2_ffn_v2, L2_ffn_Wo, L2_ffn_bo, L3_gnn_Wn, L3_gnn_bn, L3_gnn_We, L3_gnn_be, L3_gnn_attn, L3_ffn_gate_w, L3_ffn_gate_b, L3_ffn_w1, L3_ffn_b1, L3_ffn_w2, L3_ffn_b2):
    import jax
    import jax.numpy as jnp

    def _L0_gnn_ref(x, rbf, dist_cut, idx_i, idx_j, W_in2f, Wf1, bf1, Wf2, bf2, Wo1, bo1, Wo2, bo2):
        import jax, jax.numpy as jnp
        import numpy as np
        LOG2 = float(np.log(2.0))

        def ssp(x):
            return jax.nn.softplus(x) - LOG2
        N_ATOMS, N_EDGES, N_HF, N_RBF = (25000, 12500, 256, 64)
        n_atoms = x.shape[0]
        h = x @ W_in2f
        Wij = ssp(rbf @ Wf1 + bf1) @ Wf2 + bf2
        Wij = Wij * dist_cut
        x_ij = h[idx_j] * Wij
        m = jax.ops.segment_sum(x_ij, idx_i, num_segments=n_atoms)
        m = ssp(m @ Wo1 + bo1) @ Wo2 + bo2
        return x + m

    def _L0_ffn_ref(input_embeddings, router_w, w1, b1, w2, b2):
        import jax, jax.numpy as jnp
        import numpy as np
        NUM_EXPERTS = 8
        TOP_K = 2
        B, S, D = (8, 256, 256)

        def _moe(tokens, router_w, w1, b1, w2, b2):
            N = tokens.shape[0]
            E = router_w.shape[0]
            logits = tokens.astype(jnp.float32) @ router_w.astype(jnp.float32).T
            probs = jax.nn.softmax(logits, axis=-1)
            rw, re = jax.lax.top_k(probs, TOP_K)
            if TOP_K > 1:
                rw = rw / jnp.maximum(rw.sum(-1, keepdims=True), 1e-12)
            rw = rw.astype(tokens.dtype)
            combine = jnp.zeros((N, E), tokens.dtype).at[jnp.arange(N)[:, None], re].set(rw)
            out = tokens
            for e in range(E):
                h = jax.nn.gelu(tokens @ w1[e] + b1[e], approximate=False)
                y = h @ w2[e] + b2[e]
                out = out + combine[:, e:e + 1] * y
            return out
        b, s, d = input_embeddings.shape
        tokens = input_embeddings.reshape(b * s, d)
        return _moe(tokens, router_w, w1, b1, w2, b2).reshape(b, s, d)

    def _L1_gnn_ref(x, edge_index, edge_attr, W_l, b_l, W_r, b_r, W_e, att, W_res, bias):
        import jax, jax.numpy as jnp
        import numpy as np
        N_NODES = 625
        N_EDGES = 10000
        IN_DIM = 256
        HEADS = 4
        OUT_C = 64
        HC = HEADS * OUT_C
        EDGE_DIM = 16
        NEG_SLOPE = 0.2
        N = x.shape[0]
        H, C = att.shape
        src0, dst0 = (edge_index[0], edge_index[1])
        ones = jnp.ones((src0.shape[0],), dtype=x.dtype)
        cnt = jax.ops.segment_sum(ones, dst0, num_segments=N)
        loop_attr = jax.ops.segment_sum(edge_attr, dst0, num_segments=N) / jnp.maximum(cnt, 1.0)[:, None]
        loop = jnp.arange(N, dtype=src0.dtype)
        src = jnp.concatenate([src0, loop])
        dst = jnp.concatenate([dst0, loop])
        ea = jnp.concatenate([edge_attr, loop_attr], axis=0)
        x_l = (x @ W_l + b_l).reshape(N, H, C)
        x_r = (x @ W_r + b_r).reshape(N, H, C)
        e = x_l[src] + x_r[dst] + (ea @ W_e).reshape(-1, H, C)
        e = jnp.where(e > 0, e, NEG_SLOPE * e)
        logits = jnp.einsum('ehc,hc->eh', e, att)
        m = jax.ops.segment_max(logits, dst, num_segments=N)
        a = jnp.exp(logits - m[dst])
        denom = jax.ops.segment_sum(a, dst, num_segments=N)
        alpha = a / denom[dst]
        out = jax.ops.segment_sum(x_l[src] * alpha[..., None], dst, num_segments=N)
        out = out.reshape(N, H * C)
        out = out + x @ W_res + bias
        return jax.nn.elu(out)

    def _L1_ffn_ref(x, Wg, bg, W1, b1, W2, b2):
        import jax, jax.numpy as jnp
        import numpy as np
        TOP_K = 2
        B, L, D = x.shape
        E = W1.shape[0]
        xf = x.reshape(-1, D)
        gate_logits = xf @ Wg + bg
        top_w, top_i = jax.lax.top_k(gate_logits, TOP_K)
        top_w = jax.nn.softmax(top_w, axis=-1)
        w_dense = jnp.sum(jax.nn.one_hot(top_i, E, dtype=xf.dtype) * top_w[..., None], axis=1)
        out = jnp.zeros_like(xf)
        for e in range(E):
            h = jax.nn.gelu(xf @ W1[e] + b1[e], approximate=False)
            out = out + w_dense[:, e:e + 1] * (h @ W2[e] + b2[e])
        return out.reshape(B, L, D)

    def _L2_gnn_ref(x, edge_index, W1, b1, W2, b2, W3, b3, W4, b4):
        import jax, jax.numpy as jnp
        import numpy as np
        N_NODES = 50000

        def _add_self_loops(src, dst, n):
            loop = jnp.arange(n, dtype=src.dtype)
            return (jnp.concatenate([src, loop]), jnp.concatenate([dst, loop]))

        def gcn_conv(x, src, dst, W, b, n):
            h = x @ W
            deg = jnp.zeros((n,), h.dtype).at[dst].add(1.0)
            dinv = jax.lax.rsqrt(jnp.maximum(deg, 1e-12))
            norm = dinv[src] * dinv[dst]
            msg = h[src] * norm[:, None]
            return jax.ops.segment_sum(msg, dst, num_segments=n) + b
        n = x.shape[0]
        src, dst = _add_self_loops(edge_index[0], edge_index[1], n)
        h = jax.nn.relu(gcn_conv(x, src, dst, W1, b1, n))
        z = jax.nn.relu(gcn_conv(h, src, dst, W2, b2, n))
        h = jax.nn.relu(gcn_conv(z, src, dst, W3, b3, n))
        x_hat = gcn_conv(h, src, dst, W4, b4, n)
        return x_hat

    def _L2_ffn_ref(x, Wr, br, W1, b1, g1, be1, m1, v1, W2, b2, g2, be2, m2, v2, Wo, bo):
        import jax, jax.numpy as jnp
        import numpy as np
        BN_EPS = 0.001

        def _bn(h, g, b, m, v):
            return g * (h - m) * jax.lax.rsqrt(v + BN_EPS) + b
        feat = jnp.mean(x, axis=0)
        w = jax.nn.softmax(feat @ Wr + br, axis=-1)
        h = jnp.einsum('bfd,edh->bfeh', x, W1) + b1
        h = jax.nn.relu(_bn(h, g1, be1, m1, v1))
        h = jnp.einsum('bfeh,ehk->bfek', h, W2) + b2
        h = jax.nn.relu(_bn(h, g2, be2, m2, v2))
        y = jnp.einsum('bfeh,ehd->bfed', h, Wo) + bo
        return jnp.einsum('bfed,fe->bfd', y, w)

    def _L3_gnn_ref(x, edge_index, edge_attr, Wn, bn, We, be, attn):
        import jax, jax.numpy as jnp
        import numpy as np
        N_NODES = 50000
        N_EDGES = 25000
        IN_DIM = 256
        OUT_DIM = 256
        HEADS = 1
        EDGE_DIM = 128
        NEG_SLOPE = 0.01
        N = x.shape[0]
        H, C = (attn.shape[1], attn.shape[2])
        src, dst = (edge_index[0], edge_index[1])
        h = x @ Wn.T + bn
        e = edge_attr @ We.T + be
        xj = h[src].reshape(-1, H, C)
        ee = e.reshape(-1, H, C)
        a = jax.nn.leaky_relu(jnp.sum((xj + ee) * attn, axis=-1), NEG_SLOPE)
        m = jax.ops.segment_max(a, dst, num_segments=N)
        a = jnp.exp(a - m[dst])
        denom = jax.ops.segment_sum(a, dst, num_segments=N)
        a = a / (denom[dst] + 1e-16)
        msg = (xj * a[..., None]).reshape(-1, H * C)
        out = jax.ops.segment_sum(msg, dst, num_segments=N)
        return jax.nn.relu(out)

    def _L3_ffn_ref(h, gate_w, gate_b, w1, b1, w2, b2):
        import math
        import jax, jax.numpy as jnp
        import numpy as np
        CAPACITY_FACTOR = 1.25
        B, L, D = h.shape
        E = gate_w.shape[1]
        T = B * L
        C = max(1, math.ceil(CAPACITY_FACTOR * T / E))
        x = h.reshape(T, D)
        logits = x @ gate_w + gate_b
        probs = jax.nn.softmax(logits, axis=-1)
        idx = jnp.argmax(probs, axis=-1)
        prb = jnp.take_along_axis(probs, idx[:, None], axis=1)[:, 0]
        one_hot = jax.nn.one_hot(idx, E, dtype=jnp.float32)
        pos = (jnp.cumsum(one_hot, axis=0) * one_hot).sum(-1).astype(jnp.int32) - 1
        kept = pos < C
        pos_safe = jnp.where(kept, pos, C)
        buf = jnp.zeros((E, C, D), dtype=h.dtype).at[idx, pos_safe].set(x, mode='drop')
        hmid = jax.nn.relu(jnp.einsum('ecd,edf->ecf', buf, w1) + b1[:, None, :])
        ybuf = jnp.einsum('ecf,efd->ecd', hmid, w2) + b2[:, None, :]
        pos_g = jnp.minimum(pos, C - 1)
        y_tok = ybuf[idx, pos_g] * (prb * kept)[:, None]
        y = y_tok.reshape(B, L, D)
        y = jnp.nan_to_num(y, nan=0.0, posinf=10000.0, neginf=-10000.0)
        return y
    edge_index = jnp.stack([src, dst])
    x = x + _L0_gnn_ref(_layernorm(x, axis=-1), edge_attr_64, edge_weight1, src, dst, L0_gnn_W_in2f, L0_gnn_Wf1, L0_gnn_bf1, L0_gnn_Wf2, L0_gnn_bf2, L0_gnn_Wo1, L0_gnn_bo1, L0_gnn_Wo2, L0_gnn_bo2)
    x = x + _L0_ffn_ref(_layernorm(x, axis=-1)[None], L0_ffn_router_w, L0_ffn_w1, L0_ffn_b1, L0_ffn_w2, L0_ffn_b2)[0]
    x = x + _L1_gnn_ref(_layernorm(x, axis=-1), edge_index, edge_attr_16, L1_gnn_W_l, L1_gnn_b_l, L1_gnn_W_r, L1_gnn_b_r, L1_gnn_W_e, L1_gnn_att, L1_gnn_W_res, L1_gnn_bias)
    x = x + _L1_ffn_ref(_layernorm(x, axis=-1)[None], L1_ffn_Wg, L1_ffn_bg, L1_ffn_W1, L1_ffn_b1, L1_ffn_W2, L1_ffn_b2)[0]
    x = x + _L2_gnn_ref(_layernorm(x, axis=-1), edge_index, L2_gnn_W1, L2_gnn_b1, L2_gnn_W2, L2_gnn_b2, L2_gnn_W3, L2_gnn_b3, L2_gnn_W4, L2_gnn_b4)
    x = x + _L2_ffn_ref(_layernorm(x, axis=-1)[None], L2_ffn_Wr, L2_ffn_br, L2_ffn_W1, L2_ffn_b1, L2_ffn_g1, L2_ffn_be1, L2_ffn_m1, L2_ffn_v1, L2_ffn_W2, L2_ffn_b2, L2_ffn_g2, L2_ffn_be2, L2_ffn_m2, L2_ffn_v2, L2_ffn_Wo, L2_ffn_bo)[0]
    x = x + _L3_gnn_ref(_layernorm(x, axis=-1), edge_index, edge_attr_128, L3_gnn_Wn, L3_gnn_bn, L3_gnn_We, L3_gnn_be, L3_gnn_attn)
    x = x + _L3_ffn_ref(_layernorm(x, axis=-1)[None], L3_ffn_gate_w, L3_ffn_gate_b, L3_ffn_w1, L3_ffn_b1, L3_ffn_w2, L3_ffn_b2)[0]
    return x

_drawn_inputs = setup_inputs


def setup_inputs(seed=0):
    import zlib

    import numpy as np

    out = dict(_drawn_inputs(seed))
    spreads = {'L0_gnn_bf1': (0.0, 0.1),
     'L0_gnn_bf2': (0.0, 0.1),
     'L0_gnn_bo1': (0.0, 0.1),
     'L0_gnn_bo2': (0.0, 0.1),
     'L0_ffn_b1': (0.0, 0.447),
     'L0_ffn_b2': (0.0, 0.316),
     'L1_gnn_b_l': (0.0, 0.308),
     'L1_gnn_b_r': (0.0, 2.0),
     'L1_gnn_bias': (0.0, 0.278),
     'L1_ffn_bg': (0.0, 0.406),
     'L1_ffn_b1': (0.0, 0.8),
     'L1_ffn_b2': (0.0, 0.349),
     'L2_gnn_b1': (0.0, 0.8),
     'L2_gnn_b2': (0.0, 0.738),
     'L2_gnn_b3': (0.0, 0.342),
     'L2_gnn_b4': (0.0, 0.295),
     'L2_ffn_br': (0.0, 0.8),
     'L2_ffn_b1': (0.0, 0.8),
     'L2_ffn_g1': (1.0, 0.6),
     'L2_ffn_be1': (0.0, 0.8),
     'L2_ffn_m1': (0.0, 0.8),
     'L2_ffn_v1': (1.0, 0.6),
     'L2_ffn_b2': (0.0, 0.674),
     'L2_ffn_g2': (1.0, 0.6),
     'L2_ffn_be2': (0.0, 0.697),
     'L2_ffn_m2': (0.0, 0.625),
     'L2_ffn_v2': (1.0, 0.6),
     'L2_ffn_bo': (0.0, 0.497),
     'L3_gnn_bn': (0.0, 0.334),
     'L3_gnn_be': (0.0, 2.0),
     'L3_ffn_gate_b': (0.0, 0.288),
     'L3_ffn_b1': (0.0, 2.0),
     'L3_ffn_b2': (0.0, 2.0)}
    factors = {'edge_attr_16': 8.0,
     'L1_gnn_W_r': 8.0,
     'L1_gnn_W_e': 8.0,
     'L1_gnn_att': 3.641,
     'L2_gnn_W1': 6.444,
     'L2_gnn_W3': 2.691,
     'L3_ffn_w1': 2.888}
    for name, (base, spread) in spreads.items():
        noise = np.random.default_rng([zlib.crc32(name.encode()), seed]).standard_normal(out[name].shape)
        drawn = base * np.exp(spread * noise) if base else spread * noise
        out[name] = jnp.asarray(drawn.astype(out[name].dtype))
    for name, factor in factors.items():
        out[name] = (out[name] * factor).astype(out[name].dtype)
    return out
```

```python
from contextlib import ExitStack

import numpy as np

import concourse.bass as bass
from concourse import mybir

F32 = mybir.dt.float32
I32 = mybir.dt.int32
ALU = mybir.AluOpType
ACT = mybir.ActivationFunctionType
AX = mybir.AxisListType

P = 128
N = 3125
D = 256
DC = D // P
E = 50000
NT = -(-N // P)
NP = NT * P
TAIL = N - (NT - 1) * P
EC = E // P
EX = E - EC * P
BATCH = 4
ST = -(-(E // P + NT) // (2 * BATCH)) * 2 * BATCH
SLOTS = ST * P
NB = ST // BATCH
SPARE = ST - -(-E // P)
EXPERTS = 8
EPS = 1e-5
HUGE = 1.0e30

META = 4

UN = 5
NI = NT // UN
assert NT % UN == 0


def at(tensor, t, width):
    if isinstance(t, int):
        return tensor[:, t * width:(t + 1) * width]
    return tensor[:, bass.ds(t * width, width)]


class Placement:

    def __init__(self, nc, s, key, other, fields, weighted):
        self.key, self.other, self.fields, self.weighted = key, other, fields, weighted
        self.first = {}
        at_column = 0
        for name, width in fields:
            self.first[name] = at_column
            at_column += width
        self.number, self.far, self.near = at_column, at_column + 1, at_column + 2
        self.width = at_column + META
        self.records = nc.dram_tensor(f"records_by_{key}", [SLOTS, self.width], F32, kind="Internal").ap()
        self.block_row = s.sb(f"block_row_{key}", [P, ST], I32)


class Chain:

    def __init__(self, eng, sem, base=0):
        self.eng, self.sem, self.base, self.n = eng, sem, base, 0

    def __call__(self, ins):
        self.n += 1
        ins.then_inc(self.sem, 1)
        self.eng.wait_ge(self.sem, self.base + self.n)

    def steps(self, n):
        assert self.n == n, (self.n, n)


class Scope:

    def __init__(self, nc, name, ctx):
        self.nc, self.name, self.ctx, self.sems = nc, name, ctx, []
        ctx.callback(self.close)

    def close(self):
        if self.sems:
            self.nc.clear_and_free_semaphores(self.sems)
            self.nc.all_engine_barrier()

    def sb(self, name, shape, dt=F32):
        return self.ctx.enter_context(self.nc.sbuf_tensor(f"{self.name}_{name}", shape, dt))

    def ps(self, name, shape):
        return self.ctx.enter_context(self.nc.psum_tensor(f"{self.name}_{name}", shape, F32))

    def sem(self, name):
        self.sems.append(self.nc.alloc_semaphore(f"{self.name}_{name}"))
        return self.sems[-1]


class Net:

    def __init__(self, nc, arrays, ctx):
        self.nc = nc
        self.a = arrays
        s = Scope(nc, "net", ctx)
        self.x = s.sb("x", [P, NT * D])
        self.ident = s.sb("ident", [P, P])
        self.before = s.sb("before", [P, P])
        self.ones = s.sb("ones", [P, P])
        self.eps = s.sb("eps", [P, 1])
        self.columns = s.sb("columns", [P, P])
        self.rank8 = s.sb("rank8", [P, NT * EXPERTS])
        self.mean16 = s.sb("mean16", [P, NT * 16])
        self.dinv = s.sb("dinv", [P, NT])
        self.work = s.sb("work", [P, NT * 260])
        self.by_src = Placement(nc, s, "src", "dst", (("edge_attr_64", 64),), True)
        self.by_dst = Placement(nc, s, "dst", "src", (("edge_attr_128", 128), ("edge_attr_16", 16)), False)
        self.tables = {}

    def scope(self, name, ctx):
        return Scope(self.nc, name, ctx)

    def table(self, width):
        if width not in self.tables:
            self.tables[width] = self.nc.dram_tensor(f"table{width}", [NP, width], F32, kind="Internal").ap()
        return self.tables[width]


def row(vector):
    return vector.rearrange("(o n) -> o n", o=1)


def column(vector):
    return vector.rearrange("(p o) -> p o", o=1)


def spread(vector):
    return row(vector).to_broadcast([P, vector.shape[0]])


def node_rows(table, t0, n):
    return table[bass.ds(t0 * P, n * P), :].rearrange("(t p) d -> p t d", p=P)


def tiled(ap, width):
    return ap.rearrange("p (t d) -> p t d", d=width)


def chunked(weights):
    return weights.rearrange("(c p) n -> p c n", p=P)


def bank_free(q, k):
    return UN + q - 1 + (k == 0)


class Front:

    def __init__(self, s):
        self.stats = s.sb("stats", [P, UN * 6])
        self.moments = s.sb("moments", [P, UN * 2])
        self.sigma = s.sb("sigma", [P, UN])
        self.rstd = s.sb("rstd", [P, UN])
        self.xn = s.sb("xn", [P, UN * D])
        self.xT = s.sb("xT", [P, UN * D])
        self.ps = s.ps("turn", [P, 2, 512])
        self.stats_ready = s.sem("stats_ready")
        self.moments_ready = s.sem("moments_ready")
        self.rstd_ready = s.sem("rstd_ready")
        self.tick = s.sem("tick")
        self.sigma_ready = s.sem("sigma_ready")
        self.normed = s.sem("normed")
        self.turned = s.sem("turned")
        self.xT_ready = s.sem("xT_ready")
        self.projected = s.sem("projected")

    def start_tensor(self, pe):
        pe.sem_inc(self.turned, UN)
        pe.sem_inc(self.projected, UN)

    def start_scalar(self, act):
        act.sem_inc(self.xT_ready, UN)

    def moments_of(self, dve, net, i):
        for k in range(UN):
            ins = dve.bn_stats(at(self.stats, k, 6), at(net.x, i * UN + k, D))
        ins.then_inc(self.stats_ready, 1)
        dve.wait_ge(self.stats_ready, i + 1)
        dve.sem_inc(self.tick, 1)
        for k in range(UN):
            ins = dve.bn_aggr(at(self.moments, k, 2), at(self.stats, k, 6))
        ins.then_inc(self.moments_ready, 1)

    def root(self, act, net, i):
        act.wait_ge(self.moments_ready, i + 1)
        act.activation(self.sigma[:, :], tiled(self.moments[:, :], 2)[:, :, 1], ACT.Sqrt, bias=net.eps[:, :])\
            .then_inc(self.sigma_ready, 1)

    def normalize(self, dve, net, i, k):
        q = i * UN + k
        if k == 0:
            dve.wait_ge(self.sigma_ready, i + 1)
            dve.reciprocal(self.rstd[:, :], self.sigma[:, :]).then_inc(self.rstd_ready, 1)
            dve.wait_ge(self.rstd_ready, i + 1)
        dve.wait_ge(self.turned, q + 1)
        dve.tensor_scalar(at(self.xn, k, D), at(net.x, q, D), self.moments[:, 2 * k:2 * k + 1], at(self.rstd, k, 1),
                          ALU.subtract, ALU.mult).then_inc(self.normed, 1)

    def take(self, dve, q, k, fill):
        dve.wait_ge(self.turned, q + 1)
        fill(at(self.xn, k, D)).then_inc(self.normed, 1)

    def turn(self, pe, net, q, k, width=D, tick=None):
        pe.wait_ge(self.normed, q + 1)
        pe.wait_ge(self.xT_ready, bank_free(q, k))
        if tick is not None:
            pe.sem_inc(tick, 1)
        for lo in range(0, width, P):
            n = min(P, width - lo)
            ins = pe.transpose(self.ps[0:n, k % 2, lo:lo + P], self.xn[:, k * D + lo:k * D + lo + n], net.ident[:, :])
        ins.then_inc(self.turned, 1)

    def keep(self, act, q, k, rows=P, chunks=DC):
        act.wait_ge(self.turned, UN + q + 1)
        act.wait_ge(self.projected, q + 1)
        act.activation(self.xT[0:rows, k * D:k * D + chunks * P], self.ps[0:rows, k % 2, 0:chunks * P], ACT.Copy).then_inc(self.xT_ready, 1)

    def lhsT(self, k, c):
        return self.xT[:, k * D + c * P:k * D + (c + 1) * P]

    def project(self, pe, q, k, out, weights, last=True):
        for c in range(DC):
            ins = pe.matmul(out, self.lhsT(k, c), weights[:, c, :], start=c == 0, stop=c == DC - 1)
        if last:
            ins.then_inc(self.projected, 1)


def setup(net):
    nc = net.nc
    with ExitStack() as ctx:
        s = net.scope("setup", ctx)
        index = s.sb("index", [P, P], I32)
        rank = s.sb("rank", [P, NT * EXPERTS], I32)
        x_loaded = s.sem("x_loaded")
        x_cleared = s.sem("x_cleared")
        ones_set = s.sem("ones_set")
        index_set = s.sem("index_set")
        block = ctx.enter_context(nc.Block())

        @block.sync
        def _(sp):
            full = (NT - 1) * P
            sp.wait_ge(x_cleared, 1)
            sp.dma_start(net.x[:, 0:(NT - 1) * D].rearrange("p (t d) -> p t d", d=D),
                         net.a["x"][0:full, :].rearrange("(t p) d -> p t d", p=P)).then_inc(x_loaded, 16)
            sp.dma_start(net.x[0:TAIL, (NT - 1) * D:NT * D], net.a["x"][full:N, :]).then_inc(x_loaded, 16)
            sp.wait_ge(x_loaded, 32)

        @block.gpsimd
        def _(pool):
            pool.iota(index[:, :], pattern=[[1, P]], base=0, channel_multiplier=0).then_inc(index_set, 1)
            pool.iota(rank[:, :], pattern=[[0, NT], [-1, EXPERTS]], base=EXPERTS, channel_multiplier=0).then_inc(index_set, 1)
            pool.memset(net.ones[:, :], 1.0).then_inc(ones_set, 1)
            pool.wait_ge(ones_set, 1)
            pool.affine_select(out=net.ident[:, :], in_=net.ones[:, :], compare_op=ALU.is_equal, fill=0.0,
                               base=0, pattern=[[-1, P]], channel_multiplier=1)
            pool.affine_select(out=net.before[:, :], in_=net.ones[:, :], compare_op=ALU.is_gt, fill=0.0,
                               base=0, pattern=[[1, P]], channel_multiplier=-1)

        @block.vector
        def _(dve):
            dve.memset(net.eps[:, :], EPS)
            dve.memset(net.x[:, (NT - 1) * D:NT * D], 0.0).then_inc(x_cleared, 1)
            dve.wait_ge(index_set, 2)
            dve.tensor_copy(net.rank8[:, :], rank[:, :])
            dve.tensor_copy(net.columns[:, :], index[:, :])


def place_by_src(net):
    place_edges(net, net.by_src)


def place_by_dst(net):
    place_edges(net, net.by_dst)


def place_edges(net, to):
    nc, a = net.nc, net.a
    JC = 13
    CH = EC // JC
    assert EC % (2 * JC) == 0
    FILL = NT + SPARE
    with ExitStack() as ctx:
        s = net.scope(f"place_{to.key}", ctx)
        rec_w = to.width
        near = s.sb("near", [P, EC + 1], I32)
        far = s.sb("far", [P, EC + 1], I32)
        part = s.sb("part", [P, EC + 1], I32)
        blk = s.sb("blk", [P, EC + 1])
        meta = s.sb("meta", [P, (EC + 1) * META])
        weight = s.sb("weight", [P, EC + 1])
        one_row = s.sb("one_row", [P, EC + 1])
        match = s.sb("match", [P, EC + 1])
        counted = s.sb("counted", [P, NT * (EC + 1)])
        totals = s.sb("totals", [P, NT])
        count = s.sb("count", [P, NT])
        ahead = s.sb("ahead", [P, NT])
        tiles_i = s.sb("tiles_i", [P, NT], I32)
        tiles = s.sb("tiles", [P, NT])
        upto = s.sb("upto", [P, NT])
        first = s.sb("first", [P, NT])
        base = s.sb("base", [P, NT])
        pos = s.sb("pos", [P, EC + 1])
        pos_i = s.sb("pos_i", [P, EC + 1], I32)
        p_col_i = s.sb("p_col_i", [P, 1], I32)
        p_col = s.sb("p_col", [P, 1])
        spare_i = s.sb("spare_i", [P, SPARE], I32)
        spare = s.sb("spare", [P, SPARE])
        fill = s.sb("fill", [P, FILL])
        past = s.sb("past", [P, NT])
        fill_i = s.sb("fill_i", [P, FILL], I32)
        tile_no_i = s.sb("tile_no_i", [P, ST], I32)
        tile_no = s.sb("tile_no", [P, ST])
        tile_blk = s.sb("tile_blk", [P, ST])
        empty = s.sb("empty", [P, rec_w])
        fill_at = s.sb("fill_at", [P, 5], I32)
        pos_at = [s.sb(f"pos_at{b}", [P, JC], I32) for b in range(2)]
        rec = [s.sb(f"rec{b}", [P, JC * rec_w]) for b in range(2)]
        staged = [[s.sb(f"staged{n}_{b}", [P, JC * w]) for n, (_, w) in enumerate(to.fields)] for b in range(2)]
        ps = s.ps("ps", [P, 2, 512])

        ids_loaded = s.sem("ids_loaded")
        attrs_loaded = [s.sem(f"attrs_loaded{b}") for b in range(2)]
        numbers = s.sem("numbers")
        chain = s.sem("chain")
        count_step = s.sem("count_step")
        pos_step = s.sem("pos_step")
        blk_step = s.sem("blk_step")
        totals_ready = s.sem("totals_ready")
        sums_ready = s.sem("sums_ready")
        fill_ready = s.sem("fill_ready")
        fill_copied = s.sem("fill_copied")
        filled = s.sem("filled")
        wide_copied = s.sem("wide_copied")
        rest_copied = s.sem("rest_copied")
        pos_copied = s.sem("pos_copied")
        attrs_free_act = s.sem("attrs_free_act")
        attrs_free_dve = s.sem("attrs_free_dve")
        slots_ready = s.sem("slots_ready")
        scattered = [s.sem(f"scattered{b}") for b in range(2)]
        rec_free = s.sem("rec_free")
        pool_tick = s.sem("pool_tick")
        left_loaded = s.sem("left_loaded")
        left_copied = s.sem("left_copied")
        left_scattered = s.sem("left_scattered")
        block = ctx.enter_context(nc.Block())

        def three(b):
            return rec[b][:, :].rearrange("p (j r) -> p j r", r=rec_w)

        def by_edge(name, w, j0, n):
            return a[name][0:EC * P, :].rearrange("(p j) w -> p (j w)", p=P)[:, bass.ds(j0 * w, n * w)]

        @block.sync
        def _(sp):
            for name, into in ((to.key, near), (to.other, far)):
                sp.dma_start(into[:, 0:EC], a[name][0:EC * P].rearrange("(p j) -> p j", p=P)).then_inc(ids_loaded, 16)
                sp.dma_start(into[0:EX, EC:EC + 1], a[name][EC * P:E].rearrange("(p j) -> p j", j=1))\
                    .then_inc(ids_loaded, 16)
            if to.weighted:
                w = a["edge_weight1"].rearrange("e o -> (e o)")
                sp.dma_start(weight[:, 0:EC], w[0:EC * P].rearrange("(p j) -> p j", p=P)).then_inc(ids_loaded, 16)
                sp.dma_start(weight[0:EX, EC:EC + 1], w[EC * P:E].rearrange("(p j) -> p j", j=1)).then_inc(ids_loaded, 16)
            with sp.Fori(0, CH // 2) as i:
                for b in range(2):
                    q = 2 * i + b
                    sp.wait_ge(attrs_free_act, q + 1)
                    sp.wait_ge(attrs_free_dve, q + 1)
                    for n, (name, w) in enumerate(to.fields):
                        sp.dma_start(staged[b][n][:, :], by_edge(name, w, q * JC, JC)).then_inc(attrs_loaded[b], 16)
            sp.wait_ge(rec_free, CH + 1)
            for name, w in to.fields:
                c = to.first[name]
                sp.dma_start(rec[0][0:EX, c:c + w], a[name][EC * P:E, :]).then_inc(left_loaded, 16)

        @block.gpsimd
        def _(pool):
            pool.iota(p_col_i[:, :], pattern=[[0, 1]], base=0, channel_multiplier=1).then_inc(numbers, 1)
            pool.iota(spare_i[:, :], pattern=[[P, SPARE]], base=0, channel_multiplier=1).then_inc(numbers, 1)
            pool.iota(tile_no_i[:, :], pattern=[[1, ST]], base=0, channel_multiplier=0).then_inc(numbers, 1)
            pool.sem_inc(rec_free, 2)
            with pool.Fori(0, CH // 2) as i:
                for b in range(2):
                    q = 2 * i + b
                    pool.wait_ge(wide_copied, q + 1)
                    pool.wait_ge(rest_copied, q + 1)
                    pool.wait_ge(pos_copied, q + 1)
                    pool.sem_inc(pool_tick, 1)
                    for j in range(JC):
                        pool.indirect_dma_start(
                            to.records, bass.IndirectOffsetOnAxis(pos_at[b][:, j:j + 1], 0),
                            at(rec[b], j, rec_w), None).then_inc(scattered[b], 16)
                    pool.wait_ge(scattered[b], (i + 1) * 16 * JC)
                    pool.sem_inc(rec_free, 1)
            pool.wait_ge(left_copied, 2)
            pool.wait_ge(left_loaded, 16 * len(to.fields))
            pool.indirect_dma_start(to.records, bass.IndirectOffsetOnAxis(pos_at[0][0:EX, 0:1], 0),
                                    rec[0][0:EX, 0:rec_w], None).then_inc(left_scattered, 16)
            with pool.Fori(0, FILL // 5) as i:
                pool.wait_ge(fill_copied, i + 1)
                pool.sem_inc(pool_tick, 1)
                for j in range(5):
                    pool.indirect_dma_start(
                        to.records, bass.IndirectOffsetOnAxis(fill_at[:, j:j + 1], 0),
                        empty[:, :], None, bounds_check=SLOTS - 1, oob_is_err=False).then_inc(filled, 16)
                pool.wait_ge(filled, (i + 1) * 80)
                pool.sem_inc(fill_ready, 1)
            pool.wait_ge(left_scattered, 16)

        @block.tensor
        def _(pe):
            pe.wait_ge(totals_ready, 1)
            pe.matmul(ps[:, 0, 0:NT], net.before[:, :], totals[:, :], start=True, stop=True)
            pe.matmul(ps[:, 1, 0:NT], net.ones[:, :], totals[:, :], start=True, stop=True).then_inc(sums_ready, 1)

        @block.scalar
        def _(act):
            act.sem_inc(attrs_free_act, 2)
            with act.Fori(0, CH // 2) as i:
                for b in range(2):
                    act.wait_ge(attrs_loaded[b], (i + 1) * 16 * len(to.fields))
                    act.wait_ge(rec_free, 2 * i + b + 1)
                    c, w = 0, to.fields[0][1]
                    act.activation(three(b)[:, :, c:c + w], tiled(staged[b][0][:, :], w), ACT.Copy).then_inc(wide_copied, 1)
                    act.wait_ge(wide_copied, 2 * i + b + 1)
                    act.sem_inc(attrs_free_act, 1)

        @block.vector
        def _(dve):
            link = Chain(dve, chain)
            dve.wait_ge(ids_loaded, 96 if to.weighted else 64)
            link(dve.tensor_single_scalar(part[:, 0:EC], near[:, 0:EC], 7, op=ALU.arith_shift_right))
            link(dve.tensor_single_scalar(part[0:EX, EC:EC + 1], near[0:EX, EC:EC + 1], 7, op=ALU.arith_shift_right))
            link(dve.memset(blk[:, EC:EC + 1], -1.0))
            link(dve.tensor_copy(blk[:, 0:EC], part[:, 0:EC]))
            link(dve.tensor_copy(blk[0:EX, EC:EC + 1], part[0:EX, EC:EC + 1]))
            m = meta[:, :].rearrange("p (j r) -> p j r", r=META)
            link(dve.memset(meta[:, :], 1.0))
            for lo, hi, p in ((0, EC, P), (EC, EC + 1, EX)):
                if to.weighted:
                    link(dve.tensor_copy(m[0:p, lo:hi, 0], weight[0:p, lo:hi]))
                link(dve.tensor_copy(m[0:p, lo:hi, 1], far[0:p, lo:hi]))
                link(dve.tensor_single_scalar(part[0:p, lo:hi], near[0:p, lo:hi], P - 1, op=ALU.bitwise_and))
                link(dve.tensor_copy(m[0:p, lo:hi, 2], part[0:p, lo:hi]))
            link(dve.memset(one_row[:, :], 1.0))
            link(dve.memset(empty[:, :], 0.0))
            link(dve.memset(empty[:, to.near:to.near + 1], -1.0))
            with dve.Fori(0, NT) as b:
                step = Chain(dve, count_step, b * 2)
                step(dve.tensor_scalar(match[:, :], blk[:, :], at(net.columns, b, 1), None, ALU.is_equal))
                step(dve.tensor_tensor_scan(at(counted, b, EC + 1), one_row[:, :], match[:, :], 0.0, ALU.mult, ALU.add))
                step.steps(2)
            link(dve.tensor_copy(totals[:, :], counted[:, :].rearrange("p (b j) -> p b j", b=NT)[:, :, EC]))
            dve.sem_inc(totals_ready, 1)
            dve.wait_ge(sums_ready, 1)
            link(dve.tensor_copy(ahead[:, :], ps[:, 0, 0:NT]))
            link(dve.tensor_copy(count[:, :], ps[:, 1, 0:NT]))
            link(dve.tensor_scalar(base[:, :], count[:, :], float(P - 1), None, ALU.add))
            link(dve.tensor_copy(tiles_i[:, :], base[:, :]))
            link(dve.tensor_single_scalar(tiles_i[:, :], tiles_i[:, :], 7, op=ALU.arith_shift_right))
            link(dve.tensor_copy(tiles[:, :], tiles_i[:, :]))
            link(dve.tensor_tensor_scan(upto[:, :], one_row[:, 0:NT], tiles[:, :], 0.0, ALU.mult, ALU.add))
            link(dve.tensor_tensor(first[:, :], upto[:, :], tiles[:, :], ALU.subtract))
            link(dve.scalar_tensor_tensor(base[:, :], first[:, :], float(P), ahead[:, :], ALU.mult, ALU.add))
            link(dve.tensor_scalar(base[:, :], base[:, :], -1.0, None, ALU.add))
            link(dve.memset(pos[:, :], 0.0))
            with dve.Fori(0, NT) as b:
                step = Chain(dve, pos_step, b * 3)
                step(dve.tensor_scalar(match[:, :], blk[:, :], at(net.columns, b, 1), None, ALU.is_equal))
                step(dve.scalar_tensor_tensor(match[:, :], at(counted, b, EC + 1), at(base, b, 1), match[:, :],
                                              ALU.add, ALU.mult))
                step(dve.tensor_tensor(pos[:, :], pos[:, :], match[:, :], ALU.add))
                step.steps(3)
            link(dve.tensor_copy(pos_i[:, :], pos[:, :]))
            dve.wait_ge(numbers, 3)
            link(dve.tensor_copy(p_col[:, :], p_col_i[:, :]))
            link(dve.tensor_copy(spare[:, :], spare_i[:, :]))
            link(dve.tensor_copy(tile_no[:, :], tile_no_i[:, :]))
            link(dve.memset(tile_blk[:, :], -1.0))
            with dve.Fori(0, NT) as b:
                step = Chain(dve, blk_step, b)
                step(dve.scalar_tensor_tensor(tile_blk[:, :], tile_no[:, :], at(first, b, 1), tile_blk[:, :],
                                              ALU.is_ge, ALU.add))
                step.steps(1)
            link(dve.tensor_copy(to.block_row[:, :], tile_blk[:, :]))
            link(dve.scalar_tensor_tensor(fill[:, 0:NT], first[:, :], float(P), count[:, :], ALU.mult, ALU.add))
            link(dve.tensor_scalar(fill[:, 0:NT], fill[:, 0:NT], p_col[:, :], None, ALU.add))
            link(dve.tensor_scalar(past[:, :], upto[:, :], float(P), None, ALU.mult))
            link(dve.tensor_tensor(past[:, :], fill[:, 0:NT], past[:, :], ALU.is_ge))
            link(dve.scalar_tensor_tensor(fill[:, 0:NT], past[:, :], float(SLOTS), fill[:, 0:NT], ALU.mult, ALU.add))
            link(dve.tensor_scalar(past[:, 0:1], upto[:, NT - 1:NT], float(P), None, ALU.mult))
            link(dve.tensor_scalar(fill[:, NT:FILL], spare[:, :], past[:, 0:1], None, ALU.add))
            link(dve.tensor_copy(fill_i[:, :], fill[:, :]))
            dve.sem_inc(attrs_free_dve, 2)
            with dve.Fori(0, CH // 2) as i:
                for b in range(2):
                    q = 2 * i + b
                    dve.wait_ge(attrs_loaded[b], (i + 1) * 16 * len(to.fields))
                    dve.wait_ge(rec_free, q + 1)
                    dve.tensor_copy(pos_at[b][:, :], at(pos_i, q, JC)).then_inc(pos_copied, 1)
                    for n, (name, w) in enumerate(to.fields[1:], 1):
                        c = to.first[name]
                        dve.tensor_copy(three(b)[:, :, c:c + w], tiled(staged[b][n][:, :], w))
                    dve.tensor_copy(three(b)[:, :, to.number:rec_w], at(meta, q, JC * META).rearrange("p (j r) -> p j r", r=META))\
                        .then_inc(rest_copied, 1)
                    dve.wait_ge(rest_copied, q + 1)
                    dve.sem_inc(attrs_free_dve, 1)
            dve.wait_ge(rec_free, CH + 1)
            dve.tensor_copy(rec[0][0:EX, to.number:rec_w], m[0:EX, EC, :]).then_inc(left_copied, 1)
            dve.tensor_copy(pos_at[0][0:EX, 0:1], pos_i[0:EX, EC:EC + 1]).then_inc(left_copied, 1)
            dve.sem_inc(fill_ready, 1)
            with dve.Fori(0, FILL // 5) as i:
                dve.wait_ge(fill_ready, i + 1)
                dve.tensor_copy(fill_at[:, :], at(fill_i, i, 5)).then_inc(fill_copied, 1)


def batch_records(records, q, lo, hi):
    rows = records[bass.ds(q * (BATCH * P), BATCH * P), :]
    return rows.rearrange("(t p) r -> p t r", p=P)[:, :, lo:hi]


def l0_gnn_nodes(net):
    nc, a = net.nc, net.a
    table = net.table(D)
    with ExitStack() as ctx:
        s = net.scope("l0n", ctx)
        f = Front(s)
        w = s.sb("w", [P, DC * D])
        h = s.sb("h", [P, NT * D])
        ps = s.ps("ps", [P, 2, 512])
        w_loaded = s.sem("w_loaded")
        h_ready = s.sem("h_ready")
        h_stored = s.sem("h_stored")
        block = ctx.enter_context(nc.Block())
        wv = w[:, :].rearrange("p (c n) -> p c n", c=DC)

        @block.sync
        def _(sp):
            sp.dma_start(wv, chunked(a["L0_gnn_W_in2f"])).then_inc(w_loaded, 16)
            for i in range(NI):
                sp.wait_ge(h_ready, UN + (i + 1) * UN)
                sp.dma_start(node_rows(table, i * UN, UN), tiled(at(h, i, UN * D), D)).then_inc(h_stored, 16)
            sp.wait_ge(h_stored, NI * 16)

        @block.vector
        def _(dve):
            with dve.Fori(0, NI) as i:
                f.moments_of(dve, net, i)
                for k in range(UN):
                    t = i * UN + k
                    f.normalize(dve, net, i, k)
                    dve.wait_ge(f.normed, t + 1)
                    dve.tensor_tensor(at(net.x, t, D), at(net.x, t, D), at(f.xn, k, D), ALU.add)

        @block.tensor
        def _(pe):
            f.start_tensor(pe)
            pe.wait_ge(w_loaded, 16)
            with pe.Fori(0, NI) as i:
                for k in range(UN):
                    t = i * UN + k
                    f.turn(pe, net, t, k)
                    pe.wait_ge(f.xT_ready, UN + t + 1)
                    pe.wait_ge(h_ready, bank_free(t, k))
                    f.project(pe, t, k, ps[:, k % 2, 0:D], wv)

        @block.scalar
        def _(act):
            f.start_scalar(act)
            act.sem_inc(h_ready, UN)
            with act.Fori(0, NI) as i:
                f.root(act, net, i)
                for k in range(UN):
                    t = i * UN + k
                    f.keep(act, t, k)
                    act.wait_ge(f.projected, UN + t + 1)
                    act.activation(at(h, t, D), ps[:, k % 2, 0:D], ACT.Copy).then_inc(h_ready, 1)


LN2 = float(np.log(2.0))
CLAMP = 80.0


class Gather:

    def __init__(self, s, net, placed, table, width, lo):
        self.net, self.placed, self.table, self.width, self.lo, self.n = net, placed, table, width, lo, placed.width - lo
        self.rec = [s.sb(f"rec{b}", [P, BATCH * self.n]) for b in range(2)]
        self.idx = [s.sb(f"idx{b}", [P, BATCH], I32) for b in range(2)]
        self.rows = [s.sb(f"rows{b}", [P, BATCH * width]) for b in range(2)]
        self.rec_loaded = [s.sem(f"rec_loaded{b}") for b in range(2)]
        self.idx_ready = s.sem("idx_ready")
        self.rows_loaded = [s.sem(f"rows_loaded{b}") for b in range(2)]
        self.batch_done = s.sem("batch_done")
        self.pool_tick = s.sem("pool_tick")

    def load(self, sp):
        def batch(q, b):
            sp.wait_ge(self.batch_done, q + 1)
            sp.dma_start(tiled(self.rec[b][:, :], self.n), batch_records(self.placed.records, q, self.lo, self.placed.width))\
                .then_inc(self.rec_loaded[b], 16)

        with sp.Fori(0, NB // 2) as i:
            batch(2 * i, 0)
            batch(2 * i + 1, 1)

    def gather(self, pool):
        with pool.Fori(0, NB // 2) as i:
            for b in range(2):
                q = 2 * i + b
                pool.wait_ge(self.idx_ready, q + 1)
                pool.wait_ge(self.batch_done, q + 1)
                pool.sem_inc(self.pool_tick, 1)
                for k in range(BATCH):
                    pool.indirect_dma_start(at(self.rows[b], k, self.width), None, self.table,
                                            bass.IndirectOffsetOnAxis(self.idx[b][:, k:k + 1], 0))\
                        .then_inc(self.rows_loaded[b], 16)

    def start_vector(self, dve):
        dve.sem_inc(self.batch_done, 2)

    def column(self, b, c, k=None):
        c -= self.lo
        if k is None:
            return tiled(self.rec[b][:, :], self.n)[:, :, c]
        return self.rec[b][:, k * self.n + c:k * self.n + c + 1]

    def columns(self, b, k, c, w):
        c -= self.lo
        return self.rec[b][:, k * self.n + c:k * self.n + c + w]

    def sources(self, dve, i, b):
        dve.wait_ge(self.rec_loaded[b], i * 16 + 16)
        dve.tensor_copy(self.idx[b][:, :], self.column(b, self.placed.far)).then_inc(self.idx_ready, 1)

    def wait_rows(self, eng, i, b):
        eng.wait_ge(self.rows_loaded[b], i * 16 * BATCH + 16 * BATCH)


def staggered(eng, early, late):
    early(0, 0, 0)
    with eng.Fori(0, NB // 2 - 1) as i:
        early(2 * i + 1, i, 1)
        late(2 * i, i, 0)
        early(2 * i + 2, i + 1, 0)
        late(2 * i + 1, i, 1)
    early(NB - 1, NB // 2 - 1, 1)
    late(NB - 2, NB // 2 - 1, 0)
    late(NB - 1, NB // 2 - 1, 1)


def one_hots(dve, g, net, b, onehot):
    for k in range(BATCH):
        ins = dve.tensor_scalar(at(onehot, k, P), net.columns[:, :], g.column(b, g.placed.near, k), None, ALU.is_equal)
    return ins


def block_of(eng, placed, tile):
    return eng.value_load(placed.block_row[0:1, bass.ds(tile, 1)], min_val=0, max_val=NT - 1)


def l0_gnn_edges(net):
    nc, a = net.nc, net.a
    HC = D // P
    with ExitStack() as ctx:
        s = net.scope("l0e", ctx)
        g = Gather(s, net, net.by_src, net.table(D), D, 0)
        wf1 = s.sb("wf1", [64, D])
        wf2 = s.sb("wf2", [P, HC * D])
        bf1 = s.sb("bf1", [P, HC])
        bf1_ln2 = s.sb("bf1_ln2", [P, HC])
        bf2 = s.sb("bf2", [P, D])
        half = s.sb("half", [P, 1])
        rbfT = s.sb("rbfT", [64, BATCH * P])
        raised = s.sb("raised", [P, HC * BATCH * P])
        hidT = [s.sb(f"hidT{b}", [P, HC * BATCH * P]) for b in range(2)]
        onehot = [s.sb(f"onehot{b}", [P, BATCH * P]) for b in range(2)]
        msg = s.sb("msg", [P, BATCH * D])
        ps_t = s.ps("ps_t", [64, BATCH * P])
        ps_h = s.ps("ps_h", [P, HC * BATCH * P])
        ps_w = s.ps("ps_w", [P, 2, 512])
        ps_s = s.ps("ps_s", [P, 2, 512])
        loaded = s.sem("loaded")
        cleared = s.sem("cleared")
        turned = s.sem("turned")
        rbf_ready = s.sem("rbf_ready")
        hidden = s.sem("hidden")
        raise_step = s.sem("raise_step")
        powered = s.sem("powered")
        hid_ready = s.sem("hid_ready")
        onehot_ready = s.sem("onehot_ready")
        filters = s.sem("filters")
        msg_step = s.sem("msg_step")
        msg_ready = s.sem("msg_ready")
        summed = s.sem("summed")
        added = s.sem("added")
        pe_tick = s.sem("pe_tick")
        block = ctx.enter_context(nc.Block())
        sums = net.work

        @block.sync
        def _(sp):
            sp.dma_start(wf1[:, :], a["L0_gnn_Wf1"]).then_inc(loaded, 16)
            sp.dma_start(wf2[:, :].rearrange("p (c n) -> p c n", c=HC), chunked(a["L0_gnn_Wf2"])).then_inc(loaded, 16)
            for c in range(HC):
                sp.dma_start(bf1[:, c:c + 1], column(a["L0_gnn_bf1"][c * P:(c + 1) * P])).then_inc(loaded, 16)
            sp.dma_start(bf2[:, :], spread(a["L0_gnn_bf2"])).then_inc(loaded, 16)
            g.load(sp)

        @block.gpsimd
        def _(pool):
            g.gather(pool)

        @block.vector
        def _(dve):
            g.start_vector(dve)
            dve.memset(sums[:, 0:NT * D], 0.0).then_inc(cleared, 1)
            dve.memset(half[:, :], 0.5).then_inc(cleared, 1)
            dve.wait_ge(loaded, 80)
            dve.tensor_scalar(bf1_ln2[:, :], bf1[:, :], -LN2, None, ALU.add).then_inc(cleared, 1)
            dve.sem_inc(hid_ready, 1)
            dve.sem_inc(added, 2)
            dve.sem_inc(msg_step, 2)
            dve.wait_ge(cleared, 3)

            def early(q, i, b):
                g.sources(dve, i, b)
                one_hots(dve, g, net, b, onehot[b]).then_inc(onehot_ready, 1)
                dve.wait_ge(hidden, q + 1)
                for c in range(HC):
                    ins = dve.tensor_scalar(at(raised, c, BATCH * P), at(ps_h, c, BATCH * P), bf1[:, c:c + 1], CLAMP,
                                            ALU.add, ALU.min)
                ins.then_inc(raise_step, 1)
                dve.wait_ge(powered, 2 * q + 2)
                for c in range(HC):
                    ins = dve.scalar_tensor_tensor(at(hidT[b], c, BATCH * P), at(ps_h, c, BATCH * P),
                                                   bf1_ln2[:, c:c + 1], at(raised, c, BATCH * P), ALU.add, ALU.max)
                ins.then_inc(hid_ready, 1)

            def late(q, i, b):
                g.wait_rows(dve, i, b)
                for k in range(BATCH):
                    n = q * BATCH + k
                    dve.wait_ge(filters, n + 1)
                    dve.tensor_tensor(at(msg, k, D), ps_w[:, k % 2, 0:D], bf2[:, :], ALU.add).then_inc(msg_step, 1)
                    dve.wait_ge(msg_step, n + 3)
                    dve.scalar_tensor_tensor(at(msg, k, D), at(msg, k, D), g.column(b, g.placed.number, k), at(g.rows[b], k, D),
                                             ALU.mult, ALU.mult).then_inc(msg_ready, 1)
                for k in range(BATCH):
                    n = q * BATCH + k
                    blk = block_of(dve, g.placed, n)
                    dve.wait_ge(summed, n + 1)
                    dve.wait_ge(added, n + 2)
                    dve.tensor_tensor(at(sums, blk, D), at(sums, blk, D), ps_s[:, k % 2, 0:D], ALU.add)\
                        .then_inc(added, 1)
                dve.wait_ge(added, q * BATCH + BATCH + 2)
                dve.sem_inc(g.batch_done, 1)

            staggered(dve, early, late)

        @block.tensor
        def _(pe):
            pe.wait_ge(loaded, 80)

            def early(q, i, b):
                pe.wait_ge(g.rec_loaded[b], i * 16 + 16)
                pe.wait_ge(rbf_ready, q + 1)
                pe.sem_inc(pe_tick, 1)
                for k in range(BATCH):
                    ins = pe.transpose(at(ps_t, k, P), g.columns(b, k, 0, 64), net.ident[:, :])
                ins.then_inc(turned, 1)
                pe.wait_ge(rbf_ready, q + 2)
                pe.wait_ge(hid_ready, q + 1)
                for c in range(HC):
                    ins = pe.matmul(at(ps_h, c, BATCH * P), wf1[:, c * P:(c + 1) * P], rbfT[:, :], start=True, stop=True)
                ins.then_inc(hidden, 1)

            def late(q, i, b):
                pe.wait_ge(hid_ready, q + 2)
                pe.wait_ge(onehot_ready, q + 1)
                for k in range(BATCH):
                    n = q * BATCH + k
                    pe.wait_ge(msg_step, n + 1)
                    for c in range(HC):
                        ins = pe.matmul(ps_w[:, k % 2, 0:D], hidT[b][:, c * BATCH * P + k * P:c * BATCH * P + (k + 1) * P],
                                        wf2[:, c * D:(c + 1) * D], start=c == 0, stop=c == HC - 1)
                    ins.then_inc(filters, 1)
                for k in range(BATCH):
                    n = q * BATCH + k
                    pe.wait_ge(msg_ready, n + 1)
                    pe.wait_ge(added, n + 1)
                    pe.matmul(ps_s[:, k % 2, 0:D], at(onehot[b], k, P), at(msg, k, D), start=True, stop=True)\
                        .then_inc(summed, 1)

            staggered(pe, early, late)

        @block.scalar
        def _(act):
            act.sem_inc(rbf_ready, 1)
            act.wait_ge(cleared, 2)

            def batch(q):
                act.wait_ge(turned, q + 1)
                if not isinstance(q, int):
                    act.wait_ge(hidden, q)
                act.activation(rbfT[:, :], ps_t[:, :], ACT.Copy).then_inc(rbf_ready, 1)
                act.wait_ge(raise_step, q + 1)
                act.activation(raised[:, :], raised[:, :], ACT.Exp).then_inc(powered, 1)
                act.wait_ge(powered, 2 * q + 1)
                act.activation(raised[:, :], raised[:, :], ACT.Ln, bias=half[:, :], scale=0.5).then_inc(powered, 1)

            batch(0)
            with act.Fori(1, NB) as q:
                batch(q)


def l0_gnn_update(net):
    nc, a = net.nc, net.a
    with ExitStack() as ctx:
        s = net.scope("l0u", ctx)
        f = Front(s)
        wo1 = s.sb("wo1", [P, DC * D])
        wo2 = s.sb("wo2", [P, DC * D])
        bo1 = s.sb("bo1", [P, DC])
        bo1_ln2 = s.sb("bo1_ln2", [P, DC])
        bo2 = s.sb("bo2", [P, D])
        half = s.sb("half", [P, 1])
        raised = s.sb("raised", [P, D])
        hidT = s.sb("hidT", [P, D])
        ps_h = s.ps("ps_h", [P, 512])
        ps_m = s.ps("ps_m", [P, 512])
        loaded = s.sem("loaded")
        set_up = s.sem("set_up")
        raise_step = s.sem("raise_step")
        powered = s.sem("powered")
        hid_ready = s.sem("hid_ready")
        updates = s.sem("updates")
        biased = s.sem("biased")
        block = ctx.enter_context(nc.Block())

        @block.sync
        def _(sp):
            for w, into in (("L0_gnn_Wo1", wo1), ("L0_gnn_Wo2", wo2)):
                sp.dma_start(into[:, :].rearrange("p (c n) -> p c n", c=DC), chunked(a[w])).then_inc(loaded, 16)
            for c in range(DC):
                sp.dma_start(bo1[:, c:c + 1], column(a["L0_gnn_bo1"][c * P:(c + 1) * P])).then_inc(loaded, 16)
            sp.dma_start(bo2[:, :], spread(a["L0_gnn_bo2"])).then_inc(loaded, 16)

        @block.vector
        def _(dve):
            link = Chain(dve, set_up)
            dve.wait_ge(loaded, 80)
            link(dve.memset(half[:, :], 0.5))
            link(dve.tensor_scalar(bo1_ln2[:, :], bo1[:, :], -LN2, None, ALU.add))
            with dve.Fori(0, NI) as i:
                for k in range(UN):
                    t = i * UN + k
                    f.take(dve, t, k, lambda xn: dve.tensor_copy(xn, at(net.work, t, D)))
                    dve.wait_ge(f.projected, UN + t + 1)
                    for c in range(DC):
                        ins = dve.tensor_scalar(at(raised, c, P), at(ps_h, c, P), bo1[:, c:c + 1], CLAMP, ALU.add, ALU.min)
                    ins.then_inc(raise_step, 1)
                    dve.wait_ge(powered, 2 * t + 2)
                    for c in range(DC):
                        ins = dve.scalar_tensor_tensor(at(hidT, c, P), at(ps_h, c, P), bo1_ln2[:, c:c + 1],
                                                       at(raised, c, P), ALU.add, ALU.max)
                    ins.then_inc(hid_ready, 1)
                    dve.tensor_tensor(at(net.x, t, D), at(net.x, t, D), bo2[:, :], ALU.add).then_inc(biased, 1)
                    dve.wait_ge(updates, t + 1)
                    dve.wait_ge(biased, 2 * t + 1)
                    dve.tensor_tensor(at(net.x, t, D), at(net.x, t, D), ps_m[:, 0:D], ALU.add).then_inc(biased, 1)

        @block.tensor
        def _(pe):
            f.start_tensor(pe)
            pe.wait_ge(loaded, 80)
            with pe.Fori(0, NI) as i:
                for k in range(UN):
                    t = i * UN + k
                    f.turn(pe, net, t, k)
                    pe.wait_ge(f.xT_ready, UN + t + 1)
                    for m in range(DC):
                        for c in range(DC):
                            ins = pe.matmul(at(ps_h, m, P), wo1[:, c * D + m * P:c * D + (m + 1) * P], f.lhsT(k, c),
                                            start=c == 0, stop=c == DC - 1)
                    ins.then_inc(f.projected, 1)
                    pe.wait_ge(hid_ready, t + 1)
                    for c in range(DC):
                        ins = pe.matmul(ps_m[:, 0:D], at(hidT, c, P), at(wo2, c, D), start=c == 0, stop=c == DC - 1)
                    ins.then_inc(updates, 1)

        @block.scalar
        def _(act):
            f.start_scalar(act)
            act.wait_ge(set_up, 1)
            with act.Fori(0, NI) as i:
                for k in range(UN):
                    t = i * UN + k
                    f.keep(act, t, k)
                    act.wait_ge(raise_step, t + 1)
                    act.activation(raised[:, :], raised[:, :], ACT.Exp).then_inc(powered, 1)
                    act.wait_ge(powered, 2 * t + 1)
                    act.activation(raised[:, :], raised[:, :], ACT.Ln, bias=half[:, :], scale=0.5).then_inc(powered, 1)


GROUP = UN * P
PART = GROUP // 2


def turn_rows(pe, net, out, rows):
    return pe.transpose(out, rows, net.ident[0:rows.shape[0], 0:rows.shape[0]])


def moe(net, name, router, bias, choose, layers, last, last_bias, keeps_tokens=False, guarded=False):
    nc, a = net.nc, net.a
    with ExitStack() as ctx:
        s = net.scope(name, ctx)
        xT = s.sb("xT", [P, DC * NP])
        logits = s.sb("logits", [P, NT * EXPERTS])
        mix = s.sb("mix", [P, NT * EXPERTS])
        acc = net.work if guarded else net.x
        moe_front(net, name, xT, logits, router, keeps_tokens, guarded)
        choose(net, name, logits, bias, mix)
        moe_bias(net, name, mix, a[last_bias], acc)
        moe_experts(net, name, xT, mix, acc, layers, a[last])
        if guarded:
            add_guarded(net, name)


def moe_front(net, name, xT, logits, router, keeps_tokens, clears_work):
    nc, a = net.nc, net.a
    by_expert = router.shape[0] == EXPERTS
    with ExitStack() as ctx:
        s = net.scope(name + "f", ctx)
        f = Front(s)
        rows = s.sb("rows", [EXPERTS, D])
        w = s.sb("w", [P, DC * EXPERTS])
        ps = s.ps("ps", [P, 2, 512])
        w_loaded = s.sem("w_loaded")
        w_turned = s.sem("w_turned")
        w_ready = s.sem("w_ready")
        copied = s.sem("copied")
        logits_ready = s.sem("logits_ready")
        pool_tick = s.sem("pool_tick")
        block = ctx.enter_context(nc.Block())
        wv = w[:, :].rearrange("p (c n) -> p c n", c=DC)

        @block.sync
        def _(sp):
            if by_expert:
                sp.dma_start(rows[:, :], router).then_inc(w_loaded, 16)
            else:
                sp.dma_start(wv, chunked(router)).then_inc(w_loaded, 16)

        @block.gpsimd
        def _(pool):
            pool.sem_inc(copied, UN)
            with pool.Fori(0, NI) as i:
                for k in range(UN):
                    t = i * UN + k
                    pool.wait_ge(f.xT_ready, UN + t + 1)
                    pool.sem_inc(pool_tick, 1)
                    for c in range(DC):
                        ins = pool.tensor_copy(xT[:, bass.ds(c * NP + t * P, P)], f.lhsT(k, c))
                    ins.then_inc(copied, 1)

        @block.vector
        def _(dve):
            dve.sem_inc(logits_ready, UN)
            if clears_work:
                dve.memset(net.work[:, 0:NT * D], 0.0)
            dve.wait_ge(w_loaded, 16)
            if by_expert:
                dve.wait_ge(w_turned, 1)
                dve.tensor_copy(w[:, :], ps[:, 0, 0:DC * EXPERTS]).then_inc(w_ready, 1)
            else:
                dve.sem_inc(w_ready, 1)
            with dve.Fori(0, NI) as i:
                f.moments_of(dve, net, i)
                for k in range(UN):
                    t = i * UN + k
                    f.normalize(dve, net, i, k)
                for k in range(UN):
                    t = i * UN + k
                    if keeps_tokens:
                        dve.wait_ge(f.normed, t + 1)
                        dve.tensor_tensor(at(net.x, t, D), at(net.x, t, D), at(f.xn, k, D), ALU.add)
                    dve.wait_ge(f.projected, UN + t + 1)
                    dve.tensor_copy(at(logits, t, EXPERTS), ps[:, k % 2, 0:EXPERTS]).then_inc(logits_ready, 1)

        @block.tensor
        def _(pe):
            f.start_tensor(pe)
            if by_expert:
                pe.wait_ge(w_loaded, 16)
                for c in range(DC):
                    ins = turn_rows(pe, net, ps[:, 0, c * EXPERTS:(c + 1) * EXPERTS], rows[:, c * P:(c + 1) * P])
                ins.then_inc(w_turned, 1)
            pe.wait_ge(w_ready, 1)
            with pe.Fori(0, NI) as i:
                for k in range(UN):
                    t = i * UN + k
                    f.turn(pe, net, t, k)
                    pe.wait_ge(f.xT_ready, UN + t + 1)
                    pe.wait_ge(logits_ready, bank_free(t, k))
                    f.project(pe, t, k, ps[:, k % 2, 0:EXPERTS], wv)

        @block.scalar
        def _(act):
            f.start_scalar(act)
            with act.Fori(0, NI) as i:
                f.root(act, net, i)
                for k in range(UN):
                    t = i * UN + k
                    act.wait_ge(copied, t + 1)
                    f.keep(act, t, k)


def by_expert(t):
    return tiled(t[:, :], EXPERTS)


def over_experts(t):
    return t[:, :].unsqueeze(2).to_broadcast([P, NT, EXPERTS])


def first_best(dve, link, net, vals, best, onehot, score, top):
    link(dve.tensor_reduce(best[:, :], by_expert(vals), AX.X, ALU.max))
    link(dve.tensor_tensor(by_expert(score), by_expert(vals), over_experts(best), ALU.is_equal))
    link(dve.tensor_tensor(by_expert(score), by_expert(score), by_expert(net.rank8), ALU.mult))
    link(dve.tensor_reduce(top[:, :], by_expert(score), AX.X, ALU.max))
    link(dve.tensor_tensor(by_expert(onehot), by_expert(score), over_experts(top), ALU.is_equal))


def softmax_experts(dve, link, act_exp, vals, best, out, total):
    link(dve.tensor_reduce(best[:, :], by_expert(vals), AX.X, ALU.max))
    link(dve.tensor_tensor(by_expert(out), by_expert(vals), over_experts(best), ALU.subtract))
    act_exp()
    link(dve.tensor_reduce(total[:, :], by_expert(out), AX.X, ALU.add))
    link(dve.reciprocal(total[:, :], total[:, :]))
    link(dve.tensor_tensor(by_expert(out), by_expert(out), over_experts(total), ALU.mult))


def choose(kind):
    def stage(net, name, logits, bias, mix):
        nc = net.nc
        with ExitStack() as ctx:
            s = net.scope(name + "c", ctx)
            lg = s.sb("lg", [P, NT * EXPERTS])
            bias_row = s.sb("bias_row", [P, EXPERTS])
            probs = s.sb("probs", [P, NT * EXPERTS])
            score = s.sb("score", [P, NT * EXPERTS])
            one = s.sb("one", [P, NT * EXPERTS])
            two = s.sb("two", [P, NT * EXPERTS])
            rest = s.sb("rest", [P, NT * EXPERTS])
            ones_row = s.sb("ones_row", [P, NT])
            best = s.sb("best", [P, NT])
            second = s.sb("second", [P, NT])
            total = s.sb("total", [P, NT])
            top = s.sb("top", [P, NT])
            ps = s.ps("ps", [P, 2, 512])
            loaded = s.sem("loaded")
            chain = s.sem("chain")
            to_power = s.sem("to_power")
            powered = s.sem("powered")
            one_ready = s.sem("one_ready")
            counted = s.sem("counted")
            block = ctx.enter_context(nc.Block())

            @block.sync
            def _(sp):
                if bias is not None:
                    sp.dma_start(bias_row[:, :], spread(bias)).then_inc(loaded, 16)

            @block.scalar
            def _(act):
                power = {"probs": probs, "pair": total, "all": probs, "capacity": probs}[kind]
                act.wait_ge(to_power, 1)
                act.activation(power[:, :], power[:, :], ACT.Exp).then_inc(powered, 1)

            @block.tensor
            def _(pe):
                if kind == "capacity":
                    pe.wait_ge(one_ready, 1)
                    pe.matmul(ps[:, 0, 0:NT * EXPERTS], net.before[:, :], one[:, :], start=True, stop=True)
                    pe.matmul(ps[:, 1, 0:NT * EXPERTS], net.ones[:, :], one[:, :], start=True, stop=True)\
                        .then_inc(counted, 1)

            @block.vector
            def _(dve):
                link = Chain(dve, chain)

                def act_exp():
                    dve.sem_inc(to_power, 1)
                    dve.wait_ge(powered, 1)

                if bias is None:
                    link(dve.tensor_copy(lg[:, :], logits[:, :]))
                else:
                    dve.wait_ge(loaded, 16)
                    link(dve.tensor_tensor(by_expert(lg), by_expert(logits),
                                           bias_row[:, :].unsqueeze(1).to_broadcast([P, NT, EXPERTS]), ALU.add))
                if kind == "all":
                    softmax_experts(dve, link, act_exp, lg, best, probs, total)
                    link(dve.tensor_copy(mix[:, :], probs[:, :]))
                    return
                vals = lg
                if kind != "pair":
                    softmax_experts(dve, link, act_exp, lg, best, probs, total)
                    vals = probs
                first_best(dve, link, net, vals, best, one, score, top)
                if kind == "capacity":
                    dve.sem_inc(one_ready, 1)
                    dve.wait_ge(counted, 1)
                    link(dve.memset(ones_row[:, :], 1.0))
                    link(dve.tensor_copy(score[:, :], ps[:, 1, 0:NT * EXPERTS]))
                    for e in range(EXPERTS):
                        link(dve.tensor_tensor_scan(by_expert(rest)[:, :, e], ones_row[:, :], by_expert(score)[:, :, e],
                                                    0.0, ALU.mult, ALU.add))
                    link(dve.tensor_tensor(rest[:, :], rest[:, :], score[:, :], ALU.subtract))
                    link(dve.tensor_tensor(rest[:, :], rest[:, :], ps[:, 0, 0:NT * EXPERTS], ALU.add))
                    link(dve.tensor_scalar(rest[:, :], rest[:, :], float(CAPACITY), None, ALU.is_lt))
                    link(dve.tensor_tensor(one[:, :], one[:, :], rest[:, :], ALU.mult))
                    link(dve.tensor_tensor(by_expert(mix), by_expert(one), over_experts(best), ALU.mult))
                    return
                link(dve.scalar_tensor_tensor(rest[:, :], one[:, :], -HUGE, vals[:, :], ALU.mult, ALU.add))
                first_best(dve, link, net, rest, second, two, score, top)
                if kind == "pair":
                    link(dve.tensor_tensor(total[:, :], second[:, :], best[:, :], ALU.subtract))
                    act_exp()
                    link(dve.tensor_copy(second[:, :], total[:, :]))
                    link(dve.memset(best[:, :], 1.0))
                    link(dve.tensor_scalar(total[:, :], total[:, :], 1.0, None, ALU.add))
                else:
                    link(dve.tensor_tensor(total[:, :], best[:, :], second[:, :], ALU.add))
                    link(dve.tensor_scalar(total[:, :], total[:, :], 1e-12, None, ALU.max))
                link(dve.reciprocal(total[:, :], total[:, :]))
                link(dve.tensor_tensor(best[:, :], best[:, :], total[:, :], ALU.mult))
                link(dve.tensor_tensor(second[:, :], second[:, :], total[:, :], ALU.mult))
                link(dve.tensor_tensor(by_expert(one), by_expert(one), over_experts(best), ALU.mult))
                link(dve.tensor_tensor(by_expert(two), by_expert(two), over_experts(second), ALU.mult))
                link(dve.tensor_tensor(mix[:, :], one[:, :], two[:, :], ALU.add))
    return stage


def moe_bias(net, name, mix, bias, acc):
    nc = net.nc
    with ExitStack() as ctx:
        s = net.scope(name + "b", ctx)
        rows = s.sb("rows", [EXPERTS, D])
        own = s.sb("own", [P, 2 * EXPERTS])
        ownT = s.sb("ownT", [EXPERTS, 2 * P])
        ps_t = s.ps("ps_t", [EXPERTS, 2, 512])
        ps = s.ps("ps", [P, 2, 512])
        loaded = s.sem("loaded")
        taken = s.sem("taken")
        turned = s.sem("turned")
        kept = s.sem("kept")
        biases = s.sem("biases")
        added = s.sem("added")
        s_tick = s.sem("tick")
        block = ctx.enter_context(nc.Block())

        @block.sync
        def _(sp):
            sp.dma_start(rows[:, :], bias).then_inc(loaded, 16)

        @block.vector
        def _(dve):
            with dve.Fori(0, NT) as t:
                dve.tensor_copy(own[:, 0:EXPERTS], at(mix, t, EXPERTS)).then_inc(taken, 1)
                dve.wait_ge(biases, t + 1)
                dve.tensor_tensor(at(acc, t, D), at(acc, t, D), ps[:, 0, 0:D], ALU.add).then_inc(added, 1)

        @block.tensor
        def _(pe):
            pe.wait_ge(loaded, 16)
            with pe.Fori(0, NT) as t:
                pe.wait_ge(taken, t + 1)
                pe.sem_inc(s_tick, 1)
                pe.transpose(ps_t[:, 0, 0:P], own[:, 0:EXPERTS], net.ident[:, :]).then_inc(turned, 1)
                pe.wait_ge(kept, t + 1)
                pe.matmul(ps[:, 0, 0:D], ownT[:, 0:P], rows[:, :], start=True, stop=True).then_inc(biases, 1)

        @block.scalar
        def _(act):
            with act.Fori(0, NT) as t:
                act.wait_ge(turned, t + 1)
                act.activation(ownT[:, 0:P], ps_t[:, 0, 0:P], ACT.Copy).then_inc(kept, 1)


def moe_experts(net, name, xT, mix, acc, layers, last):
    nc, a = net.nc, net.a
    widths = [DC] + [a[w].shape[2] // P for w, _, _ in layers]
    halves = [2 * n for n in widths[1:]]
    starts = [sum(halves[:l]) for l in range(len(layers) + 1)]
    H = starts[-1]
    assert all(n % 4 == 0 for n in halves)
    with ExitStack() as ctx:
        s = net.scope(name + "e", ctx)
        w_in = [[s.sb(f"w{l}_{b}", [P, widths[l] * widths[l + 1] * P]) for b in range(2)] for l in range(len(layers))]
        w_out = [s.sb(f"wo_{b}", [P, widths[-1] * D]) for b in range(2)]
        hT = [s.sb(f"hT{l}", [P, widths[l + 1] * GROUP]) for l in range(len(layers))]
        vec_rows = [[s.sb(f"vr{l}_{v}", [EXPERTS * widths[l + 1], P]) for v in range(len(vs))]
                    for l, (_, vs, _) in enumerate(layers)]
        vec = [[s.sb(f"v{l}_{v}", [P, EXPERTS * widths[l + 1]]) for v in range(len(vs))]
               for l, (_, vs, _) in enumerate(layers)]
        own = [[s.sb(f"own{l}_{v}", [P, widths[l + 1]]) for v in range(min(2, len(vs)))]
               for l, (_, vs, _) in enumerate(layers)]
        ps_h = s.ps("ps_h", [P, 4, 512])
        ps_y = s.ps("ps_y", [P, 4, 512])
        vec_loaded = s.sem("vec_loaded")
        vec_turned = s.sem("vec_turned")
        vec_step = s.sem("vec_step")
        vec_rooted = s.sem("vec_rooted")
        vec_ready = s.sem("vec_ready")
        w_loaded = [s.sem(f"w_loaded{b}") for b in range(2)]
        products = s.sem("products")
        active = s.sem("active")
        outs = s.sem("outs")
        own_ready = s.sem("own_ready")
        pe_tick = s.sem("pe_tick")
        act_tick = s.sem("act_tick")
        mixed = s.sem("mixed")
        block = ctx.enter_context(nc.Block())
        vectors = [(l, v) for l, (_, vs, _) in enumerate(layers) for v in range(len(vs))]
        WL = 16 * (len(layers) + 1)

        def load(sp, e, b):
            for l, (w, _, _) in enumerate(layers):
                k, n = a[w].shape[1], a[w].shape[2]
                flat = a[w].rearrange("e k n -> (e k) n")[bass.ds(e * k, k), :]
                sp.dma_start(w_in[l][b][:, :].rearrange("p (c n) -> p c n", n=n), chunked(flat)).then_inc(w_loaded[b], 16)
            k = last.shape[1]
            flat = last.rearrange("e k n -> (e k) n")[bass.ds(e * k, k), :]
            sp.dma_start(tiled(w_out[b][:, :], D), chunked(flat)).then_inc(w_loaded[b], 16)

        @block.sync
        def _(sp):
            for l, v in vectors:
                sp.dma_start(vec_rows[l][v][:, :], a[layers[l][1][v]].rearrange("e (c p) -> (e c) p", p=P))\
                    .then_inc(vec_loaded, 16)
            for b in range(2):
                load(sp, b, b)
            with sp.Fori(1, EXPERTS // 2) as i:
                for b in range(2):
                    sp.wait_ge(outs, UN + (2 * i + b - 1) * NT)
                    load(sp, 2 * i + b, b)

        @block.tensor
        def _(pe):
            pe.sem_inc(outs, UN)
            pe.wait_ge(vec_loaded, 16 * len(vectors))
            for n, (l, v) in enumerate(vectors):
                turn_rows(pe, net, ps_h[:, n % 4, 64 * (n // 4):64 * (n // 4) + EXPERTS * widths[l + 1]],
                          vec_rows[l][v][:, :]).then_inc(vec_turned, 1)
            pe.wait_ge(vec_ready, 1)

            def expert(i, e, b):
                pe.wait_ge(w_loaded[b], i * WL + WL)
                pe.sem_inc(pe_tick, 1)
                with pe.Fori(0, NI) as g:
                    q = e * NI + g
                    for l in range(len(layers)):
                        for c in range(halves[l]):
                            m, half = c // 2, c % 2
                            n = starts[l] + c
                            if l and c == 0:
                                pe.wait_ge(active, q * H + starts[l] + 4)
                            pe.wait_ge(active, q * H + n + 1)
                            for k in range(widths[l]):
                                rhs = xT[:, bass.ds(k * NP + g * GROUP + half * PART, PART)] if l == 0 else \
                                    hT[l - 1][:, k * GROUP + half * PART:k * GROUP + (half + 1) * PART]
                                lo = (k * widths[l + 1] + m) * P
                                ins = pe.matmul(ps_h[:, c % 4, 0:PART], w_in[l][b][:, lo:lo + P], rhs,
                                                start=k == 0, stop=k == widths[l] - 1)
                            ins.then_inc(products, 1)
                    pe.wait_ge(active, q * H + H + 4)
                    for j in range(UN):
                        n = q * UN + j
                        pe.wait_ge(mixed, n + {0: UN, 4: 2}.get(j, 1))
                        for k in range(widths[-1]):
                            ins = pe.matmul(ps_y[:, j % 4, 0:D], hT[-1][:, k * GROUP + j * P:k * GROUP + (j + 1) * P],
                                            at(w_out[b], k, D), start=k == 0, stop=k == widths[-1] - 1)
                        ins.then_inc(outs, 1)

            with pe.Fori(0, EXPERTS // 2) as i:
                for b in range(2):
                    expert(i, 2 * i + b, b)

        @block.scalar
        def _(act):
            act.sem_inc(active, 4)
            for l, (_, vs, _) in enumerate(layers):
                if len(vs) > 1:
                    act.wait_ge(vec_step, len(vectors))
                    act.activation(vec[l][4][:, :], vec[l][4][:, :], ACT.Sqrt).then_inc(vec_rooted, 1)
            act.wait_ge(vec_ready, 1)

            with act.Fori(0, EXPERTS // 2) as i:
                for b in range(2):
                    e = 2 * i + b
                    act.wait_ge(active, e * NI * H + 4)
                    act.sem_inc(act_tick, 1)
                    copies = [act.activation(own[l][v][:, :], at(vec[l][v], e, widths[l + 1]), ACT.Copy)
                              for l in range(len(layers)) for v in range(len(own[l]))]
                    copies[-1].then_inc(own_ready, 1)
                    act.wait_ge(own_ready, e + 1)
                    act.sem_inc(act_tick, 1)
                    with act.Fori(0, NI) as g:
                        q = e * NI + g
                        act.wait_ge(outs, q * UN + UN)
                        for l, (_, vs, func) in enumerate(layers):
                            for c in range(halves[l]):
                                m, half = c // 2, c % 2
                                act.wait_ge(products, q * H + starts[l] + c + 1)
                                act.activation(hT[l][:, m * GROUP + half * PART:m * GROUP + (half + 1) * PART],
                                               ps_h[:, c % 4, 0:PART], func,
                                               bias=own[l][0][:, m:m + 1],
                                               scale=own[l][1][:, m:m + 1] if len(vs) > 1 else 1.0)\
                                    .then_inc(active, 1)

        @block.vector
        def _(dve):
            dve.sem_inc(mixed, UN)
            link = Chain(dve, vec_step)
            dve.wait_ge(vec_turned, len(vectors))
            for n, (l, v) in enumerate(vectors):
                from_ps = ps_h[:, n % 4, 64 * (n // 4):64 * (n // 4) + EXPERTS * widths[l + 1]]
                if v == 4:
                    link(dve.tensor_scalar(vec[l][v][:, :], from_ps, BN_EPS, None, ALU.add))
                else:
                    link(dve.tensor_copy(vec[l][v][:, :], from_ps))
            if any(len(vs) > 1 for _, vs, _ in layers):
                dve.wait_ge(vec_rooted, len(layers))
            for l, (_, vs, _) in enumerate(layers):
                if len(vs) > 1:
                    bias, gain, shift, mean, var = (t[:, :] for t in vec[l])
                    link(dve.reciprocal(var, var))
                    link(dve.tensor_tensor(gain, gain, var, ALU.mult))
                    link(dve.tensor_tensor(bias, bias, mean, ALU.subtract))
                    link(dve.tensor_tensor(bias, bias, gain, ALU.mult))
                    link(dve.tensor_tensor(bias, bias, shift, ALU.add))
            dve.sem_inc(vec_ready, 1)

            with dve.Fori(0, EXPERTS) as e:
                with dve.Fori(0, NI) as g:
                    for j in range(UN):
                        t = g * UN + j
                        n = e * NT + t
                        dve.wait_ge(outs, UN + n + 1)
                        dve.wait_ge(mixed, n + 1)
                        dve.scalar_tensor_tensor(at(acc, t, D), ps_y[:, j % 4, 0:D], at(mix, t * EXPERTS + e, 1),
                                                 at(acc, t, D), ALU.mult, ALU.add).then_inc(mixed, 1)


def add_guarded(net, name):
    nc = net.nc
    LARGEST = float(np.finfo(np.float32).max)
    with ExitStack() as ctx:
        s = net.scope(name + "g", ctx)
        y = net.work[:, 0:NT * D]
        flag = s.sb("flag", [P, NT * D], mybir.dt.uint8)
        fixed = s.sb("fixed", [P, 1])
        chain = s.sem("chain")
        block = ctx.enter_context(nc.Block())

        @block.vector
        def _(dve):
            link = Chain(dve, chain)
            link(dve.tensor_scalar(flag[:, :], y, LARGEST, None, ALU.is_gt))
            for value, test in ((1e4, None), (-1e4, lambda: dve.tensor_scalar(flag[:, :], y, -LARGEST, None, ALU.is_lt)),
                                (0.0, lambda: dve.tensor_tensor(flag[:, :], y, y, ALU.not_equal))):
                if test:
                    link(test())
                link(dve.memset(fixed[:, :], value))
                link(dve.copy_predicated(y, flag[:, :], fixed[:, :].to_broadcast([P, NT * D])))
            link(dve.tensor_tensor(net.x[:, :], net.x[:, :], y, ALU.add))


BN_EPS = 1e-3
CAPACITY = max(1, -(-5 * N // (4 * EXPERTS)))


def l0_ffn(net):
    moe(net, "l0f", net.a["L0_ffn_router_w"], None, choose("probs"),
        [("L0_ffn_w1", ("L0_ffn_b1",), ACT.Gelu)], "L0_ffn_w2", "L0_ffn_b2", keeps_tokens=True)


def l1_ffn(net):
    moe(net, "l1f", net.a["L1_ffn_Wg"], net.a["L1_ffn_bg"], choose("pair"),
        [("L1_ffn_W1", ("L1_ffn_b1",), ACT.Gelu)], "L1_ffn_W2", "L1_ffn_b2")


def l2_ffn(net):
    def names(n):
        return tuple(f"L2_ffn_{v}{n}" for v in ("b", "g", "be", "m", "v"))

    moe(net, "l2f", net.a["L2_ffn_Wr"], net.a["L2_ffn_br"], choose("all"),
        [("L2_ffn_W1", names(1), ACT.Relu), ("L2_ffn_W2", names(2), ACT.Relu)], "L2_ffn_Wo", "L2_ffn_bo")


def l3_ffn(net):
    moe(net, "l3f", net.a["L3_ffn_gate_w"], net.a["L3_ffn_gate_b"], choose("capacity"),
        [("L3_ffn_w1", ("L3_ffn_b1",), ACT.Relu)], "L3_ffn_w2", "L3_ffn_b2", guarded=True)


def edge_means(net):
    nc = net.nc
    placed = net.by_dst
    lo = placed.first["edge_attr_16"]
    W = 17
    with ExitStack() as ctx:
        s = net.scope("means", ctx)
        n = placed.width - lo
        rec = [s.sb(f"rec{b}", [P, BATCH * n]) for b in range(2)]
        onehot = [s.sb(f"onehot{b}", [P, BATCH * P]) for b in range(2)]
        found = s.sb("found", [P, NT])
        root = s.sb("root", [P, NT])
        ps = s.ps("ps", [P, 2, 512])
        loaded = [s.sem(f"loaded{b}") for b in range(2)]
        onehot_ready = s.sem("onehot_ready")
        summed = s.sem("summed")
        added = s.sem("added")
        batch_done = s.sem("batch_done")
        chain = s.sem("chain")
        to_root = s.sem("to_root")
        rooted = s.sem("rooted")
        block = ctx.enter_context(nc.Block())
        work = net.work[:, 0:NT * W]

        @block.sync
        def _(sp):
            with sp.Fori(0, NB // 2) as i:
                for b in range(2):
                    sp.wait_ge(batch_done, 2 * i + b + 1)
                    sp.dma_start(tiled(rec[b][:, :], n), batch_records(placed.records, 2 * i + b, lo, placed.width))\
                        .then_inc(loaded[b], 16)

        @block.tensor
        def _(pe):
            with pe.Fori(0, NB // 2) as i:
                for b in range(2):
                    q = 2 * i + b
                    pe.wait_ge(onehot_ready, q + 1)
                    pe.wait_ge(batch_done, q + 1)
                    for k in range(BATCH):
                        ins = pe.matmul(at(ps[:, b, :], k, W), at(onehot[b], k, P), rec[b][:, k * n:k * n + W],
                                        start=True, stop=True)
                    ins.then_inc(summed, 1)

        @block.scalar
        def _(act):
            act.wait_ge(to_root, 1)
            act.activation(root[:, :], root[:, :], ACT.Sqrt).then_inc(rooted, 1)

        @block.vector
        def _(dve):
            link = Chain(dve, chain)
            dve.sem_inc(batch_done, 2)
            link(dve.memset(work, 0.0))

            def hot(i, b):
                dve.wait_ge(loaded[b], i * 16 + 16)
                for k in range(BATCH):
                    c = k * n + placed.near - lo
                    ins = dve.tensor_scalar(at(onehot[b], k, P), net.columns[:, :], rec[b][:, c:c + 1], None, ALU.is_equal)
                ins.then_inc(onehot_ready, 1)

            def add(q, b):
                dve.wait_ge(summed, q + 1)
                for k in range(BATCH):
                    blk = block_of(dve, placed, q * BATCH + k)
                    if k or not (isinstance(q, int) and q == 0):
                        dve.wait_ge(added, q * BATCH + k)
                    dve.tensor_tensor(at(net.work, blk, W), at(net.work, blk, W), at(ps[:, b, :], k, W), ALU.add)\
                        .then_inc(added, 1)
                dve.wait_ge(added, q * BATCH + BATCH)
                dve.sem_inc(batch_done, 1)

            hot(0, 0)
            hot(0, 1)
            add(0, 0)
            add(1, 1)
            with dve.Fori(1, NB // 2) as i:
                hot(i, 0)
                hot(i, 1)
                add(2 * i, 0)
                add(2 * i + 1, 1)
            sums = tiled(work, W)
            link(dve.tensor_scalar(found[:, :], sums[:, :, 16], 1.0, None, ALU.max))
            link(dve.reciprocal(found[:, :], found[:, :]))
            link(dve.tensor_tensor(tiled(net.mean16[:, :], 16), sums[:, :, 0:16],
                                   found[:, :].unsqueeze(2).to_broadcast([P, NT, 16]), ALU.mult))
            link(dve.tensor_scalar(root[:, :], sums[:, :, 16], 1.0, None, ALU.add))
            dve.sem_inc(to_root, 1)
            dve.wait_ge(rooted, 1)
            link(dve.reciprocal(net.dinv[:, :], root[:, :]))


def gat_edges(net, name, g, heads, each, acc, top, setup_logits):
    nc = net.nc
    KH = BATCH * heads
    W = heads * (each + 1)
    with ExitStack() as ctx:
        s = net.scope(name, ctx)
        onehot = [s.sb(f"onehot{b}", [P, BATCH * P]) for b in range(2)]
        nodehot = [s.sb(f"nodehot{b}", [P, BATCH * P]) for b in range(2)]
        outside = [s.sb(f"outside{b}", [P, BATCH * P]) for b in range(2)]
        logit = s.sb("logit", [P, KH])
        masked = s.sb("masked", [P, 2 * heads * P])
        tile_top = s.sb("tile_top", [P, KH])
        new_top = s.sb("new_top", [P, KH])
        shrink = s.sb("shrink", [P, KH])
        power = s.sb("power", [P, KH])
        weighted = s.sb("weighted", [P, BATCH * W])
        ps_hot = s.ps("ps_hot", [P, BATCH * P])
        ps_x = s.ps("ps_x", [P, 2, 512])
        ps_row = s.ps("ps_row", [P, 2, 512])
        ps_top = s.ps("ps_top", [P, 512])
        onehot_ready = s.sem("onehot_ready")
        hot_turned = s.sem("hot_turned")
        nodehot_ready = s.sem("nodehot_ready")
        outside_ready = s.sem("outside_ready")
        logit_ready = s.sem("logit_ready")
        rows_turned = s.sem("rows_turned")
        topped = s.sem("topped")
        top_step = s.sem("top_step")
        shrink_ready = s.sem("shrink_ready")
        spread_top = s.sem("spread_top")
        power_step = s.sem("power_step")
        powered = s.sem("powered")
        filled = s.sem("filled")
        weighted_ready = s.sem("weighted_ready")
        summed = s.sem("summed")
        scaled = s.sem("scaled")
        added = s.sem("added")
        tick = s.sem("tick")
        logits = setup_logits(s, g, ps_x, nodehot, logit, logit_ready, added, nodehot_ready)
        block = ctx.enter_context(nc.Block())
        by_head = lambda ap, n: ap.rearrange("p (h c) -> p h c", c=n)

        @block.sync
        def _(sp):
            logits.load(sp)
            g.load(sp)

        @block.gpsimd
        def _(pool):
            g.gather(pool)

        @block.vector
        def _(dve):
            g.start_vector(dve)
            dve.sem_inc(outside_ready, 1)
            dve.sem_inc(topped, 2)
            dve.sem_inc(added, 2)
            logits.start_vector(dve)

            def early(q, i, b):
                g.sources(dve, i, b)
                one_hots(dve, g, net, b, onehot[b]).then_inc(onehot_ready, 1)
                dve.wait_ge(nodehot_ready, q + 1)
                dve.tensor_scalar(outside[b][:, :], ps_hot[:, :], HUGE, -HUGE, ALU.mult, ALU.add)\
                    .then_inc(outside_ready, 1)

            def late(q, i, b):
                g.wait_rows(dve, i, b)
                logits.vector(dve, q, i, b)
                for k in range(BATCH):
                    n = q * BATCH + k
                    dve.wait_ge(rows_turned, n + 1)
                    dve.wait_ge(topped, n + 1)
                    dve.sem_inc(tick, 1)
                    for h in range(heads):
                        c = k * heads + h
                        ins = dve.tensor_tensor_reduce(at(masked, k % 2 * heads + h, P), at(ps_row[:, k % 2, :], h, P), at(outside[b], k, P),
                                                       1.0, -HUGE, ALU.add, ALU.max, tile_top[:, c:c + 1])
                    ins.then_inc(topped, 1)
                for k in range(BATCH):
                    n = q * BATCH + k
                    blk = block_of(dve, g.placed, n)
                    dve.wait_ge(topped, n + 3)
                    dve.wait_ge(top_step, 3 * n) if k or not isinstance(q, int) or q else None
                    dve.tensor_tensor(at(new_top, k, heads), at(top, blk, heads), at(tile_top, k, heads), ALU.max)\
                        .then_inc(top_step, 1)
                    dve.wait_ge(top_step, 3 * n + 1)
                    dve.tensor_tensor(at(shrink, k, heads), at(top, blk, heads), at(new_top, k, heads), ALU.subtract)\
                        .then_inc(top_step, 1)
                    dve.wait_ge(top_step, 3 * n + 2)
                    dve.sem_inc(tick, 1)
                    dve.tensor_copy(at(top, blk, heads), at(new_top, k, heads)).then_inc(top_step, 1)
                dve.wait_ge(top_step, 3 * (q * BATCH + BATCH))
                dve.sem_inc(shrink_ready, 1)
                dve.wait_ge(spread_top, q + 1)
                dve.tensor_tensor(power[:, :], logit[:, :], ps_top[:, 0:KH], ALU.subtract).then_inc(power_step, 1)
                dve.wait_ge(power_step, 2 * q + 1)
                dve.tensor_scalar(power[:, :], power[:, :], 0.0, None, ALU.min).then_inc(power_step, 1)
                dve.wait_ge(powered, 2 * q + 2)
                for k in range(BATCH):
                    rows = at(g.rows[b], k, g.width)[:, 0:heads * each]
                    dve.tensor_tensor(by_head(at(weighted, k, W), each + 1)[:, :, 0:each], by_head(rows, each),
                                      at(power, k, heads).unsqueeze(2).to_broadcast([P, heads, each]), ALU.mult)\
                        .then_inc(weighted_ready, 1)
                for k in range(BATCH):
                    n = q * BATCH + k
                    blk = block_of(dve, g.placed, n)
                    dve.wait_ge(added, n + 2)
                    dve.tensor_tensor(by_head(at(acc, blk, W), each + 1), by_head(at(acc, blk, W), each + 1),
                                      at(shrink, k, heads).unsqueeze(2).to_broadcast([P, heads, each + 1]), ALU.mult)\
                        .then_inc(scaled, 1)
                    dve.wait_ge(scaled, n + 1)
                    dve.wait_ge(summed, n + 1)
                    dve.tensor_tensor(at(acc, blk, W), at(acc, blk, W), ps_x[:, k % 2, 0:W], ALU.add).then_inc(added, 1)
                dve.wait_ge(added, q * BATCH + BATCH + 2)
                dve.sem_inc(g.batch_done, 1)

            staggered(dve, early, late)

        @block.tensor
        def _(pe):
            logits.start_tensor(pe)

            def early(q, i, b):
                pe.wait_ge(onehot_ready, q + 1)
                pe.wait_ge(outside_ready, q + 1)
                for k in range(BATCH):
                    ins = pe.transpose(at(ps_hot, k, P), at(onehot[b], k, P), net.ident[:, :])
                ins.then_inc(hot_turned, 1)
                logits.tensor_early(pe, q, i, b)

            def late(q, i, b):
                pe.wait_ge(nodehot_ready, q + 1)
                logits.tensor(pe, q, i, b)
                pe.wait_ge(logit_ready, q + 1)
                for k in range(BATCH):
                    pe.wait_ge(topped, q * BATCH + k + 1)
                    for h in range(heads):
                        c = k * heads + h
                        ins = pe.transpose(at(ps_row[:, k % 2, :], h, P), logit[:, c:c + 1].to_broadcast([P, P]),
                                           net.ident[:, :])
                    ins.then_inc(rows_turned, 1)
                pe.wait_ge(shrink_ready, q + 1)
                for k in range(BATCH):
                    ins = pe.matmul(at(ps_top, k, heads), at(nodehot[b], k, P), at(new_top, k, heads), start=True, stop=True)
                ins.then_inc(spread_top, 1)
                pe.wait_ge(filled, q + 1)
                for k in range(BATCH):
                    n = q * BATCH + k
                    pe.wait_ge(weighted_ready, n + 1)
                    pe.wait_ge(added, n + 1)
                    pe.matmul(ps_x[:, k % 2, 0:W], at(onehot[b], k, P), at(weighted, k, W), start=True, stop=True)\
                        .then_inc(summed, 1)

            staggered(pe, early, late)

        @block.scalar
        def _(act):
            def early(q, i, b):
                act.wait_ge(hot_turned, q + 1)
                act.activation(nodehot[b][:, :], ps_hot[:, :], ACT.Copy).then_inc(nodehot_ready, 1)
                logits.scalar_early(act, q, i, b)

            def late(q, i, b):
                act.wait_ge(shrink_ready, q + 1)
                act.activation(shrink[:, :], shrink[:, :], ACT.Exp).then_inc(powered, 1)
                act.wait_ge(power_step, 2 * q + 2)
                act.activation(power[:, :], power[:, :], ACT.Exp).then_inc(powered, 1)
                act.wait_ge(powered, 2 * q + 2)
                act.activation(weighted[:, :].rearrange("p (h c) -> p h c", c=each + 1)[:, :, each], power[:, :], ACT.Copy)\
                    .then_inc(filled, 1)

            staggered(act, early, late)


class L1Logits:

    SLOPE = 0.2

    def __init__(self, net, xr, att, s, g, ps_x, nodehot, logit, logit_ready, added, nodehot_ready):
        self.net, self.xr, self.att, self.g = net, xr, att, g
        self.ps_x, self.nodehot, self.logit, self.logit_ready, self.added = ps_x, nodehot, logit, logit_ready, added
        self.we = s.sb("we", [16, D])
        self.attrT = [s.sb(f"attrT{b}", [16, BATCH * P]) for b in range(2)]
        self.e = s.sb("e", [P, BATCH * D])
        self.ps_attr = s.ps("ps_attr", [16, BATCH * P])
        self.loaded = s.sem("we_loaded")
        self.attr_turned = s.sem("attr_turned")
        self.attr_ready = s.sem("attr_ready")
        self.sums = s.sem("e_sums")
        self.step = s.sem("e_step")
        self.tick = s.sem("e_tick")

    def load(self, sp):
        sp.dma_start(self.we[:, :], self.net.a["L1_gnn_W_e"]).then_inc(self.loaded, 16)

    def start_vector(self, dve):
        dve.sem_inc(self.step, 8)

    def start_tensor(self, pe):
        pe.wait_ge(self.loaded, 16)

    def tensor_early(self, pe, q, i, b):
        pe.wait_ge(self.g.rec_loaded[b], i * 16 + 16)
        pe.wait_ge(self.attr_ready, q + 1)
        pe.sem_inc(self.tick, 1)
        for k in range(BATCH):
            ins = pe.transpose(at(self.ps_attr, k, P), self.g.columns(b, k, self.g.lo, 16), self.net.ident[:, :])
        ins.then_inc(self.attr_turned, 1)

    def scalar_early(self, act, q, i, b):
        if isinstance(q, int) and q == 0:
            act.sem_inc(self.attr_ready, 1)
        act.wait_ge(self.attr_turned, q + 1)
        act.activation(self.attrT[b][:, :], self.ps_attr[:, :], ACT.Copy).then_inc(self.attr_ready, 1)

    def tensor(self, pe, q, i, b):
        pe.wait_ge(self.attr_ready, q + 2)
        for k in range(BATCH):
            n = q * BATCH + k
            blk = block_of(pe, self.g.placed, n)
            pe.wait_ge(self.step, 4 * (n + 1))
            pe.wait_ge(self.added, q * BATCH + 2)
            pe.matmul(self.ps_x[:, k % 2, 0:D], at(self.nodehot[b], k, P), at(self.xr, blk, D), start=True, stop=False)
            pe.matmul(self.ps_x[:, k % 2, 0:D], at(self.attrT[b], k, P), self.we[:, :], start=False, stop=True)\
                .then_inc(self.sums, 1)

    def vector(self, dve, q, i, b):
        for k in range(BATCH):
            n = q * BATCH + k
            e = at(self.e, k, D)
            base = 4 * n + 8
            dve.wait_ge(self.sums, n + 1)
            dve.tensor_tensor(e, self.ps_x[:, k % 2, 0:D], at(self.g.rows[b], k, D), ALU.add).then_inc(self.step, 1)
            dve.wait_ge(self.step, base + 1)
            dve.scalar_tensor_tensor(e, e, self.SLOPE, e, ALU.mult, ALU.max).then_inc(self.step, 1)
            dve.wait_ge(self.step, base + 2)
            dve.tensor_tensor(e, e, self.att[:, :], ALU.mult).then_inc(self.step, 1)
            dve.wait_ge(self.step, base + 3)
            dve.tensor_reduce(at(self.logit, k, 4), e.rearrange("p (h c) -> p h c", h=4), AX.X, ALU.add)\
                .then_inc(self.step, 1)
        dve.wait_ge(self.step, 4 * (q * BATCH + BATCH) + 8)
        dve.sem_inc(self.logit_ready, 1)


def l1_gnn(net):
    nc, a = net.nc, net.a
    H, C = 4, 64
    W = H * (C + 1)
    with ExitStack() as ctx:
        s = net.scope("l1", ctx)
        xr = s.sb("xr", [P, NT * D])
        res = s.sb("res", [P, NT * D])
        att = s.sb("att", [P, D])
        top = s.sb("top", [P, NT * H])
        l1_nodes(net, xr, res, att, top)
        with ExitStack() as inner:
            g = Gather(net.scope("l1g", inner), net, net.by_dst, net.table(D), D, net.by_dst.first["edge_attr_16"])
            gat_edges(net, "l1e", g, H, C, net.work, top, lambda *args: L1Logits(net, xr, att, *args))
        l1_finish(net, res)


def l1_nodes(net, xr, res, att, top):
    nc, a = net.nc, net.a
    H, C = 4, 64
    W = H * (C + 1)
    table = net.table(D)
    with ExitStack() as ctx:
        s = net.scope("l1n", ctx)
        f = Front(s)
        ws = {n: s.sb(n, [P, DC * D]) for n in ("W_l", "W_r", "W_res")}
        bs = {n: s.sb(n, [P, D]) for n in ("b_l", "b_r", "bias")}
        we = s.sb("we", [16, D])
        xl = s.sb("xl", [P, 2 * UN * D])
        mean = s.sb("mean", [P, 16])
        meanT = s.sb("meanT", [16, P])
        e = s.sb("e", [P, D])
        ps = {n: s.ps(f"ps_{n}", [P, 512]) for n in ("W_l", "W_r", "W_res", "loop")}
        ps_mean = s.ps("ps_mean", [16, P])
        loaded = s.sem("loaded")
        mean_taken = s.sem("mean_taken")
        mean_turned = s.sem("mean_turned")
        mean_ready = s.sem("mean_ready")
        step = s.sem("step")
        tile_done = s.sem("tile_done")
        stored = [s.sem(f"stored{b}") for b in range(2)]
        pe_tick = s.sem("pe_tick")
        block = ctx.enter_context(nc.Block())

        @block.sync
        def _(sp):
            for n, w in ws.items():
                sp.dma_start(w[:, :].rearrange("p (c n) -> p c n", c=DC), chunked(a[f"L1_gnn_{n}"])).then_inc(loaded, 16)
            for n, v in bs.items():
                sp.dma_start(v[:, :], spread(a[f"L1_gnn_{n}"])).then_inc(loaded, 16)
            sp.dma_start(att[:, :], spread(a["L1_gnn_att"].rearrange("h c -> (h c)"))).then_inc(loaded, 16)
            sp.dma_start(we[:, :], a["L1_gnn_W_e"]).then_inc(loaded, 16)
            for i in range(NI):
                sp.wait_ge(tile_done, (i + 1) * UN)
                sp.dma_start(node_rows(table, i * UN, UN), tiled(at(xl, i % 2, UN * D), D)).then_inc(stored[i % 2], 16)
            sp.wait_ge(stored[0], 48)
            sp.wait_ge(stored[1], 32)

        @block.vector
        def _(dve):
            dve.wait_ge(loaded, 128)
            dve.memset(net.work[:, 0:NT * W], 1.0).then_inc(step, 1)
            for i in range(NI):
                f.moments_of(dve, net, i)
                for k in range(UN):
                    f.normalize(dve, net, i, k)
                if i >= 2:
                    dve.wait_ge(stored[i % 2], 16 * (i // 2))
                for k in range(UN):
                    t = i * UN + k
                    link = Chain(dve, step, 1 + t * 7)
                    own = at(xl, (i % 2) * UN + k, D)
                    dve.tensor_copy(mean[:, :], at(net.mean16, t, 16)).then_inc(mean_taken, 1)
                    dve.wait_ge(f.projected, UN + t + 1)
                    link(dve.tensor_tensor(own, ps["W_l"][:, 0:D], bs["b_l"][:, :], ALU.add))
                    link(dve.tensor_tensor(at(xr, t, D), ps["W_r"][:, 0:D], bs["b_r"][:, :], ALU.add))
                    dve.tensor_tensor(at(res, t, D), ps["W_res"][:, 0:D], bs["bias"][:, :], ALU.add)
                    link(dve.tensor_tensor(e[:, :], at(xr, t, D), own, ALU.add))
                    link(dve.tensor_tensor(e[:, :], e[:, :], ps["loop"][:, 0:D], ALU.add))
                    link(dve.scalar_tensor_tensor(e[:, :], e[:, :], L1Logits.SLOPE, e[:, :], ALU.mult, ALU.max))
                    link(dve.tensor_tensor(e[:, :], e[:, :], att[:, :], ALU.mult))
                    link(dve.tensor_reduce(at(top, t, H), e[:, :].rearrange("p (h c) -> p h c", h=H), AX.X, ALU.add))
                    dve.tensor_copy(at(net.work, t, W).rearrange("p (h c) -> p h c", h=H)[:, :, 0:C],
                                    own.rearrange("p (h c) -> p h c", h=H)).then_inc(tile_done, 1)

        @block.tensor
        def _(pe):
            f.start_tensor(pe)
            pe.wait_ge(loaded, 128)
            with pe.Fori(0, NI) as i:
                for k in range(UN):
                    t = i * UN + k
                    f.turn(pe, net, t, k)
                    pe.wait_ge(mean_taken, t + 1)
                    pe.sem_inc(pe_tick, 1)
                    pe.transpose(ps_mean[:, :], mean[:, :], net.ident[:, :]).then_inc(mean_turned, 1)
                    pe.wait_ge(f.xT_ready, UN + t + 1)
                    for n, w in ws.items():
                        f.project(pe, t, k, ps[n][:, 0:D], w[:, :].rearrange("p (c n) -> p c n", c=DC), last=False)
                    pe.wait_ge(mean_ready, t + 1)
                    pe.matmul(ps["loop"][:, 0:D], meanT[:, :], we[:, :], start=True, stop=True).then_inc(f.projected, 1)

        @block.scalar
        def _(act):
            f.start_scalar(act)
            with act.Fori(0, NI) as i:
                f.root(act, net, i)
                for k in range(UN):
                    t = i * UN + k
                    f.keep(act, t, k)
                    act.wait_ge(mean_turned, t + 1)
                    act.activation(meanT[:, :], ps_mean[:, :], ACT.Copy).then_inc(mean_ready, 1)


def l1_finish(net, res):
    nc = net.nc
    H, C = 4, 64
    W = H * (C + 1)
    with ExitStack() as ctx:
        s = net.scope("l1f", ctx)
        share = s.sb("share", [P, NT * H])
        low = s.sb("low", [P, NT * D])
        chain = s.sem("chain")
        to_power = s.sem("to_power")
        powered = s.sem("powered")
        block = ctx.enter_context(nc.Block())
        v = res[:, :]
        acc = net.work[:, 0:NT * W].rearrange("p (n c) -> p n c", c=C + 1)

        @block.scalar
        def _(act):
            act.wait_ge(to_power, 1)
            act.activation(low[:, :], low[:, :], ACT.Exp).then_inc(powered, 1)

        @block.vector
        def _(dve):
            link = Chain(dve, chain)
            link(dve.reciprocal(share[:, :], acc[:, :, C]))
            heads = low[:, :].rearrange("p (n c) -> p n c", c=C)
            link(dve.tensor_tensor(heads, acc[:, :, 0:C], share[:, :].unsqueeze(2).to_broadcast([P, NT * H, C]), ALU.mult))
            link(dve.tensor_tensor(v, v, low[:, :], ALU.add))
            link(dve.tensor_scalar(low[:, :], v, 0.0, None, ALU.min))
            dve.sem_inc(to_power, 1)
            link(dve.scalar_tensor_tensor(v, v, 0.0, net.x[:, :], ALU.max, ALU.add))
            dve.wait_ge(powered, 1)
            link(dve.scalar_tensor_tensor(net.x[:, :], low[:, :], -1.0, v, ALU.add, ALU.add))


def gcn_edges(net, name, width, acc):
    nc = net.nc
    with ExitStack() as ctx:
        s = net.scope(name, ctx)
        g = Gather(s, net, net.by_dst, net.table(width), width, net.by_dst.number)
        onehot = [s.sb(f"onehot{b}", [P, BATCH * P]) for b in range(2)]
        ps = s.ps("ps", [P, 2, 512])
        onehot_ready = s.sem("onehot_ready")
        summed = s.sem("summed")
        added = s.sem("added")
        block = ctx.enter_context(nc.Block())

        @block.sync
        def _(sp):
            g.load(sp)

        @block.gpsimd
        def _(pool):
            g.gather(pool)

        @block.vector
        def _(dve):
            g.start_vector(dve)

            def early(q, i, b):
                g.sources(dve, i, b)
                one_hots(dve, g, net, b, onehot[b]).then_inc(onehot_ready, 1)

            def late(q, i, b):
                dve.wait_ge(summed, q + 1)
                for k in range(BATCH):
                    blk = block_of(dve, g.placed, q * BATCH + k)
                    if k or not isinstance(q, int) or q:
                        dve.wait_ge(added, q * BATCH + k)
                    dve.tensor_tensor(at(acc, blk, width), at(acc, blk, width), at(ps[:, b, :], k, width), ALU.add)\
                        .then_inc(added, 1)
                dve.wait_ge(added, q * BATCH + BATCH)
                dve.sem_inc(g.batch_done, 1)

            early(0, 0, 0)
            early(1, 0, 1)
            late(0, 0, 0)
            late(1, 0, 1)
            with dve.Fori(1, NB // 2) as i:
                early(2 * i, i, 0)
                early(2 * i + 1, i, 1)
                late(2 * i, i, 0)
                late(2 * i + 1, i, 1)

        @block.tensor
        def _(pe):
            with pe.Fori(0, NB // 2) as i:
                for b in range(2):
                    q = 2 * i + b
                    pe.wait_ge(onehot_ready, q + 1)
                    g.wait_rows(pe, i, b)
                    pe.wait_ge(g.batch_done, q + 1)
                    for k in range(BATCH):
                        ins = pe.matmul(at(ps[:, b, :], k, width), at(onehot[b], k, P), at(g.rows[b], k, width),
                                        start=True, stop=True)
                    ins.then_inc(summed, 1)


def gcn_nodes(net, name, source, out, w_in=None, weights=None, before=None, after=None, final=False):
    nc, a = net.nc, net.a
    n = a[weights].shape[1] if weights else w_in
    k_in = a[weights].shape[0] if weights else w_in
    chunks = -(-k_in // P)
    kp = min(k_in, P)
    table = None if final else net.table(n)
    with ExitStack() as ctx:
        s = net.scope(name, ctx)
        f = Front(s)
        w = s.sb("w", [kp, chunks * n])
        first = s.sb("first", [P, k_in])
        second = s.sb("second", [P, n])
        held = s.sb("held", [P, UN * n])
        ps = s.ps("ps", [P, 2, 512])
        loaded = s.sem("loaded")
        step = s.sem("step")
        held_step = s.sem("held_step")
        out_done = s.sem("out_done")
        stored = s.sem("stored")
        pe_tick = s.sem("pe_tick")
        act_tick = s.sem("act_tick")
        block = ctx.enter_context(nc.Block())
        loads = sum(v is not None for v in (weights, before, after))

        @block.sync
        def _(sp):
            if weights:
                sp.dma_start(w[:, :].rearrange("p (c n) -> p c n", c=chunks), a[weights].rearrange("(c p) n -> p c n", p=kp))\
                    .then_inc(loaded, 16)
            if before:
                sp.dma_start(first[:, :], spread(a[before])).then_inc(loaded, 16)
            if after:
                sp.dma_start(second[:, :], spread(a[after])).then_inc(loaded, 16)
            if not final:
                for i in range(NI):
                    sp.wait_ge(out_done, (2 + i) * UN)
                    sp.dma_start(node_rows(table, i * UN, UN), tiled(at(out, i, UN * n), n)).then_inc(stored, 16)
                sp.wait_ge(stored, NI * 16)

        @block.vector
        def _(dve):
            dve.sem_inc(out_done, UN)
            if loads:
                dve.wait_ge(loaded, 16 * loads)

            def source_tile(t, xn):
                if before is None:
                    return dve.tensor_scalar(xn, at(source, t, k_in), at(net.dinv, t, 1), None, ALU.mult)
                dve.scalar_tensor_tensor(xn, at(source, t, k_in), at(net.dinv, t, 1), first[:, :], ALU.mult, ALU.add)\
                    .then_inc(step, 1)
                dve.wait_ge(step, 2 * t + 1)
                return dve.tensor_scalar(xn, xn, 0.0, None, ALU.max)

            with dve.Fori(0, NI) as i:
                if source is None:
                    f.moments_of(dve, net, i)
                    for k in range(UN):
                        f.normalize(dve, net, i, k)
                elif weights:
                    for k in range(UN):
                        if before is None:
                            dve.sem_inc(step, 1)
                        f.take(dve, i * UN + k, k, lambda xn: source_tile(i * UN + k, xn[:, 0:k_in]))
                        dve.sem_inc(step, 1)
                for k in range(UN):
                    t = i * UN + k
                    dve.wait_ge(out_done, t + 1)
                    if not weights:
                        dve.scalar_tensor_tensor(at(held, k, n), at(source, t, n), at(net.dinv, t, 1), first[:, :],
                                                 ALU.mult, ALU.add).then_inc(step, 1)
                        dve.wait_ge(step, t + 1)
                        dve.tensor_scalar(at(out, t, n), at(held, k, n), 0.0, at(net.dinv, t, 1), ALU.max, ALU.mult)\
                            .then_inc(out_done, 1)
                        continue
                    dve.wait_ge(f.projected, UN + t + 1)
                    if after is None:
                        dve.tensor_scalar(at(out, t, n), ps[:, k % 2, 0:n], at(net.dinv, t, 1), None, ALU.mult)\
                            .then_inc(out_done, 1)
                        continue
                    dve.tensor_tensor(at(held, k, n), ps[:, k % 2, 0:n], second[:, :], ALU.add).then_inc(held_step, 1)
                    dve.wait_ge(held_step, t + 1)
                    if final:
                        dve.tensor_tensor(at(net.x, t, D), at(net.x, t, D), at(held, k, n), ALU.add).then_inc(out_done, 1)
                    else:
                        dve.tensor_scalar(at(out, t, n), at(held, k, n), 0.0, at(net.dinv, t, 1), ALU.max, ALU.mult)\
                            .then_inc(out_done, 1)

        if not weights:
            return

        @block.tensor
        def _(pe):
            f.start_tensor(pe)
            pe.wait_ge(loaded, 16 * loads)
            with pe.Fori(0, NI) as i:
                for k in range(UN):
                    t = i * UN + k
                    f.turn(pe, net, t, k, k_in, pe_tick)
                    pe.wait_ge(f.xT_ready, UN + t + 1)
                    pe.wait_ge(out_done, bank_free(t, k))
                    pe.sem_inc(pe_tick, 1)
                    for c in range(chunks):
                        ins = pe.matmul(ps[:, k % 2, 0:n], f.lhsT(k, c)[0:kp, :], at(w, c, n), start=c == 0, stop=c == chunks - 1)
                    ins.then_inc(f.projected, 1)

        @block.scalar
        def _(act):
            f.start_scalar(act)
            with act.Fori(0, NI) as i:
                if source is None:
                    f.root(act, net, i)
                for k in range(UN):
                    f.keep(act, i * UN + k, k, kp, chunks)


def l2_gnn(net):
    with ExitStack() as ctx:
        s = net.scope("l2", ctx)
        other = s.sb("other", [P, NT * P])
        gcn_nodes(net, "l2a", None, net.work, weights="L2_gnn_W1")
        gcn_edges(net, "l2ae", 128, net.work)
        gcn_nodes(net, "l2b", net.work, other, weights="L2_gnn_W2", before="L2_gnn_b1")
        gcn_edges(net, "l2be", 64, other)
        gcn_nodes(net, "l2c", other, net.work, w_in=64, before="L2_gnn_b2")
        gcn_edges(net, "l2ce", 64, net.work)
        gcn_nodes(net, "l2d", net.work, other, weights="L2_gnn_W3", after="L2_gnn_b3")
        gcn_edges(net, "l2de", 128, other)
        gcn_nodes(net, "l2e", other, None, weights="L2_gnn_W4", after="L2_gnn_b4", final=True)


class L3Logits:

    SLOPE = 0.01

    def __init__(self, net, wide, s, g, ps_x, nodehot, logit, logit_ready, added, nodehot_ready):
        self.net, self.wide, self.g, self.logit, self.logit_ready = net, wide, g, logit, logit_ready
        self.prod = s.sb("prod", [P, BATCH * P])
        self.edge = s.sb("edge", [P, BATCH])
        self.step = s.sem("e_step")

    def load(self, sp):
        pass

    def start_vector(self, dve):
        pass

    def start_tensor(self, pe):
        pass

    def tensor_early(self, pe, q, i, b):
        pass

    def scalar_early(self, act, q, i, b):
        pass

    def tensor(self, pe, q, i, b):
        pass

    def vector(self, dve, q, i, b):
        for k in range(BATCH):
            ins = dve.tensor_tensor_reduce(at(self.prod, k, P), self.g.columns(b, k, 0, P), self.wide[:, :], 1.0, 0.0,
                                           ALU.mult, ALU.add, self.edge[:, k:k + 1])
        ins.then_inc(self.step, 1)
        dve.wait_ge(self.step, 2 * q + 1)
        dve.tensor_tensor(self.edge[:, :], self.edge[:, :], tiled(self.g.rows[b][:, :], D + 1)[:, :, D], ALU.add)\
            .then_inc(self.step, 1)
        dve.wait_ge(self.step, 2 * q + 2)
        dve.scalar_tensor_tensor(self.logit[:, :], self.edge[:, :], self.SLOPE, self.edge[:, :], ALU.mult, ALU.max)\
            .then_inc(self.logit_ready, 1)
        dve.wait_ge(self.logit_ready, q + 1)


def l3_gnn(net):
    with ExitStack() as ctx:
        s = net.scope("l3", ctx)
        wide = s.sb("wide", [P, P])
        top = s.sb("top", [P, NT])
        l3_nodes(net, wide, top)
        with ExitStack() as inner:
            g = Gather(net.scope("l3g", inner), net, net.by_dst, net.table(D + 1), D + 1, 0)
            gat_edges(net, "l3e", g, 1, D, net.work, top, lambda *args: L3Logits(net, wide, *args))
        l3_finish(net)


def l3_nodes(net, wide, top):
    nc, a = net.nc, net.a
    W = D + 1
    table = net.table(W)
    with ExitStack() as ctx:
        s = net.scope("l3n", ctx)
        f = Front(s)
        wn = s.sb("wn", [P, DC * D])
        wnT = s.sb("wnT", [P, DC * D])
        we = s.sb("we", [P, DC * P])
        be = s.sb("be", [P, DC])
        attn_col = s.sb("attn_col", [P, DC])
        attn_cols = s.sb("attn_cols", [P, DC * P])
        attn = s.sb("attn", [P, D])
        bn = s.sb("bn", [P, D])
        const = s.sb("const", [P, 1])
        h = s.sb("h", [P, NT * W])
        prod = s.sb("prod", [P, D])
        dot = s.sb("dot", [P, UN])
        held = s.sb("held", [P, UN * D])
        ps_w = s.ps("ps_w", [P, 2, 512])
        ps = s.ps("ps", [P, 2, 512])
        loaded = s.sem("loaded")
        chain = s.sem("chain")
        cols_ready = s.sem("cols_ready")
        w_turned = s.sem("w_turned")
        w_ready = s.sem("w_ready")
        step = s.sem("step")
        h_ready = s.sem("h_ready")
        stored = s.sem("stored")
        block = ctx.enter_context(nc.Block())
        vector = a["L3_gnn_attn"].rearrange("a b c -> (a b c)")

        @block.sync
        def _(sp):
            sp.dma_start(wn[:, :].rearrange("p (c n) -> p c n", c=DC), chunked(a["L3_gnn_Wn"])).then_inc(loaded, 16)
            sp.dma_start(we[:, :].rearrange("p (c n) -> p c n", c=DC), chunked(a["L3_gnn_We"])).then_inc(loaded, 16)
            for c in range(DC):
                sp.dma_start(be[:, c:c + 1], column(a["L3_gnn_be"][c * P:(c + 1) * P])).then_inc(loaded, 16)
                sp.dma_start(attn_col[:, c:c + 1], column(vector[c * P:(c + 1) * P])).then_inc(loaded, 16)
            sp.dma_start(attn[:, :], spread(vector)).then_inc(loaded, 16)
            sp.dma_start(bn[:, :], spread(a["L3_gnn_bn"])).then_inc(loaded, 16)
            for i in range(NI):
                sp.wait_ge(h_ready, (2 + i) * UN)
                sp.dma_start(node_rows(table, i * UN, UN), tiled(at(h, i, UN * W), W)).then_inc(stored, 16)
            sp.wait_ge(stored, NI * 16)

        @block.vector
        def _(dve):
            link = Chain(dve, chain)
            dve.wait_ge(loaded, 128)
            for c in range(DC):
                link(dve.tensor_scalar(at(attn_cols, c, P), net.ones[:, :], attn_col[:, c:c + 1], None, ALU.mult))
            dve.sem_inc(cols_ready, 1)
            link(dve.memset(top[:, :], -HUGE))
            link(dve.memset(net.work[:, 0:NT * W], 0.0))
            dve.wait_ge(w_turned, 1)
            for c in range(DC):
                link(dve.tensor_copy(at(wnT, c, D), ps_w[:, 0, c * D:(c + 1) * D]))
            link(dve.tensor_copy(wide[:, :], ps_w[:, 1, 0:P]))
            link(dve.tensor_copy(const[:, :], ps_w[:, 1, P:P + 1]))
            dve.sem_inc(w_ready, 1)
            dve.sem_inc(h_ready, UN)
            with dve.Fori(0, NI) as i:
                f.moments_of(dve, net, i)
                for k in range(UN):
                    f.normalize(dve, net, i, k)
                for k in range(UN):
                    t = i * UN + k
                    own = h[:, bass.ds(t * W, D)]
                    dve.wait_ge(f.projected, UN + t + 1)
                    dve.tensor_tensor(held[:, k * D:(k + 1) * D], ps[:, k % 2, 0:D], bn[:, :], ALU.add).then_inc(step, 1)
                    dve.wait_ge(step, 2 * t + 1)
                    dve.tensor_copy(own, held[:, k * D:(k + 1) * D])
                    dve.tensor_tensor_reduce(prod[:, :], held[:, k * D:(k + 1) * D], attn[:, :], 1.0, 0.0,
                                             ALU.mult, ALU.add, dot[:, k:k + 1]).then_inc(step, 1)
                    dve.wait_ge(step, 2 * t + 2)
                    dve.tensor_scalar(h[:, bass.ds(t * W + D, 1)], dot[:, k:k + 1], const[:, :], None, ALU.add)\
                        .then_inc(h_ready, 1)

        @block.tensor
        def _(pe):
            f.start_tensor(pe)
            pe.wait_ge(loaded, 128)
            for c in range(DC):
                for m in range(DC):
                    pe.transpose(ps_w[:, 0, c * D + m * P:c * D + (m + 1) * P],
                                 wn[:, m * D + c * P:m * D + (c + 1) * P], net.ident[:, :])
            pe.wait_ge(cols_ready, 1)
            for c in range(DC):
                pe.matmul(ps_w[:, 1, 0:P], at(attn_cols, c, P), at(we, c, P), start=c == 0, stop=c == DC - 1)
            for c in range(DC):
                ins = pe.matmul(ps_w[:, 1, P:P + 1], at(attn_cols, c, P), be[:, c:c + 1], start=c == 0, stop=c == DC - 1)
            ins.then_inc(w_turned, 1)
            pe.wait_ge(w_ready, 1)
            with pe.Fori(0, NI) as i:
                for k in range(UN):
                    t = i * UN + k
                    f.turn(pe, net, t, k)
                    pe.wait_ge(f.xT_ready, UN + t + 1)
                    pe.wait_ge(h_ready, bank_free(t, k))
                    f.project(pe, t, k, ps[:, k % 2, 0:D], wnT[:, :].rearrange("p (c n) -> p c n", c=DC))

        @block.scalar
        def _(act):
            f.start_scalar(act)
            with act.Fori(0, NI) as i:
                f.root(act, net, i)
                for k in range(UN):
                    f.keep(act, i * UN + k, k)


def l3_finish(net):
    nc = net.nc
    W = D + 1
    with ExitStack() as ctx:
        s = net.scope("l3f", ctx)
        share = s.sb("share", [P, NT])
        out = s.sb("out", [P, NT * D])
        chain = s.sem("chain")
        block = ctx.enter_context(nc.Block())
        acc = tiled(net.work[:, 0:NT * W], W)

        @block.vector
        def _(dve):
            link = Chain(dve, chain)
            link(dve.tensor_scalar(share[:, :], acc[:, :, D], 1e-16, None, ALU.add))
            link(dve.reciprocal(share[:, :], share[:, :]))
            link(dve.tensor_tensor(tiled(out[:, :], D), acc[:, :, 0:D], share[:, :].unsqueeze(2).to_broadcast([P, NT, D]), ALU.mult))
            link(dve.scalar_tensor_tensor(net.x[:, :], out[:, :], 0.0, net.x[:, :], ALU.max, ALU.add))


STAGES = (setup, place_by_src, l0_gnn_nodes, l0_gnn_edges, l0_gnn_update, l0_ffn, place_by_dst, edge_means,
          l1_gnn, l1_ffn, l2_gnn, l2_ffn, l3_gnn, l3_ffn)


def build(nc, arrays, out):
    with ExitStack() as ctx:
        net = Net(nc, arrays, ctx)
        for stage in STAGES:
            stage(net)
        store(net, out)


def store(net, out):
    nc = net.nc
    with ExitStack() as ctx:
        s = net.scope("store", ctx)
        stored = s.sem("stored")
        block = ctx.enter_context(nc.Block())

        @block.sync
        def _(sp):
            full = (NT - 1) * P
            sp.dma_start(out[0:full, :].rearrange("(t p) d -> p t d", p=P),
                         net.x[:, 0:(NT - 1) * D].rearrange("p (t d) -> p t d", d=D)).then_inc(stored, 16)
            sp.dma_start(out[full:N, :], net.x[0:TAIL, (NT - 1) * D:NT * D]).then_inc(stored, 16)
            sp.wait_ge(stored, 32)


def kernel(**inputs):
    from concourse import bacc
    from concourse.bass_utils import run_bass_kernel_spmd

    nc = bacc.Bacc("TRN2", target_bir_lowering=False, num_devices=1)
    arrays, aps = {}, {}
    for name, value in inputs.items():
        arrays[f"in_{name}"] = np.ascontiguousarray(value)
        aps[name] = nc.dram_tensor(f"in_{name}", value.shape, mybir.dt.from_np(arrays[f"in_{name}"].dtype),
                                   kind="ExternalInput").ap()
    out = nc.dram_tensor("out", [N, D], F32, kind="ExternalOutput").ap()
    build(nc, aps, out)
    result = run_bass_kernel_spmd(nc, [arrays], core_ids=[0])
    return result.results[0]["out"]
```

```python
from contextlib import ExitStack

import numpy as np

import concourse.bass as bass
from concourse import mybir

F32 = mybir.dt.float32
I32 = mybir.dt.int32
BF16 = mybir.dt.bfloat16
ALU = mybir.AluOpType
ACT = mybir.ActivationFunctionType
AX = mybir.AxisListType

P = 128
N = 3125
D = 256
DC = D // P
E = 50000
NT = -(-N // P)
NP = NT * P
TAIL = N - (NT - 1) * P
EC = E // P
EX = E - EC * P
PAIR = 2 * P
BATCH = 4
TWO = BATCH // 2
RING = 5
NB = -(-(E // PAIR + NT) // (TWO * RING)) * RING
ST = NB * BATCH
SLOTS = ST * P
PAIRS = NB * TWO
BLANKS = 22
assert ST % BLANKS == 0
EXPERTS = 8
EPS = 1e-5
HUGE = 1.0e30

META = 4

UN = 5
NI = NT // UN
assert NT % UN == 0


def at(tensor, t, width):
    if isinstance(t, int):
        return tensor[:, t * width:(t + 1) * width]
    return tensor[:, bass.ds(t * width, width)]


class Placement:

    def __init__(self, nc, s, key, other, fields, weighted):
        self.key, self.other, self.fields, self.weighted = key, other, fields, weighted
        self.first = {}
        at_column = 0
        for name, width in fields:
            self.first[name] = at_column
            at_column += width
        self.number, self.far, self.near = at_column, at_column + 1, at_column + 2
        self.width = at_column + META
        self.records = nc.dram_tensor(f"records_by_{key}", [SLOTS, self.width], F32, kind="Internal").ap()
        self.block_row = s.sb(f"block_row_{key}", [P, PAIRS], I32)
        self.keep = s.sb(f"keep_{key}", [P, PAIRS])


class Chain:

    def __init__(self, eng, sem, base=0):
        self.eng, self.sem, self.base, self.n = eng, sem, base, 0

    def __call__(self, ins):
        self.n += 1
        ins.then_inc(self.sem, 1)
        self.eng.wait_ge(self.sem, self.base + self.n)

    def steps(self, n):
        assert self.n == n, (self.n, n)


class Scope:

    def __init__(self, nc, name, ctx):
        self.nc, self.name, self.ctx, self.sems = nc, name, ctx, []
        ctx.callback(self.close)

    def close(self):
        if self.sems:
            self.nc.clear_and_free_semaphores(self.sems)
            self.nc.all_engine_barrier()

    def sb(self, name, shape, dt=F32):
        return self.ctx.enter_context(self.nc.sbuf_tensor(f"{self.name}_{name}", shape, dt))

    def ps(self, name, shape):
        return self.ctx.enter_context(self.nc.psum_tensor(f"{self.name}_{name}", shape, F32))

    def sem(self, name):
        self.sems.append(self.nc.alloc_semaphore(f"{self.name}_{name}"))
        return self.sems[-1]


class Net:

    def __init__(self, nc, arrays, ctx):
        self.nc = nc
        self.a = arrays
        s = Scope(nc, "net", ctx)
        self.x = s.sb("x", [P, NT * D])
        self.ident = s.sb("ident", [P, P])
        self.before = s.sb("before", [P, P])
        self.ones = s.sb("ones", [P, P])
        self.zeros = s.sb("zeros", [P, 512])
        self.eps = s.sb("eps", [P, 1])
        self.columns = s.sb("columns", [P, P])
        self.rank8 = s.sb("rank8", [P, NT * EXPERTS])
        self.mean16 = s.sb("mean16", [P, NT * 16])
        self.dinv = s.sb("dinv", [P, NT])
        self.work = s.sb("work", [P, NT * 260])
        self.by_src = Placement(nc, s, "src", "dst", (("edge_attr_64", 64),), True)
        self.by_dst = Placement(nc, s, "dst", "src", (("edge_attr_128", 128), ("edge_attr_16", 16)), False)
        self.tables = {}
        slots = (2 * N // PAIR + EXPERTS) * PAIR
        self.dispatch = {n: nc.dram_tensor(n, [slots, D], F32, kind="Internal").ap() for n in ("tokens", "outputs")}

    def scope(self, name, ctx):
        return Scope(self.nc, name, ctx)

    def table(self, width):
        if width not in self.tables:
            self.tables[width] = self.nc.dram_tensor(f"table{width}", [NP, width], F32, kind="Internal").ap()
        return self.tables[width]


def row(vector):
    return vector.rearrange("(o n) -> o n", o=1)


def column(vector):
    return vector.rearrange("(p o) -> p o", o=1)


def spread(vector):
    return row(vector).to_broadcast([P, vector.shape[0]])


def node_rows(table, t0, n):
    return table[bass.ds(t0 * P, n * P), :].rearrange("(t p) d -> p t d", p=P)


def tiled(ap, width):
    return ap.rearrange("p (t d) -> p t d", d=width)


def chunked(weights):
    return weights.rearrange("(c p) n -> p c n", p=P)


def bank_free(q, k):
    return UN + q - 1 + (k == 0)


class Front:

    def __init__(self, s):
        self.stats = s.sb("stats", [P, UN * 6])
        self.moments = s.sb("moments", [P, UN * 2])
        self.sigma = s.sb("sigma", [P, UN])
        self.rstd = s.sb("rstd", [P, UN])
        self.xn = s.sb("xn", [P, UN * D])
        self.xT = s.sb("xT", [P, UN * D])
        self.ps = s.ps("turn", [P, 2, 512])
        self.stats_ready = s.sem("stats_ready")
        self.moments_ready = s.sem("moments_ready")
        self.rstd_ready = s.sem("rstd_ready")
        self.tick = s.sem("tick")
        self.sigma_ready = s.sem("sigma_ready")
        self.normed = s.sem("normed")
        self.turned = s.sem("turned")
        self.xT_ready = s.sem("xT_ready")
        self.projected = s.sem("projected")

    def start_tensor(self, pe):
        pe.sem_inc(self.turned, UN)
        pe.sem_inc(self.projected, UN)

    def start_scalar(self, act):
        act.sem_inc(self.xT_ready, UN)

    def moments_of(self, dve, net, i):
        for k in range(UN):
            ins = dve.bn_stats(at(self.stats, k, 6), at(net.x, i * UN + k, D))
        ins.then_inc(self.stats_ready, 1)
        dve.wait_ge(self.stats_ready, i + 1)
        dve.sem_inc(self.tick, 1)
        for k in range(UN):
            ins = dve.bn_aggr(at(self.moments, k, 2), at(self.stats, k, 6))
        ins.then_inc(self.moments_ready, 1)

    def root(self, act, net, i):
        act.wait_ge(self.moments_ready, i + 1)
        act.activation(self.sigma[:, :], tiled(self.moments[:, :], 2)[:, :, 1], ACT.Sqrt, bias=net.eps[:, :])\
            .then_inc(self.sigma_ready, 1)

    def normalize(self, dve, net, i, k):
        q = i * UN + k
        if k == 0:
            dve.wait_ge(self.sigma_ready, i + 1)
            dve.reciprocal(self.rstd[:, :], self.sigma[:, :]).then_inc(self.rstd_ready, 1)
            dve.wait_ge(self.rstd_ready, i + 1)
        dve.wait_ge(self.turned, q + 1)
        dve.tensor_scalar(at(self.xn, k, D), at(net.x, q, D), self.moments[:, 2 * k:2 * k + 1], at(self.rstd, k, 1),
                          ALU.subtract, ALU.mult).then_inc(self.normed, 1)

    def take(self, dve, q, k, fill):
        dve.wait_ge(self.turned, q + 1)
        fill(at(self.xn, k, D)).then_inc(self.normed, 1)

    def turn(self, pe, net, q, k, width=D, tick=None):
        pe.wait_ge(self.normed, q + 1)
        pe.wait_ge(self.xT_ready, bank_free(q, k))
        if tick is not None:
            pe.sem_inc(tick, 1)
        for lo in range(0, width, P):
            n = min(P, width - lo)
            ins = pe.transpose(self.ps[0:n, k % 2, lo:lo + P], self.xn[:, k * D + lo:k * D + lo + n], net.ident[:, :])
        ins.then_inc(self.turned, 1)

    def keep(self, act, q, k, rows=P, chunks=DC):
        act.wait_ge(self.turned, UN + q + 1)
        act.wait_ge(self.projected, q + 1)
        act.activation(self.xT[0:rows, k * D:k * D + chunks * P], self.ps[0:rows, k % 2, 0:chunks * P], ACT.Copy).then_inc(self.xT_ready, 1)

    def lhsT(self, k, c):
        return self.xT[:, k * D + c * P:k * D + (c + 1) * P]

    def project(self, pe, q, k, out, weights, last=True):
        for c in range(DC):
            ins = pe.matmul(out, self.lhsT(k, c), weights[:, c, :], start=c == 0, stop=c == DC - 1)
        if last:
            ins.then_inc(self.projected, 1)


def setup(net):
    nc = net.nc
    with ExitStack() as ctx:
        s = net.scope("setup", ctx)
        index = s.sb("index", [P, P], I32)
        rank = s.sb("rank", [P, NT * EXPERTS], I32)
        x_loaded = s.sem("x_loaded")
        x_cleared = s.sem("x_cleared")
        ones_set = s.sem("ones_set")
        index_set = s.sem("index_set")
        block = ctx.enter_context(nc.Block())

        @block.sync
        def _(sp):
            full = (NT - 1) * P
            sp.wait_ge(x_cleared, 2)
            sp.dma_start(net.x[:, 0:(NT - 1) * D].rearrange("p (t d) -> p t d", d=D),
                         net.a["x"][0:full, :].rearrange("(t p) d -> p t d", p=P)).then_inc(x_loaded, 16)
            sp.dma_start(net.x[0:TAIL, (NT - 1) * D:NT * D], net.a["x"][full:N, :]).then_inc(x_loaded, 16)
            tokens = net.dispatch["tokens"].rearrange("(p r) d -> p (r d)", p=P)
            sp.dma_start(tokens.rearrange("p (n c) -> p n c", c=512),
                         net.zeros[:, :].unsqueeze(1).to_broadcast([P, tokens.shape[1] // 512, 512])).then_inc(x_loaded, 16)
            sp.wait_ge(x_loaded, 48)

        @block.gpsimd
        def _(pool):
            pool.iota(index[:, :], pattern=[[1, P]], base=0, channel_multiplier=0).then_inc(index_set, 1)
            pool.iota(rank[:, :], pattern=[[0, NT], [-1, EXPERTS]], base=EXPERTS, channel_multiplier=0).then_inc(index_set, 1)
            pool.memset(net.ones[:, :], 1.0).then_inc(ones_set, 1)
            pool.wait_ge(ones_set, 1)
            pool.affine_select(out=net.ident[:, :], in_=net.ones[:, :], compare_op=ALU.is_equal, fill=0.0,
                               base=0, pattern=[[-1, P]], channel_multiplier=1)
            pool.affine_select(out=net.before[:, :], in_=net.ones[:, :], compare_op=ALU.is_gt, fill=0.0,
                               base=0, pattern=[[1, P]], channel_multiplier=-1)

        @block.vector
        def _(dve):
            dve.memset(net.eps[:, :], EPS)
            dve.memset(net.zeros[:, :], 0.0).then_inc(x_cleared, 1)
            dve.memset(net.x[:, (NT - 1) * D:NT * D], 0.0).then_inc(x_cleared, 1)
            dve.wait_ge(index_set, 2)
            dve.tensor_copy(net.rank8[:, :], rank[:, :])
            dve.tensor_copy(net.columns[:, :], index[:, :])


def place_by_src(net):
    place_edges(net, net.by_src)


def place_by_dst(net):
    place_edges(net, net.by_dst)


def place_edges(net, to):
    nc, a = net.nc, net.a
    JC = 13
    CH = EC // JC
    assert EC % (2 * JC) == 0
    with ExitStack() as ctx:
        s = net.scope(f"place_{to.key}", ctx)
        rec_w = to.width
        near = s.sb("near", [P, EC + 1], I32)
        far = s.sb("far", [P, EC + 1], I32)
        part = s.sb("part", [P, EC + 1], I32)
        blk = s.sb("blk", [P, EC + 1])
        meta = s.sb("meta", [P, (EC + 1) * META])
        weight = s.sb("weight", [P, EC + 1])
        one_row = s.sb("one_row", [P, EC + 1])
        match = s.sb("match", [P, EC + 1])
        counted = s.sb("counted", [P, NT * (EC + 1)])
        totals = s.sb("totals", [P, NT])
        count = s.sb("count", [P, NT])
        ahead = s.sb("ahead", [P, NT])
        pairs_i = s.sb("pairs_i", [P, NT], I32)
        pairs = s.sb("pairs", [P, NT])
        upto = s.sb("upto", [P, NT])
        first = s.sb("first", [P, NT])
        base = s.sb("base", [P, NT])
        pos = s.sb("pos", [P, EC + 1])
        pos_i = s.sb("pos_i", [P, EC + 1], I32)
        pair_no_i = s.sb("pair_no_i", [P, PAIRS], I32)
        pair_no = s.sb("pair_no", [P, PAIRS])
        pair_blk = s.sb("pair_blk", [P, PAIRS])
        blank = s.sb("blank", [P, BLANKS * rec_w])
        pos_at = [s.sb(f"pos_at{b}", [P, JC], I32) for b in range(2)]
        rec = [s.sb(f"rec{b}", [P, JC * rec_w]) for b in range(2)]
        staged = [[s.sb(f"staged{n}_{b}", [P, JC * w]) for n, (_, w) in enumerate(to.fields)] for b in range(2)]
        ps = s.ps("ps", [P, 2, 512])

        ids_loaded = s.sem("ids_loaded")
        attrs_loaded = [s.sem(f"attrs_loaded{b}") for b in range(2)]
        numbers = s.sem("numbers")
        chain = s.sem("chain")
        count_step = s.sem("count_step")
        pos_step = s.sem("pos_step")
        blk_step = s.sem("blk_step")
        totals_ready = s.sem("totals_ready")
        sums_ready = s.sem("sums_ready")
        blank_ready = s.sem("blank_ready")
        blanked = s.sem("blanked")
        wide_copied = s.sem("wide_copied")
        rest_copied = s.sem("rest_copied")
        pos_copied = s.sem("pos_copied")
        attrs_free_act = s.sem("attrs_free_act")
        attrs_free_dve = s.sem("attrs_free_dve")
        slots_ready = s.sem("slots_ready")
        scattered = [s.sem(f"scattered{b}") for b in range(2)]
        rec_free = s.sem("rec_free")
        pool_tick = s.sem("pool_tick")
        left_loaded = s.sem("left_loaded")
        left_copied = s.sem("left_copied")
        left_scattered = s.sem("left_scattered")
        block = ctx.enter_context(nc.Block())

        def three(b):
            return rec[b][:, :].rearrange("p (j r) -> p j r", r=rec_w)

        def by_edge(name, w, j0, n):
            return a[name][0:EC * P, :].rearrange("(p j) w -> p (j w)", p=P)[:, bass.ds(j0 * w, n * w)]

        @block.sync
        def _(sp):
            for name, into in ((to.key, near), (to.other, far)):
                sp.dma_start(into[:, 0:EC], a[name][0:EC * P].rearrange("(p j) -> p j", p=P)).then_inc(ids_loaded, 16)
                sp.dma_start(into[0:EX, EC:EC + 1], a[name][EC * P:E].rearrange("(p j) -> p j", j=1))\
                    .then_inc(ids_loaded, 16)
            if to.weighted:
                w = a["edge_weight1"].rearrange("e o -> (e o)")
                sp.dma_start(weight[:, 0:EC], w[0:EC * P].rearrange("(p j) -> p j", p=P)).then_inc(ids_loaded, 16)
                sp.dma_start(weight[0:EX, EC:EC + 1], w[EC * P:E].rearrange("(p j) -> p j", j=1)).then_inc(ids_loaded, 16)
            sp.wait_ge(blank_ready, 1)
            sp.dma_start(to.records.rearrange("(p n t) r -> p n (t r)", p=P, t=BLANKS),
                         blank[:, :].unsqueeze(1).to_broadcast([P, ST // BLANKS, BLANKS * rec_w])).then_inc(blanked, 16)
            with sp.Fori(0, CH // 2) as i:
                for b in range(2):
                    q = 2 * i + b
                    sp.wait_ge(attrs_free_act, q + 1)
                    sp.wait_ge(attrs_free_dve, q + 1)
                    for n, (name, w) in enumerate(to.fields):
                        sp.dma_start(staged[b][n][:, :], by_edge(name, w, q * JC, JC)).then_inc(attrs_loaded[b], 16)
            sp.wait_ge(rec_free, CH + 1)
            for name, w in to.fields:
                c = to.first[name]
                sp.dma_start(rec[0][0:EX, c:c + w], a[name][EC * P:E, :]).then_inc(left_loaded, 16)

        @block.gpsimd
        def _(pool):
            pool.iota(pair_no_i[:, :], pattern=[[1, PAIRS]], base=0, channel_multiplier=0).then_inc(numbers, 1)
            pool.sem_inc(rec_free, 2)
            pool.wait_ge(blanked, 16)
            pool.sem_inc(pool_tick, 1)
            with pool.Fori(0, CH // 2) as i:
                for b in range(2):
                    q = 2 * i + b
                    pool.wait_ge(wide_copied, q + 1)
                    pool.wait_ge(rest_copied, q + 1)
                    pool.wait_ge(pos_copied, q + 1)
                    pool.sem_inc(pool_tick, 1)
                    for j in range(JC):
                        pool.indirect_dma_start(
                            to.records, bass.IndirectOffsetOnAxis(pos_at[b][:, j:j + 1], 0),
                            at(rec[b], j, rec_w), None).then_inc(scattered[b], 16)
                    pool.wait_ge(scattered[b], (i + 1) * 16 * JC)
                    pool.sem_inc(rec_free, 1)
            pool.wait_ge(left_copied, 2)
            pool.wait_ge(left_loaded, 16 * len(to.fields))
            pool.indirect_dma_start(to.records, bass.IndirectOffsetOnAxis(pos_at[0][0:EX, 0:1], 0),
                                    rec[0][0:EX, 0:rec_w], None).then_inc(left_scattered, 16)
            pool.wait_ge(left_scattered, 16)

        @block.tensor
        def _(pe):
            pe.wait_ge(totals_ready, 1)
            pe.matmul(ps[:, 0, 0:NT], net.before[:, :], totals[:, :], start=True, stop=True)
            pe.matmul(ps[:, 1, 0:NT], net.ones[:, :], totals[:, :], start=True, stop=True).then_inc(sums_ready, 1)

        @block.scalar
        def _(act):
            act.sem_inc(attrs_free_act, 2)
            with act.Fori(0, CH // 2) as i:
                for b in range(2):
                    act.wait_ge(attrs_loaded[b], (i + 1) * 16 * len(to.fields))
                    act.wait_ge(rec_free, 2 * i + b + 1)
                    c, w = 0, to.fields[0][1]
                    act.activation(three(b)[:, :, c:c + w], tiled(staged[b][0][:, :], w), ACT.Copy).then_inc(wide_copied, 1)
                    act.wait_ge(wide_copied, 2 * i + b + 1)
                    act.sem_inc(attrs_free_act, 1)

        @block.vector
        def _(dve):
            link = Chain(dve, chain)
            link(dve.memset(blank[:, :], 0.0))
            link(dve.memset(tiled(blank[:, :], rec_w)[:, :, to.near:to.near + 1], -1.0))
            dve.sem_inc(blank_ready, 1)
            dve.wait_ge(ids_loaded, 96 if to.weighted else 64)
            link(dve.tensor_single_scalar(part[:, 0:EC], near[:, 0:EC], 7, op=ALU.arith_shift_right))
            link(dve.tensor_single_scalar(part[0:EX, EC:EC + 1], near[0:EX, EC:EC + 1], 7, op=ALU.arith_shift_right))
            link(dve.memset(blk[:, EC:EC + 1], -1.0))
            link(dve.tensor_copy(blk[:, 0:EC], part[:, 0:EC]))
            link(dve.tensor_copy(blk[0:EX, EC:EC + 1], part[0:EX, EC:EC + 1]))
            m = meta[:, :].rearrange("p (j r) -> p j r", r=META)
            link(dve.memset(meta[:, :], 1.0))
            for lo, hi, p in ((0, EC, P), (EC, EC + 1, EX)):
                if to.weighted:
                    link(dve.tensor_copy(m[0:p, lo:hi, 0], weight[0:p, lo:hi]))
                link(dve.tensor_copy(m[0:p, lo:hi, 1], far[0:p, lo:hi]))
                link(dve.tensor_single_scalar(part[0:p, lo:hi], near[0:p, lo:hi], P - 1, op=ALU.bitwise_and))
                link(dve.tensor_copy(m[0:p, lo:hi, 2], part[0:p, lo:hi]))
            link(dve.memset(one_row[:, :], 1.0))
            with dve.Fori(0, NT) as b:
                step = Chain(dve, count_step, b * 2)
                step(dve.tensor_scalar(match[:, :], blk[:, :], at(net.columns, b, 1), None, ALU.is_equal))
                step(dve.tensor_tensor_scan(at(counted, b, EC + 1), one_row[:, :], match[:, :], 0.0, ALU.mult, ALU.add))
                step.steps(2)
            link(dve.tensor_copy(totals[:, :], counted[:, :].rearrange("p (b j) -> p b j", b=NT)[:, :, EC]))
            dve.sem_inc(totals_ready, 1)
            dve.wait_ge(sums_ready, 1)
            link(dve.tensor_copy(ahead[:, :], ps[:, 0, 0:NT]))
            link(dve.tensor_copy(count[:, :], ps[:, 1, 0:NT]))
            link(dve.tensor_scalar(base[:, :], count[:, :], float(PAIR - 1), None, ALU.add))
            link(dve.tensor_copy(pairs_i[:, :], base[:, :]))
            link(dve.tensor_single_scalar(pairs_i[:, :], pairs_i[:, :], 8, op=ALU.arith_shift_right))
            link(dve.tensor_copy(pairs[:, :], pairs_i[:, :]))
            link(dve.tensor_tensor_scan(upto[:, :], one_row[:, 0:NT], pairs[:, :], 0.0, ALU.mult, ALU.add))
            link(dve.tensor_tensor(first[:, :], upto[:, :], pairs[:, :], ALU.subtract))
            link(dve.scalar_tensor_tensor(base[:, :], first[:, :], float(PAIR), ahead[:, :], ALU.mult, ALU.add))
            link(dve.tensor_scalar(base[:, :], base[:, :], -1.0, None, ALU.add))
            link(dve.memset(pos[:, :], 0.0))
            with dve.Fori(0, NT) as b:
                step = Chain(dve, pos_step, b * 3)
                step(dve.tensor_scalar(match[:, :], blk[:, :], at(net.columns, b, 1), None, ALU.is_equal))
                step(dve.scalar_tensor_tensor(match[:, :], at(counted, b, EC + 1), at(base, b, 1), match[:, :],
                                              ALU.add, ALU.mult))
                step(dve.tensor_tensor(pos[:, :], pos[:, :], match[:, :], ALU.add))
                step.steps(3)
            link(dve.tensor_copy(pos_i[:, :], pos[:, :]))
            dve.wait_ge(numbers, 1)
            link(dve.tensor_copy(pair_no[:, :], pair_no_i[:, :]))
            link(dve.memset(pair_blk[:, :], -1.0))
            with dve.Fori(0, NT) as b:
                step = Chain(dve, blk_step, b)
                step(dve.scalar_tensor_tensor(pair_blk[:, :], pair_no[:, :], at(first, b, 1), pair_blk[:, :],
                                              ALU.is_ge, ALU.add))
                step.steps(1)
            link(dve.tensor_copy(to.block_row[:, :], pair_blk[:, :]))
            link(dve.memset(to.keep[:, 0:1], 0.0))
            link(dve.tensor_tensor(to.keep[:, 1:PAIRS], pair_blk[:, 1:PAIRS], pair_blk[:, 0:PAIRS - 1], ALU.is_equal))
            dve.sem_inc(attrs_free_dve, 2)
            with dve.Fori(0, CH // 2) as i:
                for b in range(2):
                    q = 2 * i + b
                    dve.wait_ge(attrs_loaded[b], (i + 1) * 16 * len(to.fields))
                    dve.wait_ge(rec_free, q + 1)
                    dve.tensor_copy(pos_at[b][:, :], at(pos_i, q, JC)).then_inc(pos_copied, 1)
                    for n, (name, w) in enumerate(to.fields[1:], 1):
                        c = to.first[name]
                        dve.tensor_copy(three(b)[:, :, c:c + w], tiled(staged[b][n][:, :], w))
                    dve.tensor_copy(three(b)[:, :, to.number:rec_w], at(meta, q, JC * META).rearrange("p (j r) -> p j r", r=META))\
                        .then_inc(rest_copied, 1)
                    dve.wait_ge(rest_copied, q + 1)
                    dve.sem_inc(attrs_free_dve, 1)
            dve.wait_ge(rec_free, CH + 1)
            dve.tensor_copy(rec[0][0:EX, to.number:rec_w], m[0:EX, EC, :]).then_inc(left_copied, 1)
            dve.tensor_copy(pos_at[0][0:EX, 0:1], pos_i[0:EX, EC:EC + 1]).then_inc(left_copied, 1)


def batch_records(records, q, lo, hi):
    rows = records[bass.ds(q * (BATCH * P), BATCH * P), :]
    return rows.rearrange("(t p) r -> p t r", p=P)[:, :, lo:hi]


def l0_gnn_nodes(net):
    nc, a = net.nc, net.a
    table = net.table(D)
    with ExitStack() as ctx:
        s = net.scope("l0n", ctx)
        f = Front(s)
        w = s.sb("w", [P, DC * D])
        h = s.sb("h", [P, NT * D])
        ps = s.ps("ps", [P, 2, 512])
        w_loaded = s.sem("w_loaded")
        h_ready = s.sem("h_ready")
        h_stored = s.sem("h_stored")
        block = ctx.enter_context(nc.Block())
        wv = w[:, :].rearrange("p (c n) -> p c n", c=DC)

        @block.sync
        def _(sp):
            sp.dma_start(wv, chunked(a["L0_gnn_W_in2f"])).then_inc(w_loaded, 16)
            for i in range(NI):
                sp.wait_ge(h_ready, UN + (i + 1) * UN)
                sp.dma_start(node_rows(table, i * UN, UN), tiled(at(h, i, UN * D), D)).then_inc(h_stored, 16)
            sp.wait_ge(h_stored, NI * 16)

        @block.vector
        def _(dve):
            with dve.Fori(0, NI) as i:
                f.moments_of(dve, net, i)
                for k in range(UN):
                    t = i * UN + k
                    f.normalize(dve, net, i, k)
                    dve.wait_ge(f.normed, t + 1)
                    dve.tensor_tensor(at(net.x, t, D), at(net.x, t, D), at(f.xn, k, D), ALU.add)

        @block.tensor
        def _(pe):
            f.start_tensor(pe)
            pe.wait_ge(w_loaded, 16)
            with pe.Fori(0, NI) as i:
                for k in range(UN):
                    t = i * UN + k
                    f.turn(pe, net, t, k)
                    pe.wait_ge(f.xT_ready, UN + t + 1)
                    pe.wait_ge(h_ready, bank_free(t, k))
                    f.project(pe, t, k, ps[:, k % 2, 0:D], wv)

        @block.scalar
        def _(act):
            f.start_scalar(act)
            act.sem_inc(h_ready, UN)
            with act.Fori(0, NI) as i:
                f.root(act, net, i)
                for k in range(UN):
                    t = i * UN + k
                    f.keep(act, t, k)
                    act.wait_ge(f.projected, UN + t + 1)
                    act.activation(at(h, t, D), ps[:, k % 2, 0:D], ACT.Copy).then_inc(h_ready, 1)


LN2 = float(np.log(2.0))
CLAMP = 80.0


class Gather:

    def __init__(self, s, net, placed, table, width, lo):
        self.net, self.placed, self.table, self.width, self.lo, self.n = net, placed, table, width, lo, placed.width - lo
        self.rec = [s.sb(f"rec{b}", [P, BATCH * self.n]) for b in range(RING)]
        self.idx = [s.sb(f"idx{b}", [P, BATCH], I32) for b in range(RING)]
        self.rows = [s.sb(f"rows{b}", [P, BATCH * width]) for b in range(RING)]
        self.onehot = [s.sb(f"onehot{b}", [P, BATCH * P]) for b in range(RING)]
        self.rec_loaded = [s.sem(f"rec_loaded{b}") for b in range(RING)]
        self.hot_ready = s.sem("hot_ready")
        self.rows_loaded = [s.sem(f"rows_loaded{b}") for b in range(RING)]
        self.rec_free = s.sem("rec_free")
        self.rows_free = s.sem("rows_free")
        self.hot_free = s.sem("hot_free")
        self.pool_tick = s.sem("pool_tick")
        self.pe_tick = s.sem("pe_tick")

    def load(self, sp):
        with sp.Fori(0, NB // RING) as i:
            for b in range(RING):
                q = i * RING + b
                sp.wait_ge(self.rec_free, q + 1)
                sp.dma_start(tiled(self.rec[b][:, :], self.n), batch_records(self.placed.records, q, self.lo, self.placed.width))\
                    .then_inc(self.rec_loaded[b], 16)

    def gather(self, pool):
        with pool.Fori(0, NB // RING) as i:
            for b in range(RING):
                q = i * RING + b
                pool.wait_ge(self.hot_ready, q + 1)
                pool.wait_ge(self.rows_free, q + 1)
                pool.sem_inc(self.pool_tick, 1)
                for k in range(BATCH):
                    pool.indirect_dma_start(at(self.rows[b], k, self.width), None, self.table,
                                            bass.IndirectOffsetOnAxis(self.idx[b][:, k:k + 1], 0))\
                        .then_inc(self.rows_loaded[b], 16)

    def column(self, b, c, k=None):
        c -= self.lo
        if k is None:
            return tiled(self.rec[b][:, :], self.n)[:, :, c]
        return self.rec[b][:, k * self.n + c:k * self.n + c + 1]

    def columns(self, b, k, c, w):
        c -= self.lo
        return self.rec[b][:, k * self.n + c:k * self.n + c + w]

    def hot(self, dve, q, i, b):
        dve.wait_ge(self.rec_loaded[b], i * 16 + 16)
        dve.wait_ge(self.hot_free, q + 1)
        dve.tensor_copy(self.idx[b][:, :], self.column(b, self.placed.far))
        for k in range(BATCH):
            ins = dve.tensor_scalar(at(self.onehot[b], k, P), self.net.columns[:, :], self.column(b, self.placed.near, k),
                                    None, ALU.is_equal)
        ins.then_inc(self.hot_ready, 1)

    def wait_rows(self, eng, i, b):
        eng.wait_ge(self.rows_loaded[b], i * 16 * BATCH + 16 * BATCH)


def skewed(eng, *stages, ring=RING, total=NB):
    deepest = max(lag for lag, _ in stages)
    assert deepest <= ring and total % ring == 0

    def alone(t):
        for lag, step in stages:
            q = t - lag
            if 0 <= q < total:
                step(q, q // ring, q % ring)

    for t in range(ring):
        alone(t)
    with eng.Fori(0, total // ring - 1) as j:
        for u in range(ring):
            for lag, step in stages:
                b = (u - lag) % ring
                i = j + 1 if u >= lag else j
                step(i * ring + b, i, b)
    for t in range(total, total + deepest):
        alone(t)


def block_of(eng, placed, pair):
    return eng.value_load(placed.block_row[0:1, bass.ds(pair, 1)], min_val=0, max_val=NT - 1)


def open_sums(net, pe, ps, opens):
    width = ps.shape[1]
    for lo in range(0, width, 512):
        n = min(512, width - lo)
        ins = pe.matmul(ps[:, lo:lo + n], net.zeros[:, 0:P], net.zeros[:, 0:n], start=opens, stop=not opens)
    return ins


def l0_gnn_edges(net):
    nc, a = net.nc, net.a
    HC = D // P
    WIDE = BATCH * P
    with ExitStack() as ctx:
        s = net.scope("l0e", ctx)
        g = Gather(s, net, net.by_src, net.table(D), D, 0)
        wf1 = s.sb("wf1", [64, D])
        wf2 = s.sb("wf2", [P, HC * D])
        bf1 = s.sb("bf1", [P, HC])
        bf1_ln2 = s.sb("bf1_ln2", [P, HC])
        bf2 = s.sb("bf2", [P, D])
        half = s.sb("half", [P, 1])
        rbfT = [s.sb(f"rbfT{b}", [64, WIDE]) for b in range(RING)]
        raised = [s.sb(f"raised{c}", [P, WIDE]) for c in range(HC)]
        hidT = [s.sb(f"hidT{b}", [P, HC * WIDE]) for b in range(RING)]
        shifted = s.sb("shifted", [P, BATCH * D])
        msg = [s.sb(f"msg{b}", [P, BATCH * D]) for b in range(RING)]
        total = [s.sb(f"total{k}", [P, D]) for k in range(TWO)]
        ps_t = s.ps("ps_t", [64, WIDE])
        ps_h = s.ps("ps_h", [P, HC, 512])
        ps_w = s.ps("ps_w", [P, TWO, 512])
        ps_s = s.ps("ps_s", [P, TWO, 512])
        loaded = s.sem("loaded")
        cleared = s.sem("cleared")
        turned = s.sem("turned")
        rbf_ready = s.sem("rbf_ready")
        hidden = s.sem("hidden")
        raise_step = s.sem("raise_step")
        powered = s.sem("powered")
        logged = s.sem("logged")
        hid_ready = s.sem("hid_ready")
        filters = s.sem("filters")
        shifted_ready = s.sem("shifted_ready")
        msg_ready = s.sem("msg_ready")
        summed = s.sem("summed")
        total_ready = s.sem("total_ready")
        flushed = s.sem("flushed")
        act_tick = s.sem("act_tick")
        block = ctx.enter_context(nc.Block())

        @block.sync
        def _(sp):
            sp.dma_start(wf1[:, :], a["L0_gnn_Wf1"]).then_inc(loaded, 16)
            sp.dma_start(wf2[:, :].rearrange("p (c n) -> p c n", c=HC), chunked(a["L0_gnn_Wf2"])).then_inc(loaded, 16)
            for c in range(HC):
                sp.dma_start(bf1[:, c:c + 1], column(a["L0_gnn_bf1"][c * P:(c + 1) * P])).then_inc(loaded, 16)
            sp.dma_start(bf2[:, :], spread(a["L0_gnn_bf2"])).then_inc(loaded, 16)
            g.load(sp)

        @block.gpsimd
        def _(pool):
            g.gather(pool)

        @block.vector
        def _(dve):
            dve.sem_inc(g.rec_free, RING)
            dve.sem_inc(g.rows_free, RING)
            dve.memset(net.work[:, 0:NT * D], 0.0).then_inc(cleared, 1)
            dve.memset(total[(PAIRS - 1) % TWO][:, :], 0.0).then_inc(cleared, 1)
            dve.memset(half[:, :], 0.5).then_inc(cleared, 1)
            dve.wait_ge(loaded, 80)
            dve.tensor_scalar(bf1_ln2[:, :], bf1[:, :], -LN2, None, ALU.add).then_inc(cleared, 1)
            dve.sem_inc(hid_ready, HC)
            dve.sem_inc(shifted_ready, TWO)
            dve.sem_inc(msg_ready, TWO)
            dve.sem_inc(total_ready, TWO)
            dve.wait_ge(cleared, 4)

            def clamp(q, i, b):
                for c in range(HC):
                    dve.wait_ge(hidden, HC * q + c + 1)
                    dve.tensor_scalar(raised[c][:, :], ps_h[:, c, :], bf1[:, c:c + 1], CLAMP, ALU.add, ALU.min)\
                        .then_inc(raise_step, 1)

            def hide(q, i, b):
                for c in range(HC):
                    dve.wait_ge(logged, HC * q + c + 1)
                    dve.scalar_tensor_tensor(at(hidT[b], c, WIDE), ps_h[:, c, :], bf1_ln2[:, c:c + 1], raised[c][:, :],
                                             ALU.add, ALU.max).then_inc(hid_ready, 1)

            def message(q, i, b):
                g.wait_rows(dve, i, b)
                for k in range(TWO):
                    n = q * TWO + k
                    dve.wait_ge(filters, n + 1)
                    dve.wait_ge(msg_ready, n + 1)
                    dve.tensor_tensor(tiled(at(shifted, k, 2 * D), D), tiled(ps_w[:, k, 0:2 * D], D),
                                      bf2[:, :].unsqueeze(1).to_broadcast([P, 2, D]), ALU.add).then_inc(shifted_ready, 1)
                    dve.wait_ge(shifted_ready, n + TWO + 1)
                    for m in (2 * k, 2 * k + 1):
                        ins = dve.scalar_tensor_tensor(at(msg[b], m, D), at(shifted, m, D), g.column(b, g.placed.number, m),
                                                       at(g.rows[b], m, D), ALU.mult, ALU.mult)
                    ins.then_inc(msg_ready, 1)
                dve.wait_ge(msg_ready, q * TWO + 2 * TWO)
                dve.sem_inc(g.rec_free, 1)
                dve.sem_inc(g.rows_free, 1)

            def add(q, i, b):
                for k in range(TWO):
                    n = q * TWO + k
                    dve.wait_ge(summed, n + 1)
                    dve.wait_ge(total_ready, n + TWO)
                    dve.wait_ge(flushed, n + 1)
                    dve.scalar_tensor_tensor(total[k][:, :], total[1 - k][:, :], g.placed.keep[:, bass.ds(n, 1)],
                                             ps_s[:, k, 0:D], ALU.mult, ALU.add).then_inc(total_ready, 1)

            skewed(dve, (1, clamp), (0, lambda q, i, b: g.hot(dve, q, i, b)), (2, message), (1, hide), (3, add))

        @block.tensor
        def _(pe):
            pe.sem_inc(g.hot_free, RING)
            pe.wait_ge(loaded, 80)

            def turn(q, i, b):
                pe.wait_ge(g.rec_loaded[b], i * 16 + 16)
                pe.wait_ge(rbf_ready, q + 1)
                pe.sem_inc(g.pe_tick, 1)
                for k in range(BATCH):
                    ins = pe.transpose(at(ps_t, k, P), g.columns(b, k, 0, 64), net.ident[:, :])
                ins.then_inc(turned, 1)

            def hide(q, i, b):
                pe.wait_ge(rbf_ready, q + 2)
                for c in range(HC):
                    pe.wait_ge(hid_ready, HC * q + c + 1)
                    pe.matmul(ps_h[:, c, :], wf1[:, c * P:(c + 1) * P], rbfT[b][:, :], start=True, stop=True)\
                        .then_inc(hidden, 1)

            def filter(q, i, b):
                pe.wait_ge(hid_ready, HC * q + 2 * HC)
                for k in range(TWO):
                    n = q * TWO + k
                    pe.wait_ge(shifted_ready, n + 1)
                    for m in range(2):
                        for c in range(HC):
                            ins = pe.matmul(ps_w[:, k, m * D:(m + 1) * D],
                                            hidT[b][:, c * WIDE + (2 * k + m) * P:c * WIDE + (2 * k + m + 1) * P],
                                            at(wf2, c, D), start=c == 0, stop=c == HC - 1)
                    ins.then_inc(filters, 1)

            def add(q, i, b):
                for k in range(TWO):
                    n = q * TWO + k
                    pe.wait_ge(msg_ready, n + TWO + 1)
                    pe.wait_ge(total_ready, n + 1)
                    for m in range(2):
                        ins = pe.matmul(ps_s[:, k, 0:D], at(g.onehot[b], 2 * k + m, P), at(msg[b], 2 * k + m, D),
                                        start=m == 0, stop=m == 1)
                    ins.then_inc(summed, 1)
                pe.wait_ge(summed, q * TWO + TWO)
                pe.sem_inc(g.hot_free, 1)

            skewed(pe, (1, hide), (2, filter), (0, turn), (3, add))

        @block.scalar
        def _(act):
            act.sem_inc(rbf_ready, 1)
            act.sem_inc(flushed, TWO)
            act.wait_ge(cleared, 4)

            def turn(q, i, b):
                act.wait_ge(turned, q + 1)
                act.activation(rbfT[b][:, :], ps_t[:, :], ACT.Copy).then_inc(rbf_ready, 1)

            def power(q, i, b):
                for c in range(HC):
                    act.wait_ge(raise_step, HC * q + c + 1)
                    act.activation(raised[c][:, :], raised[c][:, :], ACT.Exp).then_inc(powered, 1)
                for c in range(HC):
                    act.wait_ge(powered, HC * q + c + 1)
                    act.activation(raised[c][:, :], raised[c][:, :], ACT.Ln, bias=half[:, :], scale=0.5).then_inc(logged, 1)

            def flush(q, i, b):
                for k in range(TWO):
                    n = q * TWO + k
                    blk = block_of(act, g.placed, n)
                    act.wait_ge(total_ready, n + TWO + 1)
                    act.wait_ge(flushed, n + TWO)
                    act.sem_inc(act_tick, 1)
                    act.activation(at(net.work, blk, D), total[k][:, :], ACT.Copy).then_inc(flushed, 1)

            skewed(act, (1, power), (0, turn), (3, flush))


def l0_gnn_update(net):
    nc, a = net.nc, net.a
    with ExitStack() as ctx:
        s = net.scope("l0u", ctx)
        f = Front(s)
        wo1 = s.sb("wo1", [P, DC * D])
        wo2 = s.sb("wo2", [P, DC * D])
        bo1 = s.sb("bo1", [P, DC])
        bo1_ln2 = s.sb("bo1_ln2", [P, DC])
        bo2 = s.sb("bo2", [P, D])
        half = s.sb("half", [P, 1])
        raised = s.sb("raised", [P, D])
        hidT = s.sb("hidT", [P, D])
        ps_h = s.ps("ps_h", [P, 512])
        ps_m = s.ps("ps_m", [P, 512])
        loaded = s.sem("loaded")
        set_up = s.sem("set_up")
        raise_step = s.sem("raise_step")
        powered = s.sem("powered")
        hid_ready = s.sem("hid_ready")
        updates = s.sem("updates")
        biased = s.sem("biased")
        block = ctx.enter_context(nc.Block())

        @block.sync
        def _(sp):
            for w, into in (("L0_gnn_Wo1", wo1), ("L0_gnn_Wo2", wo2)):
                sp.dma_start(into[:, :].rearrange("p (c n) -> p c n", c=DC), chunked(a[w])).then_inc(loaded, 16)
            for c in range(DC):
                sp.dma_start(bo1[:, c:c + 1], column(a["L0_gnn_bo1"][c * P:(c + 1) * P])).then_inc(loaded, 16)
            sp.dma_start(bo2[:, :], spread(a["L0_gnn_bo2"])).then_inc(loaded, 16)

        @block.vector
        def _(dve):
            link = Chain(dve, set_up)
            dve.wait_ge(loaded, 80)
            link(dve.memset(half[:, :], 0.5))
            link(dve.tensor_scalar(bo1_ln2[:, :], bo1[:, :], -LN2, None, ALU.add))
            with dve.Fori(0, NI) as i:
                for k in range(UN):
                    t = i * UN + k
                    f.take(dve, t, k, lambda xn: dve.tensor_copy(xn, at(net.work, t, D)))
                    dve.wait_ge(f.projected, UN + t + 1)
                    for c in range(DC):
                        ins = dve.tensor_scalar(at(raised, c, P), at(ps_h, c, P), bo1[:, c:c + 1], CLAMP, ALU.add, ALU.min)
                    ins.then_inc(raise_step, 1)
                    dve.wait_ge(powered, 2 * t + 2)
                    for c in range(DC):
                        ins = dve.scalar_tensor_tensor(at(hidT, c, P), at(ps_h, c, P), bo1_ln2[:, c:c + 1],
                                                       at(raised, c, P), ALU.add, ALU.max)
                    ins.then_inc(hid_ready, 1)
                    dve.tensor_tensor(at(net.x, t, D), at(net.x, t, D), bo2[:, :], ALU.add).then_inc(biased, 1)
                    dve.wait_ge(updates, t + 1)
                    dve.wait_ge(biased, 2 * t + 1)
                    dve.tensor_tensor(at(net.x, t, D), at(net.x, t, D), ps_m[:, 0:D], ALU.add).then_inc(biased, 1)

        @block.tensor
        def _(pe):
            f.start_tensor(pe)
            pe.wait_ge(loaded, 80)
            with pe.Fori(0, NI) as i:
                for k in range(UN):
                    t = i * UN + k
                    f.turn(pe, net, t, k)
                    pe.wait_ge(f.xT_ready, UN + t + 1)
                    for m in range(DC):
                        for c in range(DC):
                            ins = pe.matmul(at(ps_h, m, P), wo1[:, c * D + m * P:c * D + (m + 1) * P], f.lhsT(k, c),
                                            start=c == 0, stop=c == DC - 1)
                    ins.then_inc(f.projected, 1)
                    pe.wait_ge(hid_ready, t + 1)
                    for c in range(DC):
                        ins = pe.matmul(ps_m[:, 0:D], at(hidT, c, P), at(wo2, c, D), start=c == 0, stop=c == DC - 1)
                    ins.then_inc(updates, 1)

        @block.scalar
        def _(act):
            f.start_scalar(act)
            act.wait_ge(set_up, 1)
            with act.Fori(0, NI) as i:
                for k in range(UN):
                    t = i * UN + k
                    f.keep(act, t, k)
                    act.wait_ge(raise_step, t + 1)
                    act.activation(raised[:, :], raised[:, :], ACT.Exp).then_inc(powered, 1)
                    act.wait_ge(powered, 2 * t + 1)
                    act.activation(raised[:, :], raised[:, :], ACT.Ln, bias=half[:, :], scale=0.5).then_inc(powered, 1)


GROUP = UN * P
PART = GROUP // 2


def turn_rows(pe, net, out, rows):
    return pe.transpose(out, rows, net.ident[0:rows.shape[0], 0:rows.shape[0]])


def moe(net, name, router, bias, choose, layers, last, last_bias, keeps_tokens=False):
    nc, a = net.nc, net.a
    with ExitStack() as ctx:
        s = net.scope(name, ctx)
        xT = s.sb("xT", [P, DC * NP])
        logits = s.sb("logits", [P, NT * EXPERTS])
        mix = s.sb("mix", [P, NT * EXPERTS])
        moe_front(net, name, logits, router, keeps_tokens, xT=xT)
        choose(net, name, logits, bias, mix)
        moe_bias(net, name, mix, a[last_bias], net.x)
        moe_experts(net, name, xT, mix, net.x, layers, a[last])


def moe_front(net, name, logits, router, keeps_tokens=False, clears_work=False, xT=None, xn=None):
    nc, a = net.nc, net.a
    by_expert = router.shape[0] == EXPERTS
    with ExitStack() as ctx:
        s = net.scope(name + "f", ctx)
        f = Front(s)
        rows = s.sb("rows", [EXPERTS, D])
        w = s.sb("w", [P, DC * EXPERTS])
        ps = s.ps("ps", [P, 2, 512])
        w_loaded = s.sem("w_loaded")
        w_turned = s.sem("w_turned")
        w_ready = s.sem("w_ready")
        copied = s.sem("copied")
        logits_ready = s.sem("logits_ready")
        pool_tick = s.sem("pool_tick")
        block = ctx.enter_context(nc.Block())
        wv = w[:, :].rearrange("p (c n) -> p c n", c=DC)

        @block.sync
        def _(sp):
            if by_expert:
                sp.dma_start(rows[:, :], router).then_inc(w_loaded, 16)
            else:
                sp.dma_start(wv, chunked(router)).then_inc(w_loaded, 16)

        @block.gpsimd
        def _(pool):
            pool.sem_inc(copied, UN)
            with pool.Fori(0, NI) as i:
                for k in range(UN):
                    t = i * UN + k
                    if xn is not None:
                        pool.wait_ge(f.normed, t + 1)
                        pool.sem_inc(pool_tick, 1)
                        pool.tensor_copy(at(xn, t, D), at(f.xn, k, D)).then_inc(copied, 1)
                        continue
                    pool.wait_ge(f.xT_ready, UN + t + 1)
                    pool.sem_inc(pool_tick, 1)
                    for c in range(DC):
                        ins = pool.tensor_copy(xT[:, bass.ds(c * NP + t * P, P)], f.lhsT(k, c))
                    ins.then_inc(copied, 1)

        @block.vector
        def _(dve):
            dve.sem_inc(logits_ready, UN)
            if clears_work:
                dve.memset(net.work[:, 0:NT * D], 0.0)
            dve.wait_ge(w_loaded, 16)
            if by_expert:
                dve.wait_ge(w_turned, 1)
                dve.tensor_copy(w[:, :], ps[:, 0, 0:DC * EXPERTS]).then_inc(w_ready, 1)
            else:
                dve.sem_inc(w_ready, 1)
            with dve.Fori(0, NI) as i:
                f.moments_of(dve, net, i)
                for k in range(UN):
                    t = i * UN + k
                    if xn is not None:
                        dve.wait_ge(copied, t + 1)
                    f.normalize(dve, net, i, k)
                for k in range(UN):
                    t = i * UN + k
                    if keeps_tokens:
                        dve.wait_ge(f.normed, t + 1)
                        dve.tensor_tensor(at(net.x, t, D), at(net.x, t, D), at(f.xn, k, D), ALU.add)
                    dve.wait_ge(f.projected, UN + t + 1)
                    dve.tensor_copy(at(logits, t, EXPERTS), ps[:, k % 2, 0:EXPERTS]).then_inc(logits_ready, 1)

        @block.tensor
        def _(pe):
            f.start_tensor(pe)
            if by_expert:
                pe.wait_ge(w_loaded, 16)
                for c in range(DC):
                    ins = turn_rows(pe, net, ps[:, 0, c * EXPERTS:(c + 1) * EXPERTS], rows[:, c * P:(c + 1) * P])
                ins.then_inc(w_turned, 1)
            pe.wait_ge(w_ready, 1)
            with pe.Fori(0, NI) as i:
                for k in range(UN):
                    t = i * UN + k
                    f.turn(pe, net, t, k)
                    pe.wait_ge(f.xT_ready, UN + t + 1)
                    pe.wait_ge(logits_ready, bank_free(t, k))
                    f.project(pe, t, k, ps[:, k % 2, 0:EXPERTS], wv)

        @block.scalar
        def _(act):
            f.start_scalar(act)
            with act.Fori(0, NI) as i:
                f.root(act, net, i)
                for k in range(UN):
                    t = i * UN + k
                    if xT is not None:
                        act.wait_ge(copied, t + 1)
                    f.keep(act, t, k)


def by_expert(t):
    return tiled(t[:, :], EXPERTS)


def over_experts(t):
    return t[:, :].unsqueeze(2).to_broadcast([P, NT, EXPERTS])


def first_best(dve, link, net, vals, best, onehot, score, top):
    link(dve.tensor_reduce(best[:, :], by_expert(vals), AX.X, ALU.max))
    link(dve.tensor_tensor(by_expert(score), by_expert(vals), over_experts(best), ALU.is_equal))
    link(dve.tensor_tensor(by_expert(score), by_expert(score), by_expert(net.rank8), ALU.mult))
    link(dve.tensor_reduce(top[:, :], by_expert(score), AX.X, ALU.max))
    link(dve.tensor_tensor(by_expert(onehot), by_expert(score), over_experts(top), ALU.is_equal))


def softmax_experts(dve, link, act_exp, vals, best, out, total):
    link(dve.tensor_reduce(best[:, :], by_expert(vals), AX.X, ALU.max))
    link(dve.tensor_tensor(by_expert(out), by_expert(vals), over_experts(best), ALU.subtract))
    act_exp()
    link(dve.tensor_reduce(total[:, :], by_expert(out), AX.X, ALU.add))
    link(dve.reciprocal(total[:, :], total[:, :]))
    link(dve.tensor_tensor(by_expert(out), by_expert(out), over_experts(total), ALU.mult))


def choose(kind):
    def stage(net, name, logits, bias, mix):
        nc = net.nc
        with ExitStack() as ctx:
            s = net.scope(name + "c", ctx)
            lg = s.sb("lg", [P, NT * EXPERTS])
            bias_row = s.sb("bias_row", [P, EXPERTS])
            probs = s.sb("probs", [P, NT * EXPERTS])
            score = s.sb("score", [P, NT * EXPERTS])
            one = s.sb("one", [P, NT * EXPERTS])
            two = s.sb("two", [P, NT * EXPERTS])
            rest = s.sb("rest", [P, NT * EXPERTS])
            ones_row = s.sb("ones_row", [P, NT])
            best = s.sb("best", [P, NT])
            second = s.sb("second", [P, NT])
            total = s.sb("total", [P, NT])
            top = s.sb("top", [P, NT])
            ps = s.ps("ps", [P, 2, 512])
            loaded = s.sem("loaded")
            chain = s.sem("chain")
            to_power = s.sem("to_power")
            powered = s.sem("powered")
            one_ready = s.sem("one_ready")
            counted = s.sem("counted")
            to = mix if isinstance(mix, Dispatch) else None
            if to:
                ahead = s.sb("ahead", [P, NT * EXPERTS])
                either = s.sb("either", [P, NT * EXPERTS])
                start = s.sb("start", [P, EXPERTS])
                groups = s.sb("groups", [P, EXPERTS])
                groups_i = s.sb("groups_i", [P, EXPERTS], I32)
                slot = s.sb("slot", [P, NT])
                room = s.sb("room", [P, NT])
                group_no_i = s.sb("group_no_i", [P, to.groups], I32)
                group_no = s.sb("group_no", [P, to.groups])
                number = s.sb("number", [P, to.groups])
                numbered = s.sem("numbered")
            block = ctx.enter_context(nc.Block())

            @block.sync
            def _(sp):
                if bias is not None:
                    sp.dma_start(bias_row[:, :], spread(bias)).then_inc(loaded, 16)

            @block.scalar
            def _(act):
                power = {"probs": probs, "pair": total, "all": probs, "capacity": probs}[kind]
                act.wait_ge(to_power, 1)
                act.activation(power[:, :], power[:, :], ACT.Exp).then_inc(powered, 1)

            @block.tensor
            def _(pe):
                if to:
                    pe.wait_ge(one_ready, 1)
                    pe.matmul(ps[:, 0, 0:NT * EXPERTS], net.before[:, :], either[:, :], start=True, stop=True)
                    pe.matmul(ps[:, 1, 0:NT * EXPERTS], net.ones[:, :], either[:, :], start=True, stop=True)\
                        .then_inc(counted, 1)

            @block.gpsimd
            def _(pool):
                if to:
                    pool.iota(group_no_i[:, :], pattern=[[1, to.groups]], base=0, channel_multiplier=0).then_inc(numbered, 1)

            @block.vector
            def _(dve):
                link = Chain(dve, chain)

                def act_exp():
                    dve.sem_inc(to_power, 1)
                    dve.wait_ge(powered, 1)

                if bias is None:
                    link(dve.tensor_copy(lg[:, :], logits[:, :]))
                else:
                    dve.wait_ge(loaded, 16)
                    link(dve.tensor_tensor(by_expert(lg), by_expert(logits),
                                           bias_row[:, :].unsqueeze(1).to_broadcast([P, NT, EXPERTS]), ALU.add))
                if kind == "all":
                    softmax_experts(dve, link, act_exp, lg, best, probs, total)
                    link(dve.tensor_copy(mix[:, :], probs[:, :]))
                    return
                vals = lg
                if kind != "pair":
                    softmax_experts(dve, link, act_exp, lg, best, probs, total)
                    vals = probs
                first_best(dve, link, net, vals, best, one, score, top)

                def rank():
                    dve.sem_inc(one_ready, 1)
                    dve.wait_ge(counted, 1)
                    link(dve.memset(ones_row[:, :], 1.0))
                    link(dve.tensor_copy(score[:, :], ps[:, 1, 0:NT * EXPERTS]))
                    for e in range(EXPERTS):
                        link(dve.tensor_tensor_scan(by_expert(rest)[:, :, e], ones_row[:, :], by_expert(score)[:, :, e],
                                                    0.0, ALU.mult, ALU.add))
                    link(dve.tensor_tensor(ahead[:, :], rest[:, :], score[:, :], ALU.subtract))
                    link(dve.tensor_tensor(ahead[:, :], ahead[:, :], ps[:, 0, 0:NT * EXPERTS], ALU.add))

                def place(onehot, places, into):
                    link(dve.tensor_tensor(score[:, :], onehot[:, :], places[:, :], ALU.mult))
                    link(dve.tensor_reduce(slot[:, :], by_expert(score), AX.X, ALU.add))
                    link(dve.tensor_copy(into, slot[:, :]))

                if kind == "capacity":
                    link(dve.tensor_copy(either[:, :], one[:, :]))
                    rank()
                    dve.wait_ge(numbered, 1)
                    link(dve.tensor_single_scalar(to.expert_row[:, :], group_no_i[:, :], (ROOM // SLICE).bit_length() - 1,
                                                  op=ALU.arith_shift_right))
                    link(dve.tensor_scalar(two[:, :], net.rank8[:, :], -float(ROOM), float(ROOM * EXPERTS), ALU.mult, ALU.add))
                    link(dve.tensor_tensor(rest[:, :], ahead[:, :], two[:, :], ALU.add))
                    link(dve.tensor_scalar(either[:, :], ahead[:, :], float(CAPACITY), None, ALU.is_ge))
                    link(dve.scalar_tensor_tensor(rest[:, :], either[:, :], float(to.groups * SLICE), rest[:, :], ALU.mult, ALU.add))
                    place(one, rest, to.slot_in[0][:, :])
                    link(dve.tensor_scalar(ahead[:, :], ahead[:, :], float(CAPACITY - 1), None, ALU.min))
                    link(dve.tensor_tensor(rest[:, :], ahead[:, :], two[:, :], ALU.add))
                    place(one, rest, to.slot_out[0][:, :])
                    link(dve.tensor_tensor(score[:, :], one[:, :], either[:, :], ALU.mult))
                    link(dve.tensor_reduce(room[:, :], by_expert(score), AX.X, ALU.add))
                    link(dve.tensor_scalar(room[:, :], room[:, :], -1.0, 1.0, ALU.mult, ALU.add))
                    link(dve.tensor_tensor(to.weight[0][:, :], best[:, :], room[:, :], ALU.mult))
                    return
                link(dve.scalar_tensor_tensor(rest[:, :], one[:, :], -HUGE, vals[:, :], ALU.mult, ALU.add))
                first_best(dve, link, net, rest, second, two, score, top)
                if kind == "pair":
                    link(dve.tensor_tensor(total[:, :], second[:, :], best[:, :], ALU.subtract))
                    act_exp()
                    link(dve.tensor_copy(second[:, :], total[:, :]))
                    link(dve.memset(best[:, :], 1.0))
                    link(dve.tensor_scalar(total[:, :], total[:, :], 1.0, None, ALU.add))
                else:
                    link(dve.tensor_tensor(total[:, :], best[:, :], second[:, :], ALU.add))
                    link(dve.tensor_scalar(total[:, :], total[:, :], 1e-12, None, ALU.max))
                link(dve.reciprocal(total[:, :], total[:, :]))
                link(dve.tensor_tensor(best[:, :], best[:, :], total[:, :], ALU.mult))
                link(dve.tensor_tensor(second[:, :], second[:, :], total[:, :], ALU.mult))
                if to:
                    link(dve.tensor_copy(to.weight[0][:, :], best[:, :]))
                    link(dve.tensor_copy(to.weight[1][:, :], second[:, :]))
                    for t in (one, two):
                        tail = at(t, NT - 1, EXPERTS)
                        link(dve.tensor_scalar(tail, tail, net.before[:, TAIL:TAIL + 1], None, ALU.mult))
                    link(dve.tensor_tensor(either[:, :], one[:, :], two[:, :], ALU.add))
                    rank()
                    link(dve.tensor_scalar(start[:, :], at(rest, NT - 1, EXPERTS), float(SLICE - 1), None, ALU.add))
                    link(dve.tensor_copy(groups_i[:, :], start[:, :]))
                    link(dve.tensor_single_scalar(groups_i[:, :], groups_i[:, :], SLICE.bit_length() - 1, op=ALU.arith_shift_right))
                    link(dve.tensor_copy(groups[:, :], groups_i[:, :]))
                    link(dve.tensor_tensor_scan(start[:, :], ones_row[:, 0:EXPERTS], groups[:, :], 0.0, ALU.mult, ALU.add))
                    link(dve.tensor_tensor(start[:, :], start[:, :], groups[:, :], ALU.subtract))
                    dve.wait_ge(numbered, 1)
                    link(dve.tensor_copy(group_no[:, :], group_no_i[:, :]))
                    link(dve.memset(number[:, :], -1.0))
                    for e in range(EXPERTS):
                        link(dve.scalar_tensor_tensor(number[:, :], group_no[:, :], start[:, e:e + 1], number[:, :],
                                                      ALU.is_ge, ALU.add))
                    link(dve.tensor_copy(to.expert_row[:, :], number[:, :]))
                    link(dve.tensor_scalar(start[:, :], start[:, :], float(SLICE), None, ALU.mult))
                    link(dve.tensor_tensor(by_expert(rest), by_expert(ahead),
                                           start[:, :].unsqueeze(1).to_broadcast([P, NT, EXPERTS]), ALU.add))
                    place(one, rest, to.slot_in[0][:, :])
                    place(two, rest, to.slot_in[1][:, :])
                    return
                link(dve.tensor_tensor(by_expert(one), by_expert(one), over_experts(best), ALU.mult))
                link(dve.tensor_tensor(by_expert(two), by_expert(two), over_experts(second), ALU.mult))
                link(dve.tensor_tensor(mix[:, :], one[:, :], two[:, :], ALU.add))
    return stage


def moe_bias(net, name, mix, bias, acc):
    nc = net.nc
    with ExitStack() as ctx:
        s = net.scope(name + "b", ctx)
        rows = s.sb("rows", [EXPERTS, D])
        own = s.sb("own", [P, 2 * EXPERTS])
        ownT = s.sb("ownT", [EXPERTS, 2 * P])
        ps_t = s.ps("ps_t", [EXPERTS, 2, 512])
        ps = s.ps("ps", [P, 2, 512])
        loaded = s.sem("loaded")
        taken = s.sem("taken")
        turned = s.sem("turned")
        kept = s.sem("kept")
        biases = s.sem("biases")
        added = s.sem("added")
        s_tick = s.sem("tick")
        block = ctx.enter_context(nc.Block())

        @block.sync
        def _(sp):
            sp.dma_start(rows[:, :], bias).then_inc(loaded, 16)

        @block.vector
        def _(dve):
            with dve.Fori(0, NT) as t:
                dve.tensor_copy(own[:, 0:EXPERTS], at(mix, t, EXPERTS)).then_inc(taken, 1)
                dve.wait_ge(biases, t + 1)
                dve.tensor_tensor(at(acc, t, D), at(acc, t, D), ps[:, 0, 0:D], ALU.add).then_inc(added, 1)

        @block.tensor
        def _(pe):
            pe.wait_ge(loaded, 16)
            with pe.Fori(0, NT) as t:
                pe.wait_ge(taken, t + 1)
                pe.sem_inc(s_tick, 1)
                pe.transpose(ps_t[:, 0, 0:P], own[:, 0:EXPERTS], net.ident[:, :]).then_inc(turned, 1)
                pe.wait_ge(kept, t + 1)
                pe.matmul(ps[:, 0, 0:D], ownT[:, 0:P], rows[:, :], start=True, stop=True).then_inc(biases, 1)

        @block.scalar
        def _(act):
            with act.Fori(0, NT) as t:
                act.wait_ge(turned, t + 1)
                act.activation(ownT[:, 0:P], ps_t[:, 0, 0:P], ACT.Copy).then_inc(kept, 1)


def moe_experts(net, name, xT, mix, acc, layers, last):
    nc, a = net.nc, net.a
    widths = [DC] + [a[w].shape[2] // P for w, _, _ in layers]
    halves = [2 * n for n in widths[1:]]
    starts = [sum(halves[:l]) for l in range(len(layers) + 1)]
    H = starts[-1]
    assert all(n % 4 == 0 for n in halves)
    with ExitStack() as ctx:
        s = net.scope(name + "e", ctx)
        w_in = [[s.sb(f"w{l}_{b}", [P, widths[l] * widths[l + 1] * P]) for b in range(2)] for l in range(len(layers))]
        w_out = [s.sb(f"wo_{b}", [P, widths[-1] * D]) for b in range(2)]
        hT = [s.sb(f"hT{l}", [P, widths[l + 1] * GROUP]) for l in range(len(layers))]
        vec_rows = [[s.sb(f"vr{l}_{v}", [EXPERTS * widths[l + 1], P]) for v in range(len(vs))]
                    for l, (_, vs, _) in enumerate(layers)]
        vec = [[s.sb(f"v{l}_{v}", [P, EXPERTS * widths[l + 1]]) for v in range(len(vs))]
               for l, (_, vs, _) in enumerate(layers)]
        own = [[s.sb(f"own{l}_{v}", [P, widths[l + 1]]) for v in range(min(2, len(vs)))]
               for l, (_, vs, _) in enumerate(layers)]
        ps_h = s.ps("ps_h", [P, 4, 512])
        ps_y = s.ps("ps_y", [P, 4, 512])
        vec_loaded = s.sem("vec_loaded")
        vec_turned = s.sem("vec_turned")
        vec_step = s.sem("vec_step")
        vec_rooted = s.sem("vec_rooted")
        vec_ready = s.sem("vec_ready")
        w_loaded = [s.sem(f"w_loaded{b}") for b in range(2)]
        products = s.sem("products")
        active = s.sem("active")
        outs = s.sem("outs")
        own_ready = s.sem("own_ready")
        pe_tick = s.sem("pe_tick")
        act_tick = s.sem("act_tick")
        mixed = s.sem("mixed")
        block = ctx.enter_context(nc.Block())
        vectors = [(l, v) for l, (_, vs, _) in enumerate(layers) for v in range(len(vs))]
        WL = 16 * (len(layers) + 1)

        def load(sp, e, b):
            for l, (w, _, _) in enumerate(layers):
                k, n = a[w].shape[1], a[w].shape[2]
                flat = a[w].rearrange("e k n -> (e k) n")[bass.ds(e * k, k), :]
                sp.dma_start(w_in[l][b][:, :].rearrange("p (c n) -> p c n", n=n), chunked(flat)).then_inc(w_loaded[b], 16)
            k = last.shape[1]
            flat = last.rearrange("e k n -> (e k) n")[bass.ds(e * k, k), :]
            sp.dma_start(tiled(w_out[b][:, :], D), chunked(flat)).then_inc(w_loaded[b], 16)

        @block.sync
        def _(sp):
            for l, v in vectors:
                sp.dma_start(vec_rows[l][v][:, :], a[layers[l][1][v]].rearrange("e (c p) -> (e c) p", p=P))\
                    .then_inc(vec_loaded, 16)
            for b in range(2):
                load(sp, b, b)
            with sp.Fori(1, EXPERTS // 2) as i:
                for b in range(2):
                    sp.wait_ge(outs, UN + (2 * i + b - 1) * NT)
                    load(sp, 2 * i + b, b)

        @block.tensor
        def _(pe):
            pe.sem_inc(outs, UN)
            pe.wait_ge(vec_loaded, 16 * len(vectors))
            for n, (l, v) in enumerate(vectors):
                turn_rows(pe, net, ps_h[:, n % 4, 64 * (n // 4):64 * (n // 4) + EXPERTS * widths[l + 1]],
                          vec_rows[l][v][:, :]).then_inc(vec_turned, 1)
            pe.wait_ge(vec_ready, 1)

            def expert(i, e, b):
                pe.wait_ge(w_loaded[b], i * WL + WL)
                pe.sem_inc(pe_tick, 1)
                with pe.Fori(0, NI) as g:
                    q = e * NI + g
                    for l in range(len(layers)):
                        for c in range(halves[l]):
                            m, half = c // 2, c % 2
                            n = starts[l] + c
                            if l and c == 0:
                                pe.wait_ge(active, q * H + starts[l] + 4)
                            pe.wait_ge(active, q * H + n + 1)
                            for k in range(widths[l]):
                                rhs = xT[:, bass.ds(k * NP + g * GROUP + half * PART, PART)] if l == 0 else \
                                    hT[l - 1][:, k * GROUP + half * PART:k * GROUP + (half + 1) * PART]
                                lo = (k * widths[l + 1] + m) * P
                                ins = pe.matmul(ps_h[:, c % 4, 0:PART], w_in[l][b][:, lo:lo + P], rhs,
                                                start=k == 0, stop=k == widths[l] - 1)
                            ins.then_inc(products, 1)
                    pe.wait_ge(active, q * H + H + 4)
                    for j in range(UN):
                        n = q * UN + j
                        pe.wait_ge(mixed, n + {0: UN, 4: 2}.get(j, 1))
                        for k in range(widths[-1]):
                            ins = pe.matmul(ps_y[:, j % 4, 0:D], hT[-1][:, k * GROUP + j * P:k * GROUP + (j + 1) * P],
                                            at(w_out[b], k, D), start=k == 0, stop=k == widths[-1] - 1)
                        ins.then_inc(outs, 1)

            with pe.Fori(0, EXPERTS // 2) as i:
                for b in range(2):
                    expert(i, 2 * i + b, b)

        @block.scalar
        def _(act):
            act.sem_inc(active, 4)
            for l, (_, vs, _) in enumerate(layers):
                if len(vs) > 1:
                    act.wait_ge(vec_step, len(vectors))
                    act.activation(vec[l][4][:, :], vec[l][4][:, :], ACT.Sqrt).then_inc(vec_rooted, 1)
            act.wait_ge(vec_ready, 1)

            with act.Fori(0, EXPERTS // 2) as i:
                for b in range(2):
                    e = 2 * i + b
                    act.wait_ge(active, e * NI * H + 4)
                    act.sem_inc(act_tick, 1)
                    copies = [act.activation(own[l][v][:, :], at(vec[l][v], e, widths[l + 1]), ACT.Copy)
                              for l in range(len(layers)) for v in range(len(own[l]))]
                    copies[-1].then_inc(own_ready, 1)
                    act.wait_ge(own_ready, e + 1)
                    act.sem_inc(act_tick, 1)
                    with act.Fori(0, NI) as g:
                        q = e * NI + g
                        act.wait_ge(outs, q * UN + UN)
                        for l, (_, vs, func) in enumerate(layers):
                            for c in range(halves[l]):
                                m, half = c // 2, c % 2
                                act.wait_ge(products, q * H + starts[l] + c + 1)
                                act.activation(hT[l][:, m * GROUP + half * PART:m * GROUP + (half + 1) * PART],
                                               ps_h[:, c % 4, 0:PART], func,
                                               bias=own[l][0][:, m:m + 1],
                                               scale=own[l][1][:, m:m + 1] if len(vs) > 1 else 1.0)\
                                    .then_inc(active, 1)

        @block.vector
        def _(dve):
            dve.sem_inc(mixed, UN)
            link = Chain(dve, vec_step)
            dve.wait_ge(vec_turned, len(vectors))
            for n, (l, v) in enumerate(vectors):
                from_ps = ps_h[:, n % 4, 64 * (n // 4):64 * (n // 4) + EXPERTS * widths[l + 1]]
                if v == 4:
                    link(dve.tensor_scalar(vec[l][v][:, :], from_ps, BN_EPS, None, ALU.add))
                else:
                    link(dve.tensor_copy(vec[l][v][:, :], from_ps))
            if any(len(vs) > 1 for _, vs, _ in layers):
                dve.wait_ge(vec_rooted, len(layers))
            for l, (_, vs, _) in enumerate(layers):
                if len(vs) > 1:
                    bias, gain, shift, mean, var = (t[:, :] for t in vec[l])
                    link(dve.reciprocal(var, var))
                    link(dve.tensor_tensor(gain, gain, var, ALU.mult))
                    link(dve.tensor_tensor(bias, bias, mean, ALU.subtract))
                    link(dve.tensor_tensor(bias, bias, gain, ALU.mult))
                    link(dve.tensor_tensor(bias, bias, shift, ALU.add))
            dve.sem_inc(vec_ready, 1)

            with dve.Fori(0, EXPERTS) as e:
                with dve.Fori(0, NI) as g:
                    for j in range(UN):
                        t = g * UN + j
                        n = e * NT + t
                        dve.wait_ge(outs, UN + n + 1)
                        dve.wait_ge(mixed, n + 1)
                        dve.scalar_tensor_tensor(at(acc, t, D), ps_y[:, j % 4, 0:D], at(mix, t * EXPERTS + e, 1),
                                                 at(acc, t, D), ALU.mult, ALU.add).then_inc(mixed, 1)


SLICE = 2 * P


class Dispatch:

    def __init__(self, net, s, choices, groups, capacity):
        self.choices, self.groups, self.capacity = choices, groups, capacity
        self.slot_in = [s.sb(f"slot_in{c}", [P, NT], I32) for c in range(choices)]
        self.slot_out = [s.sb(f"slot_out{c}", [P, NT], I32) for c in range(choices)] if capacity else self.slot_in
        self.weight = [s.sb(f"weight{c}", [P, NT]) for c in range(choices)]
        self.expert_row = s.sb("expert_row", [P, groups], I32)
        self.tokens = net.dispatch["tokens"][0:groups * SLICE, :]
        self.outputs = net.dispatch["outputs"][0:groups * SLICE, :]


def moe_sparse(net, name, router, bias, kind, choices, groups, w1, b1, func, w2, b2):
    with ExitStack() as ctx:
        s = net.scope(name, ctx)
        xn = s.sb("xn", [P, NT * D])
        logits = s.sb("logits", [P, NT * EXPERTS])
        to = Dispatch(net, s, choices, groups, kind == "capacity")
        moe_front(net, name, logits, router, xn=xn)
        choose(kind)(net, name, logits, bias, to)
        moe_scatter(net, name, xn, to)
        moe_groups(net, name, to, w1, b1, func, w2, b2)
        moe_combine(net, name, to)


def moe_scatter(net, name, xn, to):
    nc = net.nc
    with ExitStack() as ctx:
        s = net.scope(name + "s", ctx)
        scattered = s.sem("scattered")
        block = ctx.enter_context(nc.Block())

        @block.gpsimd
        def _(pool):
            for t in range(NT):
                rows = P if t < NT - 1 else TAIL
                for c in range(to.choices):
                    pool.indirect_dma_start(to.tokens, bass.IndirectOffsetOnAxis(to.slot_in[c][0:rows, t:t + 1], 0),
                                            xn[0:rows, t * D:(t + 1) * D], None, bounds_check=to.groups * SLICE - 1,
                                            oob_is_err=False).then_inc(scattered, 16)
            pool.wait_ge(scattered, 16 * NT * to.choices)


def moe_groups(net, name, to, w1, b1, func, w2, b2):
    nc, a = net.nc, net.a
    F = a[w1].shape[2]
    FC = F // P
    BANKS = FC // 2
    TILES = SLICE // P
    with ExitStack() as ctx:
        s = net.scope(name + "g", ctx)
        w_in = [s.sb(f"w_in{b}", [P, DC * F]) for b in range(2)]
        w_out = [s.sb(f"w_out{b}", [P, FC * D]) for b in range(2)]
        rows = [s.sb(f"rows{b}", [P, TILES * D]) for b in range(2)]
        xT = [s.sb(f"xT{b}", [P, DC * SLICE]) for b in range(2)]
        hT = [s.sb(f"hT{b}", [P, FC * SLICE]) for b in range(2)]
        y = [s.sb(f"y{b}", [P, TILES * D]) for b in range(2)]
        b1_rows = s.sb("b1_rows", [EXPERTS * FC, P])
        b1_cols = s.sb("b1_cols", [P, EXPERTS * FC])
        b2_all = s.sb("b2_all", [P, EXPERTS * D])
        ps_t = s.ps("ps_t", [P, DC * SLICE])
        ps_h = s.ps("ps_h", [P, BANKS, 512])
        ps_y = s.ps("ps_y", [P, TILES, 512])
        loaded = s.sem("loaded")
        b1_turned = s.sem("b1_turned")
        b1_ready = s.sem("b1_ready")
        rows_loaded = [s.sem(f"rows_loaded{b}") for b in range(2)]
        w_in_loaded = [s.sem(f"w_in_loaded{b}") for b in range(2)]
        w_out_loaded = [s.sem(f"w_out_loaded{b}") for b in range(2)]
        turned = s.sem("turned")
        xT_ready = s.sem("xT_ready")
        hidden = s.sem("hidden")
        projected = s.sem("projected")
        active = s.sem("active")
        outs = s.sem("outs")
        done = s.sem("done")
        y_ready = s.sem("y_ready")
        stored = [s.sem(f"stored{b}") for b in range(2)]
        y_free = s.sem("y_free")
        dve_tick = s.sem("dve_tick")
        act_tick = s.sem("act_tick")
        pe_tick = s.sem("pe_tick")
        pool_tick = s.sem("pool_tick")
        block = ctx.enter_context(nc.Block())
        run = dict(ring=2, total=to.groups)

        def expert_of(eng, g):
            return eng.value_load(to.expert_row[0:1, bass.ds(g, 1)], min_val=0, max_val=EXPERTS - 1)

        def of_expert(w, e):
            return chunked(a[w].rearrange("e k n -> (e k) n")[bass.ds(e * a[w].shape[1], a[w].shape[1]), :])

        @block.sync
        def _(sp):
            sp.dma_start(b1_rows[:, :], a[b1].rearrange("e (c p) -> (e c) p", p=P)).then_inc(loaded, 16)
            sp.dma_start(b2_all[:, :], spread(a[b2].rearrange("e d -> (e d)"))).then_inc(loaded, 16)

            def load(g, i, b):
                e = expert_of(sp, g)
                sp.wait_ge(turned, g + 1)
                sp.dma_start(tiled(rows[b][:, :], D),
                             to.tokens[bass.ds(g * SLICE, SLICE), :].rearrange("(t p) d -> p t d", p=P)).then_inc(rows_loaded[b], 16)
                sp.wait_ge(projected, g + 1)
                sp.dma_start(w_in[b][:, :].rearrange("p (c n) -> p c n", c=DC), of_expert(w1, e)).then_inc(w_in_loaded[b], 16)
                sp.wait_ge(done, g + 1)
                sp.dma_start(w_out[b][:, :].rearrange("p (c n) -> p c n", c=FC), of_expert(w2, e)).then_inc(w_out_loaded[b], 16)

            skewed(sp, (0, load), **run)

        @block.tensor
        def _(pe):
            pe.sem_inc(turned, 2)
            pe.sem_inc(projected, 2)
            pe.sem_inc(done, 2)
            pe.wait_ge(loaded, 32)
            turn_rows(pe, net, ps_y[:, 0, 0:EXPERTS * FC], b1_rows[:, :]).then_inc(b1_turned, 1)
            pe.wait_ge(b1_ready, 1)

            def turn(g, i, b):
                pe.wait_ge(rows_loaded[b], i * 16 + 16)
                pe.wait_ge(xT_ready, g + 1)
                pe.sem_inc(pe_tick, 1)
                for c in range(DC):
                    for t in range(TILES):
                        ins = pe.transpose(ps_t[:, c * SLICE + t * P:c * SLICE + (t + 1) * P],
                                           rows[b][:, t * D + c * P:t * D + (c + 1) * P], net.ident[:, :])
                ins.then_inc(turned, 1)

            def hide(g, i, b):
                pe.wait_ge(w_in_loaded[b], i * 16 + 16)
                pe.wait_ge(xT_ready, g + 2)
                for n in range(BANKS):
                    pe.wait_ge(active, g * BANKS + n + 1)
                    for m in (2 * n, 2 * n + 1):
                        for c in range(DC):
                            ins = pe.matmul(ps_h[:, n, (m % 2) * SLICE:(m % 2 + 1) * SLICE],
                                            w_in[b][:, c * F + m * P:c * F + (m + 1) * P], at(xT[b], c, SLICE),
                                            start=c == 0, stop=c == DC - 1)
                    ins.then_inc(hidden, 1)
                pe.wait_ge(hidden, (g + 1) * BANKS)
                pe.sem_inc(projected, 1)

            def put_out(g, i, b):
                pe.wait_ge(w_out_loaded[b], i * 16 + 16)
                pe.wait_ge(active, (g + 2) * BANKS)
                for t in range(TILES):
                    pe.wait_ge(y_ready, g * TILES + t + 1)
                    for c in range(FC):
                        ins = pe.matmul(ps_y[:, t, 0:D], hT[b][:, c * SLICE + t * P:c * SLICE + (t + 1) * P], at(w_out[b], c, D),
                                        start=c == 0, stop=c == FC - 1)
                    ins.then_inc(outs, 1)
                pe.wait_ge(outs, (g + 1) * TILES)
                pe.sem_inc(done, 1)

            skewed(pe, (1, hide), (0, turn), (2, put_out), **run)

        @block.scalar
        def _(act):
            act.sem_inc(active, BANKS)
            act.wait_ge(b1_ready, 1)
            act.sem_inc(act_tick, 1)

            def activate(g, i, b):
                e = expert_of(act, g)
                act.wait_ge(done, g + 1)
                for n in range(BANKS):
                    act.wait_ge(hidden, g * BANKS + n + 1)
                    act.sem_inc(act_tick, 1)
                    for m in (2 * n, 2 * n + 1):
                        ins = act.activation(at(hT[b], m, SLICE), ps_h[:, n, (m % 2) * SLICE:(m % 2 + 1) * SLICE], func,
                                             bias=b1_cols[:, bass.ds(e * FC + m, 1)])
                    ins.then_inc(active, 1)

            skewed(act, (0, activate), **run)

        @block.vector
        def _(dve):
            dve.sem_inc(xT_ready, 1)
            dve.sem_inc(y_ready, TILES)
            dve.wait_ge(b1_turned, 1)
            dve.tensor_copy(b1_cols[:, :], ps_y[:, 0, 0:EXPERTS * FC]).then_inc(b1_ready, 1)
            dve.wait_ge(loaded, 32)

            def keep(g, i, b):
                dve.wait_ge(turned, g + 3)
                dve.wait_ge(projected, g + 1)
                dve.tensor_copy(xT[b][:, :], ps_t[:, :]).then_inc(xT_ready, 1)

            def put_out(g, i, b):
                e = expert_of(dve, g)
                dve.wait_ge(y_free, g + 1)
                dve.sem_inc(dve_tick, 1)
                for t in range(TILES):
                    dve.wait_ge(outs, g * TILES + t + 1)
                    dve.tensor_tensor(at(y[b], t, D), ps_y[:, t, 0:D], at(b2_all, e, D), ALU.add).then_inc(y_ready, 1)

            skewed(dve, (0, keep), (2, put_out), **run)

        @block.gpsimd
        def _(pool):
            def store(g, i, b):
                pool.wait_ge(y_ready, (g + 2) * TILES)
                pool.sem_inc(pool_tick, 1)
                pool.dma_start(to.outputs[bass.ds(g * SLICE, SLICE), :].rearrange("(t p) d -> p t d", p=P),
                               tiled(y[b][:, :], D)).then_inc(stored[b], 16)
                pool.wait_ge(stored[b], i * 16 + 16)
                pool.sem_inc(y_free, 1)

            pool.sem_inc(y_free, 2)
            skewed(pool, (0, store), **run)


def moe_combine(net, name, to):
    nc = net.nc
    LARGEST = float(np.finfo(np.float32).max)
    with ExitStack() as ctx:
        s = net.scope(name + "o", ctx)
        rows = [s.sb(f"rows{c}", [P, NT * D]) for c in range(to.choices)]
        fixed = s.sb("fixed", [P, 1])
        chain = s.sem("chain")
        gathered = [s.sem(f"gathered{i}") for i in range(NI)]
        step = s.sem("step")
        block = ctx.enter_context(nc.Block())

        @block.gpsimd
        def _(pool):
            for t in range(NT):
                for c in range(to.choices):
                    pool.indirect_dma_start(at(rows[c], t, D), None, to.outputs,
                                            bass.IndirectOffsetOnAxis(to.slot_out[c][:, t:t + 1], 0)).then_inc(gathered[t // UN], 16)

        @block.vector
        def _(dve):
            if not to.capacity:
                for t in range(NT):
                    if t % UN == 0:
                        dve.wait_ge(gathered[t // UN], 16 * to.choices * UN)
                    for c in range(to.choices):
                        if c:
                            dve.wait_ge(step, t * (to.choices - 1) + c)
                        ins = dve.scalar_tensor_tensor(at(net.x, t, D), at(rows[c], t, D), to.weight[c][:, t:t + 1], at(net.x, t, D),
                                                       ALU.mult, ALU.add)
                        if c < to.choices - 1:
                            ins.then_inc(step, 1)
                return
            flag = s.sb("flag", [P, NT * D], mybir.dt.uint8)
            y = rows[0][:, :]
            link = Chain(dve, chain)
            for i in range(NI):
                dve.wait_ge(gathered[i], 16 * UN)
            link(dve.tensor_tensor(tiled(y, D), tiled(y, D), to.weight[0][:, :].unsqueeze(2).to_broadcast([P, NT, D]), ALU.mult))
            link(dve.tensor_scalar(flag[:, :], y, LARGEST, None, ALU.is_gt))
            for value, test in ((1e4, None), (-1e4, lambda: dve.tensor_scalar(flag[:, :], y, -LARGEST, None, ALU.is_lt)),
                                (0.0, lambda: dve.tensor_tensor(flag[:, :], y, y, ALU.not_equal))):
                if test:
                    link(test())
                link(dve.memset(fixed[:, :], value))
                link(dve.copy_predicated(y, flag[:, :], fixed[:, :].to_broadcast([P, NT * D])))
            link(dve.tensor_tensor(net.x[:, :], net.x[:, :], y, ALU.add))


BN_EPS = 1e-3
CAPACITY = max(1, -(-5 * N // (4 * EXPERTS)))
ROOM = -(-CAPACITY // SLICE) * SLICE
assert ROOM // SLICE == 2


def l0_ffn(net):
    moe(net, "l0f", net.a["L0_ffn_router_w"], None, choose("probs"),
        [("L0_ffn_w1", ("L0_ffn_b1",), ACT.Gelu)], "L0_ffn_w2", "L0_ffn_b2", keeps_tokens=True)


def l1_ffn(net):
    moe_sparse(net, "l1f", net.a["L1_ffn_Wg"], net.a["L1_ffn_bg"], "pair", 2, 2 * N // SLICE + EXPERTS,
               "L1_ffn_W1", "L1_ffn_b1", ACT.Gelu, "L1_ffn_W2", "L1_ffn_b2")


def l2_ffn(net):
    def names(n):
        return tuple(f"L2_ffn_{v}{n}" for v in ("b", "g", "be", "m", "v"))

    moe(net, "l2f", net.a["L2_ffn_Wr"], net.a["L2_ffn_br"], choose("all"),
        [("L2_ffn_W1", names(1), ACT.Relu), ("L2_ffn_W2", names(2), ACT.Relu)], "L2_ffn_Wo", "L2_ffn_bo")


def l3_ffn(net):
    moe_sparse(net, "l3f", net.a["L3_ffn_gate_w"], net.a["L3_ffn_gate_b"], "capacity", 1, EXPERTS * ROOM // SLICE,
               "L3_ffn_w1", "L3_ffn_b1", ACT.Relu, "L3_ffn_w2", "L3_ffn_b2")


def edge_means(net):
    nc = net.nc
    placed = net.by_dst
    lo = placed.first["edge_attr_16"]
    W = 17
    with ExitStack() as ctx:
        s = net.scope("means", ctx)
        n = placed.width - lo
        rec = [s.sb(f"rec{b}", [P, BATCH * n]) for b in range(RING)]
        onehot = [s.sb(f"onehot{b}", [P, BATCH * P]) for b in range(RING)]
        found = s.sb("found", [P, NT])
        root = s.sb("root", [P, NT])
        ps = s.ps("ps", [P, NT * W])
        loaded = [s.sem(f"loaded{b}") for b in range(RING)]
        onehot_ready = s.sem("onehot_ready")
        closed = s.sem("closed")
        summed = s.sem("summed")
        chain = s.sem("chain")
        to_root = s.sem("to_root")
        rooted = s.sem("rooted")
        block = ctx.enter_context(nc.Block())

        @block.sync
        def _(sp):
            with sp.Fori(0, NB // RING) as i:
                for b in range(RING):
                    q = i * RING + b
                    sp.wait_ge(summed, q + 1)
                    sp.dma_start(tiled(rec[b][:, :], n), batch_records(placed.records, q, lo, placed.width))\
                        .then_inc(loaded[b], 16)

        @block.tensor
        def _(pe):
            pe.sem_inc(summed, RING)
            open_sums(net, pe, ps, True)
            with pe.Fori(0, NB // RING) as i:
                for b in range(RING):
                    q = i * RING + b
                    blocks = [block_of(pe, placed, q * TWO + k) for k in range(TWO)]
                    pe.wait_ge(onehot_ready, q + 1)
                    for k in range(BATCH):
                        ins = pe.matmul(at(ps, blocks[k // 2], W), at(onehot[b], k, P), rec[b][:, k * n:k * n + W],
                                        start=False, stop=False)
                    ins.then_inc(summed, 1)
            open_sums(net, pe, ps, False).then_inc(closed, 1)

        @block.scalar
        def _(act):
            act.wait_ge(to_root, 1)
            act.activation(root[:, :], root[:, :], ACT.Sqrt).then_inc(rooted, 1)

        @block.vector
        def _(dve):
            link = Chain(dve, chain)
            with dve.Fori(0, NB // RING) as i:
                for b in range(RING):
                    dve.wait_ge(loaded[b], i * 16 + 16)
                    dve.wait_ge(summed, i * RING + b + 1)
                    for k in range(BATCH):
                        c = k * n + placed.near - lo
                        ins = dve.tensor_scalar(at(onehot[b], k, P), net.columns[:, :], rec[b][:, c:c + 1], None, ALU.is_equal)
                    ins.then_inc(onehot_ready, 1)
            dve.wait_ge(closed, 1)
            sums = tiled(ps[:, :], W)
            link(dve.tensor_scalar(found[:, :], sums[:, :, 16], 1.0, None, ALU.max))
            link(dve.reciprocal(found[:, :], found[:, :]))
            link(dve.tensor_tensor(tiled(net.mean16[:, :], 16), sums[:, :, 0:16],
                                   found[:, :].unsqueeze(2).to_broadcast([P, NT, 16]), ALU.mult))
            link(dve.tensor_scalar(root[:, :], sums[:, :, 16], 1.0, None, ALU.add))
            dve.sem_inc(to_root, 1)
            dve.wait_ge(rooted, 1)
            link(dve.reciprocal(net.dinv[:, :], root[:, :]))


def gat_edges(net, name, heads, each, table, lo, logits_of, tops=None):
    nc = net.nc
    KH = BATCH * heads
    W = heads * (each + 1)
    UNITS = -(-heads // 2)
    FLUSH = 1 if tops is None else 2
    placed = net.by_dst
    with ExitStack() as ctx:
        s = net.scope(name, ctx)
        g = Gather(s, net, placed, table, table.shape[1], lo)
        nodehot = [s.sb(f"nodehot{b}", [P, BATCH * P]) for b in range(RING)]
        outside = [s.sb(f"outside{b}", [P, BATCH * P], BF16) for b in range(RING)]
        logit = [s.sb(f"logit{b}", [P, KH]) for b in range(RING)]
        fresh = s.sb("fresh", [P, PAIRS])
        fresh_step = s.sem("fresh_step")
        masked = s.sb("masked", [P, 2 * 2 * PAIR])
        tile_top = s.sb("tile_top", [P, TWO * heads])
        top = s.sb("top", [P, RING * TWO * heads])
        shrink = [s.sb(f"shrink{b}", [P, TWO * heads]) for b in range(RING)]
        power = [s.sb(f"power{b}", [P, KH]) for b in range(RING)]
        weighted = s.sb("weighted", [P, BATCH * W])
        scaled = s.sb("scaled", [P, W])
        total = [s.sb(f"total{k}", [P, W]) for k in range(TWO)]
        ps_hot = s.ps("ps_hot", [P, BATCH * P])
        ps_x = s.ps("ps_x", [P, TWO, 512])
        ps_row = s.ps("ps_row", [P, 2, 512])
        ps_s = s.ps("ps_s", [P, TWO, 512])
        ps_top = ps_s[:, TWO - 1, 512 - KH:512]
        cleared = s.sem("cleared")
        hot_turned = s.sem("hot_turned")
        nodehot_ready = s.sem("nodehot_ready")
        logit_ready = s.sem("logit_ready")
        rows_turned = s.sem("rows_turned")
        topped = s.sem("topped")
        top_step = s.sem("top_step")
        shrink_ready = s.sem("shrink_ready")
        spread_top = s.sem("spread_top")
        power_step = s.sem("power_step")
        shrunk = s.sem("shrunk")
        powered = s.sem("powered")
        weighted_ready = s.sem("weighted_ready")
        summed = s.sem("summed")
        scale_step = s.sem("scale_step")
        total_ready = s.sem("total_ready")
        flushed = s.sem("flushed")
        act_tick = s.sem("act_tick")
        dve_tick = s.sem("dve_tick")
        logits = logits_of(s, g, ps_x, nodehot, logit, logit_ready, nodehot_ready)
        block = ctx.enter_context(nc.Block())
        by_head = lambda ap, n: ap.rearrange("p (h c) -> p h c", c=n)

        def top_at(b, k):
            return at(top, b * TWO + k, heads)

        @block.sync
        def _(sp):
            logits.load(sp)
            g.load(sp)

        @block.gpsimd
        def _(pool):
            g.gather(pool)

        @block.vector
        def _(dve):
            dve.memset(net.work[:, 0:NT * W], 0.0).then_inc(cleared, 1)
            dve.memset(top[:, :], -HUGE).then_inc(cleared, 1)
            dve.memset(total[TWO - 1][:, :], 0.0).then_inc(cleared, 1)
            if tops is not None:
                dve.memset(tops[:, :], -HUGE).then_inc(cleared, 1)
            dve.tensor_scalar(fresh[:, :], placed.keep[:, :], -1.0, HUGE, ALU.add, ALU.mult).then_inc(fresh_step, 1)
            dve.sem_inc(topped, 2)
            dve.sem_inc(total_ready, TWO)
            logits.start_vector(dve)
            dve.wait_ge(cleared, 3 if tops is None else 4)
            dve.wait_ge(fresh_step, 1)

            def tops_of(k):
                def step(q, i, b):
                    for h0 in range(0, heads, 2):
                        n = (q * TWO + k) * UNITS + h0 // 2
                        side = (k * UNITS + h0 // 2) % 2
                        dve.wait_ge(rows_turned, n + 1)
                        dve.wait_ge(topped, n + 1)
                        dve.sem_inc(dve_tick, 1)
                        for h in range(h0, min(h0 + 2, heads)):
                            c = k * heads + h
                            ins = dve.tensor_tensor_reduce(at(masked, side * 2 + h - h0, PAIR), at(ps_row[:, side, :], h - h0, PAIR),
                                                           at(outside[b], k, PAIR), 1.0, -HUGE, ALU.add, ALU.max,
                                                           tile_top[:, c:c + 1])
                        ins.then_inc(topped, 1)
                return step

            def raise_tops(q, i, b):
                for k in range(TWO):
                    n = q * TWO + k
                    old = top_at(b, k - 1) if k else top_at((b - 1) % RING, TWO - 1)
                    dve.wait_ge(topped, (n + 1) * UNITS + 2)
                    if not isinstance(n, int) or n:
                        dve.wait_ge(top_step, n)
                    dve.scalar_tensor_tensor(top_at(b, k), old, fresh[:, bass.ds(n, 1)], at(tile_top, k, heads),
                                             ALU.add, ALU.max).then_inc(top_step, 1)
                    dve.wait_ge(top_step, n + 1)
                    dve.scalar_tensor_tensor(at(shrink[b], k, heads), old, fresh[:, bass.ds(n, 1)], top_at(b, k),
                                             ALU.add, ALU.subtract).then_inc(shrink_ready, 1)

            def fall(q, i, b):
                dve.wait_ge(spread_top, q + 1)
                dve.tensor_tensor(power[b][:, :], logit[b][:, :], ps_top, ALU.subtract).then_inc(power_step, 1)
                dve.wait_ge(power_step, 2 * q + 1)
                dve.tensor_scalar(power[b][:, :], power[b][:, :], 0.0, None, ALU.min).then_inc(power_step, 1)

            def add(q, i, b):
                dve.wait_ge(shrunk, q + 1)
                for k in range(TWO):
                    n = q * TWO + k
                    dve.wait_ge(total_ready, n + TWO)
                    dve.tensor_tensor(by_head(scaled[:, :], each + 1), by_head(total[1 - k][:, :], each + 1),
                                      at(shrink[b], k, heads).unsqueeze(2).to_broadcast([P, heads, each + 1]), ALU.mult)\
                        .then_inc(scale_step, 1)
                    dve.wait_ge(scale_step, n + 1)
                    dve.wait_ge(summed, n + TWO + 1)
                    dve.wait_ge(flushed, (n + 1) * FLUSH)
                    dve.sem_inc(dve_tick, 1)
                    dve.tensor_tensor(total[k][:, :], scaled[:, :], ps_s[:, k, 0:W], ALU.add).then_inc(total_ready, 1)

            skewed(dve, (5, add), (3, tops_of(0)), (2, lambda q, i, b: logits.vector(dve, q, i, b)), (3, tops_of(1)),
                   (3, raise_tops), (0, lambda q, i, b: g.hot(dve, q, i, b)), (3, fall))

        @block.tensor
        def _(pe):
            pe.sem_inc(g.hot_free, RING)
            pe.sem_inc(summed, TWO)
            logits.start_tensor(pe)

            def turn(q, i, b):
                pe.wait_ge(g.hot_ready, q + 1)
                pe.wait_ge(nodehot_ready, q + 1)
                for k in range(BATCH):
                    ins = pe.transpose(at(ps_hot, k, P), at(g.onehot[b], k, P), net.ident[:, :])
                ins.then_inc(hot_turned, 1)
                logits.tensor_early(pe, q, i, b)

            def turn_logits(k):
                def step(q, i, b):
                    pe.wait_ge(logit_ready, q + 1)
                    for h0 in range(0, heads, 2):
                        n = (q * TWO + k) * UNITS + h0 // 2
                        side = (k * UNITS + h0 // 2) % 2
                        pe.wait_ge(topped, n + 1)
                        for h in range(h0, min(h0 + 2, heads)):
                            for m in range(2):
                                c = (2 * k + m) * heads + h
                                lo = (h - h0) * PAIR + m * P
                                ins = pe.transpose(ps_row[:, side, lo:lo + P], logit[b][:, c:c + 1].to_broadcast([P, P]),
                                                   net.ident[:, :])
                        ins.then_inc(rows_turned, 1)
                return step

            def add(q, i, b):
                for k in range(TWO):
                    n = q * TWO + k
                    pe.wait_ge(weighted_ready, n + 1)
                    pe.wait_ge(total_ready, n + 1)
                    for m in (2 * k, 2 * k + 1):
                        ins = pe.matmul(ps_s[:, k, 0:W], at(g.onehot[b], m, P), at(weighted, m, W), start=m == 2 * k, stop=m > 2 * k)
                    ins.then_inc(summed, 1)
                pe.wait_ge(summed, q * TWO + 2 * TWO)
                pe.sem_inc(g.hot_free, 1)

            def spread(q, i, b):
                pe.wait_ge(shrink_ready, q * TWO + TWO)
                for m in range(BATCH):
                    ins = pe.matmul(at(ps_top, m, heads), at(nodehot[b], m, P), top_at(b, m // 2), start=True, stop=True)
                ins.then_inc(spread_top, 1)

            skewed(pe, (3, turn_logits(0)), (2, lambda q, i, b: logits.tensor(pe, q, i, b)), (3, turn_logits(1)), (1, turn),
                   (4, add), (3, spread))

        @block.scalar
        def _(act):
            act.sem_inc(g.rows_free, RING)
            act.sem_inc(nodehot_ready, 1)
            act.sem_inc(flushed, TWO * FLUSH)
            logits.start_scalar(act)
            act.wait_ge(cleared, 3 if tops is None else 4)
            act.sem_inc(act_tick, 1)

            def turn(q, i, b):
                act.wait_ge(hot_turned, q + 1)
                act.activation(outside[b][:, :], ps_hot[:, :], ACT.Copy, bias=-HUGE, scale=HUGE)
                act.activation(nodehot[b][:, :], ps_hot[:, :], ACT.Copy).then_inc(nodehot_ready, 1)
                logits.scalar_early(act, q, i, b)

            def shrinks(q, i, b):
                act.wait_ge(shrink_ready, q * TWO + TWO)
                act.activation(shrink[b][:, :], shrink[b][:, :], ACT.Exp).then_inc(shrunk, 1)

            def weigh(q, i, b):
                act.wait_ge(power_step, 2 * q + 2)
                act.activation(power[b][:, :], power[b][:, :], ACT.Exp).then_inc(powered, 1)
                g.wait_rows(act, i, b)
                act.wait_ge(powered, q + 1)
                for k in range(TWO):
                    act.wait_ge(summed, q * TWO + k + 1)
                    for m in (2 * k, 2 * k + 1):
                        out = by_head(at(weighted, m, W), each + 1)
                        for h in range(heads):
                            lo = m * g.width + h * each
                            act.activation(out[:, h, 0:each], g.rows[b][:, lo:lo + each], ACT.Copy,
                                           scale=power[b][:, m * heads + h:m * heads + h + 1])
                        ins = act.activation(out[:, :, each], at(power[b], m, heads), ACT.Copy)
                    ins.then_inc(weighted_ready, 1)
                act.wait_ge(weighted_ready, q * TWO + TWO)
                act.sem_inc(g.rows_free, 1)

            def flush(q, i, b):
                for k in range(TWO):
                    n = q * TWO + k
                    blk = block_of(act, placed, n)
                    act.wait_ge(total_ready, n + TWO + 1)
                    act.wait_ge(flushed, (n + TWO) * FLUSH)
                    act.sem_inc(act_tick, 1)
                    if tops is not None:
                        act.activation(at(tops, blk, heads), top_at(b, k), ACT.Copy).then_inc(flushed, 1)
                    act.activation(at(net.work, blk, W), total[k][:, :], ACT.Copy).then_inc(flushed, 1)

            skewed(act, (4, weigh), (5, flush), (3, shrinks), (1, turn))


class L1Logits:

    SLOPE = 0.2

    def __init__(self, net, xr, att, s, g, ps_x, nodehot, logit, logit_ready, nodehot_ready):
        self.net, self.xr, self.att, self.g = net, xr, att, g
        self.ps_x, self.nodehot, self.logit, self.logit_ready, self.nodehot_ready = ps_x, nodehot, logit, logit_ready, nodehot_ready
        self.we = s.sb("we", [16, D])
        self.attrT = [s.sb(f"attrT{b}", [16, BATCH * P]) for b in range(RING)]
        self.e = [s.sb(f"e{k}", [P, 2 * D]) for k in range(TWO)]
        self.ps_attr = s.ps("ps_attr", [16, BATCH * P])
        self.loaded = s.sem("we_loaded")
        self.attr_turned = s.sem("attr_turned")
        self.attr_ready = s.sem("attr_ready")
        self.sums = s.sem("e_sums")
        self.x_read = s.sem("x_read")
        self.step = s.sem("e_step")
        self.tick = s.sem("e_tick")

    def load(self, sp):
        sp.dma_start(self.we[:, :], self.net.a["L1_gnn_W_e"]).then_inc(self.loaded, 16)

    def start_vector(self, dve):
        dve.sem_inc(self.x_read, TWO)

    def start_tensor(self, pe):
        pe.wait_ge(self.loaded, 16)

    def start_scalar(self, act):
        act.sem_inc(self.g.rec_free, RING)
        act.sem_inc(self.attr_ready, 1)

    def tensor_early(self, pe, q, i, b):
        pe.wait_ge(self.g.rec_loaded[b], i * 16 + 16)
        pe.wait_ge(self.attr_ready, q + 1)
        pe.sem_inc(self.tick, 1)
        for k in range(BATCH):
            ins = pe.transpose(at(self.ps_attr, k, P), self.g.columns(b, k, self.g.lo, 16), self.net.ident[:, :])
        ins.then_inc(self.attr_turned, 1)

    def scalar_early(self, act, q, i, b):
        act.wait_ge(self.attr_turned, q + 1)
        act.activation(self.attrT[b][:, :], self.ps_attr[:, :], ACT.Copy).then_inc(self.attr_ready, 1)
        act.sem_inc(self.g.rec_free, 1)

    def tensor(self, pe, q, i, b):
        pe.wait_ge(self.attr_ready, q + 2)
        pe.wait_ge(self.nodehot_ready, q + 2)
        for k in range(TWO):
            n = q * TWO + k
            blk = block_of(pe, self.g.placed, n)
            pe.wait_ge(self.x_read, n + 1)
            for m in range(2):
                out = self.ps_x[:, k, m * D:(m + 1) * D]
                pe.matmul(out, at(self.nodehot[b], 2 * k + m, P), at(self.xr, blk, D), start=True, stop=False)
                ins = pe.matmul(out, at(self.attrT[b], 2 * k + m, P), self.we[:, :], start=False, stop=True)
            ins.then_inc(self.sums, 1)

    def vector(self, dve, q, i, b):
        base = 3 * TWO * q
        self.g.wait_rows(dve, i, b)
        for k in range(TWO):
            dve.wait_ge(self.sums, q * TWO + k + 1)
            dve.tensor_tensor(self.e[k][:, :], self.ps_x[:, k, 0:2 * D], at(self.g.rows[b], k, 2 * D), ALU.add)\
                .then_inc(self.x_read, 1)
        for k in range(TWO):
            e = self.e[k][:, :]
            dve.wait_ge(self.x_read, q * TWO + TWO + k + 1)
            dve.scalar_tensor_tensor(e, e, self.SLOPE, e, ALU.mult, ALU.max).then_inc(self.step, 1)
        for k in range(TWO):
            e = tiled(self.e[k][:, :], D)
            dve.wait_ge(self.step, base + k + 1)
            dve.tensor_tensor(e, e, self.att[:, :].unsqueeze(1).to_broadcast([P, 2, D]), ALU.mult).then_inc(self.step, 1)
        for k in range(TWO):
            dve.wait_ge(self.step, base + TWO + k + 1)
            dve.tensor_reduce(at(self.logit[b], k, 8), self.e[k][:, :].rearrange("p (h c) -> p h c", c=64), AX.X, ALU.add)\
                .then_inc(self.step, 1)
        dve.wait_ge(self.step, base + 3 * TWO)
        dve.sem_inc(self.logit_ready, 1)


def l1_gnn(net):
    H, C = 4, 64
    with ExitStack() as ctx:
        s = net.scope("l1", ctx)
        res = s.sb("res", [P, NT * D])
        own_logit = s.sb("own_logit", [P, NT * H])
        top = s.sb("top", [P, NT * H])
        with ExitStack() as inner:
            t = net.scope("l1x", inner)
            xr = t.sb("xr", [P, NT * D])
            att = t.sb("att", [P, D])
            l1_nodes(net, xr, res, att, own_logit)
            gat_edges(net, "l1e", H, C, net.table(D), net.by_dst.first["edge_attr_16"],
                      lambda *args: L1Logits(net, xr, att, *args), top)
        l1_finish(net, res, own_logit, top)


def l1_nodes(net, xr, res, att, own_logit):
    nc, a = net.nc, net.a
    H, C = 4, 64
    W = H * (C + 1)
    table = net.table(D)
    with ExitStack() as ctx:
        s = net.scope("l1n", ctx)
        f = Front(s)
        ws = {n: s.sb(n, [P, DC * D]) for n in ("W_l", "W_r", "W_res")}
        bs = {n: s.sb(n, [P, D]) for n in ("b_l", "b_r", "bias")}
        we = s.sb("we", [16, D])
        xl = s.sb("xl", [P, 2 * UN * D])
        mean = s.sb("mean", [P, 16])
        meanT = s.sb("meanT", [16, P])
        e = s.sb("e", [P, D])
        ps = {n: s.ps(f"ps_{n}", [P, 512]) for n in ("W_l", "W_r", "W_res", "loop")}
        ps_mean = s.ps("ps_mean", [16, P])
        loaded = s.sem("loaded")
        mean_taken = s.sem("mean_taken")
        mean_turned = s.sem("mean_turned")
        mean_ready = s.sem("mean_ready")
        step = s.sem("step")
        tile_done = s.sem("tile_done")
        stored = [s.sem(f"stored{b}") for b in range(2)]
        pe_tick = s.sem("pe_tick")
        block = ctx.enter_context(nc.Block())

        @block.sync
        def _(sp):
            for n, w in ws.items():
                sp.dma_start(w[:, :].rearrange("p (c n) -> p c n", c=DC), chunked(a[f"L1_gnn_{n}"])).then_inc(loaded, 16)
            for n, v in bs.items():
                sp.dma_start(v[:, :], spread(a[f"L1_gnn_{n}"])).then_inc(loaded, 16)
            sp.dma_start(att[:, :], spread(a["L1_gnn_att"].rearrange("h c -> (h c)"))).then_inc(loaded, 16)
            sp.dma_start(we[:, :], a["L1_gnn_W_e"]).then_inc(loaded, 16)
            for i in range(NI):
                sp.wait_ge(tile_done, (i + 1) * UN)
                sp.dma_start(node_rows(table, i * UN, UN), tiled(at(xl, i % 2, UN * D), D)).then_inc(stored[i % 2], 16)
            sp.wait_ge(stored[0], 48)
            sp.wait_ge(stored[1], 32)

        @block.vector
        def _(dve):
            dve.wait_ge(loaded, 128)
            for i in range(NI):
                f.moments_of(dve, net, i)
                for k in range(UN):
                    f.normalize(dve, net, i, k)
                if i >= 2:
                    dve.wait_ge(stored[i % 2], 16 * (i // 2))
                for k in range(UN):
                    t = i * UN + k
                    link = Chain(dve, step, t * 7)
                    own = at(xl, (i % 2) * UN + k, D)
                    dve.tensor_copy(mean[:, :], at(net.mean16, t, 16)).then_inc(mean_taken, 1)
                    dve.wait_ge(f.projected, UN + t + 1)
                    link(dve.tensor_tensor(own, ps["W_l"][:, 0:D], bs["b_l"][:, :], ALU.add))
                    link(dve.tensor_tensor(at(xr, t, D), ps["W_r"][:, 0:D], bs["b_r"][:, :], ALU.add))
                    dve.tensor_tensor(at(res, t, D), ps["W_res"][:, 0:D], bs["bias"][:, :], ALU.add)
                    link(dve.tensor_tensor(e[:, :], at(xr, t, D), own, ALU.add))
                    link(dve.tensor_tensor(e[:, :], e[:, :], ps["loop"][:, 0:D], ALU.add))
                    link(dve.scalar_tensor_tensor(e[:, :], e[:, :], L1Logits.SLOPE, e[:, :], ALU.mult, ALU.max))
                    link(dve.tensor_tensor(e[:, :], e[:, :], att[:, :], ALU.mult))
                    link(dve.tensor_reduce(at(own_logit, t, H), e[:, :].rearrange("p (h c) -> p h c", h=H), AX.X, ALU.add))
                    dve.sem_inc(tile_done, 1)

        @block.tensor
        def _(pe):
            f.start_tensor(pe)
            pe.wait_ge(loaded, 128)
            with pe.Fori(0, NI) as i:
                for k in range(UN):
                    t = i * UN + k
                    f.turn(pe, net, t, k)
                    pe.wait_ge(mean_taken, t + 1)
                    pe.sem_inc(pe_tick, 1)
                    pe.transpose(ps_mean[:, :], mean[:, :], net.ident[:, :]).then_inc(mean_turned, 1)
                    pe.wait_ge(f.xT_ready, UN + t + 1)
                    for n, w in ws.items():
                        f.project(pe, t, k, ps[n][:, 0:D], w[:, :].rearrange("p (c n) -> p c n", c=DC), last=False)
                    pe.wait_ge(mean_ready, t + 1)
                    pe.matmul(ps["loop"][:, 0:D], meanT[:, :], we[:, :], start=True, stop=True).then_inc(f.projected, 1)

        @block.scalar
        def _(act):
            f.start_scalar(act)
            with act.Fori(0, NI) as i:
                f.root(act, net, i)
                for k in range(UN):
                    t = i * UN + k
                    f.keep(act, t, k)
                    act.wait_ge(mean_turned, t + 1)
                    act.activation(meanT[:, :], ps_mean[:, :], ACT.Copy).then_inc(mean_ready, 1)


def l1_finish(net, res, own_logit, top):
    nc = net.nc
    H, C = 4, 64
    W = H * (C + 1)
    with ExitStack() as ctx:
        s = net.scope("l1f", ctx)
        xl = s.sb("xl", [P, NT * D])
        best = s.sb("best", [P, NT * H])
        total = s.sb("total", [P, NT * H])
        low = s.sb("low", [P, NT * D])
        xl_loaded = s.sem("xl_loaded")
        chain = s.sem("chain")
        to_weigh = s.sem("to_weigh")
        weights_ready = s.sem("weights_ready")
        to_power = s.sem("to_power")
        powered = s.sem("powered")
        block = ctx.enter_context(nc.Block())
        v = res[:, :]
        acc = net.work[:, 0:NT * W].rearrange("p (n c) -> p n c", c=C + 1)

        def every(t):
            return t[:, :].unsqueeze(2).to_broadcast([P, NT * H, C])

        @block.sync
        def _(sp):
            sp.dma_start(tiled(xl[:, :], D), node_rows(net.table(D), 0, NT)).then_inc(xl_loaded, 16)

        @block.scalar
        def _(act):
            act.wait_ge(to_weigh, 1)
            act.activation(own_logit[:, :], own_logit[:, :], ACT.Exp)
            act.activation(top[:, :], top[:, :], ACT.Exp).then_inc(weights_ready, 1)
            act.wait_ge(to_power, 1)
            act.activation(low[:, :], low[:, :], ACT.Exp).then_inc(powered, 1)

        @block.vector
        def _(dve):
            link = Chain(dve, chain)
            link(dve.tensor_tensor(best[:, :], own_logit[:, :], top[:, :], ALU.max))
            link(dve.tensor_tensor(own_logit[:, :], own_logit[:, :], best[:, :], ALU.subtract))
            link(dve.tensor_tensor(top[:, :], top[:, :], best[:, :], ALU.subtract))
            dve.sem_inc(to_weigh, 1)
            dve.wait_ge(weights_ready, 1)
            link(dve.tensor_tensor(total[:, :], acc[:, :, C], top[:, :], ALU.mult))
            link(dve.tensor_tensor(total[:, :], total[:, :], own_logit[:, :], ALU.add))
            link(dve.reciprocal(total[:, :], total[:, :]))
            link(dve.tensor_tensor(top[:, :], top[:, :], total[:, :], ALU.mult))
            link(dve.tensor_tensor(own_logit[:, :], own_logit[:, :], total[:, :], ALU.mult))
            heads = low[:, :].rearrange("p (n c) -> p n c", c=C)
            link(dve.tensor_tensor(heads, acc[:, :, 0:C], every(top), ALU.mult))
            link(dve.tensor_tensor(v, v, low[:, :], ALU.add))
            dve.wait_ge(xl_loaded, 16)
            link(dve.tensor_tensor(heads, xl[:, :].rearrange("p (n c) -> p n c", c=C), every(own_logit), ALU.mult))
            link(dve.tensor_tensor(v, v, low[:, :], ALU.add))
            link(dve.tensor_scalar(low[:, :], v, 0.0, None, ALU.min))
            dve.sem_inc(to_power, 1)
            link(dve.scalar_tensor_tensor(v, v, 0.0, net.x[:, :], ALU.max, ALU.add))
            dve.wait_ge(powered, 1)
            link(dve.scalar_tensor_tensor(net.x[:, :], low[:, :], -1.0, v, ALU.add, ALU.add))


def gcn_edges(net, name, width, acc):
    nc = net.nc
    with ExitStack() as ctx:
        s = net.scope(name, ctx)
        g = Gather(s, net, net.by_dst, net.table(width), width, net.by_dst.number)
        ps = s.ps("ps", [P, NT * width])
        closed = s.sem("closed")
        block = ctx.enter_context(nc.Block())

        @block.sync
        def _(sp):
            g.load(sp)

        @block.gpsimd
        def _(pool):
            g.gather(pool)

        @block.vector
        def _(dve):
            dve.sem_inc(g.rec_free, RING)
            with dve.Fori(0, NB // RING) as i:
                for b in range(RING):
                    q = i * RING + b
                    g.hot(dve, q, i, b)
                    dve.wait_ge(g.hot_ready, q + 1)
                    dve.sem_inc(g.rec_free, 1)
            dve.wait_ge(closed, 1)
            dve.tensor_tensor(acc[:, 0:NT * width], acc[:, 0:NT * width], ps[:, :], ALU.add)

        @block.tensor
        def _(pe):
            pe.sem_inc(g.rows_free, RING)
            pe.sem_inc(g.hot_free, RING)
            open_sums(net, pe, ps, True)
            with pe.Fori(0, NB // RING) as i:
                for b in range(RING):
                    q = i * RING + b
                    blocks = [block_of(pe, g.placed, q * TWO + k) for k in range(TWO)]
                    pe.wait_ge(g.hot_ready, q + 1)
                    g.wait_rows(pe, i, b)
                    pe.sem_inc(g.pe_tick, 1)
                    for k in range(BATCH):
                        ins = pe.matmul(at(ps, blocks[k // 2], width), at(g.onehot[b], k, P), at(g.rows[b], k, width),
                                        start=False, stop=False)
                    ins.then_inc(g.hot_free, 1)
                    pe.wait_ge(g.hot_free, RING + q + 1)
                    pe.sem_inc(g.rows_free, 1)
            open_sums(net, pe, ps, False).then_inc(closed, 1)


def gcn_nodes(net, name, source, out, w_in=None, weights=None, before=None, after=None, final=False):
    nc, a = net.nc, net.a
    n = a[weights].shape[1] if weights else w_in
    k_in = a[weights].shape[0] if weights else w_in
    chunks = -(-k_in // P)
    kp = min(k_in, P)
    table = None if final else net.table(n)
    with ExitStack() as ctx:
        s = net.scope(name, ctx)
        f = Front(s)
        w = s.sb("w", [kp, chunks * n])
        first = s.sb("first", [P, k_in])
        second = s.sb("second", [P, n])
        held = s.sb("held", [P, UN * n])
        ps = s.ps("ps", [P, 2, 512])
        loaded = s.sem("loaded")
        step = s.sem("step")
        held_step = s.sem("held_step")
        out_done = s.sem("out_done")
        stored = s.sem("stored")
        pe_tick = s.sem("pe_tick")
        act_tick = s.sem("act_tick")
        block = ctx.enter_context(nc.Block())
        loads = sum(v is not None for v in (weights, before, after))

        @block.sync
        def _(sp):
            if weights:
                sp.dma_start(w[:, :].rearrange("p (c n) -> p c n", c=chunks), a[weights].rearrange("(c p) n -> p c n", p=kp))\
                    .then_inc(loaded, 16)
            if before:
                sp.dma_start(first[:, :], spread(a[before])).then_inc(loaded, 16)
            if after:
                sp.dma_start(second[:, :], spread(a[after])).then_inc(loaded, 16)
            if not final:
                for i in range(NI):
                    sp.wait_ge(out_done, (2 + i) * UN)
                    sp.dma_start(node_rows(table, i * UN, UN), tiled(at(out, i, UN * n), n)).then_inc(stored, 16)
                sp.wait_ge(stored, NI * 16)

        @block.vector
        def _(dve):
            dve.sem_inc(out_done, UN)
            if loads:
                dve.wait_ge(loaded, 16 * loads)

            def source_tile(t, xn):
                if before is None:
                    return dve.tensor_scalar(xn, at(source, t, k_in), at(net.dinv, t, 1), None, ALU.mult)
                dve.scalar_tensor_tensor(xn, at(source, t, k_in), at(net.dinv, t, 1), first[:, :], ALU.mult, ALU.add)\
                    .then_inc(step, 1)
                dve.wait_ge(step, 2 * t + 1)
                return dve.tensor_scalar(xn, xn, 0.0, None, ALU.max)

            with dve.Fori(0, NI) as i:
                if source is None:
                    f.moments_of(dve, net, i)
                    for k in range(UN):
                        f.normalize(dve, net, i, k)
                elif weights:
                    for k in range(UN):
                        if before is None:
                            dve.sem_inc(step, 1)
                        f.take(dve, i * UN + k, k, lambda xn: source_tile(i * UN + k, xn[:, 0:k_in]))
                        dve.sem_inc(step, 1)
                for k in range(UN):
                    t = i * UN + k
                    dve.wait_ge(out_done, t + 1)
                    if not weights:
                        dve.scalar_tensor_tensor(at(held, k, n), at(source, t, n), at(net.dinv, t, 1), first[:, :],
                                                 ALU.mult, ALU.add).then_inc(step, 1)
                        dve.wait_ge(step, t + 1)
                        dve.tensor_scalar(at(out, t, n), at(held, k, n), 0.0, at(net.dinv, t, 1), ALU.max, ALU.mult)\
                            .then_inc(out_done, 1)
                        continue
                    dve.wait_ge(f.projected, UN + t + 1)
                    if after is None:
                        dve.tensor_scalar(at(out, t, n), ps[:, k % 2, 0:n], at(net.dinv, t, 1), None, ALU.mult)\
                            .then_inc(out_done, 1)
                        continue
                    dve.tensor_tensor(at(held, k, n), ps[:, k % 2, 0:n], second[:, :], ALU.add).then_inc(held_step, 1)
                    dve.wait_ge(held_step, t + 1)
                    if final:
                        dve.tensor_tensor(at(net.x, t, D), at(net.x, t, D), at(held, k, n), ALU.add).then_inc(out_done, 1)
                    else:
                        dve.tensor_scalar(at(out, t, n), at(held, k, n), 0.0, at(net.dinv, t, 1), ALU.max, ALU.mult)\
                            .then_inc(out_done, 1)

        if not weights:
            return

        @block.tensor
        def _(pe):
            f.start_tensor(pe)
            pe.wait_ge(loaded, 16 * loads)
            with pe.Fori(0, NI) as i:
                for k in range(UN):
                    t = i * UN + k
                    f.turn(pe, net, t, k, k_in, pe_tick)
                    pe.wait_ge(f.xT_ready, UN + t + 1)
                    pe.wait_ge(out_done, bank_free(t, k))
                    pe.sem_inc(pe_tick, 1)
                    for c in range(chunks):
                        ins = pe.matmul(ps[:, k % 2, 0:n], f.lhsT(k, c)[0:kp, :], at(w, c, n), start=c == 0, stop=c == chunks - 1)
                    ins.then_inc(f.projected, 1)

        @block.scalar
        def _(act):
            f.start_scalar(act)
            with act.Fori(0, NI) as i:
                if source is None:
                    f.root(act, net, i)
                for k in range(UN):
                    f.keep(act, i * UN + k, k, kp, chunks)


def l2_gnn(net):
    with ExitStack() as ctx:
        s = net.scope("l2", ctx)
        other = s.sb("other", [P, NT * P])
        gcn_nodes(net, "l2a", None, net.work, weights="L2_gnn_W1")
        gcn_edges(net, "l2ae", 128, net.work)
        gcn_nodes(net, "l2b", net.work, other, weights="L2_gnn_W2", before="L2_gnn_b1")
        gcn_edges(net, "l2be", 64, other)
        gcn_nodes(net, "l2c", other, net.work, w_in=64, before="L2_gnn_b2")
        gcn_edges(net, "l2ce", 64, net.work)
        gcn_nodes(net, "l2d", net.work, other, weights="L2_gnn_W3", after="L2_gnn_b3")
        gcn_edges(net, "l2de", 128, other)
        gcn_nodes(net, "l2e", other, None, weights="L2_gnn_W4", after="L2_gnn_b4", final=True)


class L3Logits:

    SLOPE = 0.01

    def __init__(self, net, wide, s, g, ps_x, nodehot, logit, logit_ready, nodehot_ready):
        self.net, self.wide, self.g, self.logit, self.logit_ready = net, wide, g, logit, logit_ready
        self.prod = s.sb("prod", [P, BATCH * P])
        self.edge = s.sb("edge", [P, BATCH])
        self.step = s.sem("e_step")

    def load(self, sp):
        pass

    def start_vector(self, dve):
        dve.sem_inc(self.g.rec_free, RING)

    def start_tensor(self, pe):
        pass

    def start_scalar(self, act):
        pass

    def tensor_early(self, pe, q, i, b):
        pass

    def scalar_early(self, act, q, i, b):
        pass

    def tensor(self, pe, q, i, b):
        pass

    def vector(self, dve, q, i, b):
        for k in range(BATCH):
            ins = dve.tensor_tensor_reduce(at(self.prod, k, P), self.g.columns(b, k, 0, P), self.wide[:, :], 1.0, 0.0,
                                           ALU.mult, ALU.add, self.edge[:, k:k + 1])
        ins.then_inc(self.step, 1)
        dve.wait_ge(self.step, 2 * q + 1)
        dve.sem_inc(self.g.rec_free, 1)
        self.g.wait_rows(dve, i, b)
        dve.tensor_tensor(self.edge[:, :], self.edge[:, :], tiled(self.g.rows[b][:, :], D + 1)[:, :, D], ALU.add)\
            .then_inc(self.step, 1)
        dve.wait_ge(self.step, 2 * q + 2)
        dve.scalar_tensor_tensor(self.logit[b][:, :], self.edge[:, :], self.SLOPE, self.edge[:, :], ALU.mult, ALU.max)\
            .then_inc(self.logit_ready, 1)
        dve.wait_ge(self.logit_ready, q + 1)


def l3_gnn(net):
    with ExitStack() as ctx:
        s = net.scope("l3", ctx)
        wide = s.sb("wide", [P, P])
        l3_nodes(net, wide)
        gat_edges(net, "l3e", 1, D, net.table(D + 1), 0, lambda *args: L3Logits(net, wide, *args))
        l3_finish(net)


def l3_nodes(net, wide):
    nc, a = net.nc, net.a
    W = D + 1
    table = net.table(W)
    with ExitStack() as ctx:
        s = net.scope("l3n", ctx)
        f = Front(s)
        wn = s.sb("wn", [P, DC * D])
        wnT = s.sb("wnT", [P, DC * D])
        we = s.sb("we", [P, DC * P])
        be = s.sb("be", [P, DC])
        attn_col = s.sb("attn_col", [P, DC])
        attn_cols = s.sb("attn_cols", [P, DC * P])
        attn = s.sb("attn", [P, D])
        bn = s.sb("bn", [P, D])
        const = s.sb("const", [P, 1])
        h = s.sb("h", [P, NT * W])
        prod = s.sb("prod", [P, D])
        dot = s.sb("dot", [P, UN])
        held = s.sb("held", [P, UN * D])
        ps_w = s.ps("ps_w", [P, 2, 512])
        ps = s.ps("ps", [P, 2, 512])
        loaded = s.sem("loaded")
        chain = s.sem("chain")
        cols_ready = s.sem("cols_ready")
        w_turned = s.sem("w_turned")
        w_ready = s.sem("w_ready")
        step = s.sem("step")
        h_ready = s.sem("h_ready")
        stored = s.sem("stored")
        block = ctx.enter_context(nc.Block())
        vector = a["L3_gnn_attn"].rearrange("a b c -> (a b c)")

        @block.sync
        def _(sp):
            sp.dma_start(wn[:, :].rearrange("p (c n) -> p c n", c=DC), chunked(a["L3_gnn_Wn"])).then_inc(loaded, 16)
            sp.dma_start(we[:, :].rearrange("p (c n) -> p c n", c=DC), chunked(a["L3_gnn_We"])).then_inc(loaded, 16)
            for c in range(DC):
                sp.dma_start(be[:, c:c + 1], column(a["L3_gnn_be"][c * P:(c + 1) * P])).then_inc(loaded, 16)
                sp.dma_start(attn_col[:, c:c + 1], column(vector[c * P:(c + 1) * P])).then_inc(loaded, 16)
            sp.dma_start(attn[:, :], spread(vector)).then_inc(loaded, 16)
            sp.dma_start(bn[:, :], spread(a["L3_gnn_bn"])).then_inc(loaded, 16)
            for i in range(NI):
                sp.wait_ge(h_ready, (2 + i) * UN)
                sp.dma_start(node_rows(table, i * UN, UN), tiled(at(h, i, UN * W), W)).then_inc(stored, 16)
            sp.wait_ge(stored, NI * 16)

        @block.vector
        def _(dve):
            link = Chain(dve, chain)
            dve.wait_ge(loaded, 128)
            for c in range(DC):
                link(dve.tensor_scalar(at(attn_cols, c, P), net.ones[:, :], attn_col[:, c:c + 1], None, ALU.mult))
            dve.sem_inc(cols_ready, 1)
            dve.wait_ge(w_turned, 1)
            for c in range(DC):
                link(dve.tensor_copy(at(wnT, c, D), ps_w[:, 0, c * D:(c + 1) * D]))
            link(dve.tensor_copy(wide[:, :], ps_w[:, 1, 0:P]))
            link(dve.tensor_copy(const[:, :], ps_w[:, 1, P:P + 1]))
            dve.sem_inc(w_ready, 1)
            dve.sem_inc(h_ready, UN)
            with dve.Fori(0, NI) as i:
                f.moments_of(dve, net, i)
                for k in range(UN):
                    f.normalize(dve, net, i, k)
                for k in range(UN):
                    t = i * UN + k
                    own = h[:, bass.ds(t * W, D)]
                    dve.wait_ge(f.projected, UN + t + 1)
                    dve.tensor_tensor(held[:, k * D:(k + 1) * D], ps[:, k % 2, 0:D], bn[:, :], ALU.add).then_inc(step, 1)
                    dve.wait_ge(step, 2 * t + 1)
                    dve.tensor_copy(own, held[:, k * D:(k + 1) * D])
                    dve.tensor_tensor_reduce(prod[:, :], held[:, k * D:(k + 1) * D], attn[:, :], 1.0, 0.0,
                                             ALU.mult, ALU.add, dot[:, k:k + 1]).then_inc(step, 1)
                    dve.wait_ge(step, 2 * t + 2)
                    dve.tensor_scalar(h[:, bass.ds(t * W + D, 1)], dot[:, k:k + 1], const[:, :], None, ALU.add)\
                        .then_inc(h_ready, 1)

        @block.tensor
        def _(pe):
            f.start_tensor(pe)
            pe.wait_ge(loaded, 128)
            for c in range(DC):
                for m in range(DC):
                    pe.transpose(ps_w[:, 0, c * D + m * P:c * D + (m + 1) * P],
                                 wn[:, m * D + c * P:m * D + (c + 1) * P], net.ident[:, :])
            pe.wait_ge(cols_ready, 1)
            for c in range(DC):
                pe.matmul(ps_w[:, 1, 0:P], at(attn_cols, c, P), at(we, c, P), start=c == 0, stop=c == DC - 1)
            for c in range(DC):
                ins = pe.matmul(ps_w[:, 1, P:P + 1], at(attn_cols, c, P), be[:, c:c + 1], start=c == 0, stop=c == DC - 1)
            ins.then_inc(w_turned, 1)
            pe.wait_ge(w_ready, 1)
            with pe.Fori(0, NI) as i:
                for k in range(UN):
                    t = i * UN + k
                    f.turn(pe, net, t, k)
                    pe.wait_ge(f.xT_ready, UN + t + 1)
                    pe.wait_ge(h_ready, bank_free(t, k))
                    f.project(pe, t, k, ps[:, k % 2, 0:D], wnT[:, :].rearrange("p (c n) -> p c n", c=DC))

        @block.scalar
        def _(act):
            f.start_scalar(act)
            with act.Fori(0, NI) as i:
                f.root(act, net, i)
                for k in range(UN):
                    f.keep(act, i * UN + k, k)


def l3_finish(net):
    nc = net.nc
    W = D + 1
    with ExitStack() as ctx:
        s = net.scope("l3f", ctx)
        share = s.sb("share", [P, NT])
        out = s.sb("out", [P, NT * D])
        chain = s.sem("chain")
        block = ctx.enter_context(nc.Block())
        acc = tiled(net.work[:, 0:NT * W], W)

        @block.vector
        def _(dve):
            link = Chain(dve, chain)
            link(dve.tensor_scalar(share[:, :], acc[:, :, D], 1e-16, None, ALU.add))
            link(dve.reciprocal(share[:, :], share[:, :]))
            link(dve.tensor_tensor(tiled(out[:, :], D), acc[:, :, 0:D], share[:, :].unsqueeze(2).to_broadcast([P, NT, D]), ALU.mult))
            link(dve.scalar_tensor_tensor(net.x[:, :], out[:, :], 0.0, net.x[:, :], ALU.max, ALU.add))


STAGES = (setup, place_by_src, l0_gnn_nodes, l0_gnn_edges, l0_gnn_update, l0_ffn, place_by_dst, edge_means,
          l1_gnn, l1_ffn, l2_gnn, l2_ffn, l3_gnn, l3_ffn)


def build(nc, arrays, out):
    with ExitStack() as ctx:
        net = Net(nc, arrays, ctx)
        for stage in STAGES:
            stage(net)
        store(net, out)


def store(net, out):
    nc = net.nc
    with ExitStack() as ctx:
        s = net.scope("store", ctx)
        stored = s.sem("stored")
        block = ctx.enter_context(nc.Block())

        @block.sync
        def _(sp):
            full = (NT - 1) * P
            sp.dma_start(out[0:full, :].rearrange("(t p) d -> p t d", p=P),
                         net.x[:, 0:(NT - 1) * D].rearrange("p (t d) -> p t d", d=D)).then_inc(stored, 16)
            sp.dma_start(out[full:N, :], net.x[0:TAIL, (NT - 1) * D:NT * D]).then_inc(stored, 16)
            sp.wait_ge(stored, 32)


def kernel(**inputs):
    from concourse import bacc
    from concourse.bass_utils import run_bass_kernel_spmd

    nc = bacc.Bacc("TRN2", target_bir_lowering=False, num_devices=1)
    arrays, aps = {}, {}
    for name, value in inputs.items():
        arrays[f"in_{name}"] = np.ascontiguousarray(value)
        aps[name] = nc.dram_tensor(f"in_{name}", value.shape, mybir.dt.from_np(arrays[f"in_{name}"].dtype),
                                   kind="ExternalInput").ap()
    out = nc.dram_tensor("out", [N, D], F32, kind="ExternalOutput").ap()
    build(nc, aps, out)
    result = run_bass_kernel_spmd(nc, [arrays], core_ids=[0])
    return result.results[0]["out"]
```

```python
from contextlib import ExitStack

import numpy as np

import concourse.bass as bass
from concourse import mybir

F32 = mybir.dt.float32
I32 = mybir.dt.int32
BF16 = mybir.dt.bfloat16
ALU = mybir.AluOpType
ACT = mybir.ActivationFunctionType
AX = mybir.AxisListType

P = 128
N = 3125
D = 256
DC = D // P
E = 50000
NT = -(-N // P)
NP = NT * P
TAIL = N - (NT - 1) * P
EC = E // P
EX = E - EC * P
PAIR = 2 * P
BATCH = 4
TWO = BATCH // 2
RING = 5
NB = -(-(E // PAIR + NT) // (TWO * RING)) * RING
ST = NB * BATCH
SLOTS = ST * P
PAIRS = NB * TWO
BLANKS = 22
assert ST % BLANKS == 0
EXPERTS = 8
EPS = 1e-5
HUGE = 1.0e30

META = 4

UN = 5
NI = NT // UN
assert NT % UN == 0


def at(tensor, t, width):
    if isinstance(t, int):
        return tensor[:, t * width:(t + 1) * width]
    return tensor[:, bass.ds(t * width, width)]


class Placement:

    def __init__(self, nc, s, key, other, fields, weighted):
        self.key, self.other, self.fields, self.weighted = key, other, fields, weighted
        self.first = {}
        at_column = 0
        for name, width in fields:
            self.first[name] = at_column
            at_column += width
        self.number, self.far, self.near = at_column, at_column + 1, at_column + 2
        self.width = at_column + META
        self.pos = self.meta = None
        self.blanked = None
        self.records = nc.dram_tensor(f"records_by_{key}", [SLOTS, self.width], F32, kind="Internal").ap()
        self.block_row = s.sb(f"block_row_{key}", [P, PAIRS], I32)
        self.keep = s.sb(f"keep_{key}", [P, PAIRS])


class Chain:

    def __init__(self, eng, sem, base=0):
        self.eng, self.sem, self.base, self.n = eng, sem, base, 0

    def __call__(self, ins):
        self.n += 1
        ins.then_inc(self.sem, 1)
        self.eng.wait_ge(self.sem, self.base + self.n)

    def steps(self, n):
        assert self.n == n, (self.n, n)


class Scope:

    def __init__(self, nc, name, ctx):
        self.nc, self.name, self.ctx, self.sems = nc, name, ctx, []
        ctx.callback(self.close)

    def close(self):
        if self.sems:
            self.nc.clear_and_free_semaphores(self.sems)
            self.nc.all_engine_barrier()

    def sb(self, name, shape, dt=F32):
        return self.ctx.enter_context(self.nc.sbuf_tensor(f"{self.name}_{name}", shape, dt))

    def ps(self, name, shape, dtype=F32):
        return self.ctx.enter_context(self.nc.psum_tensor(f"{self.name}_{name}", shape, dtype))

    def sem(self, name):
        self.sems.append(self.nc.alloc_semaphore(f"{self.name}_{name}"))
        return self.sems[-1]


class Net:

    def __init__(self, nc, arrays, ctx):
        self.nc = nc
        self.a = arrays
        s = Scope(nc, "net", ctx)
        self.x = s.sb("x", [P, NT * D])
        self.ident = s.sb("ident", [P, P])
        self.before = s.sb("before", [P, P])
        self.ones = s.sb("ones", [P, P])
        self.zeros = s.sb("zeros", [P, 512])
        self.eps = s.sb("eps", [P, 1])
        self.columns = s.sb("columns", [P, P])
        self.rank8 = s.sb("rank8", [P, NT * EXPERTS])
        self.mean16 = s.sb("mean16", [P, NT * 16])
        self.dinv = s.sb("dinv", [P, NT])
        self.work = s.sb("work", [P, NT * 260])
        self.by_src = Placement(nc, s, "src", "dst", (("edge_attr_64", 64),), True)
        self.by_dst = Placement(nc, s, "dst", "src", (("edge_attr_128", 128), ("edge_attr_16", 16)), False)
        self.tokens_cleared = s.sem("tokens_cleared")
        self.tick = s.sem("tick")
        self.tables = {}
        slots = (2 * N // PAIR + EXPERTS) * PAIR
        self.attr_parts = nc.dram_tensor("attr_parts", [NB * P, BATCH * P], BF16, kind="Internal").ap()
        self.dispatch = {n: nc.dram_tensor(n, [slots, D], F32, kind="Internal").ap() for n in ("tokens", "outputs")}

    def scope(self, name, ctx):
        return Scope(self.nc, name, ctx)

    def table(self, width):
        if width not in self.tables:
            self.tables[width] = self.nc.dram_tensor(f"table{width}", [NP, width], F32, kind="Internal").ap()
        return self.tables[width]


def row(vector):
    return vector.rearrange("(o n) -> o n", o=1)


def column(vector):
    return vector.rearrange("(p o) -> p o", o=1)


def spread(vector):
    return row(vector).to_broadcast([P, vector.shape[0]])


def node_rows(table, t0, n):
    return table[bass.ds(t0 * P, n * P), :].rearrange("(t p) d -> p t d", p=P)


def tiled(ap, width):
    return ap.rearrange("p (t d) -> p t d", d=width)


def chunked(weights):
    return weights.rearrange("(c p) n -> p c n", p=P)


def bank_free(q, k):
    return UN + q - 1 + (k == 0)


class Front:

    def __init__(self, s):
        self.stats = s.sb("stats", [P, NT * 6])
        self.moments = s.sb("moments", [P, NT * 2])
        self.sigma = s.sb("sigma", [P, NT])
        self.rstd = s.sb("rstd", [P, NT])
        self.xn = s.sb("xn", [P, UN * D])
        self.xT = s.sb("xT", [P, UN * D])
        self.ps = s.ps("turn", [P, 2, 512])
        self.stats_ready = s.sem("stats_ready")
        self.moments_ready = s.sem("moments_ready")
        self.rstd_ready = s.sem("rstd_ready")
        self.tick = s.sem("tick")
        self.sigma_ready = s.sem("sigma_ready")
        self.normed = s.sem("normed")
        self.turned = s.sem("turned")
        self.xT_ready = s.sem("xT_ready")
        self.projected = s.sem("projected")

    def start_tensor(self, pe):
        pe.sem_inc(self.turned, UN)
        pe.sem_inc(self.projected, UN)

    def start_scalar(self, act):
        act.sem_inc(self.xT_ready, UN)

    def moments_of(self, dve, net):
        with dve.Fori(0, NI) as i:
            for k in range(UN):
                t = i * UN + k
                ins = dve.bn_stats(at(self.stats, t, 6), at(net.x, t, D))
            ins.then_inc(self.stats_ready, 1)
        dve.wait_ge(self.stats_ready, NI)
        dve.sem_inc(self.tick, 1)
        for t in range(NT):
            ins = dve.bn_aggr(at(self.moments, t, 2), at(self.stats, t, 6))
        ins.then_inc(self.moments_ready, 1)
        dve.wait_ge(self.sigma_ready, 1)
        dve.reciprocal(self.rstd[:, :], self.sigma[:, :]).then_inc(self.rstd_ready, 1)
        dve.wait_ge(self.rstd_ready, 1)
        dve.sem_inc(self.tick, 1)

    def root(self, act, net):
        act.wait_ge(self.moments_ready, 1)
        act.activation(self.sigma[:, :], tiled(self.moments[:, :], 2)[:, :, 1], ACT.Sqrt, bias=net.eps[:, :])\
            .then_inc(self.sigma_ready, 1)

    def normalize(self, dve, net, i, k):
        q = i * UN + k
        dve.wait_ge(self.turned, q + 1)
        dve.tensor_scalar(at(self.xn, k, D), at(net.x, q, D), at(self.moments, 2 * q, 1), at(self.rstd, q, 1),
                          ALU.subtract, ALU.mult).then_inc(self.normed, 1)

    def take(self, dve, q, k, fill):
        dve.wait_ge(self.turned, q + 1)
        fill(at(self.xn, k, D)).then_inc(self.normed, 1)

    def turn(self, pe, net, q, k, width=D, tick=None):
        pe.wait_ge(self.normed, q + 1)
        pe.wait_ge(self.xT_ready, bank_free(q, k))
        if tick is not None:
            pe.sem_inc(tick, 1)
        for lo in range(0, width, P):
            n = min(P, width - lo)
            ins = pe.transpose(self.ps[0:n, k % 2, lo:lo + P], self.xn[:, k * D + lo:k * D + lo + n], net.ident[:, :])
        ins.then_inc(self.turned, 1)

    def keep(self, act, q, k, rows=P, chunks=DC):
        act.wait_ge(self.turned, UN + q + 1)
        act.wait_ge(self.projected, q + 1)
        act.activation(self.xT[0:rows, k * D:k * D + chunks * P], self.ps[0:rows, k % 2, 0:chunks * P], ACT.Copy).then_inc(self.xT_ready, 1)

    def lhsT(self, k, c):
        return self.xT[:, k * D + c * P:k * D + (c + 1) * P]

    def project(self, pe, q, k, out, weights, last=True):
        for c in range(DC):
            ins = pe.matmul(out, self.lhsT(k, c), weights[:, c, :], start=c == 0, stop=c == DC - 1)
        if last:
            ins.then_inc(self.projected, 1)


def setup(net):
    nc = net.nc
    with ExitStack() as ctx:
        s = net.scope("setup", ctx)
        index = s.sb("index", [P, P], I32)
        rank = s.sb("rank", [P, NT * EXPERTS], I32)
        x_loaded = s.sem("x_loaded")
        x_cleared = s.sem("x_cleared")
        ones_set = s.sem("ones_set")
        index_set = s.sem("index_set")
        block = ctx.enter_context(nc.Block())

        @block.sync
        def _(sp):
            full = (NT - 1) * P
            sp.wait_ge(x_cleared, 2)
            sp.dma_start(net.x[:, 0:(NT - 1) * D].rearrange("p (t d) -> p t d", d=D),
                         net.a["x"][0:full, :].rearrange("(t p) d -> p t d", p=P)).then_inc(x_loaded, 16)
            sp.dma_start(net.x[0:TAIL, (NT - 1) * D:NT * D], net.a["x"][full:N, :]).then_inc(x_loaded, 16)
            tokens = net.dispatch["tokens"].rearrange("(p r) d -> p (r d)", p=P)
            sp.dma_start(tokens.rearrange("p (n c) -> p n c", c=512),
                         net.zeros[:, :].unsqueeze(1).to_broadcast([P, tokens.shape[1] // 512, 512])).then_inc(net.tokens_cleared, 16)
            sp.wait_ge(x_loaded, 32)

        @block.gpsimd
        def _(pool):
            pool.iota(index[:, :], pattern=[[1, P]], base=0, channel_multiplier=0).then_inc(index_set, 1)
            pool.iota(rank[:, :], pattern=[[0, NT], [-1, EXPERTS]], base=EXPERTS, channel_multiplier=0).then_inc(index_set, 1)
            pool.memset(net.ones[:, :], 1.0).then_inc(ones_set, 1)
            pool.wait_ge(ones_set, 1)
            pool.affine_select(out=net.ident[:, :], in_=net.ones[:, :], compare_op=ALU.is_equal, fill=0.0,
                               base=0, pattern=[[-1, P]], channel_multiplier=1)
            pool.affine_select(out=net.before[:, :], in_=net.ones[:, :], compare_op=ALU.is_gt, fill=0.0,
                               base=0, pattern=[[1, P]], channel_multiplier=-1)

        @block.vector
        def _(dve):
            dve.memset(net.eps[:, :], EPS)
            dve.memset(net.zeros[:, :], 0.0).then_inc(x_cleared, 1)
            dve.memset(net.x[:, (NT - 1) * D:NT * D], 0.0).then_inc(x_cleared, 1)
            dve.wait_ge(index_set, 2)
            dve.tensor_copy(net.rank8[:, :], rank[:, :])
            dve.tensor_copy(net.columns[:, :], index[:, :])


class Numbering:

    def __init__(self, s, shared, to, near, far, weight):
        self.to, self.near, self.far, self.weight = to, near, far, weight
        self.t = shared
        self.chain = s.sem(f"chain_{to.key}")
        self.count_step = s.sem(f"count_step_{to.key}")
        self.pos_step = s.sem(f"pos_step_{to.key}")
        self.totals_ready = s.sem(f"totals_ready_{to.key}")
        self.sums_ready = s.sem(f"sums_ready_{to.key}")
        self.numbered = s.sem(f"numbered_{to.key}")

    @staticmethod
    def shared(s):
        wide, one = [P, EC + 1], [P, NT]
        t = {n: s.sb(n, wide) for n in ("blk", "one_row", "pos_a", "pos_b")}
        t.update({f"match{k}": s.sb(f"match{k}", wide) for k in range(UN)})
        t.update({n: s.sb(n, one) for n in ("totals", "count", "ahead", "pairs", "upto", "first", "base")})
        t["part"] = s.sb("part", wide, I32)
        t["pairs_i"] = s.sb("pairs_i", one, I32)
        t["counted"] = s.sb("counted", [P, NT * (EC + 1)])
        t["pair_no_i"] = s.sb("pair_no_i", [P, PAIRS], I32)
        t["pair_no"] = s.sb("pair_no", [P, PAIRS])
        t["pair_blk"] = s.sb("pair_blk", [P, PAIRS])
        t["ps"] = s.ps("ps_sums", [P, 2, 512])
        return t

    def tensor(self, pe, net):
        t = self.t
        pe.wait_ge(self.totals_ready, 1)
        pe.matmul(t["ps"][:, 0, 0:NT], net.before[:, :], t["totals"][:, :], start=True, stop=True)
        pe.matmul(t["ps"][:, 1, 0:NT], net.ones[:, :], t["totals"][:, :], start=True, stop=True).then_inc(self.sums_ready, 1)

    def vector(self, dve, net):
        to, near, far = self.to, self.near, self.far
        t = {n: (v if n == "ps" else v[:, :]) for n, v in self.t.items()}
        part, blk, counted = t["part"], t["blk"], self.t["counted"]
        match = [t[f"match{k}"] for k in range(UN)]
        link = Chain(dve, self.chain)
        link(dve.tensor_single_scalar(part[:, 0:EC], near[:, 0:EC], 7, op=ALU.arith_shift_right))
        link(dve.tensor_single_scalar(part[0:EX, EC:EC + 1], near[0:EX, EC:EC + 1], 7, op=ALU.arith_shift_right))
        link(dve.memset(blk[:, EC:EC + 1], -1.0))
        link(dve.tensor_copy(blk[:, 0:EC], part[:, 0:EC]))
        link(dve.tensor_copy(blk[0:EX, EC:EC + 1], part[0:EX, EC:EC + 1]))
        link(dve.memset(t["one_row"], 1.0))
        with dve.Fori(0, NI) as i:
            base = i * 2 * UN
            for k in range(UN):
                dve.tensor_scalar(match[k], blk, at(net.columns, i * UN + k, 1), None, ALU.is_equal).then_inc(self.count_step, 1)
            for k in range(UN):
                dve.wait_ge(self.count_step, base + k + 1)
                dve.sem_inc(net.tick, 1)
                dve.tensor_tensor_scan(at(counted, i * UN + k, EC + 1), t["one_row"], match[k], 0.0, ALU.mult, ALU.add)\
                    .then_inc(self.count_step, 1)
            dve.wait_ge(self.count_step, base + 2 * UN)
        link(dve.tensor_copy(t["totals"], counted[:, :].rearrange("p (b j) -> p b j", b=NT)[:, :, EC]))
        dve.sem_inc(self.totals_ready, 1)
        dve.wait_ge(self.sums_ready, 1)
        link(dve.tensor_copy(t["ahead"], t["ps"][:, 0, 0:NT]))
        link(dve.tensor_copy(t["count"], t["ps"][:, 1, 0:NT]))
        base, pairs, first = t["base"], t["pairs"], t["first"]
        link(dve.tensor_scalar(base, t["count"], float(PAIR - 1), None, ALU.add))
        link(dve.tensor_copy(t["pairs_i"], base))
        link(dve.tensor_single_scalar(t["pairs_i"], t["pairs_i"], 8, op=ALU.arith_shift_right))
        link(dve.tensor_copy(pairs, t["pairs_i"]))
        link(dve.tensor_tensor_scan(t["upto"], t["one_row"][:, 0:NT], pairs, 0.0, ALU.mult, ALU.add))
        link(dve.tensor_tensor(first, t["upto"], pairs, ALU.subtract))
        link(dve.scalar_tensor_tensor(base, first, float(PAIR), t["ahead"], ALU.mult, ALU.add))
        link(dve.tensor_scalar(base, base, -1.0, None, ALU.add))
        pos = (t["pos_a"], t["pos_b"])
        for p in pos:
            link(dve.memset(p, 0.0))
        with dve.Fori(0, NI) as i:
            base3 = i * 3 * UN
            for k in range(UN):
                dve.tensor_scalar(match[k], blk, at(net.columns, i * UN + k, 1), None, ALU.is_equal).then_inc(self.pos_step, 1)
            for k in range(UN):
                b = i * UN + k
                dve.wait_ge(self.pos_step, base3 + k + 1)
                dve.scalar_tensor_tensor(match[k], at(counted, b, EC + 1), at(self.t["base"], b, 1), match[k],
                                         ALU.add, ALU.mult).then_inc(self.pos_step, 1)
            for k in range(UN):
                dve.wait_ge(self.pos_step, base3 + UN + max(k + 1, 2 * k - 1 if k < 2 else UN + k - 1))
                dve.tensor_tensor(pos[k % 2], pos[k % 2], match[k], ALU.add).then_inc(self.pos_step, 1)
            dve.wait_ge(self.pos_step, base3 + 3 * UN)
        link(dve.tensor_tensor(pos[0], pos[0], pos[1], ALU.add))
        link(dve.tensor_copy(to.pos[:, :], pos[0]))
        m = to.meta[:, :].rearrange("p (j r) -> p j r", r=META)
        link(dve.memset(to.meta[:, :], 1.0))
        for lo, hi, p in ((0, EC, P), (EC, EC + 1, EX)):
            if to.weighted:
                link(dve.tensor_copy(m[0:p, lo:hi, 0], self.weight[0:p, lo:hi]))
            link(dve.tensor_copy(m[0:p, lo:hi, 1], far[0:p, lo:hi]))
            link(dve.tensor_single_scalar(part[0:p, lo:hi], near[0:p, lo:hi], P - 1, op=ALU.bitwise_and))
            link(dve.tensor_copy(m[0:p, lo:hi, 2], part[0:p, lo:hi]))
        dve.sem_inc(self.numbered, 1)
        link(dve.tensor_copy(t["pair_no"], t["pair_no_i"]))
        link(dve.memset(t["pair_blk"], -1.0))
        for b in range(NT):
            link(dve.scalar_tensor_tensor(t["pair_blk"], t["pair_no"], at(self.t["first"], b, 1), t["pair_blk"], ALU.is_ge, ALU.add))
        link(dve.tensor_copy(to.block_row[:, :], t["pair_blk"]))
        link(dve.memset(to.keep[:, 0:1], 0.0))
        link(dve.tensor_tensor(to.keep[:, 1:PAIRS], t["pair_blk"][:, 1:PAIRS], t["pair_blk"][:, 0:PAIRS - 1], ALU.is_equal))


class Scatter:

    def __init__(self, s, net, to, columns, ring, chunks, first=0, last=True):
        self.to, self.a, self.columns, self.ring, self.chunks = to, net.a, columns, ring, chunks
        assert first % columns == 0
        self.ahead = first // columns
        self.rec = [s.sb(f"rec_{to.key}{b}", [P, columns * to.width]) for b in range(ring)]
        self.pos_at = [s.sb(f"pos_at_{to.key}{b}", [P, columns], I32) for b in range(ring)]
        self.loaded = [s.sem(f"loaded_{to.key}{b}") for b in range(ring)]
        self.scattered = [s.sem(f"scattered_{to.key}{b}") for b in range(ring)]
        self.copied = s.sem(f"copied_{to.key}")
        self.tick = s.sem(f"scatter_tick_{to.key}")
        self.left_loaded = s.sem(f"left_loaded_{to.key}")
        self.left_copied = s.sem(f"left_copied_{to.key}")
        self.left_scattered = s.sem(f"left_scattered_{to.key}")
        done = first + chunks * columns
        self.left = [(j, min(columns, EC - j), P) for j in range(done, EC, columns)] + [(EC, 1, EX)] if last else []

    def load(self, sp, q, i, b):
        if not isinstance(i, int) or i:
            sp.wait_ge(self.scattered[b], i * 16 * self.columns)
        rec = tiled(self.rec[b][:, :], self.to.width)
        for name, w in self.to.fields:
            c = self.to.first[name]
            rows = self.a[name][0:EC * P, :].rearrange("(p j) w -> p (j w)", p=P)
            sp.dma_start(rec[:, :, c:c + w], tiled(rows[:, bass.ds((q + self.ahead) * (self.columns * w), self.columns * w)], w))\
                .then_inc(self.loaded[b], 16)

    def scatter(self, pool, q, i, b):
        to = self.to
        pool.wait_ge(self.loaded[b], (i + 1) * 16 * len(to.fields))
        pool.sem_inc(self.tick, 1)
        pool.tensor_copy(tiled(self.rec[b][:, :], to.width)[:, :, to.number:to.width],
                         at(to.meta, q + self.ahead, self.columns * META).rearrange("p (j r) -> p j r", r=META)).then_inc(self.copied, 1)
        pool.tensor_copy(self.pos_at[b][:, :], at(to.pos, q + self.ahead, self.columns)).then_inc(self.copied, 1)
        pool.wait_ge(self.copied, 2 * q + 2)
        pool.sem_inc(self.tick, 1)
        for j in range(self.columns):
            pool.indirect_dma_start(to.records, bass.IndirectOffsetOnAxis(self.pos_at[b][:, j:j + 1], 0),
                                    at(self.rec[b], j, to.width), None).then_inc(self.scattered[b], 16)

    def load_left(self, sp):
        for b in range(self.ring):
            sp.wait_ge(self.scattered[b], self.chunks // self.ring * 16 * self.columns)
        for n, (j, w_j, p) in enumerate(self.left):
            rec = tiled(self.rec[n][0:p, 0:w_j * self.to.width], self.to.width)
            for name, w in self.to.fields:
                c = self.to.first[name]
                if j < EC:
                    rows = tiled(self.a[name][0:EC * P, :].rearrange("(p j) w -> p (j w)", p=P)[:, j * w:(j + w_j) * w], w)
                else:
                    rows = self.a[name][EC * P:E, :].unsqueeze(1)
                sp.dma_start(rec[:, :, c:c + w], rows).then_inc(self.left_loaded, 16)

    def scatter_left(self, pool):
        to = self.to
        pool.wait_ge(self.left_loaded, 16 * len(to.fields) * len(self.left))
        pool.sem_inc(self.tick, 1)
        for n, (j, w_j, p) in enumerate(self.left):
            pool.tensor_copy(tiled(self.rec[n][0:p, 0:w_j * to.width], to.width)[:, :, to.number:to.width],
                             to.meta[0:p, j * META:(j + w_j) * META].rearrange("p (j r) -> p j r", r=META))\
                .then_inc(self.left_copied, 1)
        pool.wait_ge(self.left_copied, len(self.left))
        for n, (j, w_j, p) in enumerate(self.left):
            for c in range(w_j):
                pool.indirect_dma_start(to.records, bass.IndirectOffsetOnAxis(to.pos[0:p, j + c:j + c + 1], 0),
                                        self.rec[n][0:p, c * to.width:(c + 1) * to.width], None).then_inc(self.left_scattered, 16)
        pool.wait_ge(self.left_scattered, 16 * sum(w_j for _, w_j, _ in self.left))


def l0_gnn(net):
    with ExitStack() as ctx:
        s = net.scope("l0", ctx)
        for to in (net.by_src, net.by_dst):
            to.pos = s.sb(f"pos_{to.key}", [P, EC + 1], I32)
            to.meta = s.sb(f"meta_{to.key}", [P, (EC + 1) * META])
            to.blanked = s.sem(f"blanked_{to.key}")
        l0_gnn_nodes(net)
        l0_gnn_edges(net)
        l0_gnn_update(net)


def batch_records(records, q, lo, hi):
    rows = records[bass.ds(q * (BATCH * P), BATCH * P), :]
    return rows.rearrange("(t p) r -> p t r", p=P)[:, :, lo:hi]


def l0_gnn_nodes(net):
    nc, a = net.nc, net.a
    table = net.table(D)
    JC = 13
    CHUNKS = EC // JC
    DEEP = 3
    assert CHUNKS % DEEP == 0
    with ExitStack() as ctx:
        s = net.scope("l0n", ctx)
        src = s.sb("src", [P, EC + 1], I32)
        dst = s.sb("dst", [P, EC + 1], I32)
        weight = s.sb("weight", [P, EC + 1])
        blank = {to.key: s.sb(f"blank_{to.key}", [P, BLANKS * to.width]) for to in (net.by_src, net.by_dst)}
        shared = Numbering.shared(s)
        by_src = Numbering(s, shared, net.by_src, src, dst, weight)
        by_dst = Numbering(s, shared, net.by_dst, dst, src, None)
        scatter = Scatter(s, net, net.by_src, JC, DEEP, CHUNKS)
        f = Front(s)
        w = s.sb("w", [P, DC * D])
        h = s.sb("h", [P, 2 * UN * D])
        ps = s.ps("ps", [P, 2, 512])
        ids_loaded = s.sem("ids_loaded")
        blank_step = s.sem("blank_step")
        pairs_numbered = s.sem("pairs_numbered")
        w_loaded = s.sem("w_loaded")
        h_ready = s.sem("h_ready")
        h_stored = [s.sem(f"h_stored{b}") for b in range(2)]
        block = ctx.enter_context(nc.Block())
        wv = w[:, :].rearrange("p (c n) -> p c n", c=DC)

        @block.sync
        def _(sp):
            for name, into in (("src", src), ("dst", dst), ("edge_weight1", weight)):
                flat = a[name] if name != "edge_weight1" else a[name].rearrange("e o -> (e o)")
                sp.dma_start(into[:, 0:EC], flat[0:EC * P].rearrange("(p j) -> p j", p=P)).then_inc(ids_loaded, 16)
                sp.dma_start(into[0:EX, EC:EC + 1], flat[EC * P:E].rearrange("(p j) -> p j", j=1)).then_inc(ids_loaded, 16)
            sp.dma_start(wv, chunked(a["L0_gnn_W_in2f"])).then_inc(w_loaded, 16)
            sp.wait_ge(blank_step, 4)
            for to in (net.by_src, net.by_dst):
                sp.dma_start(to.records.rearrange("(p n t) r -> p n (t r)", p=P, t=BLANKS),
                             blank[to.key][:, :].unsqueeze(1).to_broadcast([P, ST // BLANKS, BLANKS * to.width])).then_inc(to.blanked, 16)
                if to is net.by_src:
                    for b in range(DEEP):
                        scatter.load(sp, b, 0, b)
            with sp.Fori(1, CHUNKS // DEEP) as i:
                for b in range(DEEP):
                    scatter.load(sp, i * DEEP + b, i, b)
            scatter.load_left(sp)
            sp.wait_ge(net.by_dst.blanked, 16)

        @block.gpsimd
        def _(pool):
            pool.iota(shared["pair_no_i"][:, :], pattern=[[1, PAIRS]], base=0, channel_multiplier=0).then_inc(pairs_numbered, 1)
            pool.wait_ge(by_src.numbered, 1)
            pool.wait_ge(net.by_src.blanked, 16)
            pool.sem_inc(net.tick, 1)
            with pool.Fori(0, CHUNKS // DEEP) as i:
                for b in range(DEEP):
                    scatter.scatter(pool, i * DEEP + b, i, b)
            scatter.scatter_left(pool)

        @block.vector
        def _(dve):
            for to in (net.by_src, net.by_dst):
                dve.memset(blank[to.key][:, :], 0.0).then_inc(blank_step, 1)
            for n, to in enumerate((net.by_src, net.by_dst)):
                dve.wait_ge(blank_step, n + 1)
                dve.memset(tiled(blank[to.key][:, :], to.width)[:, :, to.near:to.near + 1], -1.0).then_inc(blank_step, 1)
            dve.wait_ge(ids_loaded, 96)
            dve.wait_ge(pairs_numbered, 1)
            dve.sem_inc(net.tick, 1)
            by_src.vector(dve, net)
            f.moments_of(dve, net)
            with dve.Fori(0, NI) as i:
                for k in range(UN):
                    t = i * UN + k
                    f.normalize(dve, net, i, k)
                    dve.wait_ge(f.normed, t + 1)
                    dve.tensor_tensor(at(net.x, t, D), at(net.x, t, D), at(f.xn, k, D), ALU.add)
            by_dst.vector(dve, net)

        @block.tensor
        def _(pe):
            by_src.tensor(pe, net)
            f.start_tensor(pe)
            pe.wait_ge(w_loaded, 16)
            with pe.Fori(0, NI) as i:
                for k in range(UN):
                    t = i * UN + k
                    f.turn(pe, net, t, k)
                    pe.wait_ge(f.xT_ready, UN + t + 1)
                    pe.wait_ge(h_ready, bank_free(t, k))
                    f.project(pe, t, k, ps[:, k % 2, 0:D], wv)
            by_dst.tensor(pe, net)

        @block.scalar
        def _(act):
            f.start_scalar(act)
            act.sem_inc(h_ready, UN)
            f.root(act, net)
            for i in range(NI):
                if i >= 2:
                    act.wait_ge(h_stored[i % 2], 16 * (i // 2))
                for k in range(UN):
                    t = i * UN + k
                    f.keep(act, t, k)
                    act.wait_ge(f.projected, UN + t + 1)
                    act.activation(at(h, i % 2 * UN + k, D), ps[:, k % 2, 0:D], ACT.Copy).then_inc(h_ready, 1)
                act.wait_ge(h_ready, UN + (i + 1) * UN)
                act.dma_start(node_rows(table, i * UN, UN), tiled(at(h, i % 2, UN * D), D)).then_inc(h_stored[i % 2], 16)
            act.wait_ge(h_stored[0], 48)
            act.wait_ge(h_stored[1], 32)


LN2 = float(np.log(2.0))
CLAMP = 80.0


def mark_nodes(eng, net, onehot, near):
    wide = [P, BATCH, P]
    return eng.tensor_tensor(tiled(onehot[:, :], P), net.columns[:, :].unsqueeze(1).to_broadcast(wide),
                             near.unsqueeze(2).to_broadcast(wide), ALU.is_equal)


class Gather:

    def __init__(self, s, net, placed, table, width, lo):
        self.net, self.placed, self.table, self.width, self.lo, self.n = net, placed, table, width, lo, placed.width - lo
        self.rec = [s.sb(f"rec{b}", [P, BATCH * self.n]) for b in range(RING)]
        self.idx = [s.sb(f"idx{b}", [P, BATCH], I32) for b in range(RING)]
        self.rows = [s.sb(f"rows{b}", [P, BATCH * width]) for b in range(RING)]
        self.onehot = [s.sb(f"onehot{b}", [P, BATCH * P]) for b in range(RING)]
        self.rec_loaded = [s.sem(f"rec_loaded{b}") for b in range(RING)]
        self.hot_ready = s.sem("hot_ready")
        self.rows_loaded = [s.sem(f"rows_loaded{b}") for b in range(RING)]
        self.rec_free = s.sem("rec_free")
        self.rows_free = s.sem("rows_free")
        self.hot_free = s.sem("hot_free")
        self.pool_tick = s.sem("pool_tick")
        self.pe_tick = s.sem("pe_tick")

    def load_batch(self, sp, q, b):
        sp.wait_ge(self.rec_free, q + 1)
        sp.dma_start(tiled(self.rec[b][:, :], self.n), batch_records(self.placed.records, q, self.lo, self.placed.width))\
            .then_inc(self.rec_loaded[b], 16)

    def load(self, sp, more=None):
        with sp.Fori(0, NB // RING) as i:
            for b in range(RING):
                self.load_batch(sp, i * RING + b, b)
                if more is not None:
                    more(sp, i * RING + b, b)

    def gather_batch(self, pool, q, b):
        pool.wait_ge(self.hot_ready, q + 1)
        pool.wait_ge(self.rows_free, q + 1)
        pool.sem_inc(self.pool_tick, 1)
        for k in range(BATCH):
            pool.indirect_dma_start(at(self.rows[b], k, self.width), None, self.table,
                                    bass.IndirectOffsetOnAxis(self.idx[b][:, k:k + 1], 0)).then_inc(self.rows_loaded[b], 16)

    def gather(self, pool):
        with pool.Fori(0, NB // RING) as i:
            for b in range(RING):
                self.gather_batch(pool, i * RING + b, b)

    def column(self, b, c, k=None):
        c -= self.lo
        if k is None:
            return tiled(self.rec[b][:, :], self.n)[:, :, c]
        return self.rec[b][:, k * self.n + c:k * self.n + c + 1]

    def columns(self, b, k, c, w):
        c -= self.lo
        return self.rec[b][:, k * self.n + c:k * self.n + c + w]

    def hot(self, eng, q, i, b, tick=None):
        eng.wait_ge(self.rec_loaded[b], i * 16 + 16)
        eng.wait_ge(self.hot_free, q + 1)
        if tick is not None:
            eng.sem_inc(tick, 1)
            eng.tensor_copy(self.idx[b][:, :], self.column(b, self.placed.far))
            for k in range(BATCH):
                ins = eng.tensor_scalar(at(self.onehot[b], k, P), self.net.columns[:, :], self.column(b, self.placed.near, k),
                                        None, ALU.is_equal)
            ins.then_inc(self.hot_ready, 1)
            return
        eng.tensor_copy(self.idx[b][:, :], self.column(b, self.placed.far))
        mark_nodes(eng, self.net, self.onehot[b], self.column(b, self.placed.near)).then_inc(self.hot_ready, 1)

    def wait_rows(self, eng, i, b):
        eng.wait_ge(self.rows_loaded[b], i * 16 * BATCH + 16 * BATCH)


def skewed(eng, *stages, ring=RING, total=NB):
    deepest = max(lag for lag, _ in stages)
    assert deepest <= ring and total % ring == 0

    def alone(t):
        for lag, step in stages:
            q = t - lag
            if 0 <= q < total:
                step(q, q // ring, q % ring)

    for t in range(ring):
        alone(t)
    with eng.Fori(0, total // ring - 1) as j:
        for u in range(ring):
            for lag, step in stages:
                b = (u - lag) % ring
                i = j + 1 if u >= lag else j
                step(i * ring + b, i, b)
    for t in range(total, total + deepest):
        alone(t)


def block_of(eng, placed, pair):
    return eng.value_load(placed.block_row[0:1, bass.ds(pair, 1)], min_val=0, max_val=NT - 1)


def open_sums(net, pe, ps, opens):
    width = ps.shape[1]
    for lo in range(0, width, 512):
        n = min(512, width - lo)
        ins = pe.matmul(ps[:, lo:lo + n], net.zeros[:, 0:P], net.zeros[:, 0:n], start=opens, stop=not opens)
    return ins


BESIDE = EC // NB * NB


def l0_gnn_edges(net):
    nc, a = net.nc, net.a
    HC = D // P
    WIDE = BATCH * P
    with ExitStack() as ctx:
        s = net.scope("l0e", ctx)
        g = Gather(s, net, net.by_src, net.table(D), D, 0)
        scatter = Scatter(s, net, net.by_dst, BESIDE // NB, RING, NB, last=False)
        wf1 = s.sb("wf1", [64, D])
        wf2 = s.sb("wf2", [P, HC * D])
        bf1 = s.sb("bf1", [P, HC])
        bf1_ln2 = s.sb("bf1_ln2", [P, HC])
        bf2 = s.sb("bf2", [P, D])
        half = s.sb("half", [P, 1])
        rbfT = [s.sb(f"rbfT{b}", [64, WIDE]) for b in range(RING)]
        raised = [s.sb(f"raised{c}", [P, WIDE]) for c in range(HC)]
        hidT = [s.sb(f"hidT{b}", [P, HC * WIDE]) for b in range(RING)]
        shifted = s.sb("shifted", [P, BATCH * D])
        msg = [s.sb(f"msg{b}", [P, BATCH * D]) for b in range(RING)]
        total = [s.sb(f"total{k}", [P, D]) for k in range(TWO)]
        ps_t = s.ps("ps_t", [64, WIDE])
        ps_h = s.ps("ps_h", [P, HC, 512])
        ps_w = s.ps("ps_w", [P, TWO, 512])
        ps_s = s.ps("ps_s", [P, TWO, 512])
        loaded = s.sem("loaded")
        cleared = s.sem("cleared")
        turned = s.sem("turned")
        rbf_ready = s.sem("rbf_ready")
        hidden = s.sem("hidden")
        raise_step = s.sem("raise_step")
        powered = s.sem("powered")
        logged = s.sem("logged")
        hid_ready = s.sem("hid_ready")
        filters = s.sem("filters")
        shifted_ready = s.sem("shifted_ready")
        msg_ready = s.sem("msg_ready")
        summed = s.sem("summed")
        total_ready = s.sem("total_ready")
        flushed = s.sem("flushed")
        act_tick = s.sem("act_tick")
        block = ctx.enter_context(nc.Block())

        @block.sync
        def _(sp):
            sp.dma_start(wf1[:, :], a["L0_gnn_Wf1"]).then_inc(loaded, 16)
            sp.dma_start(wf2[:, :].rearrange("p (c n) -> p c n", c=HC), chunked(a["L0_gnn_Wf2"])).then_inc(loaded, 16)
            for c in range(HC):
                sp.dma_start(bf1[:, c:c + 1], column(a["L0_gnn_bf1"][c * P:(c + 1) * P])).then_inc(loaded, 16)
            sp.dma_start(bf2[:, :], spread(a["L0_gnn_bf2"])).then_inc(loaded, 16)
            for b in range(RING):
                g.load_batch(sp, b, b)
                scatter.load(sp, b, 0, b)
            with sp.Fori(1, NB // RING) as i:
                for b in range(RING):
                    g.load_batch(sp, i * RING + b, b)
                    scatter.load(sp, i * RING + b, i, b)
            scatter.load_left(sp)

        @block.gpsimd
        def _(pool):
            with pool.Fori(0, NB // RING) as i:
                for b in range(RING):
                    g.gather_batch(pool, i * RING + b, b)
                    scatter.scatter(pool, i * RING + b, i, b)

        @block.vector
        def _(dve):
            dve.sem_inc(g.rec_free, RING)
            dve.sem_inc(g.rows_free, RING)
            dve.memset(net.work[:, 0:NT * D], 0.0).then_inc(cleared, 1)
            dve.memset(total[(PAIRS - 1) % TWO][:, :], 0.0).then_inc(cleared, 1)
            dve.memset(half[:, :], 0.5).then_inc(cleared, 1)
            dve.wait_ge(loaded, 80)
            dve.tensor_scalar(bf1_ln2[:, :], bf1[:, :], -LN2, None, ALU.add).then_inc(cleared, 1)
            dve.sem_inc(hid_ready, HC)
            dve.sem_inc(shifted_ready, TWO)
            dve.sem_inc(msg_ready, TWO)
            dve.sem_inc(total_ready, TWO)
            dve.wait_ge(cleared, 4)

            def clamp(q, i, b):
                for c in range(HC):
                    dve.wait_ge(hidden, HC * q + c + 1)
                    dve.tensor_scalar(raised[c][:, :], ps_h[:, c, :], bf1[:, c:c + 1], CLAMP, ALU.add, ALU.min)\
                        .then_inc(raise_step, 1)

            def hide(q, i, b):
                for c in range(HC):
                    dve.wait_ge(logged, HC * q + c + 1)
                    dve.scalar_tensor_tensor(at(hidT[b], c, WIDE), ps_h[:, c, :], bf1_ln2[:, c:c + 1], raised[c][:, :],
                                             ALU.add, ALU.max).then_inc(hid_ready, 1)

            def message(q, i, b):
                g.wait_rows(dve, i, b)
                for k in range(TWO):
                    n = q * TWO + k
                    dve.wait_ge(filters, n + 1)
                    dve.wait_ge(msg_ready, n + 1)
                    dve.tensor_tensor(tiled(at(shifted, k, 2 * D), D), tiled(ps_w[:, k, 0:2 * D], D),
                                      bf2[:, :].unsqueeze(1).to_broadcast([P, 2, D]), ALU.add).then_inc(shifted_ready, 1)
                    dve.wait_ge(shifted_ready, n + TWO + 1)
                    for m in (2 * k, 2 * k + 1):
                        ins = dve.scalar_tensor_tensor(at(msg[b], m, D), at(shifted, m, D), g.column(b, g.placed.number, m),
                                                       at(g.rows[b], m, D), ALU.mult, ALU.mult)
                    ins.then_inc(msg_ready, 1)
                dve.wait_ge(msg_ready, q * TWO + 2 * TWO)
                dve.sem_inc(g.rec_free, 1)
                dve.sem_inc(g.rows_free, 1)

            def add(q, i, b):
                for k in range(TWO):
                    n = q * TWO + k
                    dve.wait_ge(summed, n + 1)
                    dve.wait_ge(total_ready, n + TWO)
                    dve.wait_ge(flushed, n + 1)
                    dve.scalar_tensor_tensor(total[k][:, :], total[1 - k][:, :], g.placed.keep[:, bass.ds(n, 1)],
                                             ps_s[:, k, 0:D], ALU.mult, ALU.add).then_inc(total_ready, 1)

            skewed(dve, (1, clamp), (0, lambda q, i, b: g.hot(dve, q, i, b)), (2, message), (1, hide), (3, add))

        @block.tensor
        def _(pe):
            pe.sem_inc(g.hot_free, RING)
            pe.wait_ge(loaded, 80)

            def turn(q, i, b):
                pe.wait_ge(g.rec_loaded[b], i * 16 + 16)
                pe.wait_ge(rbf_ready, q + 1)
                pe.sem_inc(g.pe_tick, 1)
                for k in range(BATCH):
                    ins = pe.transpose(at(ps_t, k, P), g.columns(b, k, 0, 64), net.ident[:, :])
                ins.then_inc(turned, 1)

            def hide(q, i, b):
                pe.wait_ge(rbf_ready, q + 2)
                for c in range(HC):
                    pe.wait_ge(hid_ready, HC * q + c + 1)
                    pe.matmul(ps_h[:, c, :], wf1[:, c * P:(c + 1) * P], rbfT[b][:, :], start=True, stop=True)\
                        .then_inc(hidden, 1)

            def filter(q, i, b):
                pe.wait_ge(hid_ready, HC * q + 2 * HC)
                for k in range(TWO):
                    n = q * TWO + k
                    pe.wait_ge(shifted_ready, n + 1)
                    for m in range(2):
                        for c in range(HC):
                            ins = pe.matmul(ps_w[:, k, m * D:(m + 1) * D],
                                            hidT[b][:, c * WIDE + (2 * k + m) * P:c * WIDE + (2 * k + m + 1) * P],
                                            at(wf2, c, D), start=c == 0, stop=c == HC - 1)
                    ins.then_inc(filters, 1)

            def add(q, i, b):
                for k in range(TWO):
                    n = q * TWO + k
                    pe.wait_ge(msg_ready, n + TWO + 1)
                    pe.wait_ge(total_ready, n + 1)
                    for m in range(2):
                        ins = pe.matmul(ps_s[:, k, 0:D], at(g.onehot[b], 2 * k + m, P), at(msg[b], 2 * k + m, D),
                                        start=m == 0, stop=m == 1)
                    ins.then_inc(summed, 1)
                pe.wait_ge(summed, q * TWO + TWO)
                pe.sem_inc(g.hot_free, 1)

            skewed(pe, (1, hide), (2, filter), (0, turn), (3, add))

        @block.scalar
        def _(act):
            act.sem_inc(rbf_ready, 1)
            act.sem_inc(flushed, TWO)
            act.wait_ge(cleared, 4)

            def turn(q, i, b):
                act.wait_ge(turned, q + 1)
                act.activation(rbfT[b][:, :], ps_t[:, :], ACT.Copy).then_inc(rbf_ready, 1)

            def power(q, i, b):
                for c in range(HC):
                    act.wait_ge(raise_step, HC * q + c + 1)
                    act.activation(raised[c][:, :], raised[c][:, :], ACT.Exp).then_inc(powered, 1)
                for c in range(HC):
                    act.wait_ge(powered, HC * q + c + 1)
                    act.activation(raised[c][:, :], raised[c][:, :], ACT.Ln, bias=half[:, :], scale=0.5).then_inc(logged, 1)

            def flush(q, i, b):
                for k in range(TWO):
                    n = q * TWO + k
                    blk = block_of(act, g.placed, n)
                    act.wait_ge(total_ready, n + TWO + 1)
                    act.wait_ge(flushed, n + TWO)
                    act.sem_inc(act_tick, 1)
                    act.activation(at(net.work, blk, D), total[k][:, :], ACT.Copy).then_inc(flushed, 1)

            skewed(act, (1, power), (0, turn), (4, flush))


THIRD = (0, 1, 2, 0, 1)


def third_free(q):
    return UN + q - 1


def l0_gnn_update(net):
    nc, a = net.nc, net.a
    JC = 10
    DEEP = 3
    CHUNKS = (EC - BESIDE) // JC // DEEP * DEEP
    with ExitStack() as ctx:
        s = net.scope("l0u", ctx)
        f = Front(s)
        scatter = Scatter(s, net, net.by_dst, JC, DEEP, CHUNKS, first=BESIDE)
        wo1 = s.sb("wo1", [P, DC * D])
        wo2 = s.sb("wo2", [P, DC * D])
        bo1 = s.sb("bo1", [P, DC])
        bo1_ln2 = s.sb("bo1_ln2", [P, DC])
        bo2 = s.sb("bo2", [P, D])
        half = s.sb("half", [P, 1])
        raised = net.work[:, 0:NT * D]
        lowered = s.sb("lowered", [P, NT * D])
        hidT = [s.sb(f"hidT{b}", [P, D]) for b in range(UN)]
        ps_h = s.ps("ps_h", [P, 3, 512])
        ps_m = s.ps("ps_m", [P, 3, 512])
        loaded = s.sem("loaded")
        set_up = s.sem("set_up")
        raise_step = s.sem("raise_step")
        powered = s.sem("powered")
        logged = s.sem("logged")
        hid_ready = s.sem("hid_ready")
        updates = s.sem("updates")
        biased = s.sem("biased")
        added = s.sem("added")
        block = ctx.enter_context(nc.Block())

        @block.sync
        def _(sp):
            for w, into in (("L0_gnn_Wo1", wo1), ("L0_gnn_Wo2", wo2)):
                sp.dma_start(into[:, :].rearrange("p (c n) -> p c n", c=DC), chunked(a[w])).then_inc(loaded, 16)
            for c in range(DC):
                sp.dma_start(bo1[:, c:c + 1], column(a["L0_gnn_bo1"][c * P:(c + 1) * P])).then_inc(loaded, 16)
            sp.dma_start(bo2[:, :], spread(a["L0_gnn_bo2"])).then_inc(loaded, 16)
            for q in range(CHUNKS):
                scatter.load(sp, q, q // DEEP, q % DEEP)
            scatter.load_left(sp)

        @block.gpsimd
        def _(pool):
            with pool.Fori(0, CHUNKS // DEEP) as i:
                for b in range(DEEP):
                    scatter.scatter(pool, i * DEEP + b, i, b)
            scatter.scatter_left(pool)

        @block.vector
        def _(dve):
            link = Chain(dve, set_up)
            dve.wait_ge(loaded, 80)
            link(dve.memset(half[:, :], 0.5))
            link(dve.tensor_scalar(bo1_ln2[:, :], bo1[:, :], -LN2, None, ALU.add))
            dve.sem_inc(raise_step, UN)
            dve.sem_inc(added, UN)

            def take(t, i, b):
                f.take(dve, t, b, lambda xn: dve.tensor_copy(xn, at(net.work, t, D)))
                dve.tensor_tensor(at(net.x, t, D), at(net.x, t, D), bo2[:, :], ALU.add).then_inc(biased, 1)

            def clamp(t, i, b):
                dve.wait_ge(f.projected, UN + t + 1)
                for c in range(DC):
                    of_ps = at(ps_h[:, THIRD[b], :], c, P)
                    dve.tensor_scalar(at(lowered, t * DC + c, P), of_ps, bo1_ln2[:, c:c + 1], None, ALU.add)
                    ins = dve.tensor_scalar(at(raised, t * DC + c, P), of_ps, bo1[:, c:c + 1], CLAMP, ALU.add, ALU.min)
                ins.then_inc(raise_step, 1)

            def hide(t, i, b):
                dve.wait_ge(logged, i + 1)
                dve.wait_ge(updates, t + 1)
                dve.tensor_tensor(hidT[b][:, :], at(raised, t, D), at(lowered, t, D), ALU.max).then_inc(hid_ready, 1)

            def add(t, i, b):
                dve.wait_ge(updates, UN + t + 1)
                dve.wait_ge(biased, t + 1)
                dve.tensor_tensor(at(net.x, t, D), at(net.x, t, D), ps_m[:, THIRD[b], 0:D], ALU.add).then_inc(added, 1)

            skewed(dve, (2, clamp), (0, take), ring=UN, total=NT)
            skewed(dve, (0, hide), (2, add), ring=UN, total=NT)

        @block.tensor
        def _(pe):
            f.start_tensor(pe)
            pe.wait_ge(loaded, 80)

            def hide(t, i, b):
                pe.wait_ge(f.xT_ready, UN + t + 1)
                pe.wait_ge(raise_step, third_free(t))
                for m in range(DC):
                    for c in range(DC):
                        ins = pe.matmul(at(ps_h[:, THIRD[b], :], m, P), wo1[:, c * D + m * P:c * D + (m + 1) * P], f.lhsT(b, c),
                                        start=c == 0, stop=c == DC - 1)
                ins.then_inc(f.projected, 1)

            def update(t, i, b):
                pe.wait_ge(hid_ready, t + 1)
                pe.wait_ge(added, third_free(t))
                for c in range(DC):
                    ins = pe.matmul(ps_m[:, THIRD[b], 0:D], at(hidT[b], c, P), at(wo2, c, D), start=c == 0, stop=c == DC - 1)
                ins.then_inc(updates, 1)

            skewed(pe, (0, lambda t, i, b: f.turn(pe, net, t, b)), (1, hide), ring=UN, total=NT)
            pe.sem_inc(updates, UN)
            skewed(pe, (0, update), ring=UN, total=NT)

        @block.scalar
        def _(act):
            f.start_scalar(act)
            act.wait_ge(set_up, 1)

            def power(i):
                act.wait_ge(raise_step, (i + 2) * UN)
                act.activation(at(raised, i, UN * D), at(raised, i, UN * D), ACT.Exp).then_inc(powered, 1)

            for i in range(NI):
                for b in range(UN):
                    f.keep(act, i * UN + b, b)
                if i:
                    power(i - 1)
            power(NI - 1)
            for i in range(NI):
                act.wait_ge(powered, i + 1)
                act.activation(at(raised, i, UN * D), at(raised, i, UN * D), ACT.Ln, bias=half[:, :], scale=0.5).then_inc(logged, 1)


GROUP = UN * P
PART = GROUP // 2


def turn_rows(pe, net, out, rows):
    return pe.transpose(out, rows, net.ident[0:rows.shape[0], 0:rows.shape[0]])


def moe(net, name, router, bias, layers, last, last_bias):
    nc, a = net.nc, net.a
    with ExitStack() as ctx:
        s = net.scope(name, ctx)
        xT = s.sb("xT", [P, DC * NP])
        logits = s.sb("logits", [P, NT * EXPERTS])
        mix = s.sb("mix", [P, NT * EXPERTS])
        moe_front(net, name, logits, router, xT=xT)
        choose("all")(net, name, logits, bias, mix)
        moe_bias(net, name, mix, a[last_bias], net.x)
        moe_experts(net, name, xT, mix, net.x, layers, a[last])


def moe_front(net, name, logits, router, keeps_tokens=False, xT=None, xn=None):
    nc, a = net.nc, net.a
    by_expert = router.shape[0] == EXPERTS
    with ExitStack() as ctx:
        s = net.scope(name + "f", ctx)
        f = Front(s)
        rows = s.sb("rows", [EXPERTS, D])
        w = s.sb("w", [P, DC * EXPERTS])
        ps = s.ps("ps", [P, 3, 512])
        w_loaded = s.sem("w_loaded")
        w_turned = s.sem("w_turned")
        w_ready = s.sem("w_ready")
        copied = s.sem("copied")
        kept = s.sem("kept")
        logits_ready = s.sem("logits_ready")
        pool_tick = s.sem("pool_tick")
        dve_tick = s.sem("dve_tick")
        block = ctx.enter_context(nc.Block())
        wv = w[:, :].rearrange("p (c n) -> p c n", c=DC)

        @block.sync
        def _(sp):
            if by_expert:
                sp.dma_start(rows[:, :], router).then_inc(w_loaded, 16)
            else:
                sp.dma_start(wv, chunked(router)).then_inc(w_loaded, 16)

        @block.gpsimd
        def _(pool):
            pool.sem_inc(copied, UN)
            with pool.Fori(0, NI) as i:
                for k in range(UN):
                    t = i * UN + k
                    if xn is not None:
                        pool.wait_ge(f.normed, t + 1)
                        pool.sem_inc(pool_tick, 1)
                        pool.tensor_copy(at(xn, t, D), at(f.xn, k, D)).then_inc(copied, 1)
                        continue
                    pool.wait_ge(f.xT_ready, UN + t + 1)
                    pool.sem_inc(pool_tick, 1)
                    for c in range(DC):
                        ins = pool.tensor_copy(xT[:, bass.ds(c * NP + t * P, P)], f.lhsT(k, c))
                    ins.then_inc(copied, 1)

        @block.vector
        def _(dve):
            dve.sem_inc(logits_ready, UN)
            if keeps_tokens:
                dve.sem_inc(kept, UN)
            dve.wait_ge(w_loaded, 16)
            if by_expert:
                dve.wait_ge(w_turned, 1)
                dve.tensor_copy(w[:, :], ps[:, 0, 0:DC * EXPERTS]).then_inc(w_ready, 1)
            else:
                dve.sem_inc(w_ready, 1)
            f.moments_of(dve, net)

            def normalize(t, i, k):
                if xn is not None:
                    dve.wait_ge(copied, t + 1)
                if keeps_tokens:
                    dve.wait_ge(kept, t + 1)
                f.normalize(dve, net, i, k)

            def keep(t, i, k):
                if keeps_tokens:
                    dve.wait_ge(f.normed, t + 1)
                    dve.tensor_tensor(at(net.x, t, D), at(net.x, t, D), at(f.xn, k, D), ALU.add).then_inc(kept, 1)

            def logit(t, i, k):
                dve.wait_ge(f.projected, UN + t + 1)
                dve.sem_inc(dve_tick, 1)
                dve.tensor_copy(at(logits, t, EXPERTS), ps[:, THIRD[k], 0:EXPERTS]).then_inc(logits_ready, 1)

            skewed(dve, (0, normalize), (1, keep), (3, logit), ring=UN, total=NT)

        @block.tensor
        def _(pe):
            f.start_tensor(pe)
            if by_expert:
                pe.wait_ge(w_loaded, 16)
                for c in range(DC):
                    ins = turn_rows(pe, net, ps[:, 0, c * EXPERTS:(c + 1) * EXPERTS], rows[:, c * P:(c + 1) * P])
                ins.then_inc(w_turned, 1)
            pe.wait_ge(w_ready, 1)

            def project(t, i, k):
                pe.wait_ge(f.xT_ready, UN + t + 1)
                pe.wait_ge(logits_ready, third_free(t))
                f.project(pe, t, k, ps[:, THIRD[k], 0:EXPERTS], wv)

            skewed(pe, (0, lambda t, i, k: f.turn(pe, net, t, k)), (1, project), ring=UN, total=NT)

        @block.scalar
        def _(act):
            f.start_scalar(act)
            f.root(act, net)
            with act.Fori(0, NI) as i:
                for k in range(UN):
                    t = i * UN + k
                    if xT is not None:
                        act.wait_ge(copied, t + 1)
                    f.keep(act, t, k)


def by_expert(t):
    return tiled(t[:, :], EXPERTS)


def over_experts(t):
    return t[:, :].unsqueeze(2).to_broadcast([P, NT, EXPERTS])


def first_best(dve, link, net, vals, best, onehot, score, top):
    link(dve.tensor_reduce(best[:, :], by_expert(vals), AX.X, ALU.max))
    link(dve.tensor_tensor(by_expert(score), by_expert(vals), over_experts(best), ALU.is_equal))
    link(dve.tensor_tensor(by_expert(score), by_expert(score), by_expert(net.rank8), ALU.mult))
    link(dve.tensor_reduce(top[:, :], by_expert(score), AX.X, ALU.max))
    link(dve.tensor_tensor(by_expert(onehot), by_expert(score), over_experts(top), ALU.is_equal))


def softmax_experts(dve, link, act_exp, vals, best, out, total):
    link(dve.tensor_reduce(best[:, :], by_expert(vals), AX.X, ALU.max))
    link(dve.tensor_tensor(by_expert(out), by_expert(vals), over_experts(best), ALU.subtract))
    act_exp()
    link(dve.tensor_reduce(total[:, :], by_expert(out), AX.X, ALU.add))
    link(dve.reciprocal(total[:, :], total[:, :]))
    link(dve.tensor_tensor(by_expert(out), by_expert(out), over_experts(total), ALU.mult))


def choose(kind):
    def stage(net, name, logits, bias, mix):
        nc = net.nc
        with ExitStack() as ctx:
            s = net.scope(name + "c", ctx)
            lg = s.sb("lg", [P, NT * EXPERTS])
            bias_row = s.sb("bias_row", [P, EXPERTS])
            probs = s.sb("probs", [P, NT * EXPERTS])
            score = s.sb("score", [P, NT * EXPERTS])
            one = s.sb("one", [P, NT * EXPERTS])
            two = s.sb("two", [P, NT * EXPERTS])
            rest = s.sb("rest", [P, NT * EXPERTS])
            ones_row = s.sb("ones_row", [P, NT])
            best = s.sb("best", [P, NT])
            second = s.sb("second", [P, NT])
            total = s.sb("total", [P, NT])
            top = s.sb("top", [P, NT])
            ps = s.ps("ps", [P, 2, 512])
            loaded = s.sem("loaded")
            chain = s.sem("chain")
            to_power = s.sem("to_power")
            powered = s.sem("powered")
            one_ready = s.sem("one_ready")
            counted = s.sem("counted")
            to = mix if isinstance(mix, Dispatch) else None
            if to:
                ahead = s.sb("ahead", [P, NT * EXPERTS])
                either = s.sb("either", [P, NT * EXPERTS])
                start = s.sb("start", [P, EXPERTS])
                groups = s.sb("groups", [P, EXPERTS])
                groups_i = s.sb("groups_i", [P, EXPERTS], I32)
                slot = s.sb("slot", [P, NT])
                room = s.sb("room", [P, NT])
                group_no_i = s.sb("group_no_i", [P, to.groups], I32)
                group_no = s.sb("group_no", [P, to.groups])
                number = s.sb("number", [P, to.groups])
                numbered = s.sem("numbered")
            block = ctx.enter_context(nc.Block())

            @block.sync
            def _(sp):
                if bias is not None:
                    sp.dma_start(bias_row[:, :], spread(bias)).then_inc(loaded, 16)

            @block.scalar
            def _(act):
                power = {"probs": probs, "pair": total, "all": probs, "capacity": probs}[kind]
                act.wait_ge(to_power, 1)
                act.activation(power[:, :], power[:, :], ACT.Exp).then_inc(powered, 1)

            @block.tensor
            def _(pe):
                if to:
                    pe.wait_ge(one_ready, 1)
                    pe.matmul(ps[:, 0, 0:NT * EXPERTS], net.before[:, :], either[:, :], start=True, stop=True)
                    pe.matmul(ps[:, 1, 0:NT * EXPERTS], net.ones[:, :], either[:, :], start=True, stop=True)\
                        .then_inc(counted, 1)

            @block.gpsimd
            def _(pool):
                if to:
                    pool.iota(group_no_i[:, :], pattern=[[1, to.groups]], base=0, channel_multiplier=0).then_inc(numbered, 1)

            @block.vector
            def _(dve):
                link = Chain(dve, chain)

                def act_exp():
                    dve.sem_inc(to_power, 1)
                    dve.wait_ge(powered, 1)

                if bias is None:
                    link(dve.tensor_copy(lg[:, :], logits[:, :]))
                else:
                    dve.wait_ge(loaded, 16)
                    link(dve.tensor_tensor(by_expert(lg), by_expert(logits),
                                           bias_row[:, :].unsqueeze(1).to_broadcast([P, NT, EXPERTS]), ALU.add))
                if kind == "all":
                    softmax_experts(dve, link, act_exp, lg, best, probs, total)
                    link(dve.tensor_copy(mix[:, :], probs[:, :]))
                    return
                vals = lg
                if kind != "pair":
                    softmax_experts(dve, link, act_exp, lg, best, probs, total)
                    vals = probs
                first_best(dve, link, net, vals, best, one, score, top)

                def rank():
                    dve.sem_inc(one_ready, 1)
                    dve.wait_ge(counted, 1)
                    link(dve.memset(ones_row[:, :], 1.0))
                    link(dve.tensor_copy(score[:, :], ps[:, 1, 0:NT * EXPERTS]))
                    for e in range(EXPERTS):
                        link(dve.tensor_tensor_scan(by_expert(rest)[:, :, e], ones_row[:, :], by_expert(score)[:, :, e],
                                                    0.0, ALU.mult, ALU.add))
                    link(dve.tensor_tensor(ahead[:, :], rest[:, :], score[:, :], ALU.subtract))
                    link(dve.tensor_tensor(ahead[:, :], ahead[:, :], ps[:, 0, 0:NT * EXPERTS], ALU.add))

                def place(onehot, places, into):
                    link(dve.tensor_tensor(score[:, :], onehot[:, :], places[:, :], ALU.mult))
                    link(dve.tensor_reduce(slot[:, :], by_expert(score), AX.X, ALU.add))
                    link(dve.tensor_copy(into, slot[:, :]))

                if kind == "capacity":
                    link(dve.tensor_copy(either[:, :], one[:, :]))
                    rank()
                    dve.wait_ge(numbered, 1)
                    link(dve.tensor_single_scalar(to.expert_row[:, :], group_no_i[:, :], (ROOM // SLICE).bit_length() - 1,
                                                  op=ALU.arith_shift_right))
                    link(dve.tensor_scalar(two[:, :], net.rank8[:, :], -float(ROOM), float(ROOM * EXPERTS), ALU.mult, ALU.add))
                    link(dve.tensor_tensor(rest[:, :], ahead[:, :], two[:, :], ALU.add))
                    link(dve.tensor_scalar(either[:, :], ahead[:, :], float(CAPACITY), None, ALU.is_ge))
                    link(dve.scalar_tensor_tensor(rest[:, :], either[:, :], float(to.groups * SLICE), rest[:, :], ALU.mult, ALU.add))
                    place(one, rest, to.slot_in[0][:, :])
                    link(dve.tensor_scalar(ahead[:, :], ahead[:, :], float(CAPACITY - 1), None, ALU.min))
                    link(dve.tensor_tensor(rest[:, :], ahead[:, :], two[:, :], ALU.add))
                    place(one, rest, to.slot_out[0][:, :])
                    link(dve.tensor_tensor(score[:, :], one[:, :], either[:, :], ALU.mult))
                    link(dve.tensor_reduce(room[:, :], by_expert(score), AX.X, ALU.add))
                    link(dve.tensor_scalar(room[:, :], room[:, :], -1.0, 1.0, ALU.mult, ALU.add))
                    link(dve.tensor_tensor(to.weight[0][:, :], best[:, :], room[:, :], ALU.mult))
                    return
                link(dve.scalar_tensor_tensor(rest[:, :], one[:, :], -HUGE, vals[:, :], ALU.mult, ALU.add))
                first_best(dve, link, net, rest, second, two, score, top)
                if kind == "pair":
                    link(dve.tensor_tensor(total[:, :], second[:, :], best[:, :], ALU.subtract))
                    act_exp()
                    link(dve.tensor_copy(second[:, :], total[:, :]))
                    link(dve.memset(best[:, :], 1.0))
                    link(dve.tensor_scalar(total[:, :], total[:, :], 1.0, None, ALU.add))
                else:
                    link(dve.tensor_tensor(total[:, :], best[:, :], second[:, :], ALU.add))
                    link(dve.tensor_scalar(total[:, :], total[:, :], 1e-12, None, ALU.max))
                link(dve.reciprocal(total[:, :], total[:, :]))
                link(dve.tensor_tensor(best[:, :], best[:, :], total[:, :], ALU.mult))
                link(dve.tensor_tensor(second[:, :], second[:, :], total[:, :], ALU.mult))
                if to:
                    link(dve.tensor_copy(to.weight[0][:, :], best[:, :]))
                    link(dve.tensor_copy(to.weight[1][:, :], second[:, :]))
                    for t in (one, two):
                        tail = at(t, NT - 1, EXPERTS)
                        link(dve.tensor_scalar(tail, tail, net.before[:, TAIL:TAIL + 1], None, ALU.mult))
                    link(dve.tensor_tensor(either[:, :], one[:, :], two[:, :], ALU.add))
                    rank()
                    link(dve.tensor_scalar(start[:, :], at(rest, NT - 1, EXPERTS), float(SLICE - 1), None, ALU.add))
                    link(dve.tensor_copy(groups_i[:, :], start[:, :]))
                    link(dve.tensor_single_scalar(groups_i[:, :], groups_i[:, :], SLICE.bit_length() - 1, op=ALU.arith_shift_right))
                    link(dve.tensor_copy(groups[:, :], groups_i[:, :]))
                    link(dve.tensor_tensor_scan(start[:, :], ones_row[:, 0:EXPERTS], groups[:, :], 0.0, ALU.mult, ALU.add))
                    link(dve.tensor_tensor(start[:, :], start[:, :], groups[:, :], ALU.subtract))
                    dve.wait_ge(numbered, 1)
                    link(dve.tensor_copy(group_no[:, :], group_no_i[:, :]))
                    link(dve.memset(number[:, :], -1.0))
                    for e in range(EXPERTS):
                        link(dve.scalar_tensor_tensor(number[:, :], group_no[:, :], start[:, e:e + 1], number[:, :],
                                                      ALU.is_ge, ALU.add))
                    link(dve.tensor_copy(to.expert_row[:, :], number[:, :]))
                    link(dve.tensor_scalar(start[:, :], start[:, :], float(SLICE), None, ALU.mult))
                    link(dve.tensor_tensor(by_expert(rest), by_expert(ahead),
                                           start[:, :].unsqueeze(1).to_broadcast([P, NT, EXPERTS]), ALU.add))
                    place(one, rest, to.slot_in[0][:, :])
                    place(two, rest, to.slot_in[1][:, :])
                    return
                link(dve.tensor_tensor(by_expert(one), by_expert(one), over_experts(best), ALU.mult))
                link(dve.tensor_tensor(by_expert(two), by_expert(two), over_experts(second), ALU.mult))
                link(dve.tensor_tensor(mix[:, :], one[:, :], two[:, :], ALU.add))
    return stage


def moe_bias(net, name, mix, bias, acc):
    nc = net.nc
    with ExitStack() as ctx:
        s = net.scope(name + "b", ctx)
        rows = s.sb("rows", [EXPERTS, D])
        own = [s.sb(f"own{b}", [P, EXPERTS]) for b in range(UN)]
        ownT = [s.sb(f"ownT{b}", [EXPERTS, P]) for b in range(UN)]
        ps_t = s.ps("ps_t", [EXPERTS, 3, 512])
        ps = s.ps("ps", [P, 3, 512])
        loaded = s.sem("loaded")
        taken = s.sem("taken")
        turned = s.sem("turned")
        kept = s.sem("kept")
        biases = s.sem("biases")
        added = s.sem("added")
        tick = s.sem("tick")
        dve_tick = s.sem("dve_tick")
        block = ctx.enter_context(nc.Block())

        @block.sync
        def _(sp):
            sp.dma_start(rows[:, :], bias).then_inc(loaded, 16)

        @block.vector
        def _(dve):
            dve.sem_inc(added, UN)

            def take(t, i, b):
                dve.wait_ge(turned, t + 1)
                dve.sem_inc(dve_tick, 1)
                dve.tensor_copy(own[b][:, :], at(mix, t, EXPERTS)).then_inc(taken, 1)

            def add(t, i, b):
                dve.wait_ge(biases, UN + t + 1)
                dve.tensor_tensor(at(acc, t, D), at(acc, t, D), ps[:, THIRD[b], 0:D], ALU.add).then_inc(added, 1)

            skewed(dve, (0, take), (3, add), ring=UN, total=NT)

        @block.tensor
        def _(pe):
            pe.sem_inc(turned, UN)
            pe.sem_inc(biases, UN)
            pe.wait_ge(loaded, 16)

            def turn(t, i, b):
                pe.wait_ge(taken, t + 1)
                pe.wait_ge(kept, third_free(t))
                pe.sem_inc(tick, 1)
                pe.transpose(ps_t[:, THIRD[b], 0:P], own[b][:, :], net.ident[:, :]).then_inc(turned, 1)

            def weigh(t, i, b):
                pe.wait_ge(kept, UN + t + 1)
                pe.wait_ge(added, third_free(t))
                pe.matmul(ps[:, THIRD[b], 0:D], ownT[b][:, :], rows[:, :], start=True, stop=True).then_inc(biases, 1)

            skewed(pe, (0, turn), (1, weigh), ring=UN, total=NT)

        @block.scalar
        def _(act):
            act.sem_inc(kept, UN)

            def keep(t, i, b):
                act.wait_ge(turned, UN + t + 1)
                act.wait_ge(biases, t + 1)
                act.activation(ownT[b][:, :], ps_t[:, THIRD[b], 0:P], ACT.Copy).then_inc(kept, 1)

            skewed(act, (0, keep), ring=UN, total=NT)


def moe_experts(net, name, xT, mix, acc, layers, last):
    nc, a = net.nc, net.a
    widths = [DC] + [a[w].shape[2] // P for w, _, _ in layers]
    halves = [2 * n for n in widths[1:]]
    starts = [sum(halves[:l]) for l in range(len(layers) + 1)]
    H = starts[-1]
    assert all(n % 4 == 0 for n in halves)
    with ExitStack() as ctx:
        s = net.scope(name + "e", ctx)
        w_in = [[s.sb(f"w{l}_{b}", [P, widths[l] * widths[l + 1] * P]) for b in range(2)] for l in range(len(layers))]
        w_out = [s.sb(f"wo_{b}", [P, widths[-1] * D]) for b in range(2)]
        hT = [s.sb(f"hT{l}", [P, widths[l + 1] * GROUP]) for l in range(len(layers))]
        vec_rows = [[s.sb(f"vr{l}_{v}", [EXPERTS * widths[l + 1], P]) for v in range(len(vs))]
                    for l, (_, vs, _) in enumerate(layers)]
        vec = [[s.sb(f"v{l}_{v}", [P, EXPERTS * widths[l + 1]]) for v in range(len(vs))]
               for l, (_, vs, _) in enumerate(layers)]
        own = [[s.sb(f"own{l}_{v}", [P, widths[l + 1]]) for v in range(min(2, len(vs)))]
               for l, (_, vs, _) in enumerate(layers)]
        ps_h = s.ps("ps_h", [P, 4, 512])
        ps_y = s.ps("ps_y", [P, 4, 512])
        vec_loaded = s.sem("vec_loaded")
        vec_turned = s.sem("vec_turned")
        vec_step = s.sem("vec_step")
        vec_rooted = s.sem("vec_rooted")
        vec_ready = s.sem("vec_ready")
        w_loaded = [s.sem(f"w_loaded{b}") for b in range(2)]
        products = s.sem("products")
        active = s.sem("active")
        outs = s.sem("outs")
        own_ready = s.sem("own_ready")
        pe_tick = s.sem("pe_tick")
        act_tick = s.sem("act_tick")
        mixed = s.sem("mixed")
        block = ctx.enter_context(nc.Block())
        vectors = [(l, v) for l, (_, vs, _) in enumerate(layers) for v in range(len(vs))]
        WL = 16 * (len(layers) + 1)

        def load(sp, e, b):
            for l, (w, _, _) in enumerate(layers):
                k, n = a[w].shape[1], a[w].shape[2]
                flat = a[w].rearrange("e k n -> (e k) n")[bass.ds(e * k, k), :]
                sp.dma_start(w_in[l][b][:, :].rearrange("p (c n) -> p c n", n=n), chunked(flat)).then_inc(w_loaded[b], 16)
            k = last.shape[1]
            flat = last.rearrange("e k n -> (e k) n")[bass.ds(e * k, k), :]
            sp.dma_start(tiled(w_out[b][:, :], D), chunked(flat)).then_inc(w_loaded[b], 16)

        @block.sync
        def _(sp):
            for l, v in vectors:
                sp.dma_start(vec_rows[l][v][:, :], a[layers[l][1][v]].rearrange("e (c p) -> (e c) p", p=P))\
                    .then_inc(vec_loaded, 16)
            for b in range(2):
                load(sp, b, b)
            with sp.Fori(1, EXPERTS // 2) as i:
                for b in range(2):
                    sp.wait_ge(outs, UN + (2 * i + b - 1) * NT)
                    load(sp, 2 * i + b, b)

        @block.tensor
        def _(pe):
            pe.sem_inc(outs, UN)
            pe.wait_ge(vec_loaded, 16 * len(vectors))
            for n, (l, v) in enumerate(vectors):
                turn_rows(pe, net, ps_h[:, n % 4, 64 * (n // 4):64 * (n // 4) + EXPERTS * widths[l + 1]],
                          vec_rows[l][v][:, :]).then_inc(vec_turned, 1)
            pe.wait_ge(vec_ready, 1)

            def expert(i, e, b):
                pe.wait_ge(w_loaded[b], i * WL + WL)
                pe.sem_inc(pe_tick, 1)
                with pe.Fori(0, NI) as g:
                    q = e * NI + g
                    for l in range(len(layers)):
                        for c in range(halves[l]):
                            half, m = divmod(c, widths[l + 1])
                            n = starts[l] + c
                            if l and m == 0:
                                pe.wait_ge(active, q * H + starts[l - 1] + (half + 1) * widths[l] + 4)
                            pe.wait_ge(active, q * H + n + 1)
                            for k in range(widths[l]):
                                rhs = xT[:, bass.ds(k * NP + g * GROUP + half * PART, PART)] if l == 0 else \
                                    hT[l - 1][:, k * GROUP + half * PART:k * GROUP + (half + 1) * PART]
                                lo = (k * widths[l + 1] + m) * P
                                ins = pe.matmul(ps_h[:, c % 4, 0:PART], w_in[l][b][:, lo:lo + P], rhs,
                                                start=k == 0, stop=k == widths[l] - 1)
                            ins.then_inc(products, 1)
                    for j in range(UN):
                        n = q * UN + j
                        if j == 0:
                            pe.wait_ge(active, q * H + H - widths[-1] + 4)
                        if (j + 1) * P > PART:
                            pe.wait_ge(active, q * H + H + 4)
                        pe.wait_ge(mixed, n + {0: UN, 4: 2}.get(j, 1))
                        for k in range(widths[-1]):
                            ins = pe.matmul(ps_y[:, j % 4, 0:D], hT[-1][:, k * GROUP + j * P:k * GROUP + (j + 1) * P],
                                            at(w_out[b], k, D), start=k == 0, stop=k == widths[-1] - 1)
                        ins.then_inc(outs, 1)

            with pe.Fori(0, EXPERTS // 2) as i:
                for b in range(2):
                    expert(i, 2 * i + b, b)

        @block.scalar
        def _(act):
            act.sem_inc(active, 4)
            for l, (_, vs, _) in enumerate(layers):
                if len(vs) > 1:
                    act.wait_ge(vec_step, len(vectors))
                    act.activation(vec[l][4][:, :], vec[l][4][:, :], ACT.Sqrt).then_inc(vec_rooted, 1)
            act.wait_ge(vec_ready, 1)

            with act.Fori(0, EXPERTS // 2) as i:
                for b in range(2):
                    e = 2 * i + b
                    act.wait_ge(active, e * NI * H + 4)
                    act.sem_inc(act_tick, 1)
                    copies = [act.activation(own[l][v][:, :], at(vec[l][v], e, widths[l + 1]), ACT.Copy)
                              for l in range(len(layers)) for v in range(len(own[l]))]
                    copies[-1].then_inc(own_ready, 1)
                    act.wait_ge(own_ready, e + 1)
                    act.sem_inc(act_tick, 1)
                    with act.Fori(0, NI) as g:
                        q = e * NI + g
                        for l, (_, vs, func) in enumerate(layers):
                            if l == len(layers) - 1:
                                act.wait_ge(outs, q * UN + UN)
                                act.sem_inc(act_tick, 1)
                            for c in range(halves[l]):
                                half, m = divmod(c, widths[l + 1])
                                act.wait_ge(products, q * H + starts[l] + c + 1)
                                act.activation(hT[l][:, m * GROUP + half * PART:m * GROUP + (half + 1) * PART],
                                               ps_h[:, c % 4, 0:PART], func,
                                               bias=own[l][0][:, m:m + 1],
                                               scale=own[l][1][:, m:m + 1] if len(vs) > 1 else 1.0)\
                                    .then_inc(active, 1)

        @block.vector
        def _(dve):
            dve.sem_inc(mixed, UN)
            link = Chain(dve, vec_step)
            dve.wait_ge(vec_turned, len(vectors))
            for n, (l, v) in enumerate(vectors):
                from_ps = ps_h[:, n % 4, 64 * (n // 4):64 * (n // 4) + EXPERTS * widths[l + 1]]
                if v == 4:
                    link(dve.tensor_scalar(vec[l][v][:, :], from_ps, BN_EPS, None, ALU.add))
                else:
                    link(dve.tensor_copy(vec[l][v][:, :], from_ps))
            if any(len(vs) > 1 for _, vs, _ in layers):
                dve.wait_ge(vec_rooted, len(layers))
            for l, (_, vs, _) in enumerate(layers):
                if len(vs) > 1:
                    bias, gain, shift, mean, var = (t[:, :] for t in vec[l])
                    link(dve.reciprocal(var, var))
                    link(dve.tensor_tensor(gain, gain, var, ALU.mult))
                    link(dve.tensor_tensor(bias, bias, mean, ALU.subtract))
                    link(dve.tensor_tensor(bias, bias, gain, ALU.mult))
                    link(dve.tensor_tensor(bias, bias, shift, ALU.add))
            dve.sem_inc(vec_ready, 1)

            with dve.Fori(0, EXPERTS) as e:
                with dve.Fori(0, NI) as g:
                    for j in range(UN):
                        t = g * UN + j
                        n = e * NT + t
                        dve.wait_ge(outs, UN + n + 1)
                        dve.wait_ge(mixed, n + 1)
                        dve.scalar_tensor_tensor(at(acc, t, D), ps_y[:, j % 4, 0:D], at(mix, t * EXPERTS + e, 1),
                                                 at(acc, t, D), ALU.mult, ALU.add).then_inc(mixed, 1)


SLICE = 2 * P


class Dispatch:

    def __init__(self, net, s, choices, groups, capacity):
        self.choices, self.groups, self.capacity = choices, groups, capacity
        self.slot_in = [s.sb(f"slot_in{c}", [P, NT], I32) for c in range(choices)]
        self.slot_out = [s.sb(f"slot_out{c}", [P, NT], I32) for c in range(choices)] if capacity else self.slot_in
        self.weight = [s.sb(f"weight{c}", [P, NT]) for c in range(choices)]
        self.expert_row = s.sb("expert_row", [P, groups], I32)
        self.tokens = net.dispatch["tokens"][0:groups * SLICE, :]
        self.outputs = net.dispatch["outputs"][0:groups * SLICE, :]


def moe_sparse(net, name, router, bias, kind, choices, groups, w1, b1, func, w2, b2, keeps_tokens=False):
    with ExitStack() as ctx:
        s = net.scope(name, ctx)
        xn = s.sb("xn", [P, NT * D])
        logits = s.sb("logits", [P, NT * EXPERTS])
        to = Dispatch(net, s, choices, groups, kind == "capacity")
        moe_front(net, name, logits, router, keeps_tokens, xn=xn)
        choose(kind)(net, name, logits, bias, to)
        moe_scatter(net, name, xn, to)
        moe_groups(net, name, to, w1, b1, func, w2, b2)
        moe_combine(net, name, to)


def moe_scatter(net, name, xn, to):
    nc = net.nc
    with ExitStack() as ctx:
        s = net.scope(name + "s", ctx)
        scattered = s.sem("scattered")
        block = ctx.enter_context(nc.Block())

        @block.gpsimd
        def _(pool):
            pool.wait_ge(net.tokens_cleared, 16)
            pool.sem_inc(net.tick, 1)
            for t in range(NT):
                rows = P if t < NT - 1 else TAIL
                for c in range(to.choices):
                    pool.indirect_dma_start(to.tokens, bass.IndirectOffsetOnAxis(to.slot_in[c][0:rows, t:t + 1], 0),
                                            xn[0:rows, t * D:(t + 1) * D], None, bounds_check=to.groups * SLICE - 1,
                                            oob_is_err=False).then_inc(scattered, 16)
            pool.wait_ge(scattered, 16 * NT * to.choices)


def moe_groups(net, name, to, w1, b1, func, w2, b2):
    nc, a = net.nc, net.a
    F = a[w1].shape[2]
    FC = F // P
    BANKS = FC // 2
    TILES = SLICE // P
    with ExitStack() as ctx:
        s = net.scope(name + "g", ctx)
        w_in = [s.sb(f"w_in{b}", [P, DC * F]) for b in range(2)]
        w_out = [s.sb(f"w_out{b}", [P, FC * D]) for b in range(2)]
        rows = [s.sb(f"rows{b}", [P, TILES * D]) for b in range(2)]
        xT = [s.sb(f"xT{b}", [P, DC * SLICE]) for b in range(2)]
        hT = [s.sb(f"hT{b}", [P, FC * SLICE]) for b in range(2)]
        y = [s.sb(f"y{b}", [P, TILES * D]) for b in range(2)]
        b1_rows = s.sb("b1_rows", [EXPERTS * FC, P])
        b1_cols = s.sb("b1_cols", [P, EXPERTS * FC])
        b2_all = s.sb("b2_all", [P, EXPERTS * D])
        ps_t = s.ps("ps_t", [P, DC * SLICE])
        ps_h = s.ps("ps_h", [P, BANKS, 512])
        ps_y = s.ps("ps_y", [P, TILES, 512])
        loaded = s.sem("loaded")
        b1_turned = s.sem("b1_turned")
        b1_ready = s.sem("b1_ready")
        rows_loaded = [s.sem(f"rows_loaded{b}") for b in range(2)]
        w_in_loaded = [s.sem(f"w_in_loaded{b}") for b in range(2)]
        w_out_loaded = [s.sem(f"w_out_loaded{b}") for b in range(2)]
        turned = s.sem("turned")
        xT_ready = s.sem("xT_ready")
        hidden = s.sem("hidden")
        active = s.sem("active")
        outs = s.sem("outs")
        y_ready = s.sem("y_ready")
        stored = [s.sem(f"stored{b}") for b in range(2)]
        y_free = s.sem("y_free")
        dve_tick = s.sem("dve_tick")
        act_tick = s.sem("act_tick")
        pe_tick = s.sem("pe_tick")
        pool_tick = s.sem("pool_tick")
        block = ctx.enter_context(nc.Block())
        run = dict(ring=2, total=to.groups)

        def expert_of(eng, g):
            return eng.value_load(to.expert_row[0:1, bass.ds(g, 1)], min_val=0, max_val=EXPERTS - 1)

        def of_expert(w, e):
            return chunked(a[w].rearrange("e k n -> (e k) n")[bass.ds(e * a[w].shape[1], a[w].shape[1]), :])

        @block.sync
        def _(sp):
            sp.dma_start(b1_rows[:, :], a[b1].rearrange("e (c p) -> (e c) p", p=P)).then_inc(loaded, 16)
            sp.dma_start(b2_all[:, :], spread(a[b2].rearrange("e d -> (e d)"))).then_inc(loaded, 16)

            def load_in(g, i, b):
                e = expert_of(sp, g)
                sp.wait_ge(turned, g + 1)
                sp.dma_start(tiled(rows[b][:, :], D),
                             to.tokens[bass.ds(g * SLICE, SLICE), :].rearrange("(t p) d -> p t d", p=P)).then_inc(rows_loaded[b], 16)
                sp.wait_ge(hidden, (g + 1) * BANKS)
                sp.dma_start(w_in[b][:, :].rearrange("p (c n) -> p c n", c=DC), of_expert(w1, e)).then_inc(w_in_loaded[b], 16)

            def load_out(g, i, b):
                e = expert_of(sp, g)
                sp.wait_ge(outs, (g + 1) * TILES)
                sp.dma_start(w_out[b][:, :].rearrange("p (c n) -> p c n", c=FC), of_expert(w2, e)).then_inc(w_out_loaded[b], 16)

            skewed(sp, (0, load_in), (1, load_out), **run)

        @block.tensor
        def _(pe):
            pe.sem_inc(turned, 2)
            pe.sem_inc(hidden, 2 * BANKS)
            pe.sem_inc(outs, 2 * TILES)
            pe.wait_ge(loaded, 32)
            turn_rows(pe, net, ps_y[:, 0, 0:EXPERTS * FC], b1_rows[:, :]).then_inc(b1_turned, 1)
            pe.wait_ge(b1_ready, 1)

            def turn(g, i, b):
                pe.wait_ge(rows_loaded[b], i * 16 + 16)
                pe.wait_ge(xT_ready, g + 1)
                pe.sem_inc(pe_tick, 1)
                for c in range(DC):
                    for t in range(TILES):
                        ins = pe.transpose(ps_t[:, c * SLICE + t * P:c * SLICE + (t + 1) * P],
                                           rows[b][:, t * D + c * P:t * D + (c + 1) * P], net.ident[:, :])
                ins.then_inc(turned, 1)

            def hide(g, i, b):
                pe.wait_ge(w_in_loaded[b], i * 16 + 16)
                pe.wait_ge(xT_ready, g + 2)
                for n in range(BANKS):
                    pe.wait_ge(active, g * BANKS + n + 1)
                    for m in (2 * n, 2 * n + 1):
                        for c in range(DC):
                            ins = pe.matmul(ps_h[:, n, (m % 2) * SLICE:(m % 2 + 1) * SLICE],
                                            w_in[b][:, c * F + m * P:c * F + (m + 1) * P], at(xT[b], c, SLICE),
                                            start=c == 0, stop=c == DC - 1)
                    ins.then_inc(hidden, 1)

            def put_out(g, i, b):
                pe.wait_ge(w_out_loaded[b], i * 16 + 16)
                pe.wait_ge(active, (g + 2) * BANKS)
                for t in range(TILES):
                    pe.wait_ge(y_ready, g * TILES + t + 1)
                    for c in range(FC):
                        ins = pe.matmul(ps_y[:, t, 0:D], hT[b][:, c * SLICE + t * P:c * SLICE + (t + 1) * P], at(w_out[b], c, D),
                                        start=c == 0, stop=c == FC - 1)
                    ins.then_inc(outs, 1)

            skewed(pe, (1, hide), (0, turn), (2, put_out), **run)

        @block.scalar
        def _(act):
            act.sem_inc(active, BANKS)
            act.wait_ge(b1_ready, 1)
            act.sem_inc(act_tick, 1)

            def activate(g, i, b):
                e = expert_of(act, g)
                act.wait_ge(outs, (g + 1) * TILES)
                for n in range(BANKS):
                    act.wait_ge(hidden, (g + 2) * BANKS + n + 1)
                    act.sem_inc(act_tick, 1)
                    for m in (2 * n, 2 * n + 1):
                        ins = act.activation(at(hT[b], m, SLICE), ps_h[:, n, (m % 2) * SLICE:(m % 2 + 1) * SLICE], func,
                                             bias=b1_cols[:, bass.ds(e * FC + m, 1)])
                    ins.then_inc(active, 1)

            skewed(act, (0, activate), **run)

        @block.vector
        def _(dve):
            dve.sem_inc(xT_ready, 1)
            dve.sem_inc(y_ready, TILES)
            dve.wait_ge(b1_turned, 1)
            dve.tensor_copy(b1_cols[:, :], ps_y[:, 0, 0:EXPERTS * FC]).then_inc(b1_ready, 1)
            dve.wait_ge(loaded, 32)

            def keep(g, i, b):
                dve.wait_ge(turned, g + 3)
                dve.wait_ge(hidden, (g + 1) * BANKS)
                dve.tensor_copy(xT[b][:, :], ps_t[:, :]).then_inc(xT_ready, 1)

            def put_out(g, i, b):
                e = expert_of(dve, g)
                dve.wait_ge(y_free, g + 1)
                dve.sem_inc(dve_tick, 1)
                for t in range(TILES):
                    dve.wait_ge(outs, (g + 2) * TILES + t + 1)
                    dve.tensor_tensor(at(y[b], t, D), ps_y[:, t, 0:D], at(b2_all, e, D), ALU.add).then_inc(y_ready, 1)

            skewed(dve, (0, keep), (2, put_out), **run)

        @block.gpsimd
        def _(pool):
            def store(g, i, b):
                pool.wait_ge(y_ready, (g + 2) * TILES)
                pool.sem_inc(pool_tick, 1)
                pool.dma_start(to.outputs[bass.ds(g * SLICE, SLICE), :].rearrange("(t p) d -> p t d", p=P),
                               tiled(y[b][:, :], D)).then_inc(stored[b], 16)
                pool.wait_ge(stored[b], i * 16 + 16)
                pool.sem_inc(y_free, 1)

            pool.sem_inc(y_free, 2)
            skewed(pool, (0, store), **run)


def moe_combine(net, name, to):
    nc = net.nc
    LARGEST = float(np.finfo(np.float32).max)
    with ExitStack() as ctx:
        s = net.scope(name + "o", ctx)
        rows = [s.sb(f"rows{c}", [P, NT * D]) for c in range(to.choices)]
        fixed = s.sb("fixed", [P, 3])
        chain = s.sem("chain")
        gathered = [s.sem(f"gathered{i}") for i in range(NI)]
        step = s.sem("step")
        block = ctx.enter_context(nc.Block())

        @block.gpsimd
        def _(pool):
            for t in range(NT):
                for c in range(to.choices):
                    pool.indirect_dma_start(at(rows[c], t, D), None, to.outputs,
                                            bass.IndirectOffsetOnAxis(to.slot_out[c][:, t:t + 1], 0)).then_inc(gathered[t // UN], 16)

        @block.vector
        def _(dve):
            if not to.capacity:
                for t in range(NT):
                    if t % UN == 0:
                        dve.wait_ge(gathered[t // UN], 16 * to.choices * UN)
                    for c in range(to.choices):
                        if c:
                            dve.wait_ge(step, t * (to.choices - 1) + c)
                        ins = dve.scalar_tensor_tensor(at(net.x, t, D), at(rows[c], t, D), to.weight[c][:, t:t + 1], at(net.x, t, D),
                                                       ALU.mult, ALU.add)
                        if c < to.choices - 1:
                            ins.then_inc(step, 1)
                return
            flag = s.sb("flag", [P, UN * D], mybir.dt.uint8)
            link = Chain(dve, chain)
            for n, value in enumerate((1e4, -1e4, 0.0)):
                link(dve.memset(fixed[:, n:n + 1], value))
            for i in range(NI):
                y, x = at(rows[0], i, UN * D), at(net.x, i, UN * D)
                dve.wait_ge(gathered[i], 16 * UN)
                link(dve.tensor_tensor(tiled(y, D), tiled(y, D), at(to.weight[0], i, UN).unsqueeze(2).to_broadcast([P, UN, D]), ALU.mult))
                for n, test in enumerate((lambda: dve.tensor_scalar(flag[:, :], y, LARGEST, None, ALU.is_gt),
                                          lambda: dve.tensor_scalar(flag[:, :], y, -LARGEST, None, ALU.is_lt),
                                          lambda: dve.tensor_tensor(flag[:, :], y, y, ALU.not_equal))):
                    link(test())
                    link(dve.copy_predicated(y, flag[:, :], fixed[:, n:n + 1].to_broadcast([P, UN * D])))
                link(dve.tensor_tensor(x, x, y, ALU.add))


BN_EPS = 1e-3
CAPACITY = max(1, -(-5 * N // (4 * EXPERTS)))
ROOM = -(-CAPACITY // SLICE) * SLICE
assert ROOM // SLICE == 2


def l0_ffn(net):
    moe_sparse(net, "l0f", net.a["L0_ffn_router_w"], None, "probs", 2, 2 * N // SLICE + EXPERTS,
               "L0_ffn_w1", "L0_ffn_b1", ACT.Gelu, "L0_ffn_w2", "L0_ffn_b2", keeps_tokens=True)


def l1_ffn(net):
    moe_sparse(net, "l1f", net.a["L1_ffn_Wg"], net.a["L1_ffn_bg"], "pair", 2, 2 * N // SLICE + EXPERTS,
               "L1_ffn_W1", "L1_ffn_b1", ACT.Gelu, "L1_ffn_W2", "L1_ffn_b2")


def l2_ffn(net):
    def names(n):
        return tuple(f"L2_ffn_{v}{n}" for v in ("b", "g", "be", "m", "v"))

    moe(net, "l2f", net.a["L2_ffn_Wr"], net.a["L2_ffn_br"],
        [("L2_ffn_W1", names(1), ACT.Relu), ("L2_ffn_W2", names(2), ACT.Relu)], "L2_ffn_Wo", "L2_ffn_bo")


def l3_ffn(net):
    moe_sparse(net, "l3f", net.a["L3_ffn_gate_w"], net.a["L3_ffn_gate_b"], "capacity", 1, EXPERTS * ROOM // SLICE,
               "L3_ffn_w1", "L3_ffn_b1", ACT.Relu, "L3_ffn_w2", "L3_ffn_b2")


ATTR_PRODUCTS = ((0, 0), (0, 1), (0, 2), (1, 0), (1, 1), (1, 2), (2, 0), (2, 1))


def edge_means(net):
    nc = net.nc
    placed = net.by_dst
    lo = placed.first["edge_attr_16"]
    W = 17
    firsts = [sum(1 for a, _ in ATTR_PRODUCTS if a < n) for n in range(4)]
    with ExitStack() as ctx:
        s = net.scope("means", ctx)
        n = placed.width - lo
        rec = [s.sb(f"rec{b}", [P, BATCH * n]) for b in range(RING)]
        onehot = [s.sb(f"onehot{b}", [P, BATCH * P]) for b in range(RING)]
        ident = s.sb("ident_bf16", [P, P], BF16)
        parts = [s.sb(f"parts{b}", [P, BATCH * P], BF16) for b in range(RING)]
        rest = [s.sb(f"rest{b}", [P, BATCH * 16]) for b in range(RING)]
        partsT = [s.sb(f"partsT{b}", [P, BATCH * P], BF16) for b in range(RING)]
        found = s.sb("found", [P, NT])
        root = s.sb("root", [P, NT])
        ps = s.ps("ps", [P, NT * W])
        ps_t = s.ps("ps_t", [P, RING, 1024], BF16)
        ident_ready = s.sem("ident_ready")
        loaded = [s.sem(f"loaded{b}") for b in range(RING)]
        onehot_ready = s.sem("onehot_ready")
        first_ready = s.sem("first_ready")
        rest_ready = s.sem("rest_ready")
        second_ready = s.sem("second_ready")
        third_ready = s.sem("third_ready")
        turned = s.sem("turned")
        kept = s.sem("kept")
        stored = [s.sem(f"stored{b}") for b in range(RING)]
        closed = s.sem("closed")
        chain = s.sem("chain")
        to_root = s.sem("to_root")
        rooted = s.sem("rooted")
        pe_tick = s.sem("pe_tick")
        act_tick = s.sem("act_tick")
        block = ctx.enter_context(nc.Block())

        def copies(t, part):
            return t[:, :].rearrange("p (t s c) -> p t s c", t=BATCH, c=16)[:, :, firsts[part]:firsts[part + 1], :]

        def repeated(ap, part):
            count = firsts[part + 1] - firsts[part]
            return ap.unsqueeze(2).to_broadcast([P, BATCH, count, 16])

        @block.sync
        def _(sp):
            def load(q, i, b):
                sp.wait_ge(turned, q + 1)
                sp.dma_start(tiled(rec[b][:, :], n), batch_records(placed.records, q, lo, placed.width))\
                    .then_inc(loaded[b], 16)

            def keep(q, i, b):
                sp.wait_ge(kept, RING + q + 1)
                sp.dma_start(net.attr_parts[bass.ds(q * P, P), :], partsT[b][:, :]).then_inc(stored[b], 16)

            skewed(sp, (0, load), (4, keep))
            for b in range(RING):
                sp.wait_ge(stored[b], NB // RING * 16)

        @block.tensor
        def _(pe):
            pe.sem_inc(turned, RING)
            open_sums(net, pe, ps, True)
            pe.wait_ge(ident_ready, 1)

            def add(q, i, b):
                blocks = [block_of(pe, placed, q * TWO + k) for k in range(TWO)]
                pe.wait_ge(onehot_ready, q + 1)
                for k in range(BATCH):
                    ins = pe.matmul(at(ps, blocks[k // 2], W), at(onehot[b], k, P), rec[b][:, k * n:k * n + W],
                                    start=False, stop=False)
                pe.wait_ge(third_ready, q + 1)
                pe.wait_ge(kept, q + 1)
                pe.sem_inc(pe_tick, 1)
                for k in range(BATCH):
                    ins = pe.transpose(at(ps_t[:, b, :], k, P), at(parts[b], k, P), ident[:, :])
                ins.then_inc(turned, 1)

            skewed(pe, (2, add))
            open_sums(net, pe, ps, False).then_inc(closed, 1)

        @block.scalar
        def _(act):
            act.sem_inc(kept, RING)

            def first(q, i, b):
                act.wait_ge(loaded[b], i * 16 + 16)
                act.wait_ge(turned, q + 1)
                act.activation(copies(parts[b], 0), repeated(tiled(rec[b][:, :], n)[:, :, 0:16], 0), ACT.Copy).then_inc(first_ready, 1)

            def second(q, i, b):
                act.wait_ge(rest_ready, q + 1)
                act.activation(copies(parts[b], 1), repeated(tiled(rest[b][:, :], 16), 1), ACT.Copy).then_inc(second_ready, 1)

            def keep(q, i, b):
                act.wait_ge(turned, RING + q + 1)
                if not isinstance(i, int) or i:
                    act.wait_ge(stored[b], i * 16)
                act.sem_inc(act_tick, 1)
                act.activation(partsT[b][:, :], ps_t[:, b, 0:BATCH * P], ACT.Copy).then_inc(kept, 1)

            skewed(act, (0, first), (1, second), (3, keep))
            act.wait_ge(to_root, 1)
            act.activation(root[:, :], root[:, :], ACT.Sqrt).then_inc(rooted, 1)

        @block.vector
        def _(dve):
            link = Chain(dve, chain)
            dve.tensor_copy(ident[:, :], net.ident[:, :]).then_inc(ident_ready, 1)

            def hot(q, i, b):
                dve.wait_ge(loaded[b], i * 16 + 16)
                dve.wait_ge(turned, q + 1)
                mark_nodes(dve, net, onehot[b], tiled(rec[b][:, :], n)[:, :, placed.near - lo]).then_inc(onehot_ready, 1)

            def take(q, i, b):
                dve.wait_ge(first_ready, q + 1)
                dve.tensor_tensor(tiled(rest[b][:, :], 16), tiled(rec[b][:, :], n)[:, :, 0:16],
                                  copies(parts[b], 0)[:, :, 0, :], ALU.subtract).then_inc(rest_ready, 1)

            def last(q, i, b):
                dve.wait_ge(second_ready, q + 1)
                dve.tensor_tensor(copies(parts[b], 2), repeated(tiled(rest[b][:, :], 16), 2),
                                  copies(parts[b], 1)[:, :, 0:firsts[3] - firsts[2], :], ALU.subtract).then_inc(third_ready, 1)

            skewed(dve, (2, last), (1, take), (0, hot))
            dve.wait_ge(closed, 1)
            sums = tiled(ps[:, :], W)
            link(dve.tensor_scalar(found[:, :], sums[:, :, 16], 1.0, None, ALU.max))
            link(dve.reciprocal(found[:, :], found[:, :]))
            link(dve.tensor_tensor(tiled(net.mean16[:, :], 16), sums[:, :, 0:16],
                                   found[:, :].unsqueeze(2).to_broadcast([P, NT, 16]), ALU.mult))
            link(dve.tensor_scalar(root[:, :], sums[:, :, 16], 1.0, None, ALU.add))
            dve.sem_inc(to_root, 1)
            dve.wait_ge(rooted, 1)
            link(dve.reciprocal(net.dinv[:, :], root[:, :]))


def gat_edges(net, name, heads, each, table, lo, logits_of, tops=None):
    nc = net.nc
    KH = BATCH * heads
    W = heads * (each + 1)
    UNITS = -(-heads // 2)
    FLUSH = 1 if tops is None else 2
    placed = net.by_dst
    with ExitStack() as ctx:
        s = net.scope(name, ctx)
        g = Gather(s, net, placed, table, table.shape[1], lo)
        nodehot = [s.sb(f"nodehot{b}", [P, BATCH * P]) for b in range(RING)]
        outside = [s.sb(f"outside{b}", [P, BATCH * P], BF16) for b in range(RING)]
        logit = [s.sb(f"logit{b}", [P, KH]) for b in range(RING)]
        fresh = s.sb("fresh", [P, PAIRS])
        fresh_step = s.sem("fresh_step")
        masked = s.sb("masked", [P, 2 * 2 * PAIR])
        tile_top = s.sb("tile_top", [P, TWO * heads])
        top = s.sb("top", [P, RING * TWO * heads])
        shrink = [s.sb(f"shrink{b}", [P, TWO * heads]) for b in range(RING)]
        power = [s.sb(f"power{b}", [P, KH]) for b in range(RING)]
        weighted = s.sb("weighted", [P, BATCH * W])
        total = [s.sb(f"total{k}", [P, W]) for k in range(TWO)]
        ps_hot = s.ps("ps_hot", [P, BATCH * P])
        ps_x = s.ps("ps_x", [P, TWO, 512])
        ps_row = s.ps("ps_row", [P, 2, 512])
        ps_s = s.ps("ps_s", [P, TWO, 512])
        ps_top = s.ps("ps_top", [P, 512])[:, 0:KH]
        cleared = s.sem("cleared")
        hot_turned = s.sem("hot_turned")
        nodehot_ready = s.sem("nodehot_ready")
        logit_ready = s.sem("logit_ready")
        rows_turned = s.sem("rows_turned")
        topped = s.sem("topped")
        top_step = s.sem("top_step")
        shrink_ready = s.sem("shrink_ready")
        spread_top = s.sem("spread_top")
        power_step = s.sem("power_step")
        shrunk = s.sem("shrunk")
        powered = s.sem("powered")
        weighted_ready = s.sem("weighted_ready")
        summed = s.sem("summed")
        total_ready = s.sem("total_ready")
        flushed = s.sem("flushed")
        act_tick = s.sem("act_tick")
        dve_tick = s.sem("dve_tick")
        logits = logits_of(s, g, ps_x, nodehot, logit, logit_ready, nodehot_ready)
        block = ctx.enter_context(nc.Block())
        by_head = lambda ap, n: ap.rearrange("p (h c) -> p h c", c=n)

        def top_at(b, k):
            return at(top, b * TWO + k, heads)

        @block.sync
        def _(sp):
            logits.load(sp)
            g.load(sp, logits.load_batch)

        @block.gpsimd
        def _(pool):
            logits.gather(pool)

        @block.vector
        def _(dve):
            dve.memset(net.work[:, 0:NT * W], 0.0).then_inc(cleared, 1)
            dve.memset(top[:, :], -HUGE).then_inc(cleared, 1)
            dve.memset(total[TWO - 1][:, :], 0.0).then_inc(cleared, 1)
            if tops is not None:
                dve.memset(tops[:, :], -HUGE).then_inc(cleared, 1)
            dve.tensor_scalar(fresh[:, :], placed.keep[:, :], -1.0, HUGE, ALU.add, ALU.mult).then_inc(fresh_step, 1)
            dve.sem_inc(topped, 2)
            dve.sem_inc(total_ready, TWO)
            dve.sem_inc(top_step, 1)
            logits.start_vector(dve)
            dve.wait_ge(cleared, 3 if tops is None else 4)
            dve.wait_ge(fresh_step, 1)

            def tops_of(k, h0):
                def step(q, i, b):
                    n = (q * TWO + k) * UNITS + h0 // 2
                    side = (k * UNITS + h0 // 2) % 2
                    dve.wait_ge(rows_turned, n + 1)
                    dve.wait_ge(topped, n + 1)
                    dve.sem_inc(dve_tick, 1)
                    for h in range(h0, min(h0 + 2, heads)):
                        c = k * heads + h
                        ins = dve.tensor_tensor_reduce(at(masked, side * 2 + h - h0, PAIR), at(ps_row[:, side, :], h - h0, PAIR),
                                                       at(outside[b], k, PAIR), 1.0, -HUGE, ALU.add, ALU.max,
                                                       tile_top[:, c:c + 1])
                    ins.then_inc(topped, 1)
                return 3, step

            def raise_first(q, i, b):
                n = q * TWO
                dve.wait_ge(topped, (n + 1) * UNITS + 2)
                dve.wait_ge(top_step, n + 1)
                dve.scalar_tensor_tensor(top_at(b, 0), top_at((b - 1) % RING, TWO - 1), fresh[:, bass.ds(n, 1)],
                                         at(tile_top, 0, heads), ALU.add, ALU.max).then_inc(top_step, 1)

            def raise_second(q, i, b):
                n = q * TWO
                dve.wait_ge(topped, (n + TWO) * UNITS + 2)
                dve.wait_ge(top_step, n + 2)
                dve.scalar_tensor_tensor(top_at(b, 1), top_at(b, 0), fresh[:, bass.ds(n + 1, 1)], at(tile_top, 1, heads),
                                         ALU.add, ALU.max).then_inc(top_step, 1)
                dve.scalar_tensor_tensor(at(shrink[b], 0, heads), top_at((b - 1) % RING, TWO - 1), fresh[:, bass.ds(n, 1)],
                                         top_at(b, 0), ALU.add, ALU.subtract).then_inc(shrink_ready, 1)
                dve.wait_ge(top_step, n + 3)
                dve.scalar_tensor_tensor(at(shrink[b], 1, heads), top_at(b, 0), fresh[:, bass.ds(n + 1, 1)], top_at(b, 1),
                                         ALU.add, ALU.subtract).then_inc(shrink_ready, 1)

            def fall(q, i, b):
                dve.wait_ge(spread_top, q + 1)
                dve.tensor_tensor(power[b][:, :], logit[b][:, :], ps_top, ALU.subtract).then_inc(power_step, 1)
                dve.wait_ge(power_step, 2 * q + 1)
                dve.tensor_scalar(power[b][:, :], power[b][:, :], 0.0, None, ALU.min).then_inc(power_step, 1)

            def add(k):
                def step(q, i, b):
                    n = q * TWO + k
                    if k == 0:
                        dve.wait_ge(shrunk, q + 1)
                    dve.wait_ge(summed, n + TWO + 1)
                    dve.wait_ge(flushed, (n + 1) * FLUSH)
                    dve.wait_ge(total_ready, n + TWO)
                    for h in range(heads):
                        own = slice(h * (each + 1), (h + 1) * (each + 1))
                        ins = dve.scalar_tensor_tensor(total[k][:, own], total[1 - k][:, own], shrink[b][:, k * heads + h:k * heads + h + 1],
                                                       ps_s[:, k, own], ALU.mult, ALU.add)
                    ins.then_inc(total_ready, 1)
                return 4, step

            units = [tops_of(k, h0) for k in range(TWO) for h0 in range(0, heads, 2)]
            early, middle, late, hot = ((2, lambda q, i, b, part=part: part(dve, q, i, b)) for part in logits.vector_steps())
            ends = ((3, fall), add(0), late, add(1)) if UNITS > 1 else (late, (0, hot[1]), (3, fall), add(0), add(1))
            skewed(dve, *units[:UNITS + 1], (3, raise_first), *units[UNITS + 1:], early, (3, raise_second), middle, *ends)

        @block.tensor
        def _(pe):
            pe.sem_inc(g.hot_free, RING)
            pe.sem_inc(summed, TWO)
            logits.start_tensor(pe)

            def turn(q, i, b):
                pe.wait_ge(g.hot_ready, q + 1)
                pe.wait_ge(nodehot_ready, q + 1)
                for k in range(BATCH):
                    ins = pe.transpose(at(ps_hot, k, P), at(g.onehot[b], k, P), net.ident[:, :])
                ins.then_inc(hot_turned, 1)

            def turn_logits(k):
                def step(q, i, b):
                    pe.wait_ge(logit_ready, q + 1)
                    for h0 in range(0, heads, 2):
                        n = (q * TWO + k) * UNITS + h0 // 2
                        side = (k * UNITS + h0 // 2) % 2
                        pe.wait_ge(topped, n + 1)
                        for h in range(h0, min(h0 + 2, heads)):
                            for m in range(2):
                                c = (2 * k + m) * heads + h
                                lo = (h - h0) * PAIR + m * P
                                ins = pe.transpose(ps_row[:, side, lo:lo + P], logit[b][:, c:c + 1].to_broadcast([P, P]),
                                                   net.ident[:, :])
                        ins.then_inc(rows_turned, 1)
                return step

            def add(q, i, b):
                for k in range(TWO):
                    n = q * TWO + k
                    pe.wait_ge(weighted_ready, n + 1)
                    pe.wait_ge(total_ready, n + 1)
                    for m in (2 * k, 2 * k + 1):
                        ins = pe.matmul(ps_s[:, k, 0:W], at(g.onehot[b], m, P), at(weighted, m, W), start=m == 2 * k, stop=m > 2 * k)
                    ins.then_inc(summed, 1)

            def spread(q, i, b):
                pe.wait_ge(shrink_ready, q * TWO + TWO)
                for m in range(BATCH):
                    ins = pe.matmul(at(ps_top, m, heads), at(nodehot[b], m, P), top_at(b, m // 2), start=True, stop=True)
                    if m == 0 and (not isinstance(q, int) or q):
                        ins.then_inc(g.hot_free, 1)
                ins.then_inc(spread_top, 1)

            skewed(pe, *([(3, turn_logits(1))] if UNITS > 1 else []), (4, add), (1, lambda q, i, b: logits.blocks(pe, q)), (3, spread),
                   (1, lambda q, i, b: logits.tensor(pe, q, i, b)), (2, turn_logits(0)),
                   *([(2, turn_logits(1))] if UNITS == 1 else []), (0, turn))

        @block.scalar
        def _(act):
            act.sem_inc(g.rows_free, RING)
            act.sem_inc(nodehot_ready, 1)
            act.sem_inc(flushed, TWO * FLUSH)
            logits.start_scalar(act)
            act.wait_ge(cleared, 3 if tops is None else 4)
            act.sem_inc(act_tick, 1)

            def turn(q, i, b):
                act.wait_ge(hot_turned, q + 1)
                act.activation(outside[b][:, :], ps_hot[:, :], ACT.Copy, bias=-HUGE, scale=HUGE)
                act.activation(nodehot[b][:, :], ps_hot[:, :], ACT.Copy).then_inc(nodehot_ready, 1)

            def shrinks(q, i, b):
                act.wait_ge(shrink_ready, q * TWO + TWO)
                act.activation(shrink[b][:, :], shrink[b][:, :], ACT.Exp).then_inc(shrunk, 1)

            def weigh(q, i, b):
                act.wait_ge(power_step, 2 * q + 2)
                act.activation(power[b][:, :], power[b][:, :], ACT.Exp).then_inc(powered, 1)
                g.wait_rows(act, i, b)
                act.wait_ge(powered, q + 1)
                for k in range(TWO):
                    act.wait_ge(summed, q * TWO + k + 1)
                    for m in (2 * k, 2 * k + 1):
                        out = by_head(at(weighted, m, W), each + 1)
                        for h in range(heads):
                            lo = m * g.width + h * each
                            act.activation(out[:, h, 0:each], g.rows[b][:, lo:lo + each], ACT.Copy,
                                           scale=power[b][:, m * heads + h:m * heads + h + 1])
                        ins = act.activation(out[:, :, each], at(power[b], m, heads), ACT.Copy)
                    ins.then_inc(weighted_ready, 1)
                act.wait_ge(weighted_ready, q * TWO + TWO)
                act.sem_inc(g.rows_free, 1)

            def flush(q, i, b):
                for k in range(TWO):
                    n = q * TWO + k
                    blk = block_of(act, placed, n)
                    act.wait_ge(total_ready, n + TWO + 1)
                    act.wait_ge(flushed, (n + TWO) * FLUSH)
                    act.sem_inc(act_tick, 1)
                    if tops is not None:
                        act.activation(at(tops, blk, heads), top_at(b, k), ACT.Copy).then_inc(flushed, 1)
                    act.activation(at(net.work, blk, W), total[k][:, :], ACT.Copy).then_inc(flushed, 1)

            skewed(act, (3, shrinks), (3, weigh), (0, turn), (4, flush))


class L1Logits:

    SLOPE = 0.2

    def __init__(self, net, xr, att, s, g, ps_x, nodehot, logit, logit_ready, nodehot_ready):
        self.net, self.xr, self.att, self.g = net, xr, att, g
        self.ps_x, self.nodehot, self.logit, self.logit_ready, self.nodehot_ready = ps_x, nodehot, logit, logit_ready, nodehot_ready
        self.we = s.sb("we", [16, D])
        self.we_part = [s.sb(f"we_part{n}", [16, D], BF16) for n in range(3)]
        self.we_parts = s.sb("we_parts", [P, D], BF16)
        self.attrT = [s.sb(f"attrT{b}", [P, BATCH * P], BF16) for b in range(RING)]
        self.e = [s.sb(f"e{k}", [P, 2 * D]) for k in range(TWO)]
        self.loaded = s.sem("we_loaded")
        self.split_step = s.sem("split_step")
        self.parts_laid = s.sem("parts_laid")
        self.attr_loaded = [s.sem(f"attr_loaded{b}") for b in range(RING)]
        self.sums = s.sem("e_sums")
        self.x_read = s.sem("x_read")
        self.bent = s.sem("bent")
        self.times_att = s.sem("times_att")
        self.tick = s.sem("e_tick")
        self.pool_tick = s.sem("e_pool_tick")

    def load(self, sp):
        sp.dma_start(self.we[:, :], self.net.a["L1_gnn_W_e"]).then_inc(self.loaded, 16)
        sp.wait_ge(self.split_step, 5)
        for n, (_, part) in enumerate(ATTR_PRODUCTS):
            sp.dma_start(self.we_parts[n * 16:(n + 1) * 16, :], self.we_part[part][:, :]).then_inc(self.parts_laid, 16)

    def load_batch(self, sp, q, b):
        sp.dma_start(self.attrT[b][:, :], self.net.attr_parts[bass.ds(q * P, P), :]).then_inc(self.attr_loaded[b], 16)

    def gather(self, pool):
        skewed(pool, (0, lambda q, i, b: self.g.hot(pool, q, i, b, self.pool_tick)), (0, lambda q, i, b: self.g.gather_batch(pool, q, b)),
               (2, lambda q, i, b: self.multiply(pool, q)))

    def hot(self, dve, q, i, b):
        pass

    def start_vector(self, dve):
        dve.sem_inc(self.x_read, TWO)
        dve.sem_inc(self.g.rec_free, RING)
        dve.wait_ge(self.loaded, 16)
        for n in range(3):
            dve.tensor_copy(self.we_part[n][:, :], self.we[:, :]).then_inc(self.split_step, 1)
            dve.wait_ge(self.split_step, 2 * n + 1)
            if n < 2:
                dve.tensor_tensor(self.we[:, :], self.we[:, :], self.we_part[n][:, :], ALU.subtract).then_inc(self.split_step, 1)
                dve.wait_ge(self.split_step, 2 * n + 2)

    def start_tensor(self, pe):
        pe.wait_ge(self.parts_laid, 16 * len(ATTR_PRODUCTS))

    def start_scalar(self, act):
        pass

    def blocks(self, pe, q):
        self.block = [block_of(pe, self.g.placed, q * TWO + k) for k in range(TWO)]

    def tensor(self, pe, q, i, b):
        pe.wait_ge(self.attr_loaded[b], i * 16 + 16)
        pe.wait_ge(self.nodehot_ready, q + 2)
        pe.sem_inc(self.tick, 1)
        for k in range(TWO):
            n = q * TWO + k
            pe.wait_ge(self.x_read, n + 1)
            for m in range(2):
                out = self.ps_x[:, k, m * D:(m + 1) * D]
                pe.matmul(out, at(self.nodehot[b], 2 * k + m, P), at(self.xr, self.block[k], D), start=True, stop=False)
                ins = pe.matmul(out, at(self.attrT[b], 2 * k + m, P), self.we_parts[:, :], start=False, stop=True)
            ins.then_inc(self.sums, 1)

    def vector_steps(self):
        return self.vector_early, self.vector_middle, self.vector_late, self.hot

    def join(self, dve, q, b, k):
        dve.wait_ge(self.sums, q * TWO + k + 1)
        dve.tensor_tensor(self.e[k][:, :], self.ps_x[:, k, 0:2 * D], at(self.g.rows[b], k, 2 * D), ALU.add).then_inc(self.x_read, 1)

    def bend(self, dve, q, k):
        e = self.e[k][:, :]
        dve.wait_ge(self.x_read, q * TWO + TWO + k + 1)
        dve.scalar_tensor_tensor(e, e, self.SLOPE, e, ALU.mult, ALU.max).then_inc(self.bent, 1)

    def vector_early(self, dve, q, i, b):
        self.g.wait_rows(dve, i, b)
        self.join(dve, q, b, 0)

    def vector_middle(self, dve, q, i, b):
        self.bend(dve, q, 0)
        self.join(dve, q, b, 1)
        dve.sem_inc(self.g.rec_free, 1)
        self.bend(dve, q, 1)

    def multiply(self, pool, q):
        for k in range(TWO):
            e = tiled(self.e[k][:, :], D)
            pool.wait_ge(self.bent, q * TWO + k + 1)
            pool.sem_inc(self.pool_tick, 1)
            pool.tensor_tensor(e, e, self.att[:, :].unsqueeze(1).to_broadcast([P, 2, D]), ALU.mult).then_inc(self.times_att, 1)

    def vector_late(self, dve, q, i, b):
        for k in range(TWO):
            dve.wait_ge(self.times_att, q * TWO + k + 1)
            ins = dve.tensor_reduce(at(self.logit[b], k, 8), self.e[k][:, :].rearrange("p (h c) -> p h c", c=64), AX.X, ALU.add)
        ins.then_inc(self.logit_ready, 1)


def l1_gnn(net):
    H, C = 4, 64
    with ExitStack() as ctx:
        s = net.scope("l1", ctx)
        res = s.sb("res", [P, NT * D])
        own_logit = s.sb("own_logit", [P, NT * H])
        top = s.sb("top", [P, NT * H])
        with ExitStack() as inner:
            t = net.scope("l1x", inner)
            xr = t.sb("xr", [P, NT * D])
            att = t.sb("att", [P, D])
            l1_nodes(net, xr, res, att, own_logit)
            gat_edges(net, "l1e", H, C, net.table(D), net.by_dst.number,
                      lambda *args: L1Logits(net, xr, att, *args), top)
        l1_finish(net, res, own_logit, top)


def l1_nodes(net, xr, res, att, own_logit):
    nc, a = net.nc, net.a
    H, C = 4, 64
    W = H * (C + 1)
    table = net.table(D)
    with ExitStack() as ctx:
        s = net.scope("l1n", ctx)
        f = Front(s)
        ws = {n: s.sb(n, [P, DC * D]) for n in ("W_l", "W_r", "W_res")}
        bs = {n: s.sb(n, [P, D]) for n in ("b_l", "b_r", "bias")}
        we = s.sb("we", [16, D])
        xl = s.sb("xl", [P, NT * D])
        mean = [s.sb(f"mean{k}", [P, 16]) for k in range(UN)]
        meanT = [s.sb(f"meanT{k}", [16, P]) for k in range(UN)]
        e = [s.sb(f"e{k}", [P, D]) for k in range(UN)]
        ps = s.ps("ps", [P, 3, 2 * 512])
        loaded = s.sem("loaded")
        mean_taken = s.sem("mean_taken")
        xl_ready = s.sem("xl_ready")
        xr_ready = s.sem("xr_ready")
        joined = s.sem("joined")
        e_step = s.sem("e_step")
        stored = s.sem("stored")
        pe_tick = s.sem("pe_tick")
        block = ctx.enter_context(nc.Block())

        @block.sync
        def _(sp):
            for n, w in ws.items():
                sp.dma_start(w[:, :].rearrange("p (c n) -> p c n", c=DC), chunked(a[f"L1_gnn_{n}"])).then_inc(loaded, 16)
            for n, v in bs.items():
                sp.dma_start(v[:, :], spread(a[f"L1_gnn_{n}"])).then_inc(loaded, 16)
            sp.dma_start(att[:, :], spread(a["L1_gnn_att"].rearrange("h c -> (h c)"))).then_inc(loaded, 16)
            sp.dma_start(we[:, :], a["L1_gnn_W_e"]).then_inc(loaded, 16)
            for i in range(NI):
                sp.wait_ge(xl_ready, (i + 1) * UN)
                sp.dma_start(node_rows(table, i * UN, UN), tiled(at(xl, i, UN * D), D)).then_inc(stored, 16)
            sp.wait_ge(stored, NI * 16)

        @block.vector
        def _(dve):
            dve.wait_ge(loaded, 128)
            dve.sem_inc(joined, UN)
            f.moments_of(dve, net)

            def normalize(t, i, k):
                f.normalize(dve, net, i, k)
                dve.tensor_copy(mean[k][:, :], at(net.mean16, t, 16)).then_inc(mean_taken, 1)

            def left(t, i, k):
                dve.wait_ge(f.projected, UN + t + 1)
                dve.tensor_tensor(at(xl, t, D), ps[:, THIRD[k], 0:D], bs["b_l"][:, :], ALU.add).then_inc(xl_ready, 1)

            def right(t, i, k):
                dve.tensor_tensor(at(xr, t, D), ps[:, THIRD[k], D:2 * D], bs["b_r"][:, :], ALU.add).then_inc(xr_ready, 1)

            def residual(t, i, k):
                dve.tensor_tensor(at(res, t, D), ps[:, THIRD[k], 512:512 + D], bs["bias"][:, :], ALU.add)

            def join_left(t, i, k):
                dve.wait_ge(xl_ready, t + 1)
                dve.tensor_tensor(e[k][:, :], ps[:, THIRD[k], 512 + D:512 + 2 * D], at(xl, t, D), ALU.add).then_inc(joined, 1)

            def join_right(t, i, k):
                dve.wait_ge(joined, UN + t + 1)
                dve.wait_ge(xr_ready, t + 1)
                dve.tensor_tensor(e[k][:, :], e[k][:, :], at(xr, t, D), ALU.add).then_inc(e_step, 1)

            def bend(t, i, k):
                dve.wait_ge(e_step, 3 * t + 1)
                dve.scalar_tensor_tensor(e[k][:, :], e[k][:, :], L1Logits.SLOPE, e[k][:, :], ALU.mult, ALU.max).then_inc(e_step, 1)

            def attend(t, i, k):
                dve.wait_ge(e_step, 3 * t + 2)
                dve.tensor_tensor(e[k][:, :], e[k][:, :], att[:, :], ALU.mult).then_inc(e_step, 1)

            def reduce(t, i, k):
                dve.wait_ge(e_step, 3 * t + 3)
                dve.tensor_reduce(at(own_logit, t, H), e[k][:, :].rearrange("p (h c) -> p h c", h=H), AX.X, ALU.add)

            skewed(dve, (0, normalize), (3, join_right), (2, left), (3, bend), (2, right), (3, attend), (2, residual),
                   (3, reduce), (2, join_left), ring=UN, total=NT)

        @block.tensor
        def _(pe):
            f.start_tensor(pe)
            pe.wait_ge(loaded, 128)

            def turn(t, i, k):
                pe.wait_ge(mean_taken, t + 1)
                pe.wait_ge(f.xT_ready, bank_free(t, k))
                pe.sem_inc(pe_tick, 1)
                pe.transpose(f.ps[0:16, k % 2, D:D + P], mean[k][:, :], net.ident[:, :])
                f.turn(pe, net, t, k)

            def project(t, i, k):
                pe.wait_ge(f.xT_ready, UN + t + 1)
                pe.wait_ge(joined, third_free(t))
                for n, (name, w) in enumerate(ws.items()):
                    f.project(pe, t, k, at(ps[:, THIRD[k], :], n, D), w[:, :].rearrange("p (c n) -> p c n", c=DC), last=False)
                pe.matmul(at(ps[:, THIRD[k], :], len(ws), D), meanT[k][:, :], we[:, :], start=True, stop=True).then_inc(f.projected, 1)

            skewed(pe, (0, turn), (1, project), ring=UN, total=NT)

        @block.scalar
        def _(act):
            f.start_scalar(act)
            f.root(act, net)

            def keep(t, i, k):
                act.wait_ge(f.turned, UN + t + 1)
                act.wait_ge(f.projected, t + 1)
                act.activation(meanT[k][:, :], f.ps[0:16, k % 2, D:D + P], ACT.Copy)
                f.keep(act, t, k)

            skewed(act, (0, keep), ring=UN, total=NT)


def l1_finish(net, res, own_logit, top):
    nc = net.nc
    H, C = 4, 64
    W = H * (C + 1)
    with ExitStack() as ctx:
        s = net.scope("l1f", ctx)
        xl = s.sb("xl", [P, NT * D])
        best = s.sb("best", [P, NT * H])
        total = s.sb("total", [P, NT * H])
        low = s.sb("low", [P, NT * D])
        xl_loaded = s.sem("xl_loaded")
        chain = s.sem("chain")
        to_weigh = s.sem("to_weigh")
        weights_ready = s.sem("weights_ready")
        to_power = s.sem("to_power")
        powered = s.sem("powered")
        block = ctx.enter_context(nc.Block())
        v = res[:, :]
        acc = net.work[:, 0:NT * W].rearrange("p (n c) -> p n c", c=C + 1)

        def every(t):
            return t[:, :].unsqueeze(2).to_broadcast([P, NT * H, C])

        @block.sync
        def _(sp):
            sp.dma_start(tiled(xl[:, :], D), node_rows(net.table(D), 0, NT)).then_inc(xl_loaded, 16)

        @block.scalar
        def _(act):
            act.wait_ge(to_weigh, 1)
            act.activation(own_logit[:, :], own_logit[:, :], ACT.Exp)
            act.activation(top[:, :], top[:, :], ACT.Exp).then_inc(weights_ready, 1)
            act.wait_ge(to_power, 1)
            act.activation(low[:, :], low[:, :], ACT.Exp).then_inc(powered, 1)

        @block.vector
        def _(dve):
            link = Chain(dve, chain)
            link(dve.tensor_tensor(best[:, :], own_logit[:, :], top[:, :], ALU.max))
            link(dve.tensor_tensor(own_logit[:, :], own_logit[:, :], best[:, :], ALU.subtract))
            link(dve.tensor_tensor(top[:, :], top[:, :], best[:, :], ALU.subtract))
            dve.sem_inc(to_weigh, 1)
            dve.wait_ge(weights_ready, 1)
            link(dve.tensor_tensor(total[:, :], acc[:, :, C], top[:, :], ALU.mult))
            link(dve.tensor_tensor(total[:, :], total[:, :], own_logit[:, :], ALU.add))
            link(dve.reciprocal(total[:, :], total[:, :]))
            link(dve.tensor_tensor(top[:, :], top[:, :], total[:, :], ALU.mult))
            link(dve.tensor_tensor(own_logit[:, :], own_logit[:, :], total[:, :], ALU.mult))
            heads = low[:, :].rearrange("p (n c) -> p n c", c=C)
            link(dve.tensor_tensor(heads, acc[:, :, 0:C], every(top), ALU.mult))
            link(dve.tensor_tensor(v, v, low[:, :], ALU.add))
            dve.wait_ge(xl_loaded, 16)
            link(dve.tensor_tensor(heads, xl[:, :].rearrange("p (n c) -> p n c", c=C), every(own_logit), ALU.mult))
            link(dve.tensor_tensor(v, v, low[:, :], ALU.add))
            link(dve.tensor_scalar(low[:, :], v, 0.0, None, ALU.min))
            dve.sem_inc(to_power, 1)
            link(dve.scalar_tensor_tensor(v, v, 0.0, net.x[:, :], ALU.max, ALU.add))
            dve.wait_ge(powered, 1)
            link(dve.scalar_tensor_tensor(net.x[:, :], low[:, :], -1.0, v, ALU.add, ALU.add))


def gcn_edges(net, name, width, acc):
    nc = net.nc
    with ExitStack() as ctx:
        s = net.scope(name, ctx)
        g = Gather(s, net, net.by_dst, net.table(width), width, net.by_dst.number)
        ps = s.ps("ps", [P, NT * width])
        closed = s.sem("closed")
        block = ctx.enter_context(nc.Block())

        @block.sync
        def _(sp):
            g.load(sp)

        @block.gpsimd
        def _(pool):
            g.gather(pool)

        @block.vector
        def _(dve):
            dve.sem_inc(g.rec_free, RING)
            with dve.Fori(0, NB // RING) as i:
                for b in range(RING):
                    q = i * RING + b
                    g.hot(dve, q, i, b)
                    dve.wait_ge(g.hot_ready, q + 1)
                    dve.sem_inc(g.rec_free, 1)
            dve.wait_ge(closed, 1)
            dve.tensor_tensor(acc[:, 0:NT * width], acc[:, 0:NT * width], ps[:, :], ALU.add)

        @block.tensor
        def _(pe):
            pe.sem_inc(g.rows_free, RING)
            pe.sem_inc(g.hot_free, RING)
            open_sums(net, pe, ps, True)
            with pe.Fori(0, NB // RING) as i:
                for b in range(RING):
                    q = i * RING + b
                    blocks = [block_of(pe, g.placed, q * TWO + k) for k in range(TWO)]
                    pe.wait_ge(g.hot_ready, q + 1)
                    g.wait_rows(pe, i, b)
                    pe.sem_inc(g.pe_tick, 1)
                    for k in range(BATCH):
                        ins = pe.matmul(at(ps, blocks[k // 2], width), at(g.onehot[b], k, P), at(g.rows[b], k, width),
                                        start=False, stop=False)
                    ins.then_inc(g.hot_free, 1)
                    pe.wait_ge(g.hot_free, RING + q + 1)
                    pe.sem_inc(g.rows_free, 1)
            open_sums(net, pe, ps, False).then_inc(closed, 1)


def gcn_nodes(net, name, source, out, w_in=None, weights=None, before=None, after=None, final=False):
    nc, a = net.nc, net.a
    n = a[weights].shape[1] if weights else w_in
    k_in = a[weights].shape[0] if weights else w_in
    chunks = -(-k_in // P)
    kp = min(k_in, P)
    table = None if final else net.table(n)
    with ExitStack() as ctx:
        s = net.scope(name, ctx)
        f = Front(s)
        w = s.sb("w", [kp, chunks * n])
        first = s.sb("first", [P, k_in])
        second = s.sb("second", [P, n])
        held = s.sb("held", [P, UN * n])
        ps = s.ps("ps", [P, 3, 512])
        loaded = s.sem("loaded")
        step = s.sem("step")
        held_step = s.sem("held_step")
        out_done = s.sem("out_done")
        stored = s.sem("stored")
        pe_tick = s.sem("pe_tick")
        act_tick = s.sem("act_tick")
        block = ctx.enter_context(nc.Block())
        loads = sum(v is not None for v in (weights, before, after))

        @block.sync
        def _(sp):
            if weights:
                sp.dma_start(w[:, :].rearrange("p (c n) -> p c n", c=chunks), a[weights].rearrange("(c p) n -> p c n", p=kp))\
                    .then_inc(loaded, 16)
            if before:
                sp.dma_start(first[:, :], spread(a[before])).then_inc(loaded, 16)
            if after:
                sp.dma_start(second[:, :], spread(a[after])).then_inc(loaded, 16)
            if not final:
                for i in range(NI):
                    sp.wait_ge(out_done, (2 + i) * UN)
                    sp.dma_start(node_rows(table, i * UN, UN), tiled(at(out, i, UN * n), n)).then_inc(stored, 16)
                sp.wait_ge(stored, NI * 16)

        @block.vector
        def _(dve):
            dve.sem_inc(out_done, UN)
            dve.sem_inc(held_step, UN)
            if loads:
                dve.wait_ge(loaded, 16 * loads)

            def source_tile(t, xn):
                if before is None:
                    return dve.tensor_scalar(xn, at(source, t, k_in), at(net.dinv, t, 1), None, ALU.mult)
                dve.scalar_tensor_tensor(xn, at(source, t, k_in), at(net.dinv, t, 1), first[:, :], ALU.mult, ALU.add)\
                    .then_inc(step, 1)
                dve.wait_ge(step, 2 * t + 1)
                return dve.tensor_scalar(xn, xn, 0.0, None, ALU.max)

            if source is None:
                f.moments_of(dve, net)

            def start(t, i, k):
                if source is None:
                    f.normalize(dve, net, i, k)
                    return
                if before is None:
                    dve.sem_inc(step, 1)
                f.take(dve, t, k, lambda xn: source_tile(t, xn[:, 0:k_in]))
                dve.sem_inc(step, 1)

            def scale(t, i, k):
                dve.wait_ge(out_done, t + 1)
                dve.scalar_tensor_tensor(at(held, k, n), at(source, t, n), at(net.dinv, t, 1), first[:, :],
                                         ALU.mult, ALU.add).then_inc(step, 1)

            def bend(t, i, k):
                dve.wait_ge(step, t + 1)
                dve.tensor_scalar(at(out, t, n), at(held, k, n), 0.0, at(net.dinv, t, 1), ALU.max, ALU.mult).then_inc(out_done, 1)

            def take_out(t, i, k):
                dve.wait_ge(f.projected, UN + t + 1)
                if after is None:
                    dve.tensor_scalar(at(out, t, n), ps[:, THIRD[k], 0:n], at(net.dinv, t, 1), None, ALU.mult).then_inc(out_done, 1)
                else:
                    dve.wait_ge(out_done, t + 1)
                    dve.tensor_tensor(at(held, k, n), ps[:, THIRD[k], 0:n], second[:, :], ALU.add).then_inc(held_step, 1)

            def finish(t, i, k):
                if after is None:
                    return
                dve.wait_ge(held_step, UN + t + 1)
                if final:
                    dve.tensor_tensor(at(net.x, t, D), at(net.x, t, D), at(held, k, n), ALU.add).then_inc(out_done, 1)
                else:
                    dve.tensor_scalar(at(out, t, n), at(held, k, n), 0.0, at(net.dinv, t, 1), ALU.max, ALU.mult).then_inc(out_done, 1)

            if weights:
                skewed(dve, (4, finish), (0, start), (3, take_out), ring=UN, total=NT)
            else:
                skewed(dve, (0, scale), (1, bend), ring=UN, total=NT)

        if not weights:
            return

        @block.tensor
        def _(pe):
            f.start_tensor(pe)
            pe.wait_ge(loaded, 16 * loads)

            def project(t, i, k):
                pe.wait_ge(f.xT_ready, UN + t + 1)
                if after is None:
                    pe.wait_ge(out_done, third_free(t))
                else:
                    pe.wait_ge(held_step, third_free(t))
                pe.sem_inc(pe_tick, 1)
                for c in range(chunks):
                    ins = pe.matmul(ps[:, THIRD[k], 0:n], f.lhsT(k, c)[0:kp, :], at(w, c, n), start=c == 0, stop=c == chunks - 1)
                ins.then_inc(f.projected, 1)

            skewed(pe, (0, lambda t, i, k: f.turn(pe, net, t, k, k_in, pe_tick)), (1, project), ring=UN, total=NT)

        @block.scalar
        def _(act):
            f.start_scalar(act)
            if source is None:
                f.root(act, net)
            with act.Fori(0, NI) as i:
                for k in range(UN):
                    f.keep(act, i * UN + k, k, kp, chunks)


def l2_gnn(net):
    with ExitStack() as ctx:
        s = net.scope("l2", ctx)
        other = s.sb("other", [P, NT * P])
        gcn_nodes(net, "l2a", None, net.work, weights="L2_gnn_W1")
        gcn_edges(net, "l2ae", 128, net.work)
        gcn_nodes(net, "l2b", net.work, other, weights="L2_gnn_W2", before="L2_gnn_b1")
        gcn_edges(net, "l2be", 64, other)
        gcn_nodes(net, "l2c", other, net.work, w_in=64, before="L2_gnn_b2")
        gcn_edges(net, "l2ce", 64, net.work)
        gcn_nodes(net, "l2d", net.work, other, weights="L2_gnn_W3", after="L2_gnn_b3")
        gcn_edges(net, "l2de", 128, other)
        gcn_nodes(net, "l2e", other, None, weights="L2_gnn_W4", after="L2_gnn_b4", final=True)


class L3Logits:

    SLOPE = 0.01

    def __init__(self, net, wide, s, g, ps_x, nodehot, logit, logit_ready, nodehot_ready):
        self.net, self.wide, self.g, self.logit, self.logit_ready = net, wide, g, logit, logit_ready
        self.prod = s.sb("prod", [P, BATCH * P])
        self.edge = s.sb("edge", [P, BATCH])
        self.step = s.sem("e_step")
        self.tick = s.sem("e_tick")

    def load(self, sp):
        pass

    def load_batch(self, sp, q, b):
        pass

    def gather(self, pool):
        self.g.gather(pool)

    def hot(self, dve, q, i, b):
        self.g.hot(dve, q, i, b)

    def start_vector(self, dve):
        dve.sem_inc(self.g.rec_free, RING)

    def start_tensor(self, pe):
        pass

    def start_scalar(self, act):
        pass

    def blocks(self, pe, q):
        pass

    def tensor(self, pe, q, i, b):
        pass

    def vector_steps(self):
        return self.vector_early, self.vector_middle, self.vector_late, self.hot

    def vector_middle(self, dve, q, i, b):
        self.g.wait_rows(dve, i, b)
        dve.wait_ge(self.step, 2 * q + 1)
        dve.tensor_tensor(self.edge[:, :], self.edge[:, :], tiled(self.g.rows[b][:, :], D + 1)[:, :, D], ALU.add)\
            .then_inc(self.step, 1)
        dve.sem_inc(self.g.rec_free, 1)

    def vector_late(self, dve, q, i, b):
        dve.wait_ge(self.step, 2 * q + 2)
        dve.scalar_tensor_tensor(self.logit[b][:, :], self.edge[:, :], self.SLOPE, self.edge[:, :], ALU.mult, ALU.max)\
            .then_inc(self.logit_ready, 1)

    def vector_early(self, dve, q, i, b):
        if not isinstance(q, int) or q:
            dve.wait_ge(self.logit_ready, q)
        dve.sem_inc(self.tick, 1)
        for k in range(BATCH):
            ins = dve.tensor_tensor_reduce(at(self.prod, k, P), self.g.columns(b, k, 0, P), self.wide[:, :], 1.0, 0.0,
                                           ALU.mult, ALU.add, self.edge[:, k:k + 1])
        ins.then_inc(self.step, 1)


def l3_gnn(net):
    with ExitStack() as ctx:
        s = net.scope("l3", ctx)
        wide = s.sb("wide", [P, P])
        l3_nodes(net, wide)
        gat_edges(net, "l3e", 1, D, net.table(D + 1), 0, lambda *args: L3Logits(net, wide, *args))
        l3_finish(net)


def l3_nodes(net, wide):
    nc, a = net.nc, net.a
    W = D + 1
    table = net.table(W)
    with ExitStack() as ctx:
        s = net.scope("l3n", ctx)
        f = Front(s)
        wn = s.sb("wn", [P, DC * D])
        wnT = s.sb("wnT", [P, DC * D])
        we = s.sb("we", [P, DC * P])
        be = s.sb("be", [P, DC])
        attn_col = s.sb("attn_col", [P, DC])
        attn_cols = s.sb("attn_cols", [P, DC * P])
        attn = s.sb("attn", [P, D])
        bn = s.sb("bn", [P, D])
        const = s.sb("const", [P, 1])
        h = s.sb("h", [P, NT * W])
        prod = s.sb("prod", [P, UN * D])
        dot = s.sb("dot", [P, UN])
        held = s.sb("held", [P, UN * D])
        ps_w = s.ps("ps_w", [P, 2, 512])
        ps = s.ps("ps", [P, 3, 512])
        loaded = s.sem("loaded")
        chain = s.sem("chain")
        cols_ready = s.sem("cols_ready")
        w_turned = s.sem("w_turned")
        w_ready = s.sem("w_ready")
        biased = s.sem("biased")
        dotted = s.sem("dotted")
        h_ready = s.sem("h_ready")
        dve_tick = s.sem("dve_tick")
        stored = s.sem("stored")
        block = ctx.enter_context(nc.Block())
        vector = a["L3_gnn_attn"].rearrange("a b c -> (a b c)")

        @block.sync
        def _(sp):
            sp.dma_start(wn[:, :].rearrange("p (c n) -> p c n", c=DC), chunked(a["L3_gnn_Wn"])).then_inc(loaded, 16)
            sp.dma_start(we[:, :].rearrange("p (c n) -> p c n", c=DC), chunked(a["L3_gnn_We"])).then_inc(loaded, 16)
            for c in range(DC):
                sp.dma_start(be[:, c:c + 1], column(a["L3_gnn_be"][c * P:(c + 1) * P])).then_inc(loaded, 16)
                sp.dma_start(attn_col[:, c:c + 1], column(vector[c * P:(c + 1) * P])).then_inc(loaded, 16)
            sp.dma_start(attn[:, :], spread(vector)).then_inc(loaded, 16)
            sp.dma_start(bn[:, :], spread(a["L3_gnn_bn"])).then_inc(loaded, 16)
            for i in range(NI):
                sp.wait_ge(h_ready, (2 + i) * UN)
                sp.dma_start(node_rows(table, i * UN, UN), tiled(at(h, i, UN * W), W)).then_inc(stored, 16)
            sp.wait_ge(stored, NI * 16)

        @block.vector
        def _(dve):
            link = Chain(dve, chain)
            dve.wait_ge(loaded, 128)
            for c in range(DC):
                link(dve.tensor_scalar(at(attn_cols, c, P), net.ones[:, :], attn_col[:, c:c + 1], None, ALU.mult))
            dve.sem_inc(cols_ready, 1)
            dve.wait_ge(w_turned, 1)
            for c in range(DC):
                link(dve.tensor_copy(at(wnT, c, D), ps_w[:, 0, c * D:(c + 1) * D]))
            link(dve.tensor_copy(wide[:, :], ps_w[:, 1, 0:P]))
            link(dve.tensor_copy(const[:, :], ps_w[:, 1, P:P + 1]))
            dve.sem_inc(w_ready, 1)
            dve.sem_inc(h_ready, UN)
            dve.sem_inc(biased, UN)
            f.moments_of(dve, net)

            def bias(t, i, k):
                dve.wait_ge(f.projected, UN + t + 1)
                dve.wait_ge(h_ready, t + 1)
                dve.tensor_tensor(at(held, k, D), ps[:, THIRD[k], 0:D], bn[:, :], ALU.add).then_inc(biased, 1)

            def attend(t, i, k):
                dve.wait_ge(biased, UN + t + 1)
                dve.sem_inc(dve_tick, 1)
                dve.tensor_copy(h[:, bass.ds(t * W, D)], at(held, k, D))
                dve.tensor_tensor_reduce(at(prod, k, D), at(held, k, D), attn[:, :], 1.0, 0.0,
                                         ALU.mult, ALU.add, dot[:, k:k + 1]).then_inc(dotted, 1)

            def finish(t, i, k):
                dve.wait_ge(dotted, t + 1)
                dve.tensor_scalar(h[:, bass.ds(t * W + D, 1)], dot[:, k:k + 1], const[:, :], None, ALU.add).then_inc(h_ready, 1)

            skewed(dve, (0, lambda t, i, k: f.normalize(dve, net, i, k)), (4, finish), (3, attend), (2, bias), ring=UN, total=NT)

        @block.tensor
        def _(pe):
            f.start_tensor(pe)
            pe.wait_ge(loaded, 128)
            for c in range(DC):
                for m in range(DC):
                    pe.transpose(ps_w[:, 0, c * D + m * P:c * D + (m + 1) * P],
                                 wn[:, m * D + c * P:m * D + (c + 1) * P], net.ident[:, :])
            pe.wait_ge(cols_ready, 1)
            for c in range(DC):
                pe.matmul(ps_w[:, 1, 0:P], at(attn_cols, c, P), at(we, c, P), start=c == 0, stop=c == DC - 1)
            for c in range(DC):
                ins = pe.matmul(ps_w[:, 1, P:P + 1], at(attn_cols, c, P), be[:, c:c + 1], start=c == 0, stop=c == DC - 1)
            ins.then_inc(w_turned, 1)
            pe.wait_ge(w_ready, 1)

            def project(t, i, k):
                pe.wait_ge(f.xT_ready, UN + t + 1)
                pe.wait_ge(biased, third_free(t))
                f.project(pe, t, k, ps[:, THIRD[k], 0:D], wnT[:, :].rearrange("p (c n) -> p c n", c=DC))

            skewed(pe, (0, lambda t, i, k: f.turn(pe, net, t, k)), (1, project), ring=UN, total=NT)

        @block.scalar
        def _(act):
            f.start_scalar(act)
            f.root(act, net)
            with act.Fori(0, NI) as i:
                for k in range(UN):
                    f.keep(act, i * UN + k, k)


def l3_finish(net):
    nc = net.nc
    W = D + 1
    with ExitStack() as ctx:
        s = net.scope("l3f", ctx)
        share = s.sb("share", [P, NT])
        out = s.sb("out", [P, NT * D])
        chain = s.sem("chain")
        block = ctx.enter_context(nc.Block())
        acc = tiled(net.work[:, 0:NT * W], W)

        @block.vector
        def _(dve):
            link = Chain(dve, chain)
            link(dve.tensor_scalar(share[:, :], acc[:, :, D], 1e-16, None, ALU.add))
            link(dve.reciprocal(share[:, :], share[:, :]))
            link(dve.tensor_tensor(tiled(out[:, :], D), acc[:, :, 0:D], share[:, :].unsqueeze(2).to_broadcast([P, NT, D]), ALU.mult))
            link(dve.scalar_tensor_tensor(net.x[:, :], out[:, :], 0.0, net.x[:, :], ALU.max, ALU.add))


STAGES = (setup, l0_gnn, l0_ffn, edge_means, l1_gnn, l1_ffn, l2_gnn, l2_ffn, l3_gnn, l3_ffn)


def build(nc, arrays, out):
    with ExitStack() as ctx:
        net = Net(nc, arrays, ctx)
        for stage in STAGES:
            stage(net)
        store(net, out)


def store(net, out):
    nc = net.nc
    with ExitStack() as ctx:
        s = net.scope("store", ctx)
        stored = s.sem("stored")
        block = ctx.enter_context(nc.Block())

        @block.sync
        def _(sp):
            full = (NT - 1) * P
            sp.dma_start(out[0:full, :].rearrange("(t p) d -> p t d", p=P),
                         net.x[:, 0:(NT - 1) * D].rearrange("p (t d) -> p t d", d=D)).then_inc(stored, 16)
            sp.dma_start(out[full:N, :], net.x[0:TAIL, (NT - 1) * D:NT * D]).then_inc(stored, 16)
            sp.wait_ge(stored, 32)


def kernel(**inputs):
    from concourse import bacc
    from concourse.bass_utils import run_bass_kernel_spmd

    nc = bacc.Bacc("TRN2", target_bir_lowering=False, num_devices=1)
    arrays, aps = {}, {}
    for name, value in inputs.items():
        arrays[f"in_{name}"] = np.ascontiguousarray(value)
        aps[name] = nc.dram_tensor(f"in_{name}", value.shape, mybir.dt.from_np(arrays[f"in_{name}"].dtype),
                                   kind="ExternalInput").ap()
    out = nc.dram_tensor("out", [N, D], F32, kind="ExternalOutput").ap()
    build(nc, aps, out)
    result = run_bass_kernel_spmd(nc, [arrays], core_ids=[0])
    return result.results[0]["out"]
```
